# Optimizing a Trainium2 kernel written in Bass

```python
import numpy as np
import jax
import jax.numpy as jnp

def _softmax(x, axis=-1):
    return jax.nn.softmax(x, axis=axis)

def _gelu(x):
    return jax.nn.gelu(x, approximate=True)

def _silu(x):
    return jax.nn.silu(x)

def _sigmoid(x):
    return jax.nn.sigmoid(x)

def _layernorm(x, axis=-1, eps=1e-05):
    m = jnp.mean(x, axis=axis, keepdims=True)
    v = jnp.var(x, axis=axis, keepdims=True)
    return (x - m) / jnp.sqrt(v + eps)

def _scatter_add(tgt, idx, src, axis=0):
    return tgt.at[idx].add(src)

def _segment_sum(src, seg, n):
    return jax.ops.segment_sum(src, seg, n)
kernel_name = 'mk_gps_d2_gnn_r8_0b2cc1'

def setup_inputs(seed: int=0):
    np.random.seed(seed)
    _w = jnp.asarray

    def _rec_inputs():
        import jax
        import jax.numpy as jnp
        _gk = jax.random.key(seed)
        x = -0.0003713 + 1 * jax.random.normal(jax.random.fold_in(_gk, 1), (6250, 256), jnp.float32)
        src = jax.random.randint(jax.random.fold_in(_gk, 2), (100000,), 0, 6250, jnp.int32)
        dst = jax.random.randint(jax.random.fold_in(_gk, 3), (100000,), 0, 6250, jnp.int32)
        _o = jnp.argsort(dst, stable=True)
        src = src[_o]
        dst = dst[_o]
        edge_type_8 = jax.random.randint(jax.random.fold_in(_gk, 13), (100000,), 0, 8, jnp.int32)
        edge_weight = jax.random.uniform(jax.random.fold_in(_gk, 14), (100000,), jnp.float32, 0.0, 1)
        return (x, src, dst, edge_type_8, edge_weight)
    x, src, dst, edge_type_8, edge_weight = _rec_inputs()

    def _L0_gnn_setup():
        import jax, jax.numpy as jnp
        import numpy as np
        N, E, DIN, DH, H, HD, L = (6250, 125000, 256, 256, 4, 64, 3)
        EPS = 1e-05

        def layer_norm(x, g, b):
            mu = jnp.mean(x, axis=-1, keepdims=True)
            var = jnp.var(x, axis=-1, keepdims=True)
            return (x - mu) * jax.lax.rsqrt(var + EPS) * g + b

        def gat_conv(x, src, dst, w, a_src, a_dst, bias):
            h = (x @ w).reshape(N, H, HD)
            s = jnp.sum(h * a_src, axis=-1)
            d = jnp.sum(h * a_dst, axis=-1)
            e = jax.nn.leaky_relu(s[src] + d[dst], negative_slope=0.2)
            m = jax.ops.segment_max(e, dst, num_segments=N)
            ex = jnp.exp(e - m[dst])
            denom = jax.ops.segment_sum(ex, dst, num_segments=N)
            alpha = ex / (denom[dst] + 1e-16)
            msg = h[src] * alpha[:, :, None]
            out = jax.ops.segment_sum(msg, dst, num_segments=N)
            return out.reshape(N, H * HD) + bias
        key = jax.random.key(seed)
        ks = jax.random.split(key, 12)
        sc = 1.0 / np.sqrt(DH)
        return {'x': jax.random.normal(ks[0], (N, DIN), dtype=jnp.float32), 'edge_index': jax.random.randint(ks[1], (2, E), 0, N, dtype=jnp.int64), 'w_in': jax.random.normal(ks[2], (DIN, DH), dtype=jnp.float32) * sc, 'b_in': jnp.zeros((DH,), jnp.float32), 'g_in': jnp.ones((DH,), jnp.float32), 'bt_in': jnp.zeros((DH,), jnp.float32), 'w_l': jax.random.normal(ks[3], (L, DH, H * HD), dtype=jnp.float32) * sc, 'a_s': jax.random.normal(ks[4], (L, H, HD), dtype=jnp.float32) * sc, 'a_d': jax.random.normal(ks[5], (L, H, HD), dtype=jnp.float32) * sc, 'b_l': jnp.zeros((L, H * HD), jnp.float32), 'g_l': jnp.ones((L, H * HD), jnp.float32), 'bt_l': jnp.zeros((L, H * HD), jnp.float32)}
    _L0_gnn_all = _L0_gnn_setup()
    _L0_gnn_in = {k: v for k, v in _L0_gnn_all.items() if k in ('w_in', 'b_in', 'g_in', 'bt_in', 'w_l', 'a_s', 'a_d', 'b_l', 'g_l', 'bt_l')}
    del _L0_gnn_all

    def _L0_mix_setup():
        import jax, jax.numpy as jnp
        import numpy as np
        D_MODEL = 256
        NHEAD = 8
        D_HEAD = D_MODEL // NHEAD
        DIM_FF = 1024
        B, L = (4, 2048)
        LN_EPS = 1e-05

        def _layernorm(x, g, b):
            mu = jnp.mean(x, axis=-1, keepdims=True)
            var = jnp.mean((x - mu) ** 2, axis=-1, keepdims=True)
            return (x - mu) * jax.lax.rsqrt(var + LN_EPS) * g + b

        def _phi(x):
            return jnp.where(x > 0, x + 1.0, jnp.exp(x))
        key = jax.random.key(seed)
        ks = jax.random.split(key, 16)
        s_in = 1.0 / np.sqrt(D_MODEL)
        s_ff = 1.0 / np.sqrt(DIM_FF)
        inp = {'x': jax.random.normal(ks[0], (B, L, D_MODEL), dtype=jnp.float32), 'Wq': jax.random.normal(ks[1], (D_MODEL, D_MODEL), dtype=jnp.float32) * s_in, 'bq': jnp.zeros((D_MODEL,), jnp.float32), 'Wk': jax.random.normal(ks[2], (D_MODEL, D_MODEL), dtype=jnp.float32) * s_in, 'bk': jnp.zeros((D_MODEL,), jnp.float32), 'Wv': jax.random.normal(ks[3], (D_MODEL, D_MODEL), dtype=jnp.float32) * s_in, 'bv': jnp.zeros((D_MODEL,), jnp.float32), 'Wo': jax.random.normal(ks[4], (D_MODEL, D_MODEL), dtype=jnp.float32) * s_in, 'bo': jnp.zeros((D_MODEL,), jnp.float32), 'W1': jax.random.normal(ks[5], (D_MODEL, DIM_FF), dtype=jnp.float32) * s_in, 'b1': jnp.zeros((DIM_FF,), jnp.float32), 'W2': jax.random.normal(ks[6], (DIM_FF, D_MODEL), dtype=jnp.float32) * s_ff, 'b2': jnp.zeros((D_MODEL,), jnp.float32), 'ln1_g': jnp.ones((D_MODEL,), jnp.float32), 'ln1_b': jnp.zeros((D_MODEL,), jnp.float32), 'ln2_g': jnp.ones((D_MODEL,), jnp.float32), 'ln2_b': jnp.zeros((D_MODEL,), jnp.float32)}
        return inp
    _L0_mix_all = _L0_mix_setup()
    _L0_mix_in = {k: v for k, v in _L0_mix_all.items() if k in ('Wq', 'bq', 'Wk', 'bk', 'Wv', 'bv', 'Wo', 'bo', 'W1', 'b1', 'W2', 'b2', 'ln1_g', 'ln1_b', 'ln2_g', 'ln2_b')}
    del _L0_mix_all

    def _L0_ffn_setup():
        import jax, jax.numpy as jnp
        import numpy as np
        BN_EPS = 0.001

        def _bn(h, g, b, m, v):
            return g * (h - m) * jax.lax.rsqrt(v + BN_EPS) + b
        key = jax.random.key(seed)
        ks = jax.random.split(key, 8)
        B, F, Df = (256, 64, 256)
        E, H, D = (8, 256, 256)
        s1 = 1.0 / np.sqrt(Df)
        s2 = 1.0 / np.sqrt(H)
        return {'x': jax.random.normal(ks[0], (B, F, Df), jnp.float32), 'Wr': jax.random.normal(ks[1], (Df, E), jnp.float32) * s1, 'br': jnp.zeros((E,), jnp.float32), 'W1': jax.random.normal(ks[2], (E, Df, H), jnp.float32) * s1, 'b1': jnp.zeros((E, H), jnp.float32), 'g1': jnp.ones((E, H), jnp.float32), 'be1': jnp.zeros((E, H), jnp.float32), 'm1': jnp.zeros((E, H), jnp.float32), 'v1': jnp.ones((E, H), jnp.float32), 'W2': jax.random.normal(ks[3], (E, H, H), jnp.float32) * s2, 'b2': jnp.zeros((E, H), jnp.float32), 'g2': jnp.ones((E, H), jnp.float32), 'be2': jnp.zeros((E, H), jnp.float32), 'm2': jnp.zeros((E, H), jnp.float32), 'v2': jnp.ones((E, H), jnp.float32), 'Wo': jax.random.normal(ks[4], (E, H, D), jnp.float32) * s2, 'bo': jnp.zeros((E, D), jnp.float32)}
    _L0_ffn_all = _L0_ffn_setup()
    _L0_ffn_in = {k: v for k, v in _L0_ffn_all.items() if k in ('Wr', 'br', 'W1', 'b1', 'g1', 'be1', 'm1', 'v1', 'W2', 'b2', 'g2', 'be2', 'm2', 'v2', 'Wo', 'bo')}
    del _L0_ffn_all

    def _L1_gnn_setup():
        import jax, jax.numpy as jnp
        import numpy as np
        N_NODES = 6250
        N_EDGES = 100000
        IN_FEAT = 256
        OUT_FEAT = 256
        NUM_RELS = 8
        NUM_BASES = 8
        SUBMAT_IN = IN_FEAT // NUM_BASES
        SUBMAT_OUT = OUT_FEAT // NUM_BASES
        key = jax.random.key(seed)
        k_h, k_w, k_src, k_dst, k_rel, k_norm = jax.random.split(key, 6)
        h = jax.random.normal(k_h, (N_NODES, IN_FEAT), dtype=jnp.float32)
        weight = jax.random.normal(k_w, (NUM_RELS, NUM_BASES * SUBMAT_IN * SUBMAT_OUT), dtype=jnp.float32) * 0.05
        edge_src = jax.random.randint(k_src, (N_EDGES,), 0, N_NODES, dtype=jnp.int32)
        edge_dst = jax.random.randint(k_dst, (N_EDGES,), 0, N_NODES, dtype=jnp.int32)
        edge_rel = jax.random.randint(k_rel, (N_EDGES,), 0, NUM_RELS, dtype=jnp.int32)
        edge_norm = jax.random.uniform(k_norm, (N_EDGES,), dtype=jnp.float32)
        return {'h': h, 'weight': weight, 'edge_src': edge_src, 'edge_dst': edge_dst, 'edge_rel': edge_rel, 'edge_norm': edge_norm}
    _L1_gnn_all = _L1_gnn_setup()
    _L1_gnn_in = {k: v for k, v in _L1_gnn_all.items() if k in ('weight',)}
    del _L1_gnn_all

    def _L1_mix_setup():
        import jax, jax.numpy as jnp
        import numpy as np
        N, F, C, H = (32, 512, 256, 8)
        D = C // H
        EPS_ATTN = 1e-06
        EPS_LN = 1e-05

        def layer_norm(x, g, b):
            mu = jnp.mean(x, axis=-1, keepdims=True)
            var = jnp.var(x, axis=-1, keepdims=True)
            return (x - mu) * jax.lax.rsqrt(var + EPS_LN) * g + b
        key = jax.random.key(seed)
        ks = jax.random.split(key, 8)
        s = 1.0 / np.sqrt(C)
        return {'x': jax.random.normal(ks[0], (N, F, C), jnp.float32), 'Wqkv': jax.random.uniform(ks[1], (3 * C, C), jnp.float32, -s, s), 'ln1_g': jnp.ones((C,), jnp.float32), 'ln1_b': jnp.zeros((C,), jnp.float32), 'W1': jax.random.uniform(ks[2], (C, C), jnp.float32, -s, s), 'b1': jax.random.uniform(ks[3], (C,), jnp.float32, -s, s), 'W2': jax.random.uniform(ks[4], (C, C), jnp.float32, -s, s), 'b2': jax.random.uniform(ks[5], (C,), jnp.float32, -s, s), 'ln2_g': jnp.ones((C,), jnp.float32), 'ln2_b': jnp.zeros((C,), jnp.float32)}
    _L1_mix_all = _L1_mix_setup()
    _L1_mix_in = {k: v for k, v in _L1_mix_all.items() if k in ('Wqkv', 'ln1_g', 'ln1_b', 'W1', 'b1', 'W2', 'b2', 'ln2_g', 'ln2_b')}
    del _L1_mix_all

    def _L1_ffn_setup():
        import jax, jax.numpy as jnp
        import numpy as np
        DIM = 256
        H = 8
        D = 64
        G = 64
        INNER = H * D
        SCALE = D ** (-0.5)
        key = jax.random.key(seed)
        ks = jax.random.split(key, 12)
        B, N = (4, 2048)
        x = jax.random.normal(ks[0], (B, N, DIM), dtype=jnp.float32)
        s = lambda fan_in: 1.0 / np.sqrt(fan_in)
        W_fx = jax.random.normal(ks[1], (DIM, INNER), dtype=jnp.float32) * s(DIM)
        b_fx = jnp.zeros((INNER,), dtype=jnp.float32)
        W_x = jax.random.normal(ks[2], (DIM, INNER), dtype=jnp.float32) * s(DIM)
        b_x = jnp.zeros((INNER,), dtype=jnp.float32)
        A = jax.random.normal(ks[3], (G, D), dtype=jnp.float32)
        Q, _ = jnp.linalg.qr(A.T)
        W_slice = Q[:, :G].astype(jnp.float32)
        b_slice = jnp.zeros((G,), dtype=jnp.float32)
        W_q = jax.random.normal(ks[4], (D, D), dtype=jnp.float32) * s(D)
        W_k = jax.random.normal(ks[5], (D, D), dtype=jnp.float32) * s(D)
        W_v = jax.random.normal(ks[6], (D, D), dtype=jnp.float32) * s(D)
        W_out = jax.random.normal(ks[7], (INNER, DIM), dtype=jnp.float32) * s(INNER)
        b_out = jnp.zeros((DIM,), dtype=jnp.float32)
        temperature = jnp.ones((1, H, 1, 1), dtype=jnp.float32) * 0.5
        return {'x': x, 'W_fx': W_fx, 'b_fx': b_fx, 'W_x': W_x, 'b_x': b_x, 'W_slice': W_slice, 'b_slice': b_slice, 'W_q': W_q, 'W_k': W_k, 'W_v': W_v, 'W_out': W_out, 'b_out': b_out, 'temperature': temperature}
    _L1_ffn_all = _L1_ffn_setup()
    _L1_ffn_in = {k: v for k, v in _L1_ffn_all.items() if k in ('W_fx', 'b_fx', 'W_x', 'b_x', 'W_slice', 'b_slice', 'W_q', 'W_k', 'W_v', 'W_out', 'b_out', 'temperature')}
    del _L1_ffn_all
    return {'x': x, 'src': src, 'dst': dst, 'edge_type_8': edge_type_8, 'edge_weight': edge_weight, 'L0_gnn_w_in': _L0_gnn_in['w_in'], 'L0_gnn_b_in': _L0_gnn_in['b_in'], 'L0_gnn_g_in': _L0_gnn_in['g_in'], 'L0_gnn_bt_in': _L0_gnn_in['bt_in'], 'L0_gnn_w_l': _L0_gnn_in['w_l'], 'L0_gnn_a_s': _L0_gnn_in['a_s'], 'L0_gnn_a_d': _L0_gnn_in['a_d'], 'L0_gnn_b_l': _L0_gnn_in['b_l'], 'L0_gnn_g_l': _L0_gnn_in['g_l'], 'L0_gnn_bt_l': _L0_gnn_in['bt_l'], 'L0_mix_Wq': _L0_mix_in['Wq'], 'L0_mix_bq': _L0_mix_in['bq'], 'L0_mix_Wk': _L0_mix_in['Wk'], 'L0_mix_bk': _L0_mix_in['bk'], 'L0_mix_Wv': _L0_mix_in['Wv'], 'L0_mix_bv': _L0_mix_in['bv'], 'L0_mix_Wo': _L0_mix_in['Wo'], 'L0_mix_bo': _L0_mix_in['bo'], 'L0_mix_W1': _L0_mix_in['W1'], 'L0_mix_b1': _L0_mix_in['b1'], 'L0_mix_W2': _L0_mix_in['W2'], 'L0_mix_b2': _L0_mix_in['b2'], 'L0_mix_ln1_g': _L0_mix_in['ln1_g'], 'L0_mix_ln1_b': _L0_mix_in['ln1_b'], 'L0_mix_ln2_g': _L0_mix_in['ln2_g'], 'L0_mix_ln2_b': _L0_mix_in['ln2_b'], 'L0_ffn_Wr': _L0_ffn_in['Wr'], 'L0_ffn_br': _L0_ffn_in['br'], 'L0_ffn_W1': _L0_ffn_in['W1'], 'L0_ffn_b1': _L0_ffn_in['b1'], 'L0_ffn_g1': _L0_ffn_in['g1'], 'L0_ffn_be1': _L0_ffn_in['be1'], 'L0_ffn_m1': _L0_ffn_in['m1'], 'L0_ffn_v1': _L0_ffn_in['v1'], 'L0_ffn_W2': _L0_ffn_in['W2'], 'L0_ffn_b2': _L0_ffn_in['b2'], 'L0_ffn_g2': _L0_ffn_in['g2'], 'L0_ffn_be2': _L0_ffn_in['be2'], 'L0_ffn_m2': _L0_ffn_in['m2'], 'L0_ffn_v2': _L0_ffn_in['v2'], 'L0_ffn_Wo': _L0_ffn_in['Wo'], 'L0_ffn_bo': _L0_ffn_in['bo'], 'L1_gnn_weight': _L1_gnn_in['weight'], 'L1_mix_Wqkv': _L1_mix_in['Wqkv'], 'L1_mix_ln1_g': _L1_mix_in['ln1_g'], 'L1_mix_ln1_b': _L1_mix_in['ln1_b'], 'L1_mix_W1': _L1_mix_in['W1'], 'L1_mix_b1': _L1_mix_in['b1'], 'L1_mix_W2': _L1_mix_in['W2'], 'L1_mix_b2': _L1_mix_in['b2'], 'L1_mix_ln2_g': _L1_mix_in['ln2_g'], 'L1_mix_ln2_b': _L1_mix_in['ln2_b'], 'L1_ffn_W_fx': _L1_ffn_in['W_fx'], 'L1_ffn_b_fx': _L1_ffn_in['b_fx'], 'L1_ffn_W_x': _L1_ffn_in['W_x'], 'L1_ffn_b_x': _L1_ffn_in['b_x'], 'L1_ffn_W_slice': _L1_ffn_in['W_slice'], 'L1_ffn_b_slice': _L1_ffn_in['b_slice'], 'L1_ffn_W_q': _L1_ffn_in['W_q'], 'L1_ffn_W_k': _L1_ffn_in['W_k'], 'L1_ffn_W_v': _L1_ffn_in['W_v'], 'L1_ffn_W_out': _L1_ffn_in['W_out'], 'L1_ffn_b_out': _L1_ffn_in['b_out'], 'L1_ffn_temperature': _L1_ffn_in['temperature']}

def reference(x, src, dst, edge_type_8, edge_weight, L0_gnn_w_in, L0_gnn_b_in, L0_gnn_g_in, L0_gnn_bt_in, L0_gnn_w_l, L0_gnn_a_s, L0_gnn_a_d, L0_gnn_b_l, L0_gnn_g_l, L0_gnn_bt_l, L0_mix_Wq, L0_mix_bq, L0_mix_Wk, L0_mix_bk, L0_mix_Wv, L0_mix_bv, L0_mix_Wo, L0_mix_bo, L0_mix_W1, L0_mix_b1, L0_mix_W2, L0_mix_b2, L0_mix_ln1_g, L0_mix_ln1_b, L0_mix_ln2_g, L0_mix_ln2_b, L0_ffn_Wr, L0_ffn_br, L0_ffn_W1, L0_ffn_b1, L0_ffn_g1, L0_ffn_be1, L0_ffn_m1, L0_ffn_v1, L0_ffn_W2, L0_ffn_b2, L0_ffn_g2, L0_ffn_be2, L0_ffn_m2, L0_ffn_v2, L0_ffn_Wo, L0_ffn_bo, L1_gnn_weight, L1_mix_Wqkv, L1_mix_ln1_g, L1_mix_ln1_b, L1_mix_W1, L1_mix_b1, L1_mix_W2, L1_mix_b2, L1_mix_ln2_g, L1_mix_ln2_b, L1_ffn_W_fx, L1_ffn_b_fx, L1_ffn_W_x, L1_ffn_b_x, L1_ffn_W_slice, L1_ffn_b_slice, L1_ffn_W_q, L1_ffn_W_k, L1_ffn_W_v, L1_ffn_W_out, L1_ffn_b_out, L1_ffn_temperature):
    import jax
    import jax.numpy as jnp

    def _L0_gnn_ref(x, edge_index, w_in, b_in, g_in, bt_in, w_l, a_s, a_d, b_l, g_l, bt_l):
        import jax, jax.numpy as jnp
        import numpy as np
        N, E, DIN, DH, H, HD, L = (6250, 125000, 256, 256, 4, 64, 3)
        EPS = 1e-05

        def layer_norm(x, g, b):
            mu = jnp.mean(x, axis=-1, keepdims=True)
            var = jnp.var(x, axis=-1, keepdims=True)
            return (x - mu) * jax.lax.rsqrt(var + EPS) * g + b

        def gat_conv(x, src, dst, w, a_src, a_dst, bias):
            h = (x @ w).reshape(N, H, HD)
            s = jnp.sum(h * a_src, axis=-1)
            d = jnp.sum(h * a_dst, axis=-1)
            e = jax.nn.leaky_relu(s[src] + d[dst], negative_slope=0.2)
            m = jax.ops.segment_max(e, dst, num_segments=N)
            ex = jnp.exp(e - m[dst])
            denom = jax.ops.segment_sum(ex, dst, num_segments=N)
            alpha = ex / (denom[dst] + 1e-16)
            msg = h[src] * alpha[:, :, None]
            out = jax.ops.segment_sum(msg, dst, num_segments=N)
            return out.reshape(N, H * HD) + bias
        loops = jnp.arange(N, dtype=edge_index.dtype)
        src = jnp.concatenate([edge_index[0], loops])
        dst = jnp.concatenate([edge_index[1], loops])
        h = jax.nn.elu(layer_norm(x @ w_in + b_in, g_in, bt_in))
        for i in range(L):
            identity = h
            y = gat_conv(h, src, dst, w_l[i], a_s[i], a_d[i], b_l[i])
            y = jax.nn.elu(y)
            y = layer_norm(y, g_l[i], bt_l[i])
            h = y + identity
        return h

    def _L0_mix_ref(x, Wq, bq, Wk, bk, Wv, bv, Wo, bo, W1, b1, W2, b2, ln1_g, ln1_b, ln2_g, ln2_b):
        import jax, jax.numpy as jnp
        import numpy as np
        D_MODEL = 256
        NHEAD = 8
        D_HEAD = D_MODEL // NHEAD
        DIM_FF = 1024
        B, L = (4, 2048)
        LN_EPS = 1e-05

        def _layernorm(x, g, b):
            mu = jnp.mean(x, axis=-1, keepdims=True)
            var = jnp.mean((x - mu) ** 2, axis=-1, keepdims=True)
            return (x - mu) * jax.lax.rsqrt(var + LN_EPS) * g + b

        def _phi(x):
            return jnp.where(x > 0, x + 1.0, jnp.exp(x))
        Bq, Lq, _ = x.shape
        q = (x @ Wq + bq).reshape(Bq, Lq, NHEAD, D_HEAD)
        k = (x @ Wk + bk).reshape(Bq, Lq, NHEAD, D_HEAD)
        v = (x @ Wv + bv).reshape(Bq, Lq, NHEAD, D_HEAD)
        q_phi = _phi(q)
        k_phi = _phi(k)
        kv = jnp.einsum('blhd,blhe->bhde', k_phi, v)
        k_sum = k_phi.sum(axis=1)
        z = 1.0 / (jnp.einsum('blhd,bhd->blh', q_phi, k_sum) + 1e-06)
        out = jnp.einsum('blhd,bhde,blh->blhe', q_phi, kv, z)
        out = out.reshape(Bq, Lq, D_MODEL) @ Wo + bo
        x = _layernorm(x + out, ln1_g, ln1_b)
        ff = jax.nn.relu(x @ W1 + b1) @ W2 + b2
        x = _layernorm(x + ff, ln2_g, ln2_b)
        return x

    def _L0_ffn_ref(x, Wr, br, W1, b1, g1, be1, m1, v1, W2, b2, g2, be2, m2, v2, Wo, bo):
        import jax, jax.numpy as jnp
        import numpy as np
        BN_EPS = 0.001

        def _bn(h, g, b, m, v):
            return g * (h - m) * jax.lax.rsqrt(v + BN_EPS) + b
        feat = jnp.mean(x, axis=0)
        w = jax.nn.softmax(feat @ Wr + br, axis=-1)
        h = jnp.einsum('bfd,edh->bfeh', x, W1) + b1
        h = jax.nn.relu(_bn(h, g1, be1, m1, v1))
        h = jnp.einsum('bfeh,ehk->bfek', h, W2) + b2
        h = jax.nn.relu(_bn(h, g2, be2, m2, v2))
        y = jnp.einsum('bfeh,ehd->bfed', h, Wo) + bo
        return jnp.einsum('bfed,fe->bfd', y, w)

    def _L1_gnn_ref(h, weight, edge_src, edge_dst, edge_rel, edge_norm):
        import jax, jax.numpy as jnp
        import numpy as np
        N_NODES = 6250
        N_EDGES = 100000
        IN_FEAT = 256
        OUT_FEAT = 256
        NUM_RELS = 8
        NUM_BASES = 8
        SUBMAT_IN = IN_FEAT // NUM_BASES
        SUBMAT_OUT = OUT_FEAT // NUM_BASES
        'RGCNBlockLayer forward (self_loop=False, bias=None, activation=None).\n\n            Per relation r: agg_r[v] = sum_{(u->v) in rel r} norm_e * h[u]\n            then block-diagonal matmul out_r = blockmm(agg_r, W_r); output = sum_r out_r.\n            '
        N, in_feat = h.shape
        R = weight.shape[0]
        msg = h[edge_src] * edge_norm[:, None]
        seg = edge_rel * N + edge_dst
        agg = jax.ops.segment_sum(msg, seg, num_segments=R * N)
        agg = agg.reshape(R, N, NUM_BASES, SUBMAT_IN)
        W = weight.reshape(R, NUM_BASES, SUBMAT_IN, SUBMAT_OUT)
        out = jnp.einsum('rnbi,rbio->nbo', agg, W)
        return out.reshape(N, NUM_BASES * SUBMAT_OUT)

    def _L1_mix_ref(x, Wqkv, ln1_g, ln1_b, W1, b1, W2, b2, ln2_g, ln2_b):
        import jax, jax.numpy as jnp
        import numpy as np
        N, F, C, H = (32, 512, 256, 8)
        D = C // H
        EPS_ATTN = 1e-06
        EPS_LN = 1e-05

        def layer_norm(x, g, b):
            mu = jnp.mean(x, axis=-1, keepdims=True)
            var = jnp.var(x, axis=-1, keepdims=True)
            return (x - mu) * jax.lax.rsqrt(var + EPS_LN) * g + b
        n, f, c = x.shape
        qkv = jnp.einsum('nfc,oc->nfo', x, Wqkv)
        q, k, v = jnp.split(qkv, 3, axis=-1)
        q = q.reshape(n, f, H, D)
        k = k.reshape(n, f, H, D)
        v = v.reshape(n, f, H, D)
        q = jax.nn.elu(q) + 1.0
        k = jax.nn.elu(k) + 1.0
        kv = jnp.einsum('nshd,nshm->nhmd', k, v)
        ksum = jnp.sum(k, axis=1)
        z = 1.0 / (jnp.einsum('nlhd,nhd->nlh', q, ksum) + EPS_ATTN)
        t = jnp.einsum('nlhd,nhmd,nlh->nlhm', q, kv, z)
        t = t.reshape(n, f, c)
        x1 = layer_norm(t + x, ln1_g, ln1_b)
        h = jax.nn.gelu(jnp.einsum('nfc,oc->nfo', x1, W1) + b1, approximate=False)
        y = jnp.einsum('nfc,oc->nfo', h, W2) + b2
        return layer_norm(y + x1, ln2_g, ln2_b)

    def _L1_ffn_ref(x, W_fx, b_fx, W_x, b_x, W_slice, b_slice, W_q, W_k, W_v, W_out, b_out, temperature):
        import jax, jax.numpy as jnp
        import numpy as np
        DIM = 256
        H = 8
        D = 64
        G = 64
        INNER = H * D
        SCALE = D ** (-0.5)
        B, N, _ = x.shape
        fx_mid = (x @ W_fx + b_fx).reshape(B, N, H, D).transpose(0, 2, 1, 3)
        x_mid = (x @ W_x + b_x).reshape(B, N, H, D).transpose(0, 2, 1, 3)
        temp = jnp.clip(temperature, 0.1, 5.0)
        slice_weights = jax.nn.softmax((x_mid @ W_slice + b_slice) / temp, axis=-1)
        slice_norm = slice_weights.sum(axis=2)
        slice_token = jnp.einsum('bhnc,bhng->bhgc', fx_mid, slice_weights)
        slice_token = slice_token / (slice_norm[..., None] + 1e-05)
        q = slice_token @ W_q
        k = slice_token @ W_k
        v = slice_token @ W_v
        attn = jax.nn.softmax(jnp.einsum('bhgc,bhkc->bhgk', q, k) * SCALE, axis=-1)
        out_slice = jnp.einsum('bhgk,bhkc->bhgc', attn, v)
        out_x = jnp.einsum('bhgc,bhng->bhnc', out_slice, slice_weights)
        out_x = out_x.transpose(0, 2, 1, 3).reshape(B, N, INNER)
        return out_x @ W_out + b_out
    edge_index = jnp.stack([src, dst])
    xn = _layernorm(x, axis=-1)
    x = x + _L0_gnn_ref(xn, edge_index, L0_gnn_w_in, L0_gnn_b_in, L0_gnn_g_in, L0_gnn_bt_in, L0_gnn_w_l, L0_gnn_a_s, L0_gnn_a_d, L0_gnn_b_l, L0_gnn_g_l, L0_gnn_bt_l) + _L0_mix_ref(xn[None], L0_mix_Wq, L0_mix_bq, L0_mix_Wk, L0_mix_bk, L0_mix_Wv, L0_mix_bv, L0_mix_Wo, L0_mix_bo, L0_mix_W1, L0_mix_b1, L0_mix_W2, L0_mix_b2, L0_mix_ln1_g, L0_mix_ln1_b, L0_mix_ln2_g, L0_mix_ln2_b)[0]
    x = x + _L0_ffn_ref(_layernorm(x, axis=-1)[None], L0_ffn_Wr, L0_ffn_br, L0_ffn_W1, L0_ffn_b1, L0_ffn_g1, L0_ffn_be1, L0_ffn_m1, L0_ffn_v1, L0_ffn_W2, L0_ffn_b2, L0_ffn_g2, L0_ffn_be2, L0_ffn_m2, L0_ffn_v2, L0_ffn_Wo, L0_ffn_bo)[0]
    xn = _layernorm(x, axis=-1)
    x = x + _L1_gnn_ref(xn, L1_gnn_weight, src, dst, edge_type_8, edge_weight) + _L1_mix_ref(xn[None], L1_mix_Wqkv, L1_mix_ln1_g, L1_mix_ln1_b, L1_mix_W1, L1_mix_b1, L1_mix_W2, L1_mix_b2, L1_mix_ln2_g, L1_mix_ln2_b)[0]
    x = x + _L1_ffn_ref(_layernorm(x, axis=-1)[None], L1_ffn_W_fx, L1_ffn_b_fx, L1_ffn_W_x, L1_ffn_b_x, L1_ffn_W_slice, L1_ffn_b_slice, L1_ffn_W_q, L1_ffn_W_k, L1_ffn_W_v, L1_ffn_W_out, L1_ffn_b_out, L1_ffn_temperature)[0]
    return x

_drawn_inputs = setup_inputs


def setup_inputs(seed=0):
    import zlib

    import numpy as np

    out = dict(_drawn_inputs(seed))
    spreads = {'L0_gnn_b_in': (0.0, 0.1),
     'L0_gnn_g_in': (1.0, 0.2),
     'L0_gnn_bt_in': (0.0, 0.1),
     'L0_gnn_b_l': (0.0, 0.1),
     'L0_gnn_g_l': (1.0, 0.2),
     'L0_gnn_bt_l': (0.0, 0.1),
     'L0_mix_bq': (0.0, 2.0),
     'L0_mix_bk': (0.0, 2.0),
     'L0_mix_bv': (0.0, 0.1),
     'L0_mix_bo': (0.0, 0.1),
     'L0_mix_b1': (0.0, 0.362),
     'L0_mix_b2': (0.0, 0.1),
     'L0_mix_ln1_g': (1.0, 0.2),
     'L0_mix_ln1_b': (0.0, 0.1),
     'L0_mix_ln2_g': (1.0, 0.2),
     'L0_mix_ln2_b': (0.0, 0.1),
     'L0_ffn_br': (0.0, 0.669),
     'L0_ffn_b1': (0.0, 0.8),
     'L0_ffn_g1': (1.0, 0.6),
     'L0_ffn_be1': (0.0, 0.8),
     'L0_ffn_m1': (0.0, 0.8),
     'L0_ffn_v1': (1.0, 0.6),
     'L0_ffn_b2': (0.0, 0.602),
     'L0_ffn_g2': (1.0, 0.6),
     'L0_ffn_be2': (0.0, 0.665),
     'L0_ffn_m2': (0.0, 0.617),
     'L0_ffn_v2': (1.0, 0.6),
     'L0_ffn_bo': (0.0, 0.461),
     'L1_mix_ln1_g': (1.0, 0.2),
     'L1_mix_ln1_b': (0.0, 0.274),
     'L1_mix_ln2_g': (1.0, 0.2),
     'L1_mix_ln2_b': (0.0, 0.313),
     'L1_ffn_b_fx': (0.0, 0.302),
     'L1_ffn_b_x': (0.0, 0.8),
     'L1_ffn_b_slice': (0.0, 0.8),
     'L1_ffn_b_out': (0.0, 0.312),
     'L1_ffn_temperature': (0.5, 0.6)}
    factors = {'L0_mix_Wq': 8.0,
     'L0_mix_Wk': 8.0,
     'L0_mix_Wv': 8.0,
     'L1_mix_b1': 8.0,
     'L1_mix_b2': 5.79,
     'L1_ffn_W_x': 8.0,
     'L1_ffn_W_slice': 8.0,
     'L1_ffn_W_q': 8.0,
     'L1_ffn_W_k': 8.0}
    for name, (base, spread) in spreads.items():
        noise = np.random.default_rng([zlib.crc32(name.encode()), seed]).standard_normal(out[name].shape)
        drawn = base * np.exp(spread * noise) if base else spread * noise
        out[name] = jnp.asarray(drawn.astype(out[name].dtype))
    for name, factor in factors.items():
        out[name] = (out[name] * factor).astype(out[name].dtype)
    return out
```

```python
from contextlib import ExitStack

import numpy as np

import concourse.bass as bass
from concourse import mybir

F32 = mybir.dt.float32
I32 = mybir.dt.int32
ALU = mybir.AluOpType
ACT = mybir.ActivationFunctionType
AX = mybir.AxisListType

P = 128
N_NODES = 6250
N_EDGES = 100000
D = 256
HALVES = D // P
N_TILES = 50
N_PAD = N_TILES * P
LAST_TILE = N_NODES // P
PAIR = 2
UNITS = N_TILES // PAIR
UNROLL = 5
ROUNDS = UNITS // UNROLL
GAT_LAYERS, GAT_HEADS, GAT_DIM = 3, 4, 64
MIX_DIM = 32
GAT_ROW = D + GAT_HEADS
LN_EPS = 1e-5
BIG = 1e30
OUT_OF_RANGE = 1 << 20

CHUNKS = -(-N_EDGES // P)
STEPS = CHUNKS + LAST_TILE
SLOTS = 8
STEP_ROUNDS = -(-STEPS // SLOTS)
STEPS_RUN = STEP_ROUNDS * SLOTS
BLOCKS = -(-STEPS_RUN // P)
STEPS_PAD = BLOCKS * P


class Count:

    def __init__(self, engine, sem):
        self.engine, self.sem, self.base, self.n = engine, sem, 0, 0

    def done(self, instruction):
        instruction.then_inc(self.sem, 1)
        self.n += 1
        self.engine.wait_ge(self.sem, self.base + self.n)

    def enter(self, i, per):
        self.before, self.per = self.base + self.n, per
        self.base, self.n = self.before + i * per, 0

    def leave(self, trips):
        assert self.n == self.per, (self.n, self.per)
        self.base, self.n = self.before + trips * self.per, 0


FIRST_SEM, LAST_SEM = 100, 229
GATHER_SEMS = 26


class Space:

    def __init__(self, nc, stack, tag, gathers=None):
        self.nc, self.stack, self.tag, self.next, self.gathers = nc, stack, tag, FIRST_SEM, gathers
        stack.callback(self.close)

    def close(self):
        if self.next > FIRST_SEM:
            self.nc.all_engine_barrier(sems_to_clear=range(FIRST_SEM, self.next))

    def sb(self, name, shape, dt=F32):
        return self.stack.enter_context(self.nc.sbuf_tensor(f"{self.tag}_{name}", shape, dt))

    def ps(self, name, shape, dt=F32):
        return self.stack.enter_context(self.nc.psum_tensor(f"{self.tag}_{name}", shape, dt))

    def sem(self, name):
        assert self.next <= LAST_SEM
        self.next += 1
        return self.stack.enter_context(self.nc.semaphore(f"{self.tag}_{name}", num=self.next - 1))

    def sems(self, name, n):
        return [self.sem(f"{name}{i}") for i in range(n)]


class Gathers:

    def __init__(self, nc):
        self.sems = [nc.alloc_semaphore(f"gather{i}", num=LAST_SEM + 1 + i) for i in range(GATHER_SEMS)]
        self.had = [0] * GATHER_SEMS

    def start(self, slots):
        return [(self.sems[i], self.had[i]) for i in slots]

    def count(self, slots, dmas):
        for i in slots:
            self.had[i] += 16 * dmas


def rows_of(vector):
    return vector.partition_broadcast(P)


def build_tables(nc, io, dram, keep, gathers):
    with ExitStack() as stack:
        sp_ = Space(nc, stack, "tab")
        sb, ps, sem = sp_.sb, sp_.ps, sp_.sem
        ident, iota_row = keep["ident"], keep["iota_row"]
        pad_int = sb("pad_int", [1, 4, P], I32)
        zeros = sb("zeros", [P, D])
        minus_big = sb("minus_big", [P, 2048])
        iota_int = sb("iota_int", [P, P], I32)
        chunk_int = sb("chunk_int", [1, CHUNKS], I32)
        chunk_no = sb("chunk_no", [1, CHUNKS])
        step_int = sb("step_int", [P, BLOCKS], I32)
        step_no = sb("step_no", [P, BLOCKS])
        node_int = sb("node_int", [P, N_TILES], I32)
        node_no = sb("node_no", [P, N_TILES])
        ones = sb("ones", [1, P])
        ends = sb("ends", [1, 2, CHUNKS], I32)
        path = sb("path", [1, 2, CHUNKS])
        tile_int = sb("tile_int", [1, CHUNKS], I32)
        path_all = sb("path_all", [P, 2, CHUNKS])
        junk = sb("junk", [P, CHUNKS])
        chunk_of = sb("chunk_of", [P, BLOCKS])
        chunk_idx = sb("chunk_idx", [P, BLOCKS], I32)
        tile_of = sb("tile_of", [P, BLOCKS])
        tile_clip = sb("tile_clip", [P, BLOCKS])
        first_of = sb("first_of", [P, BLOCKS])
        raw = sb("raw", [P, 5, BLOCKS, P], I32)
        weight = sb("weight", [P, BLOCKS, P])
        as_f = sb("as_f", [P, 5, BLOCKS, P])
        rel = sb("rel", [P, BLOCKS, P])
        low = sb("low", [P, BLOCKS, P])
        valid = sb("valid", [P, BLOCKS, P])
        flags = sb("flags", [P, 5, BLOCKS, P])
        differs = sb("differs", [P, BLOCKS, P])
        zero_row = sb("zero_row", [P, P])
        any_reset = sb("any_reset", [P, 2, BLOCKS, 8])
        node_chunk = sb("node_chunk", [P, N_TILES])
        node_chunk_idx = sb("node_chunk_idx", [P, N_TILES], I32)
        node_rows = sb("node_rows", [P, UNROLL, P], I32)
        node_stage = sb("node_stage", [P, UNROLL], I32)
        node_rows_f = sb("node_rows_f", [P, UNROLL, P])
        before = sb("before", [P, N_TILES])
        has = sb("has", [P, N_TILES])
        position = sb("position", [P, N_TILES])
        bank = [ps(f"bank{i}", [P, 512]) for i in range(8)]
        s_pads, s_fill, s_consts, s_iota = sem("pads"), sem("fill"), sem("consts"), sem("iota")
        s_flat, s_ends, s_path, s_bcast = sem("flat"), sem("ends"), sem("path"), sem("bcast")
        s_index, s_rows, s_dve, s_tabs, s_psum = sem("index"), gathers.start([UNROLL])[0][0], sem("dve"), sem("tabs"), sem("psum")
        s_nidx, s_ncopy, s_nused, s_const = sem("nidx"), sem("ncopy"), sem("nused"), sem("const")
        s_nrow = [s for s, _ in gathers.start(range(UNROLL))]
        s_flags = sem("flags")

        src, dst, kind, wt = io["src"], io["dst"], io["edge_type_8"], io["edge_weight"]
        names = ["src", "dst", "prev", "next", "kind"]
        flat = {n: dram[f"{n}_rows"].rearrange("c e -> (c e)") for n in names + ["weight"]}
        tail = CHUNKS * P - N_EDGES
        n_flat = 13
        n_fill = 1 + 1 + 2 * BLOCKS

        def line(ap):
            return ap.rearrange("(a n) -> a n", a=1)

        gathers.count(range(UNROLL), N_TILES // UNROLL)
        gathers.count([UNROLL], 6 * BLOCKS)
        with nc.Block() as block:

            @block.gpsimd
            def _(pool):
                nc.gpsimd.memset(pad_int[:, 0, :], 0)
                nc.gpsimd.memset(pad_int[:, 1, :], OUT_OF_RANGE)
                nc.gpsimd.memset(pad_int[:, 2, :], -2)
                nc.gpsimd.memset(zeros[:, :], 0.0)
                nc.gpsimd.memset(minus_big[:, :], -BIG).then_inc(s_pads, 1)
                nc.gpsimd.memset(ident[:, :], 0.0)
                nc.gpsimd.memset(ones[:, :], 1.0)
                nc.gpsimd.memset(keep["eps"][:, :], LN_EPS)
                nc.gpsimd.memset(zero_row[:, :], 0.0)
                nc.gpsimd.iota(chunk_int[:, :], [[1, CHUNKS]], base=0, channel_multiplier=0)
                nc.gpsimd.iota(step_int[:, :], [[P, BLOCKS]], base=0, channel_multiplier=1)
                nc.gpsimd.iota(node_int[:, :], [[P, N_TILES]], base=0, channel_multiplier=1)
                nc.gpsimd.iota(iota_int[:, :], [[1, P]], base=0, channel_multiplier=0).then_inc(s_iota, 1)
                pool.wait_ge(s_iota, 1)
                nc.gpsimd.affine_select(out=ident[:, :], in_=ident[:, :], compare_op=ALU.not_equal, fill=1.0,
                                        base=0, pattern=[[-1, P]], channel_multiplier=1).then_inc(s_consts, 1)
                pool.wait_ge(s_index, 1)
                pool.wait_ge(s_flat, 16 * n_flat)
                for b in range(BLOCKS):
                    for j, n in enumerate(names):
                        nc.gpsimd.indirect_dma_start(
                            out=raw[:, j, b, :], out_offset=None, in_=dram[f"{n}_rows"],
                            in_offset=bass.IndirectOffsetOnAxis(ap=chunk_idx[:, b:b + 1], axis=0)).then_inc(s_rows, 16)
                    nc.gpsimd.indirect_dma_start(
                        out=weight[:, b, :], out_offset=None, in_=dram["weight_rows"],
                        in_offset=bass.IndirectOffsetOnAxis(ap=chunk_idx[:, b:b + 1], axis=0)).then_inc(s_rows, 16)
                with pool.Fori(0, N_TILES // UNROLL) as r:
                    pool.wait_ge(s_nidx, r * UNROLL + UNROLL)
                    pool.wait_ge(s_nused, r * UNROLL + UNROLL)
                    nc.gpsimd.tensor_copy(node_stage[:, :], node_chunk_idx[:, bass.ts(r, UNROLL)]).then_inc(s_ncopy, 1)
                    pool.wait_ge(s_ncopy, r + 1)
                    pool.sem_inc(s_const, 1)
                    for u in range(UNROLL):
                        nc.gpsimd.indirect_dma_start(
                            out=node_rows[:, u, :], out_offset=None, in_=dram["dst_rows"],
                            in_offset=bass.IndirectOffsetOnAxis(ap=node_stage[:, u:u + 1], axis=0)).then_inc(s_nrow[u], 16)

            @block.sync
            def _(sp):
                sp.wait_ge(s_pads, 1)
                for n, ap, pad in (("src", src, 0), ("dst", dst, 1), ("kind", kind, 0)):
                    sp.dma_start(line(flat[n][0:N_EDGES]), line(ap)).then_inc(s_flat, 16)
                    sp.dma_start(line(flat[n][N_EDGES:]), pad_int[:, pad, 0:tail]).then_inc(s_flat, 16)
                sp.dma_start(line(flat["weight"][0:N_EDGES]), line(wt)).then_inc(s_flat, 16)
                sp.dma_start(line(flat["weight"][N_EDGES:]), zeros[0:1, 0:tail]).then_inc(s_flat, 16)
                sp.dma_start(line(flat["prev"][0:1]), pad_int[:, 2, 0:1]).then_inc(s_flat, 16)
                sp.dma_start(line(flat["prev"][1:N_EDGES + 1]), line(dst)).then_inc(s_flat, 16)
                sp.dma_start(line(flat["prev"][N_EDGES + 1:]), pad_int[:, 2, 0:tail - 1]).then_inc(s_flat, 16)
                sp.dma_start(line(flat["next"][0:N_EDGES - 1]), line(dst[1:])).then_inc(s_flat, 16)
                sp.dma_start(line(flat["next"][N_EDGES - 1:]), pad_int[:, 2, 0:tail + 1]).then_inc(s_flat, 16)
                sp.dma_start(dram["x0"][0:N_NODES, :], io["x"]).then_inc(s_fill, 16)
                rest = N_PAD - N_NODES
                assert rest <= 2 * P
                sp.dma_start(dram["x0"][N_NODES:N_NODES + rest // 2, :], zeros[0:rest // 2, :]).then_inc(s_fill, 16)
                sp.dma_start(dram["x0"][N_NODES + rest // 2:, :], zeros[0:rest - rest // 2, :]).then_inc(s_fill, 16)
                for b in range(BLOCKS):
                    sp.dma_start(dram["first"][b * P * P:(b + 1) * P * P, :].rearrange("(p e) q -> p (e q)", p=P),
                                 minus_big[:, 0:P * 8]).then_inc(s_fill, 16)
                sp.wait_ge(s_flat, 16 * n_flat)
                with nc.allow_non_contiguous_dma(reason="one destination per chunk"):
                    sp.dma_start(ends[:, 0, :], dram["dst_rows"][:, 0:1].rearrange("c e -> e c")).then_inc(s_ends, 16)
                    sp.dma_start(ends[:, 1, :], dram["dst_rows"][:, P - 1:P].rearrange("c e -> e c")).then_inc(s_ends, 16)
                sp.wait_ge(s_flags, 1)
                sp.dma_start(dram["flags"], flags[:, :, :, :].rearrange("p f b e -> p (f b e)")).then_inc(s_fill, 16)
                sp.dma_start(dram["any_reset"], any_reset[:, :, :, :].rearrange("p f b e -> p (f b e)")).then_inc(s_fill, 16)
                sp.wait_ge(s_fill, 16 * (3 + BLOCKS + 2))

            @block.vector
            def _(dve):
                dve.sem_inc(s_nused, UNROLL)
                c = Count(dve, s_dve)
                nc.vector.memset(keep["same_head"][:, :], 0.0)
                c.done(nc.vector.memset(keep["head_of"][:, :], 0.0))
                for h in range(P // MIX_DIM):
                    rows = slice(h * MIX_DIM, (h + 1) * MIX_DIM)
                    nc.vector.memset(keep["same_head"][rows, rows], 1.0)
                    nc.vector.memset(keep["head_of"][rows, h:h + 1], 1.0)
                dve.wait_ge(s_iota, 1)
                nc.vector.tensor_copy(chunk_no[:, :], chunk_int[:, :])
                nc.vector.tensor_copy(step_no[:, :], step_int[:, :])
                nc.vector.tensor_copy(node_no[:, :], node_int[:, :])
                c.done(nc.vector.tensor_copy(iota_row[:, :], iota_int[:, :]))
                nc.vector.tensor_scalar(keep["mask"][:, :], node_no[:, :], float(N_NODES), None, ALU.is_lt)
                dve.wait_ge(s_ends, 32)
                c.done(nc.vector.tensor_single_scalar(tile_int[:, :], ends[:, 0, :], 7, ALU.arith_shift_right))
                c.done(nc.vector.tensor_copy(path[:, 0, :], tile_int[:, :]))
                nc.vector.tensor_copy(path[:, 1, :], ends[:, 1, :])
                nc.vector.tensor_tensor(path[:, 0, :], path[:, 0, :], chunk_no[:, :], ALU.add).then_inc(s_path, 1)
                dve.wait_ge(s_bcast, 1)
                half = CHUNKS // 2
                for f in range(2):
                    for h in range(2):
                        last = nc.vector.tensor_copy(path_all[:, f, h * half:(h + 1) * half], bank[2 * f + h][:, 0:half])
                c.done(last)
                for b in range(BLOCKS):
                    last = nc.vector.tensor_scalar(junk[:, 0:CHUNKS - 1], path_all[:, 0, 1:CHUNKS], step_no[:, b:b + 1],
                                                   0.0, ALU.is_le, ALU.add, accum_out=chunk_of[:, b:b + 1])
                    c.done(last)
                nc.vector.tensor_copy(chunk_idx[:, :], chunk_of[:, :]).then_inc(s_index, 1)
                c.done(nc.vector.tensor_tensor(tile_of[:, :], step_no[:, :], chunk_of[:, :], ALU.subtract))
                nc.vector.tensor_scalar(first_of[:, :], tile_of[:, :], float(P), None, ALU.mult)
                c.done(nc.vector.tensor_scalar(tile_clip[:, :], tile_of[:, :], float(LAST_TILE), None, ALU.min))
                with dve.Fori(0, N_TILES) as t:
                    c.enter(t, 1)
                    c.done(nc.vector.tensor_scalar(junk[:, :], path_all[:, 1, :], node_no[:, bass.ts(t, 1)], 0.0,
                                                   ALU.is_lt, ALU.add, accum_out=node_chunk[:, bass.ts(t, 1)]))
                    nc.vector.tensor_copy(node_chunk_idx[:, bass.ts(t, 1)], node_chunk[:, bass.ts(t, 1)]).then_inc(s_nidx, 1)
                c.leave(N_TILES)
                dve.wait_ge(s_rows, 16 * 6 * BLOCKS)
                c.done(nc.vector.tensor_copy(as_f[:, :, :, :].rearrange("p j b e -> p (j b e)"),
                                             raw[:, :, :, :].rearrange("p j b e -> p (j b e)")))
                for b in range(BLOCKS):
                    last = nc.vector.tensor_scalar(rel[:, b, :], as_f[:, 1, b, :], first_of[:, b:b + 1], None, ALU.subtract)
                c.done(last)
                c.done(nc.vector.tensor_scalar(low[:, :, :], rel[:, :, :], 0.0, None, ALU.is_ge))
                c.done(nc.vector.scalar_tensor_tensor(valid[:, :, :], rel[:, :, :], float(P), low[:, :, :], ALU.is_lt, ALU.mult))
                c.done(nc.vector.scalar_tensor_tensor(as_f[:, 4, :, :], as_f[:, 4, :, :], float(N_PAD), as_f[:, 0, :, :],
                                                      ALU.mult, ALU.add))
                c.done(nc.vector.tensor_scalar(flags[:, 4, :, :], valid[:, :, :], -1.0, BIG, ALU.add, ALU.mult))
                for f in range(2):
                    c.done(nc.vector.tensor_tensor(differs[:, :, :], as_f[:, 1, :, :], as_f[:, 2 + f, :, :], ALU.not_equal))
                    c.done(nc.vector.tensor_tensor(differs[:, :, :], differs[:, :, :], valid[:, :, :], ALU.mult))
                    c.done(nc.vector.tensor_scalar(flags[:, f, :, :], differs[:, :, :], -BIG, None, ALU.mult))
                for b in range(BLOCKS):
                    nc.vector.tensor_tensor_scan(flags[:, 2, b, :], zero_row[:, :], flags[:, 0, b, :], 0.0, ALU.add, ALU.min)
                    last = nc.vector.tensor_tensor_scan(flags[:, 3, b, ::-1], zero_row[:, :], flags[:, 1, b, ::-1], 0.0,
                                                        ALU.add, ALU.min)
                c.done(last)
                for f, e in ((0, P - 1), (1, 0)):
                    last = nc.vector.tensor_copy(any_reset[:, f, :, :],
                                                 flags[:, 2 + f, :, e:e + 1].to_broadcast([P, BLOCKS, 8]))
                last.then_inc(s_flags, 1)
                tables = (keep["src_tab"], keep["rel_tab"], keep["wt_tab"], keep["dst_tab"])
                for i in range(4 * BLOCKS):
                    j, b = i // BLOCKS, i % BLOCKS
                    dve.wait_ge(s_psum, i + 1)
                    nc.vector.tensor_copy(tables[j][:, b * P:(b + 1) * P], bank[i % 8][:, 0:P]).then_inc(s_tabs, 1)
                for b in range(BLOCKS):
                    dve.wait_ge(s_psum, 4 * BLOCKS + 1 + b)
                    last = nc.vector.tensor_copy(keep["tile_row"][:, b * P:(b + 1) * P], bank[b % 8][0:1, 128:256])
                c.done(last)
                with dve.Fori(0, N_TILES // UNROLL) as r:
                    c.enter(r, 3 * UNROLL)
                    for u in range(UNROLL):
                        dve.wait_ge(s_nrow[u], r * 16 + 16)
                        c.done(nc.vector.tensor_copy(node_rows_f[:, u, :], node_rows[:, u, :]))
                        dve.sem_inc(s_nused, 1)
                        c.done(nc.vector.tensor_scalar(junk[:, 0:P], node_rows_f[:, u, :], node_no[:, bass.ds(r * UNROLL + u, 1)],
                                                       0.0, ALU.is_lt, ALU.add, accum_out=before[:, bass.ds(r * UNROLL + u, 1)]))
                        c.done(nc.vector.tensor_scalar(junk[:, 0:P], node_rows_f[:, u, :], node_no[:, bass.ds(r * UNROLL + u, 1)],
                                                       0.0, ALU.is_equal, ALU.max, accum_out=has[:, bass.ds(r * UNROLL + u, 1)]))
                c.leave(N_TILES // UNROLL)
                c.done(nc.vector.scalar_tensor_tensor(position[:, :], node_chunk[:, :], float(P), before[:, :], ALU.mult, ALU.add))
                c.done(nc.vector.scalar_tensor_tensor(position[:, :], has[:, :], -float(OUT_OF_RANGE), position[:, :],
                                                      ALU.mult, ALU.add))
                for t in range(N_TILES):
                    last = nc.vector.tensor_scalar(position[:, t:t + 1], position[:, t:t + 1], float(OUT_OF_RANGE + P * t), None,
                                                   ALU.add)
                c.done(last)
                c.done(nc.vector.tensor_copy(keep["first_pos"][:, :], position[:, :]))

            @block.tensor
            def _(pe):
                pe.wait_ge(s_path, 1)
                pe.wait_ge(s_consts, 1)
                half = CHUNKS // 2
                for f in range(2):
                    for h in range(2):
                        last = nc.tensor.matmul(bank[2 * f + h][:, 0:half], ones[:, :], path[:, f, h * half:(h + 1) * half],
                                                start=True, stop=True)
                last.then_inc(s_bcast, 1)
                pe.wait_ge(s_flags, 1)
                sources = (as_f[:, 0], as_f[:, 4], weight, rel)
                for i in range(4 * BLOCKS):
                    j, b = i // BLOCKS, i % BLOCKS
                    if i >= 8:
                        pe.wait_ge(s_tabs, i - 7)
                    nc.tensor.transpose(bank[i % 8][:, 0:P], sources[j][:, b, :], ident[:, :]).then_inc(s_psum, 1)
                pe.wait_ge(s_tabs, 4 * BLOCKS)
                for b in range(BLOCKS):
                    nc.tensor.matmul(bank[b % 8][0:1, 128:256], tile_clip[:, b:b + 1], ident[:, :],
                                     start=True, stop=True).then_inc(s_psum, 1)


REL = 8
L0_FF, L1_FF = 1024, 256
MOE_E = 8
INNER = 512

_INS = ['x', 'src', 'dst', 'edge_type_8', 'edge_weight', 'L0_gnn_w_in', 'L0_gnn_b_in', 'L0_gnn_g_in', 'L0_gnn_bt_in',
        'L0_gnn_w_l', 'L0_gnn_a_s', 'L0_gnn_a_d', 'L0_gnn_b_l', 'L0_gnn_g_l', 'L0_gnn_bt_l',
        'L0_mix_Wq', 'L0_mix_bq', 'L0_mix_Wk', 'L0_mix_bk', 'L0_mix_Wv', 'L0_mix_bv', 'L0_mix_Wo', 'L0_mix_bo',
        'L0_mix_W1', 'L0_mix_b1', 'L0_mix_W2', 'L0_mix_b2', 'L0_mix_ln1_g', 'L0_mix_ln1_b', 'L0_mix_ln2_g', 'L0_mix_ln2_b',
        'L0_ffn_Wr', 'L0_ffn_br', 'L0_ffn_W1', 'L0_ffn_b1', 'L0_ffn_g1', 'L0_ffn_be1', 'L0_ffn_m1', 'L0_ffn_v1',
        'L0_ffn_W2', 'L0_ffn_b2', 'L0_ffn_g2', 'L0_ffn_be2', 'L0_ffn_m2', 'L0_ffn_v2', 'L0_ffn_Wo', 'L0_ffn_bo',
        'L1_gnn_weight', 'L1_mix_Wqkv', 'L1_mix_ln1_g', 'L1_mix_ln1_b', 'L1_mix_W1', 'L1_mix_b1', 'L1_mix_W2', 'L1_mix_b2',
        'L1_mix_ln2_g', 'L1_mix_ln2_b', 'L1_ffn_W_fx', 'L1_ffn_b_fx', 'L1_ffn_W_x', 'L1_ffn_b_x', 'L1_ffn_W_slice',
        'L1_ffn_b_slice', 'L1_ffn_W_q', 'L1_ffn_W_k', 'L1_ffn_W_v', 'L1_ffn_W_out', 'L1_ffn_b_out', 'L1_ffn_temperature']


class Normalise:

    def __init__(self, space, tag, eps):
        self.stats = space.sb(f"{tag}_stats", [P, UNROLL, PAIR, 6])
        self.mv = space.sb(f"{tag}_mv", [P, UNROLL, PAIR, 2])
        self.std = space.sb(f"{tag}_std", [P, UNROLL, PAIR])
        self.rstd = space.sb(f"{tag}_rstd", [P, UNROLL, PAIR])
        self.eps = eps
        self.s_stats, self.s_mv = space.sem(f"{tag}_s_stats"), space.sem(f"{tag}_s_mv")
        self.s_go = space.sem(f"{tag}_s_go")
        self.s_std, self.s_rstd = space.sem(f"{tag}_s_std"), space.sem(f"{tag}_s_rstd")

    def statistics(self, nc, u, n, data):
        for i in range(PAIR):
            last = nc.vector.bn_stats(self.stats[:, u, i, :], data[:, i, :])
        last.then_inc(self.s_stats, 1)

    def aggregate(self, nc, u, n):
        nc.vector.wait_ge(self.s_stats, n)
        nc.vector.sem_inc(self.s_go, 1)
        for i in range(PAIR):
            last = nc.vector.bn_aggr(self.mv[:, u, i, :], self.stats[:, u, i, :])
        last.then_inc(self.s_mv, 1)

    def root(self, nc, u, n):
        nc.scalar.wait_ge(self.s_mv, n)
        nc.scalar.activation(self.std[:, u, :], self.mv[:, u, :, 1], ACT.Sqrt, bias=self.eps[:, 0:1]).then_inc(self.s_std, 1)

    def invert(self, nc, u, n):
        nc.vector.wait_ge(self.s_std, n)
        nc.vector.reciprocal(self.rstd[:, u, :], self.std[:, u, :]).then_inc(self.s_rstd, 1)

    def scale(self, nc, u, n, out, data):
        nc.vector.wait_ge(self.s_rstd, n)
        for i in range(PAIR):
            last = nc.vector.tensor_scalar(out[:, i, :], data[:, i, :], self.mv[:, u, i, 0:1], self.rstd[:, u, i:i + 1],
                                           ALU.subtract, ALU.mult)
        return last


def transpose_pair(nc, bank, data, ident):
    for i in range(PAIR):
        for a in range(HALVES):
            last = nc.tensor.transpose(bank[:, a * D + i * P:a * D + i * P + P], data[:, i, a * P:(a + 1) * P], ident[:, :])
    return last


def project_pair(nc, bank, data_t, weight):
    for i in range(PAIR):
        for a in range(HALVES):
            last = nc.tensor.matmul(bank[:, i * D:(i + 1) * D], data_t[:, a, i * P:(i + 1) * P], weight[:, a, :],
                                    start=(a == 0), stop=(a == HALVES - 1))
    return last


def pair_rows(ap):
    return ap.rearrange("(t p) d -> p t d", p=P)


def both(rows):
    return rows.unsqueeze(1).to_broadcast([P, PAIR, rows.shape[-1]])


def gnn_input(nc, io, dram, keep, hidden):
    with ExitStack() as stack:
        space = Space(nc, stack, "gin")
        sb, sem = space.sb, space.sem
        w = sb("w", [P, HALVES, D])
        rows = {n: sb(n, [P, D]) for n in ("b_in", "g_in", "bt_in")}
        x = sb("x", [P, UNROLL, PAIR, D])
        xn = sb("xn", [P, UNROLL, PAIR, D])
        xt = sb("xt", [P, UNROLL, HALVES, PAIR * P])
        y = sb("y", [P, UNROLL, PAIR, D])
        neg = sb("neg", [P, UNROLL, PAIR, D])
        bank = [space.ps(f"bank{u}", [P, 512]) for u in range(UNROLL)]
        ln0, ln1 = Normalise(space, "ln0", keep["eps"]), Normalise(space, "ln1", keep["eps"])
        s_w, s_x, s_free = sem("s_w"), space.sems("s_x", UNROLL), sem("s_free")
        s_xn, s_xt, s_xtc, s_y, s_yb, s_yn = (sem(n) for n in ("s_xn", "s_xt", "s_xtc", "s_y", "s_yb", "s_yn"))
        s_yg, s_ya, s_neg, s_exp, s_pos = (sem(n) for n in ("s_yg", "s_ya", "s_neg", "s_exp", "s_pos"))
        tiles = pair_rows(dram["x0"])
        with nc.Block() as block:

            @block.sync
            def _(sp):
                sp.dma_start(w[:, :, :], io["L0_gnn_w_in"].rearrange("(a p) n -> p a n", p=P)).then_inc(s_w, 16)
                for n, t in rows.items():
                    sp.dma_start(t[:, :], rows_of(io[f"L0_gnn_{n}"])).then_inc(s_w, 16)
                with sp.Fori(0, ROUNDS) as r:
                    for u in range(UNROLL):
                        n = r * UNROLL + u + 1
                        sp.wait_ge(s_free, n)
                        sp.dma_start(x[:, u, :, :], tiles[:, bass.ds(r * (UNROLL * PAIR) + u * PAIR, PAIR), :]).then_inc(s_x[u], 16)

            @block.vector
            def _(dve):
                dve.sem_inc(s_free, UNROLL)
                dve.wait_ge(s_w, 64)
                with dve.Fori(0, ROUNDS) as r:
                    at = lambda u: r * UNROLL + u + 1
                    for u in range(UNROLL):
                        dve.wait_ge(s_x[u], r * 16 + 16)
                        ln0.statistics(nc, u, at(u), x[:, u])
                    for u in range(UNROLL):
                        ln0.aggregate(nc, u, at(u))
                    for u in range(UNROLL):
                        ln0.invert(nc, u, at(u))
                    for u in range(UNROLL):
                        ln0.scale(nc, u, at(u), xn[:, u], x[:, u]).then_inc(s_xn, 1)
                    for u in range(UNROLL):
                        dve.wait_ge(s_y, at(u))
                        nc.vector.tensor_tensor(y[:, u], bank[u][:, :].rearrange("p (i d) -> p i d", i=PAIR), both(rows["b_in"][:, :]),
                                                ALU.add).then_inc(s_yb, 1)
                    for u in range(UNROLL):
                        dve.wait_ge(s_yb, at(u))
                        ln1.statistics(nc, u, at(u), y[:, u])
                    for u in range(UNROLL):
                        ln1.aggregate(nc, u, at(u))
                    for u in range(UNROLL):
                        ln1.invert(nc, u, at(u))
                    for u in range(UNROLL):
                        ln1.scale(nc, u, at(u), y[:, u], y[:, u]).then_inc(s_yn, 1)
                    for u in range(UNROLL):
                        dve.wait_ge(s_ya, at(u))
                        nc.vector.tensor_scalar(neg[:, u], y[:, u], 0.0, None, ALU.min).then_inc(s_neg, 1)
                    for u in range(UNROLL):
                        nc.vector.tensor_scalar(y[:, u], y[:, u], 0.0, -1.0, ALU.max, ALU.add).then_inc(s_pos, 1)
                    for u in range(UNROLL):
                        dve.wait_ge(s_exp, at(u))
                        dve.wait_ge(s_pos, at(u))
                        nc.vector.tensor_tensor(hidden[:, bass.ds(r * (UNROLL * PAIR) + u * PAIR, PAIR), :], y[:, u], neg[:, u],
                                                ALU.add).then_inc(s_free, 1)

            @block.scalar
            def _(act):
                with act.Fori(0, ROUNDS) as r:
                    at = lambda u: r * UNROLL + u + 1
                    for u in range(UNROLL):
                        ln0.root(nc, u, at(u))
                    for u in range(UNROLL):
                        act.wait_ge(s_xt, at(u))
                        nc.scalar.copy(xt[:, u].rearrange("p a n -> p (a n)"), bank[u][:, :]).then_inc(s_xtc, 1)
                    for u in range(UNROLL):
                        ln1.root(nc, u, at(u))
                    for u in range(UNROLL):
                        act.wait_ge(s_neg, at(u))
                        nc.scalar.activation(neg[:, u], neg[:, u], ACT.Exp).then_inc(s_exp, 1)

            @block.tensor
            def _(pe):
                pe.wait_ge(s_w, 64)
                with pe.Fori(0, ROUNDS) as r:
                    at = lambda u: r * UNROLL + u + 1
                    for u in range(UNROLL):
                        pe.wait_ge(s_xn, at(u))
                        transpose_pair(nc, bank[u], xn[:, u], keep["ident"]).then_inc(s_xt, 1)
                    for u in range(UNROLL):
                        pe.wait_ge(s_xtc, at(u))
                        project_pair(nc, bank[u], xt[:, u], w).then_inc(s_y, 1)

            @block.gpsimd
            def _(pool):
                pool.wait_ge(s_w, 64)
                with pool.Fori(0, ROUNDS) as r:
                    at = lambda u: r * UNROLL + u + 1
                    for u in range(UNROLL):
                        pool.wait_ge(s_yn, at(u))
                        nc.gpsimd.tensor_tensor(y[:, u], y[:, u], both(rows["g_in"][:, :]), ALU.mult).then_inc(s_yg, 1)
                        pool.wait_ge(s_yg, at(u))
                        nc.gpsimd.tensor_tensor(y[:, u], y[:, u], both(rows["bt_in"][:, :]), ALU.add).then_inc(s_ya, 1)


def gat_project(nc, io, dram, keep, layer, hidden, scores):
    with ExitStack() as stack:
        space = Space(nc, stack, f"gp{layer}")
        sb, sem = space.sb, space.sem
        w = sb("w", [P, HALVES, D])
        a = sb("a", [P, 2, D])
        prod = sb("prod", [P, HALVES, 2, D])
        wa = sb("wa", [P, HALVES, 2 * GAT_HEADS])
        h = sb("h", [P, UNROLL, PAIR, D])
        ht = sb("ht", [P, UNROLL, HALVES, PAIR * P])
        row = sb("row", [P, UNROLL, PAIR, GAT_ROW])
        src_score = sb("src_score", [P, UNROLL, PAIR, GAT_HEADS])
        bank = [space.ps(f"bank{u}", [P, 512]) for u in range(UNROLL)]
        score_bank = [space.ps(f"score_bank{i}", [P, 512]) for i in range(3)]
        s_w, s_prod, s_wa, s_h, s_ht, s_htc = (sem(n) for n in ("s_w", "s_prod", "s_wa", "s_h", "s_ht", "s_htc"))
        s_mm, s_row, s_sc, s_sent, s_used = sem("s_mm"), sem("s_row"), sem("s_sc"), space.sems("s_sent", UNROLL), sem("s_used")
        feat, score = pair_rows(dram["feat"]), pair_rows(dram["score"])
        with nc.Block() as block:

            @block.sync
            def _(sp):
                sp.dma_start(w[:, :, :], io["L0_gnn_w_l"][layer].rearrange("(a p) n -> p a n", p=P)).then_inc(s_w, 16)
                for j, n in enumerate(("a_s", "a_d")):
                    sp.dma_start(a[:, j, :], rows_of(io[f"L0_gnn_{n}"][layer].rearrange("h d -> (h d)"))).then_inc(s_w, 16)
                sp.sem_inc(s_used, UNROLL)
                with sp.Fori(0, ROUNDS) as r:
                    for u in range(UNROLL):
                        n = r * UNROLL + u + 1
                        pair = bass.ds(r * (UNROLL * PAIR) + u * PAIR, PAIR)
                        sp.wait_ge(s_row, n + UNROLL)
                        sp.wait_ge(s_sc, n + UNROLL)
                        sp.dma_start(feat[:, pair, :], row[:, u, :, :]).then_inc(s_sent[u], 16)
                        sp.dma_start(score[:, pair, :], src_score[:, u, :, :]).then_inc(s_sent[u], 16)
                    for u in range(UNROLL):
                        sp.wait_ge(s_sent[u], r * 32 + 32)
                        sp.sem_inc(s_used, 1)

            @block.vector
            def _(dve):
                dve.sem_inc(s_sc, UNROLL)
                dve.wait_ge(s_w, 48)
                for i in range(HALVES):
                    for j in range(2):
                        last = nc.vector.tensor_tensor(prod[:, i, j, :], w[:, i, :], a[:, j, :], ALU.mult)
                last.then_inc(s_prod, 1)
                dve.wait_ge(s_prod, 1)
                nc.vector.tensor_reduce(wa[:, :, :].rearrange("p i s -> p (i s)"),
                                        prod[:, :, :, :].rearrange("p i j (h d) -> p (i j h) d", d=GAT_DIM), AX.X, ALU.add).then_inc(s_wa, 1)
                with dve.Fori(0, ROUNDS) as r:
                    for u in range(UNROLL):
                        n = r * UNROLL + u + 1
                        pair = bass.ds(r * (UNROLL * PAIR) + u * PAIR, PAIR)
                        dve.wait_ge(s_mm, n)
                        dve.wait_ge(s_used, n)
                        sc = score_bank[u % 3][:, 0:16].rearrange("p (i s) -> p i s", i=PAIR)
                        nc.vector.tensor_copy(row[:, u, :, D:], sc[:, :, 0:GAT_HEADS])
                        nc.vector.tensor_copy(src_score[:, u, :, :], sc[:, :, 0:GAT_HEADS])
                        nc.vector.tensor_copy(scores[:, pair, :], sc).then_inc(s_sc, 1)

            @block.scalar
            def _(act):
                act.sem_inc(s_row, UNROLL)
                with act.Fori(0, ROUNDS) as r:
                    for u in range(UNROLL):
                        n = r * UNROLL + u + 1
                        act.wait_ge(s_used, n)
                        nc.scalar.copy(h[:, u], hidden[:, bass.ds(r * (UNROLL * PAIR) + u * PAIR, PAIR), :]).then_inc(s_h, 1)
                    for u in range(UNROLL):
                        n = r * UNROLL + u + 1
                        act.wait_ge(s_ht, n)
                        nc.scalar.copy(ht[:, u].rearrange("p a n -> p (a n)"), bank[u][:, :]).then_inc(s_htc, 1)
                    for u in range(UNROLL):
                        n = r * UNROLL + u + 1
                        act.wait_ge(s_mm, n)
                        nc.scalar.copy(row[:, u, :, 0:D], bank[u][:, :].rearrange("p (i d) -> p i d", i=PAIR)).then_inc(s_row, 1)

            @block.tensor
            def _(pe):
                pe.wait_ge(s_wa, 1)
                with pe.Fori(0, ROUNDS) as r:
                    for u in range(UNROLL):
                        pe.wait_ge(s_h, r * UNROLL + u + 1)
                        transpose_pair(nc, bank[u], h[:, u], keep["ident"]).then_inc(s_ht, 1)
                    for u in range(UNROLL):
                        pe.wait_ge(s_htc, r * UNROLL + u + 1)
                        project_pair(nc, bank[u], ht[:, u], w)
                        pe.wait_ge(s_sc, r * UNROLL + (4, 5, 3, 6, 7)[u])
                        for i in range(PAIR):
                            c = 8 * i
                            for k in range(HALVES):
                                last = nc.tensor.matmul(score_bank[u % 3][:, c:c + 8], ht[:, u, k, i * P:(i + 1) * P], wa[:, k, :],
                                                        start=(k == 0), stop=(k == HALVES - 1))
                        last.then_inc(s_mm, 1)


def gat_softmax(nc, dram, keep, gathers, layer, scores, weights, self_weight):
    Q = 2 * GAT_HEADS
    H = GAT_HEADS
    SG = 2 * SLOTS
    with ExitStack() as stack:
        space = Space(nc, stack, f"sm{layer}")
        sb, sem = space.sb, space.sem
        flags = sb("flags", [P, 5, BLOCKS, P])
        any_reset = sb("any_reset", [P, 2, BLOCKS, Q])
        by_edge = sb("by_edge", [P, STEPS_PAD, H])
        s_step = sb("s_step", [P, BLOCKS, P, H])
        seg = sb("seg", [P, BLOCKS, P, Q])
        top = sb("top", [P, BLOCKS, P, H])
        carry_in = sb("carry_in", [P, BLOCKS, Q])
        chain = sb("chain", [Q, 4, STEPS_PAD])
        got = sb("got", [P, SG, H])
        idx = sb("idx", [P, SG], I32)
        node_score = sb("node_score", [P, UNROLL, Q])
        node_pos = sb("node_pos", [P, UNROLL], I32)
        node_top = sb("node_top", [P, UNROLL, H])
        node_max = sb("node_max", [P, N_TILES, H])
        node_e = sb("node_e", [P, 2, N_TILES, H])
        bank = [space.ps(f"bank{i}", [P, 512]) for i in range(8)]
        s_load, s_zero, s_copy, s_sent, s_free = sem("s_load"), sem("s_zero"), sem("s_copy"), gathers.start(range(SG, SG + UNROLL)), sem("s_free")
        s_got, s_used, s_dummy, s_idx = gathers.start(range(SG)), sem("s_used"), sem("s_dummy"), sem("s_idx")
        s_dve, s_seg, s_pe, s_ev = sem("s_dve"), sem("s_seg"), sem("s_pe"), sem("s_ev")
        s_top, s_ntop, s_nfree, s_exp, s_want = sem("s_top"), gathers.start(range(SG + UNROLL, SG + 2 * UNROLL)), sem("s_nfree"), sem("s_exp"), sem("s_want")
        s_fill, s_npos, s_nmax, s_ne = sem("s_fill"), sem("s_npos"), sem("s_nmax"), sem("s_ne")
        s_scat = sem("s_scat")
        first = dram["first"].rearrange("(b p e) q -> p b (e q)", p=P, e=P)
        top_rows = dram["seg_max"].rearrange("(b p e) h -> p b (e h)", p=P, e=P)
        R = N_TILES // UNROLL
        GR = -(-STEPS_RUN // SG)
        assert GR * SG == STEPS_RUN
        gathers.count(range(SG), GR)
        gathers.count(range(SG, SG + 2 * UNROLL), R)

        with nc.Block() as block:

            @block.gpsimd
            def _(pool):
                with pool.Fori(0, R) as r:
                    pool.wait_ge(s_free, r * UNROLL + UNROLL)
                    nc.gpsimd.tensor_copy(node_score[:, :, :], scores[:, bass.ts(r, UNROLL), :])
                    nc.gpsimd.tensor_copy(node_pos[:, :], keep["first_pos"][:, bass.ts(r, UNROLL)]).then_inc(s_copy, 1)
                    pool.wait_ge(s_copy, r + 1)
                    pool.sem_inc(s_dummy, 1)
                    for u in range(UNROLL):
                        nc.gpsimd.indirect_dma_start(
                            out=dram["first"], out_offset=bass.IndirectOffsetOnAxis(ap=node_pos[:, u:u + 1], axis=0),
                            in_=node_score[:, u, :], in_offset=None, bounds_check=STEPS_PAD * P - 1,
                            oob_is_err=False).then_inc(s_sent[u][0], 16)
                with pool.Fori(0, GR) as r:
                    for q in range(2):
                        half = slice(q * SLOTS, (q + 1) * SLOTS)
                        pool.wait_ge(s_used, r * SG + (q + 1) * SLOTS)
                        nc.gpsimd.tensor_copy(idx[:, half], keep["src_tab"][:, bass.ds(r * SG + q * SLOTS, SLOTS)]).then_inc(s_idx, 1)
                        pool.wait_ge(s_idx, r * 2 + q + 1)
                        pool.sem_inc(s_dummy, 1)
                        for u in range(q * SLOTS, (q + 1) * SLOTS):
                            nc.gpsimd.indirect_dma_start(
                                out=got[:, u, :], out_offset=None, in_=dram["score"],
                                in_offset=bass.IndirectOffsetOnAxis(ap=idx[:, u:u + 1], axis=0)).then_inc(s_got[u][0], 16)
                pool.wait_ge(s_top, 16)
                with pool.Fori(0, R) as r:
                    pool.wait_ge(s_nfree, r * UNROLL + UNROLL)
                    pool.sem_inc(s_dummy, 1)
                    nc.gpsimd.memset(node_top[:, :, :], -BIG)
                    nc.gpsimd.tensor_copy(node_pos[:, :], keep["first_pos"][:, bass.ts(r, UNROLL)]).then_inc(s_npos, 1)
                    pool.wait_ge(s_npos, r + 1)
                    pool.sem_inc(s_dummy, 1)
                    for u in range(UNROLL):
                        nc.gpsimd.indirect_dma_start(
                            out=node_top[:, u, :], out_offset=None, in_=dram["seg_max"],
                            in_offset=bass.IndirectOffsetOnAxis(ap=node_pos[:, u:u + 1], axis=0),
                            bounds_check=STEPS_PAD * P - 1, oob_is_err=False).then_inc(s_ntop[u][0], 16)

            @block.sync
            def _(sp):
                sp.dma_start(flags[:, :, :, :].rearrange("p f b e -> p (f b e)"), dram["flags"]).then_inc(s_load, 16)
                sp.dma_start(any_reset[:, :, :, :].rearrange("p f b e -> p (f b e)"), dram["any_reset"]).then_inc(s_load, 16)
                sp.sem_inc(s_free, UNROLL)
                with sp.Fori(0, R) as r:
                    for u in range(UNROLL):
                        sp.wait_ge(s_sent[u][0], r * 16 + (s_sent[u][1] + 16))
                        sp.sem_inc(s_free, 1)
                sp.wait_ge(s_free, UNROLL + N_TILES)
                sp.dma_start(seg[:, :, :, :].rearrange("p b e q -> p b (e q)"), first).then_inc(s_seg, 16)
                sp.wait_ge(s_want, 1)
                sp.dma_start(top_rows, top[:, :, :, :].rearrange("p b e h -> p b (e h)")).then_inc(s_top, 16)

            @block.scalar
            def _(act):
                act.sem_inc(s_used, SG)
                act.wait_ge(s_zero, 1)
                with act.Fori(0, GR) as r:
                    for u in range(SG):
                        act.wait_ge(s_got[u][0], r * 16 + (s_got[u][1] + 16))
                        nc.scalar.copy(by_edge[:, bass.ds(r * SG + u, 1), :], got[:, u:u + 1, :]).then_inc(s_used, 1)
                act.wait_ge(s_exp, 1)
                nc.scalar.activation(top[:, :, :, :], top[:, :, :, :], ACT.Exp).then_inc(s_exp, 1)
                act.wait_ge(s_ne, 1)
                nc.scalar.activation(self_weight[:, :, :], node_e[:, 0], ACT.Exp).then_inc(s_ne, 1)

            @block.vector
            def _(dve):
                c = Count(dve, s_dve)
                dve.sem_inc(s_nfree, UNROLL)
                nc.vector.memset(by_edge[:, STEPS_RUN:, :], 0.0).then_inc(s_zero, 1)
                dve.wait_ge(s_load, 32)
                for b in range(BLOCKS):
                    dve.wait_ge(s_pe, b + 1)
                    nc.vector.tensor_copy(s_step[:, b].rearrange("p e h -> p h e"),
                                          bank[b][:, :].rearrange("p (h e) -> p h e", h=H)).then_inc(s_ev, 1)
                dve.wait_ge(s_ev, BLOCKS)
                dve.wait_ge(s_seg, 16)
                for h in range(H):
                    last = nc.vector.tensor_tensor(top[:, :, :, h], s_step[:, :, :, h], flags[:, 4], ALU.add)
                c.done(last)
                c.done(nc.vector.tensor_tensor(seg[:, :, :, 0:H], seg[:, :, :, 0:H], top[:, :, :, :], ALU.max))
                for b in range(BLOCKS):
                    for q in range(Q):
                        last = nc.vector.tensor_tensor_scan(seg[:, b, :, q], flags[:, 0, b, :], seg[:, b, :, q], -BIG, ALU.add, ALU.max)
                c.done(last)
                n_pe, n_ev = BLOCKS, BLOCKS
                nc.vector.tensor_copy(carry_in[:, :, :], seg[:, :, P - 1, :]).then_inc(s_ev, 1)
                n_ev += 1

                def chained(direction, rows, n_pe, n_ev):
                    for b in range(BLOCKS):
                        dve.wait_ge(s_pe, n_pe + b + 1)
                        last = nc.vector.tensor_copy(chain[0:rows, 0:2, b * P:(b + 1) * P],
                                                     bank[b][0:rows, 0:2 * P].rearrange("q (j k) -> q j k", j=2))
                    c.done(last)
                    way = slice(None, None, direction)
                    c.done(nc.vector.tensor_tensor_scan(chain[0:rows, 2, way], chain[0:rows, 1, way], chain[0:rows, 0, way], -BIG,
                                                        ALU.add, ALU.max))
                    edge, to, frm = (0, slice(1, None), slice(0, -1)) if direction > 0 else (STEPS_PAD - 1, slice(0, -1), slice(1, None))
                    nc.vector.memset(chain[0:rows, 3, edge:edge + 1], -BIG)
                    nc.vector.tensor_copy(chain[0:rows, 3, to], chain[0:rows, 2, frm]).then_inc(s_ev, 1)
                    dve.wait_ge(s_pe, n_pe + 2 * BLOCKS)
                    for b in range(BLOCKS):
                        last = nc.vector.tensor_copy(carry_in[:, b, 0:rows], bank[b][:, 256:256 + rows])
                    c.done(last)

                chained(1, Q, n_pe, n_ev)
                n_pe, n_ev = n_pe + 2 * BLOCKS, n_ev + 1
                for b in range(BLOCKS):
                    for q in range(Q):
                        last = nc.vector.scalar_tensor_tensor(seg[:, b, :, q], flags[:, 2, b, :], carry_in[:, b, q:q + 1], seg[:, b, :, q],
                                                              ALU.add, ALU.max)
                c.done(last)
                for b in range(BLOCKS):
                    for h in range(H):
                        last = nc.vector.tensor_tensor_scan(top[:, b, ::-1, h], flags[:, 1, b, ::-1], seg[:, b, ::-1, h], -BIG,
                                                            ALU.add, ALU.max)
                c.done(last)
                nc.vector.tensor_copy(carry_in[:, :, 0:H], top[:, :, 0, :]).then_inc(s_ev, 1)
                n_ev += 1
                chained(-1, H, n_pe, n_ev)
                n_pe, n_ev = n_pe + 2 * BLOCKS, n_ev + 1
                for b in range(BLOCKS):
                    for h in range(H):
                        last = nc.vector.scalar_tensor_tensor(top[:, b, :, h], flags[:, 3, b, :], carry_in[:, b, h:h + 1], top[:, b, :, h],
                                                              ALU.add, ALU.max)
                last.then_inc(s_want, 1)
                dve.wait_ge(s_want, 1)
                c.done(nc.vector.tensor_tensor(s_step[:, :, :, :], s_step[:, :, :, :], seg[:, :, :, H:], ALU.add))
                c.done(nc.vector.scalar_tensor_tensor(s_step[:, :, :, :], s_step[:, :, :, :], 0.2, s_step[:, :, :, :], ALU.mult, ALU.max))
                c.done(nc.vector.tensor_tensor(seg[:, :, :, 0:H], top[:, :, :, :], seg[:, :, :, H:], ALU.add))
                c.done(nc.vector.scalar_tensor_tensor(seg[:, :, :, 0:H], seg[:, :, :, 0:H], 0.2, seg[:, :, :, 0:H], ALU.mult, ALU.max))
                c.done(nc.vector.tensor_tensor(s_step[:, :, :, :], s_step[:, :, :, :], seg[:, :, :, 0:H], ALU.subtract))
                dve.wait_ge(s_top, 16)
                nc.vector.tensor_scalar(top[:, :, :, :], s_step[:, :, :, :], 0.0, None, ALU.min).then_inc(s_exp, 1)
                with dve.Fori(0, R) as r:
                    for u in range(UNROLL):
                        dve.wait_ge(s_ntop[u][0], r * 16 + (s_ntop[u][1] + 16))
                        nc.vector.tensor_tensor(node_max[:, bass.ds(r * UNROLL + u, 1), :], node_top[:, u:u + 1, :],
                                                scores[:, bass.ds(r * UNROLL + u, 1), 0:H], ALU.max).then_inc(s_nfree, 1)
                dve.wait_ge(s_nfree, UNROLL + N_TILES)
                c.done(nc.vector.tensor_tensor(node_e[:, 0], scores[:, :, 0:H], scores[:, :, H:], ALU.add))
                c.done(nc.vector.tensor_tensor(node_e[:, 1], node_max[:, :, :], scores[:, :, H:], ALU.add))
                for j in range(2):
                    c.done(nc.vector.scalar_tensor_tensor(node_e[:, j], node_e[:, j], 0.2, node_e[:, j], ALU.mult, ALU.max))
                c.done(nc.vector.tensor_tensor(node_e[:, 0], node_e[:, 0], node_e[:, 1], ALU.subtract))
                nc.vector.tensor_scalar(node_e[:, 0], node_e[:, 0], 0.0, None, ALU.min).then_inc(s_ne, 1)
                for b in range(BLOCKS):
                    dve.wait_ge(s_pe, n_pe + b + 1)
                    nc.vector.tensor_copy(weights[:, b * P:(b + 1) * P, :].rearrange("p k h -> p h k"),
                                          bank[b][:, :].rearrange("p (h k) -> p h k", h=H)).then_inc(s_ev, 1)

            @block.tensor
            def _(pe):
                ident = keep["ident"]
                pe.wait_ge(s_used, SG + STEPS_RUN)
                pe.wait_ge(s_zero, 1)
                for b in range(BLOCKS):
                    for h in range(H):
                        last = nc.tensor.transpose(bank[b][:, h * P:(h + 1) * P], by_edge[:, b * P:(b + 1) * P, h], ident[:, :])
                    last.then_inc(s_pe, 1)
                n_ev = BLOCKS + 1

                def carries(rows, direction, n_ev):
                    pe.wait_ge(s_ev, n_ev)
                    for b in range(BLOCKS):
                        nc.tensor.transpose(bank[b][0:rows, 0:P], carry_in[:, b, 0:rows], ident[:, :])
                        nc.tensor.transpose(bank[b][0:rows, P:2 * P], any_reset[:, 0 if direction > 0 else 1, b, 0:rows],
                                            ident[:, :]).then_inc(s_pe, 1)
                    pe.wait_ge(s_ev, n_ev + 1)
                    for b in range(BLOCKS):
                        nc.tensor.transpose(bank[b][:, 256:256 + rows], chain[0:rows, 3, b * P:(b + 1) * P],
                                            ident[0:rows, 0:rows]).then_inc(s_pe, 1)

                carries(Q, 1, n_ev)
                carries(H, -1, n_ev + 2)
                pe.wait_ge(s_exp, 2)
                for b in range(BLOCKS):
                    for h in range(H):
                        last = nc.tensor.transpose(bank[b][:, h * P:(h + 1) * P], top[:, b, :, h], ident[:, :])
                    last.then_inc(s_pe, 1)


def add_messages(nc, keep, gathers, tag, table, width, idx_tab, acc, weights=None, edge_weight=None):
    HALF = SLOTS // 2
    with ExitStack() as stack:
        space = Space(nc, stack, tag)
        sb, sem = space.sb, space.sem
        got = sb("got", [P, SLOTS, width])
        idx = sb("idx", [P, SLOTS], I32)
        onehot = sb("onehot", [P, SLOTS, P])
        bank = [space.ps(f"bank{u}", [P, 512]) for u in range(SLOTS)]
        s_got, s_idx, s_dummy = gathers.start(range(SLOTS)), sem("s_idx"), sem("s_dummy")
        gathers.count(range(SLOTS), STEP_ROUNDS)
        s_msg, s_sum, s_acc, s_zero = sem("s_msg"), sem("s_sum"), sem("s_acc"), sem("s_zero")
        with nc.Block() as block:

            @block.gpsimd
            def _(pool):
                with pool.Fori(0, STEP_ROUNDS) as r:
                    for q in range(2):
                        half = slice(q * HALF, (q + 1) * HALF)
                        pool.wait_ge(s_sum, r * SLOTS + (q + 1) * HALF)
                        nc.gpsimd.tensor_copy(idx[:, half], idx_tab[:, bass.ds(r * SLOTS + q * HALF, HALF)]).then_inc(s_idx, 1)
                        pool.wait_ge(s_idx, r * 2 + q + 1)
                        pool.sem_inc(s_dummy, 1)
                        for u in range(q * HALF, (q + 1) * HALF):
                            nc.gpsimd.indirect_dma_start(
                                out=got[:, u, :], out_offset=None, in_=table,
                                in_offset=bass.IndirectOffsetOnAxis(ap=idx[:, u:u + 1], axis=0)).then_inc(s_got[u][0], 16)

            @block.vector
            def _(dve):
                dve.sem_inc(s_acc, SLOTS)
                nc.vector.memset(acc[:, :, :], 0.0).then_inc(s_zero, 1)
                dve.wait_ge(s_zero, 1)

                def prepare(r, u):
                    k = bass.ds(r * SLOTS + u, 1)
                    dve.wait_ge(s_sum, r * SLOTS + u + 1)
                    if edge_weight is None:
                        nc.vector.tensor_scalar(onehot[:, u, :], keep["iota_row"][:, :], keep["dst_tab"][:, k], None, ALU.is_equal)
                    else:
                        nc.vector.tensor_scalar(onehot[:, u, :], keep["iota_row"][:, :], keep["dst_tab"][:, k], edge_weight[:, k],
                                                ALU.is_equal, ALU.mult).then_inc(s_msg, 1)

                def scale(r, u):
                    w = weights[:, bass.ds(r * SLOTS + u, 1), :].rearrange("p k h -> p (k h)")
                    dve.wait_ge(s_got[u][0], r * 16 + (s_got[u][1] + 16))
                    rows = got[:, u, 0:D].rearrange("p (h d) -> p h d", h=GAT_HEADS)
                    nc.vector.tensor_tensor(rows, rows, w.unsqueeze(2).to_broadcast([P, GAT_HEADS, GAT_DIM]), ALU.mult)
                    nc.vector.tensor_copy(got[:, u, D:], w).then_inc(s_msg, 1)

                def add(r, u, tile):
                    n = r * SLOTS + u + 1
                    dve.wait_ge(s_sum, n + SLOTS)
                    dve.wait_ge(s_acc, n + SLOTS - 1)
                    rows = acc[:, bass.ds(tile, 1), 0:width].rearrange("p t d -> p (t d)")
                    nc.vector.tensor_tensor(rows, rows, bank[u][:, 0:width], ALU.add).then_inc(s_acc, 1)

                with dve.Fori(0, STEP_ROUNDS) as r:
                    _, tiles = nc.values_load_multi_w_load_instructions(
                        keep["tile_row"][0:1, bass.ds(r * SLOTS, SLOTS)], engines=[mybir.EngineType.DVE], min_val=0,
                        max_val=LAST_TILE)
                    for u in range(SLOTS):
                        prepare(r, u)
                    for u in range(SLOTS):
                        if weights is not None:
                            scale(r, u)
                        if u >= 1:
                            add(r, u - 1, tiles[u - 1])
                    add(r, SLOTS - 1, tiles[SLOTS - 1])

            @block.tensor
            def _(pe):
                pe.sem_inc(s_sum, SLOTS)
                with pe.Fori(0, STEP_ROUNDS) as r:
                    for u in range(SLOTS):
                        n = r * SLOTS + u + 1
                        pe.wait_ge(s_msg, n)
                        pe.wait_ge(s_acc, n)
                        if weights is None:
                            pe.wait_ge(s_got[u][0], r * 16 + (s_got[u][1] + 16))
                        nc.tensor.matmul(bank[u][:, 0:width], onehot[:, u, :], got[:, u, :], start=True, stop=True).then_inc(s_sum, 1)


def gat_finish(nc, io, dram, keep, layer, hidden, acc, self_weight):
    with ExitStack() as stack:
        space = Space(nc, stack, f"gf{layer}")
        sb, sem = space.sb, space.sem
        rows = {n: sb(n, [P, D]) for n in ("b_l", "g_l", "bt_l")}
        feat = sb("feat", [P, UNROLL, PAIR, D])
        den = sb("den", [P, UNROLL, PAIR, GAT_HEADS])
        y = sb("y", [P, UNROLL, PAIR, D])
        neg = sb("neg", [P, UNROLL, PAIR, D])
        ln = Normalise(space, "ln", keep["eps"])
        names = ("s_w", "s_free", "s_self", "s_sum", "s_den", "s_den1", "s_rden", "s_y", "s_yb", "s_neg", "s_pos", "s_exp",
                 "s_elu", "s_yn", "s_yg", "s_ya")
        (s_w, s_free, s_self, s_sum, s_den, s_den1, s_rden, s_y, s_yb, s_neg, s_pos, s_exp, s_elu, s_yn, s_yg,
         s_ya) = (sem(n) for n in names)
        s_feat = space.sems("s_feat", UNROLL)
        tiles = pair_rows(dram["feat"])

        def pair(r, u):
            return bass.ds(r * (UNROLL * PAIR) + u * PAIR, PAIR)

        def heads(ap):
            return ap.rearrange("p i (h d) -> p i h d", h=GAT_HEADS)

        def spread(ap):
            return ap.unsqueeze(3).to_broadcast([P, PAIR, GAT_HEADS, GAT_DIM])

        with nc.Block() as block:

            @block.sync
            def _(sp):
                for n, t in rows.items():
                    sp.dma_start(t[:, :], rows_of(io[f"L0_gnn_{n}"][layer])).then_inc(s_w, 16)
                with sp.Fori(0, ROUNDS) as r:
                    for u in range(UNROLL):
                        sp.wait_ge(s_free, r * UNROLL + u + 1)
                        sp.dma_start(feat[:, u, :, :], tiles[:, pair(r, u), 0:D]).then_inc(s_feat[u], 16)

            @block.gpsimd
            def _(pool):
                pool.wait_ge(s_w, 48)
                with pool.Fori(0, ROUNDS) as r:
                    at = lambda u: r * UNROLL + u + 1
                    for u in range(UNROLL):
                        pool.wait_ge(s_feat[u], r * 16 + 16)
                        for i in range(PAIR):
                            t = bass.ds(r * (UNROLL * PAIR) + u * PAIR + i, 1)
                            last = nc.gpsimd.tensor_tensor(
                                feat[:, u, i].rearrange("p (h d) -> p h d", h=GAT_HEADS),
                                feat[:, u, i].rearrange("p (h d) -> p h d", h=GAT_HEADS),
                                self_weight[:, t, :].rearrange("p t h -> p (t h)").unsqueeze(2).to_broadcast([P, GAT_HEADS, GAT_DIM]),
                                ALU.mult)
                        last.then_inc(s_self, 1)
                    for u in range(UNROLL):
                        pool.wait_ge(s_self, at(u))
                        nc.gpsimd.tensor_tensor(y[:, u], feat[:, u], acc[:, pair(r, u), 0:D], ALU.add).then_inc(s_sum, 1)
                    for u in range(UNROLL):
                        pool.wait_ge(s_yn, at(u))
                        nc.gpsimd.tensor_tensor(y[:, u], y[:, u], both(rows["g_l"][:, :]), ALU.mult).then_inc(s_yg, 1)
                    for u in range(UNROLL):
                        pool.wait_ge(s_yg, at(u))
                        nc.gpsimd.tensor_tensor(y[:, u], y[:, u], both(rows["bt_l"][:, :]), ALU.add).then_inc(s_ya, 1)

            @block.vector
            def _(dve):
                dve.sem_inc(s_free, UNROLL)
                dve.wait_ge(s_w, 48)
                with dve.Fori(0, ROUNDS) as r:
                    at = lambda u: r * UNROLL + u + 1
                    for u in range(UNROLL):
                        dve.wait_ge(s_free, at(u))
                        nc.vector.tensor_tensor(den[:, u], acc[:, pair(r, u), D:], self_weight[:, pair(r, u), :], ALU.add).then_inc(s_den, 1)
                    for u in range(UNROLL):
                        dve.wait_ge(s_den, at(u))
                        nc.vector.tensor_scalar(den[:, u], den[:, u], 1e-16, None, ALU.add).then_inc(s_den1, 1)
                    for u in range(UNROLL):
                        dve.wait_ge(s_den1, at(u))
                        nc.vector.reciprocal(den[:, u], den[:, u]).then_inc(s_rden, 1)
                    for u in range(UNROLL):
                        dve.wait_ge(s_rden, at(u))
                        dve.wait_ge(s_sum, at(u))
                        nc.vector.tensor_tensor(heads(y[:, u]), heads(y[:, u]), spread(den[:, u]), ALU.mult).then_inc(s_y, 1)
                    for u in range(UNROLL):
                        dve.wait_ge(s_y, at(u))
                        nc.vector.tensor_tensor(y[:, u], y[:, u], both(rows["b_l"][:, :]), ALU.add).then_inc(s_yb, 1)
                    for u in range(UNROLL):
                        dve.wait_ge(s_yb, at(u))
                        nc.vector.tensor_scalar(neg[:, u], y[:, u], 0.0, None, ALU.min).then_inc(s_neg, 1)
                    for u in range(UNROLL):
                        nc.vector.tensor_scalar(y[:, u], y[:, u], 0.0, -1.0, ALU.max, ALU.add).then_inc(s_pos, 1)
                    for u in range(UNROLL):
                        dve.wait_ge(s_exp, at(u))
                        dve.wait_ge(s_pos, at(u))
                        nc.vector.tensor_tensor(y[:, u], y[:, u], neg[:, u], ALU.add).then_inc(s_elu, 1)
                    for u in range(UNROLL):
                        dve.wait_ge(s_elu, at(u))
                        ln.statistics(nc, u, at(u), y[:, u])
                    for u in range(UNROLL):
                        ln.aggregate(nc, u, at(u))
                    for u in range(UNROLL):
                        ln.invert(nc, u, at(u))
                    for u in range(UNROLL):
                        ln.scale(nc, u, at(u), y[:, u], y[:, u]).then_inc(s_yn, 1)
                    for u in range(UNROLL):
                        dve.wait_ge(s_ya, at(u))
                        nc.vector.tensor_tensor(hidden[:, pair(r, u), :], hidden[:, pair(r, u), :], y[:, u], ALU.add).then_inc(s_free, 1)

            @block.scalar
            def _(act):
                with act.Fori(0, ROUNDS) as r:
                    at = lambda u: r * UNROLL + u + 1
                    for u in range(UNROLL):
                        act.wait_ge(s_neg, at(u))
                        nc.scalar.activation(neg[:, u], neg[:, u], ACT.Exp).then_inc(s_exp, 1)
                    for u in range(UNROLL):
                        ln.root(nc, u, at(u))


def pair_of(r, u):
    return bass.ds(r * (UNROLL * PAIR) + u * PAIR, PAIR)


def units(r):
    return [(u, r * UNROLL + u + 1) for u in range(UNROLL)]


def linear_attention_sums(nc, io, dram, keep, cfg, kv_sum):
    with ExitStack() as stack:
        space = Space(nc, stack, cfg["tag"] + "a")
        sb, sem = space.sb, space.sem
        wk, wv = sb("wk", [P, HALVES, D]), sb("wv", [P, HALVES, D])
        raw = sb("raw", [P, 4, D])
        bk, bv = sb("bk", [P, D]), sb("bv", [P, D])
        x = sb("x", [P, UNROLL, PAIR, D])
        xt = sb("xt", [P, UNROLL, HALVES, PAIR * P])
        k = sb("k", [P, UNROLL, PAIR, D])
        neg = sb("neg", [P, UNROLL, PAIR, D])
        v = sb("v", [P, UNROLL, PAIR, D])
        va = sb("va", [P, UNROLL, PAIR, HALVES, P + 1])
        bank = [space.ps(f"bank{u}", [P, 512]) for u in range(UNROLL)]
        ln = Normalise(space, "ln", keep["eps"])
        s_x = space.sems("s_x", UNROLL)
        (s_w, s_free, s_xn, s_xt, s_xtc, s_k, s_kb, s_neg, s_exp, s_phi, s_v, s_vb, s_va, s_kv, s_zero, s_turn, s_turned) = (
            sem(n) for n in ("s_w", "s_free", "s_xn", "s_xt", "s_xtc", "s_k", "s_kb", "s_neg", "s_exp", "s_phi", "s_v", "s_vb",
                             "s_va", "s_kv", "s_zero", "s_turn", "s_turned"))
        tiles = pair_rows(cfg["x"])
        turned = cfg["Wqkv"] is not None
        n_w = 1 if turned else 4

        with nc.Block() as block:

            @block.sync
            def _(sp):
                if turned:
                    sp.dma_start(raw[:, :, :], cfg["Wqkv"][D:3 * D, :].rearrange("(b p) i -> p b i", p=P)).then_inc(s_w, 16)
                else:
                    sp.dma_start(wk[:, :, :], cfg["Wk"].rearrange("(a p) n -> p a n", p=P)).then_inc(s_w, 16)
                    sp.dma_start(wv[:, :, :], cfg["Wv"].rearrange("(a p) n -> p a n", p=P)).then_inc(s_w, 16)
                    sp.dma_start(bk[:, :], rows_of(cfg["bk"])).then_inc(s_w, 16)
                    sp.dma_start(bv[:, :], rows_of(cfg["bv"])).then_inc(s_w, 16)
                with sp.Fori(0, ROUNDS) as r:
                    for u, n in units(r):
                        sp.wait_ge(s_free, n)
                        sp.dma_start(x[:, u, :, :], tiles[:, pair_of(r, u), :]).then_inc(s_x[u], 16)

            @block.vector
            def _(dve):
                dve.sem_inc(s_free, UNROLL)
                if turned:
                    nc.vector.memset(bk[:, :], 0.0)
                    nc.vector.memset(bv[:, :], 0.0)
                nc.vector.memset(kv_sum[:, :, :], 0.0).then_inc(s_zero, 1)
                dve.wait_ge(s_zero, 1)
                dve.wait_ge(s_w, 16 * n_w)
                with dve.Fori(0, ROUNDS) as r:
                    for u, n in units(r):
                        dve.wait_ge(s_x[u], r * 16 + 16)
                        ln.statistics(nc, u, n, x[:, u])
                    for u, n in units(r):
                        ln.aggregate(nc, u, n)
                    for u, n in units(r):
                        ln.invert(nc, u, n)
                    for u, n in units(r):
                        ln.scale(nc, u, n, x[:, u], x[:, u]).then_inc(s_xn, 1)
                    for u, n in units(r):
                        dve.wait_ge(s_k, n)
                        nc.vector.tensor_tensor(k[:, u], bank[u][:, :].rearrange("p (i d) -> p i d", i=PAIR), both(bk[:, :]),
                                                ALU.add).then_inc(s_kb, 1)
                    for u, n in units(r):
                        dve.wait_ge(s_kb, n)
                        nc.vector.tensor_scalar(neg[:, u], k[:, u], 0.0, None, ALU.min).then_inc(s_neg, 1)
                    for u, n in units(r):
                        dve.wait_ge(s_v, n)
                        nc.vector.tensor_tensor(v[:, u], bank[u][:, :].rearrange("p (i d) -> p i d", i=PAIR), both(bv[:, :]),
                                                ALU.add).then_inc(s_vb, 1)
                    for u, n in units(r):
                        dve.wait_ge(s_exp, n)
                        nc.vector.scalar_tensor_tensor(k[:, u], k[:, u], 0.0, neg[:, u], ALU.max, ALU.add).then_inc(s_phi, 1)
                    for u, n in units(r):
                        dve.wait_ge(s_kv, n)
                        dve.wait_ge(s_free, n + UNROLL - 1)
                        nc.vector.tensor_tensor(kv_sum[:, :, :], kv_sum[:, :, :],
                                                bank[u][:, 0:HALVES * (P + 1)].rearrange("p (a d) -> p a d", a=HALVES),
                                                ALU.add).then_inc(s_free, 1)

            @block.scalar
            def _(act):
                if turned:
                    for j in range(4):
                        act.wait_ge(s_turn, j + 1)
                        w, a = (wk, wv)[j // 2], j % 2
                        nc.scalar.copy(w[:, :, a * P:(a + 1) * P], bank[j][:, 0:2 * P].rearrange("p (k n) -> p k n", k=HALVES)).then_inc(s_turned, 1)
                with act.Fori(0, ROUNDS) as r:
                    for u, n in units(r):
                        ln.root(nc, u, n)
                    for u, n in units(r):
                        act.wait_ge(s_xt, n)
                        nc.scalar.copy(xt[:, u].rearrange("p a n -> p (a n)"), bank[u][:, :]).then_inc(s_xtc, 1)
                    for u, n in units(r):
                        act.wait_ge(s_neg, n)
                        nc.scalar.activation(neg[:, u], neg[:, u], ACT.Exp).then_inc(s_exp, 1)
                    for u, n in units(r):
                        act.wait_ge(s_vb, n)
                        for i in range(PAIR):
                            mask = keep["mask"][:, bass.ds(r * (UNROLL * PAIR) + u * PAIR + i, 1)]
                            nc.scalar.activation(va[:, u, i, :, 0:P], v[:, u, i, :].rearrange("p (a d) -> p a d", a=HALVES), ACT.Copy,
                                                 scale=mask)
                            last = nc.scalar.copy(va[:, u, i, :, P:P + 1], mask.unsqueeze(1).to_broadcast([P, HALVES, 1]))
                        last.then_inc(s_va, 1)

            @block.tensor
            def _(pe):
                pe.wait_ge(s_w, 16 * n_w)
                if turned:
                    for j in range(4):
                        for h in range(HALVES):
                            last = nc.tensor.transpose(bank[j][:, h * P:(h + 1) * P], raw[:, j, h * P:(h + 1) * P], keep["ident"][:, :])
                        last.then_inc(s_turn, 1)
                    pe.wait_ge(s_turned, 4)
                with pe.Fori(0, ROUNDS) as r:
                    for u, n in units(r):
                        pe.wait_ge(s_xn, n)
                        transpose_pair(nc, bank[u], x[:, u], keep["ident"]).then_inc(s_xt, 1)
                    for u, n in units(r):
                        pe.wait_ge(s_xtc, n)
                        project_pair(nc, bank[u], xt[:, u], wk).then_inc(s_k, 1)
                    for u, n in units(r):
                        pe.wait_ge(s_kb, n)
                        project_pair(nc, bank[u], xt[:, u], wv).then_inc(s_v, 1)
                    for u, n in units(r):
                        pe.wait_ge(s_phi, n)
                        pe.wait_ge(s_va, n)
                        for a in range(HALVES):
                            for i in range(PAIR):
                                last = nc.tensor.matmul(bank[u][:, a * (P + 1):(a + 1) * (P + 1)], k[:, u, i, a * P:(a + 1) * P],
                                                        va[:, u, i, a, :], start=(i == 0), stop=(i == PAIR - 1))
                        last.then_inc(s_kv, 1)


def linear_attention(nc, io, dram, keep, cfg, kv_sum, added=None):
    ff = cfg["ff"]
    NF = ff // P
    turned = cfg["Wqkv"] is not None
    has_out = cfg["Wo"] is not None
    ACT_FF = ACT.Gelu if turned else ACT.Relu
    with ExitStack() as stack:
        space = Space(nc, stack, cfg["tag"] + "b")
        sb, sem = space.sb, space.sem
        wq, w1, w2 = sb("wq", [P, HALVES, D]), sb("w1", [P, HALVES, ff]), sb("w2", [P, NF, D])
        wo = sb("wo", [P, HALVES, D])
        raw = sb("raw", [P, 6, D])
        bq, b1 = sb("bq", [P, HALVES]), sb("b1", [P, NF])
        rows = {n: sb(n, [P, D]) for n in ("bo", "b2", "ln1_g", "ln1_b", "ln2_g", "ln2_b")}
        kv = sb("kv", [P, HALVES, P])
        ks = sb("ks", [P, HALVES, 4])
        x = sb("x", [P, UNROLL, PAIR, D])
        xn = sb("xn", [P, UNROLL, PAIR, D])
        xt = sb("xt", [P, UNROLL, HALVES, PAIR * P])
        neg = sb("neg", [P, UNROLL, HALVES, PAIR * P])
        y = sb("y", [P, UNROLL, PAIR, D])
        z = sb("z", [P, UNROLL, PAIR * 8])
        fft = sb("fft", [P, UNROLL, NF, PAIR * P])
        bank = [space.ps(f"bank{u}", [P, 512]) for u in range(UNROLL)]
        ln0, ln1, ln2 = (Normalise(space, f"ln{i}", keep["eps"]) for i in range(3))
        s_x, s_sent = space.sems("s_x", UNROLL), space.sems("s_sent", UNROLL)
        (s_w, s_free, s_xn, s_xt, s_xtc, s_q, s_neg, s_pos, s_exp, s_phi, s_den, s_z0, s_z, s_num, s_att, s_att_t, s_att_c, s_o,
         s_ob, s_y, s_yn, s_yg, s_y1, s_y1t, s_y1c, s_ff, s_ffc, s_o2, s_o2b, s_y2, s_y2n, s_y2g, s_y2a, s_add, s_kv, s_turn,
         s_turned, s_done) = (
            sem(n) for n in ("s_w", "s_free", "s_xn", "s_xt", "s_xtc", "s_q", "s_neg", "s_pos", "s_exp", "s_phi", "s_den", "s_z0",
                             "s_z", "s_num", "s_att", "s_att_t", "s_att_c", "s_o", "s_ob", "s_y", "s_yn", "s_yg", "s_y1", "s_y1t",
                             "s_y1c", "s_ff", "s_ffc", "s_o2", "s_o2b", "s_y2", "s_y2n", "s_y2g", "s_y2a", "s_add", "s_kv",
                             "s_turn", "s_turned", "s_done"))
        tiles, out_tiles = pair_rows(cfg["x"]), pair_rows(cfg["out"])
        FF_ROUNDS = NF // 2
        loads = []
        if turned:
            loads += [(raw[:, 0:2], cfg["Wqkv"][0:D, :].rearrange("(b p) i -> p b i", p=P)),
                      (raw[:, 2:4], cfg["W1"].rearrange("(b p) i -> p b i", p=P)),
                      (raw[:, 4:6], cfg["W2"].rearrange("(b p) i -> p b i", p=P))]
        else:
            loads += [(wq[:, :, :], cfg["Wq"].rearrange("(a p) n -> p a n", p=P)),
                      (w1[:, :, :], cfg["W1"].rearrange("(a p) n -> p a n", p=P)),
                      (w2[:, :, :], cfg["W2"].rearrange("(a p) n -> p a n", p=P)),
                      (wo[:, :, :], cfg["Wo"].rearrange("(a p) n -> p a n", p=P)),
                      (bq[:, :], cfg["bq"].rearrange("(a p) -> p a", p=P)),
                      (rows["bo"][:, :], rows_of(cfg["bo"]))]
        loads += [(b1[:, :], cfg["b1"].rearrange("(a p) -> p a", p=P))]
        loads += [(rows[n][:, :], rows_of(cfg[n])) for n in ("b2", "ln1_g", "ln1_b", "ln2_g", "ln2_b")]

        def node_rows(u):
            return bank[u][:, :].rearrange("p (i d) -> p i d", i=PAIR)

        def by_head(ap):
            return ap.rearrange("p i (h d) -> p (i h) d", d=32)

        with nc.Block() as block:

            @block.sync
            def _(sp):
                with nc.allow_non_contiguous_dma(reason="biases by partition"):
                    for to, frm in loads:
                        sp.dma_start(to, frm).then_inc(s_w, 16)
                with sp.Fori(0, ROUNDS) as r:
                    for u, n in units(r):
                        sp.wait_ge(s_free, n)
                        sp.dma_start(x[:, u, :, :], tiles[:, pair_of(r, u), :]).then_inc(s_x[u], 16)
                    for u, n in units(r):
                        sp.wait_ge(s_done, n)
                        sp.dma_start(out_tiles[:, pair_of(r, u), :], x[:, u, :, :]).then_inc(s_sent[u], 16)
                    for u, n in units(r):
                        sp.wait_ge(s_sent[u], r * 16 + 16)
                        sp.sem_inc(s_free, 1)

            @block.vector
            def _(dve):
                dve.sem_inc(s_free, UNROLL)
                if turned:
                    nc.vector.memset(bq[:, :], 0.0)
                dve.wait_ge(s_w, 16 * len(loads))
                for a in range(HALVES):
                    nc.vector.tensor_tensor(kv[:, a, :], kv_sum[:, a, 0:P], keep["same_head"][:, :], ALU.mult)
                    last = nc.vector.tensor_scalar(ks[:, a, :], keep["head_of"][:, :], kv_sum[:, a, P:P + 1], None, ALU.mult)
                last.then_inc(s_kv, 1)
                with dve.Fori(0, ROUNDS) as r:
                    for u, n in units(r):
                        dve.wait_ge(s_x[u], r * 16 + 16)
                        ln0.statistics(nc, u, n, x[:, u])
                    for u, n in units(r):
                        ln0.aggregate(nc, u, n)
                    for u, n in units(r):
                        ln0.invert(nc, u, n)
                    for u, n in units(r):
                        ln0.scale(nc, u, n, xn[:, u], x[:, u]).then_inc(s_xn, 1)
                    for u, n in units(r):
                        dve.wait_ge(s_q, n)
                        for a in range(HALVES):
                            last = nc.vector.tensor_scalar(neg[:, u, a], bank[u][:, a * D:(a + 1) * D], bq[:, a:a + 1], 0.0, ALU.add,
                                                           ALU.min)
                        last.then_inc(s_neg, 1)
                        for a in range(HALVES):
                            last = nc.vector.tensor_scalar(xt[:, u, a], bank[u][:, a * D:(a + 1) * D], bq[:, a:a + 1], 0.0, ALU.add,
                                                           ALU.max)
                        last.then_inc(s_pos, 1)
                    for u, n in units(r):
                        dve.wait_ge(s_exp, n)
                        dve.wait_ge(s_pos, n)
                        nc.vector.tensor_tensor(xt[:, u], xt[:, u], neg[:, u], ALU.add).then_inc(s_phi, 1)
                    for u, n in units(r):
                        dve.wait_ge(s_den, n)
                        nc.vector.tensor_scalar(z[:, u, :], bank[u][:, 0:PAIR * 8], 1e-6, None, ALU.add).then_inc(s_z0, 1)
                    for u, n in units(r):
                        dve.wait_ge(s_z0, n)
                        nc.vector.reciprocal(z[:, u, :], z[:, u, :]).then_inc(s_z, 1)
                    for u, n in units(r):
                        dve.wait_ge(s_num, n)
                        dve.wait_ge(s_z, n)
                        nc.vector.tensor_tensor(by_head(y[:, u]), by_head(node_rows(u)),
                                                z[:, u, :].unsqueeze(2).to_broadcast([P, PAIR * 8, 32]), ALU.mult).then_inc(s_att, 1)
                    if has_out:
                        for u, n in units(r):
                            dve.wait_ge(s_o, n)
                            nc.vector.tensor_tensor(y[:, u], node_rows(u), both(rows["bo"][:, :]), ALU.add).then_inc(s_ob, 1)
                    for u, n in units(r):
                        dve.wait_ge(s_ob if has_out else s_att, n)
                        nc.vector.tensor_tensor(y[:, u], y[:, u], xn[:, u], ALU.add).then_inc(s_y, 1)
                    for u, n in units(r):
                        dve.wait_ge(s_y, n)
                        ln1.statistics(nc, u, n, y[:, u])
                    for u, n in units(r):
                        ln1.aggregate(nc, u, n)
                    for u, n in units(r):
                        ln1.invert(nc, u, n)
                    for u, n in units(r):
                        ln1.scale(nc, u, n, y[:, u], y[:, u]).then_inc(s_yn, 1)
                    for u, n in units(r):
                        dve.wait_ge(s_o2, n)
                        nc.vector.tensor_tensor(xn[:, u], node_rows(u), both(rows["b2"][:, :]), ALU.add).then_inc(s_o2b, 1)
                    for u, n in units(r):
                        dve.wait_ge(s_o2b, n)
                        nc.vector.tensor_tensor(y[:, u], y[:, u], xn[:, u], ALU.add).then_inc(s_y2, 1)
                    for u, n in units(r):
                        dve.wait_ge(s_y2, n)
                        ln2.statistics(nc, u, n, y[:, u])
                    for u, n in units(r):
                        ln2.aggregate(nc, u, n)
                    for u, n in units(r):
                        ln2.invert(nc, u, n)
                    for u, n in units(r):
                        ln2.scale(nc, u, n, y[:, u], y[:, u]).then_inc(s_y2n, 1)
                    if added is not None:
                        for u, n in units(r):
                            nc.vector.tensor_tensor(x[:, u], x[:, u], added[:, pair_of(r, u), 0:D], ALU.add).then_inc(s_add, 1)
                    for u, n in units(r):
                        dve.wait_ge(s_y2a, n)
                        if added is not None:
                            dve.wait_ge(s_add, n)
                        nc.vector.tensor_tensor(x[:, u], x[:, u], y[:, u], ALU.add).then_inc(s_done, 1)

            @block.gpsimd
            def _(pool):
                pool.wait_ge(s_w, 16 * len(loads))
                with pool.Fori(0, ROUNDS) as r:
                    for s_in, g, s_mid, b, s_out in ((s_yn, "ln1_g", s_yg, "ln1_b", s_y1), (s_y2n, "ln2_g", s_y2g, "ln2_b", s_y2a)):
                        for u, n in units(r):
                            pool.wait_ge(s_in, n)
                            nc.gpsimd.tensor_tensor(y[:, u], y[:, u], both(rows[g][:, :]), ALU.mult).then_inc(s_mid, 1)
                            pool.wait_ge(s_mid, n)
                            nc.gpsimd.tensor_tensor(y[:, u], y[:, u], both(rows[b][:, :]), ALU.add).then_inc(s_out, 1)

            @block.scalar
            def _(act):
                if turned:
                    for j in range(6):
                        w, a = (wq, w1, w2)[j // 2], j % 2
                        act.wait_ge(s_turn, j + 1)
                        nc.scalar.copy(w[:, :, a * P:(a + 1) * P], bank[j % UNROLL][:, 0:2 * P].rearrange("p (k n) -> p k n", k=HALVES)).then_inc(s_turned, 1)
                with act.Fori(0, ROUNDS) as r:
                    for u, n in units(r):
                        ln0.root(nc, u, n)
                    for u, n in units(r):
                        act.wait_ge(s_xt, n)
                        nc.scalar.copy(xt[:, u].rearrange("p a n -> p (a n)"), bank[u][:, :]).then_inc(s_xtc, 1)
                    for u, n in units(r):
                        act.wait_ge(s_neg, n)
                        nc.scalar.activation(neg[:, u], neg[:, u], ACT.Exp).then_inc(s_exp, 1)
                    if has_out:
                        for u, n in units(r):
                            act.wait_ge(s_att_t, n)
                            nc.scalar.copy(xt[:, u].rearrange("p a n -> p (a n)"), bank[u][:, :]).then_inc(s_att_c, 1)
                    for u, n in units(r):
                        ln1.root(nc, u, n)
                    for u, n in units(r):
                        act.wait_ge(s_y1t, n)
                        nc.scalar.copy(xt[:, u].rearrange("p a n -> p (a n)"), bank[u][:, :]).then_inc(s_y1c, 1)
                    for f in range(FF_ROUNDS):
                        for u, n in units(r):
                            act.wait_ge(s_ff, r * (UNROLL * FF_ROUNDS) + (f * UNROLL + u + 1))
                            for j in range(2):
                                c = 2 * f + j
                                last = nc.scalar.activation(fft[:, u, c], bank[u][:, j * D:(j + 1) * D], ACT_FF, bias=b1[:, c:c + 1])
                            last.then_inc(s_ffc, 1)
                    for u, n in units(r):
                        ln2.root(nc, u, n)

            @block.tensor
            def _(pe):
                pe.wait_ge(s_w, 16 * len(loads))
                if turned:
                    for j in range(6):
                        if j >= UNROLL:
                            pe.wait_ge(s_turned, j - UNROLL + 1)
                        for h in range(HALVES):
                            last = nc.tensor.transpose(bank[j % UNROLL][:, h * P:(h + 1) * P], raw[:, j, h * P:(h + 1) * P], keep["ident"][:, :])
                        last.then_inc(s_turn, 1)
                    pe.wait_ge(s_turned, 6)
                pe.wait_ge(s_kv, 1)
                with pe.Fori(0, ROUNDS) as r:
                    for u, n in units(r):
                        pe.wait_ge(s_xn, n)
                        transpose_pair(nc, bank[u], xn[:, u], keep["ident"]).then_inc(s_xt, 1)
                    for u, n in units(r):
                        pe.wait_ge(s_xtc, n)
                        for a in range(HALVES):
                            for k in range(HALVES):
                                last = nc.tensor.matmul(bank[u][:, a * D:(a + 1) * D], wq[:, k, a * P:(a + 1) * P], xt[:, u, k, :],
                                                        start=(k == 0), stop=(k == HALVES - 1))
                        last.then_inc(s_q, 1)
                    for u, n in units(r):
                        pe.wait_ge(s_phi, n)
                        for i in range(PAIR):
                            for a in range(HALVES):
                                c = 8 * i + 4 * a
                                last = nc.tensor.matmul(bank[u][:, c:c + 4], xt[:, u, a, i * P:(i + 1) * P], ks[:, a, :], start=True, stop=True)
                        last.then_inc(s_den, 1)
                    for u, n in units(r):
                        pe.wait_ge(s_z0, n)
                        for i in range(PAIR):
                            for a in range(HALVES):
                                c = i * D + a * P
                                last = nc.tensor.matmul(bank[u][:, c:c + P], xt[:, u, a, i * P:(i + 1) * P], kv[:, a, :], start=True, stop=True)
                        last.then_inc(s_num, 1)
                    if has_out:
                        for u, n in units(r):
                            pe.wait_ge(s_att, n)
                            transpose_pair(nc, bank[u], y[:, u], keep["ident"]).then_inc(s_att_t, 1)
                        for u, n in units(r):
                            pe.wait_ge(s_att_c, n)
                            project_pair(nc, bank[u], xt[:, u], wo).then_inc(s_o, 1)
                    for u, n in units(r):
                        pe.wait_ge(s_y1, n)
                        transpose_pair(nc, bank[u], y[:, u], keep["ident"]).then_inc(s_y1t, 1)
                    for f in range(FF_ROUNDS):
                        for u, n in units(r):
                            if f == 0:
                                pe.wait_ge(s_y1c, n)
                            else:
                                pe.wait_ge(s_ffc, r * (UNROLL * FF_ROUNDS) + ((f - 1) * UNROLL + u + 1))
                            for j in range(2):
                                c = 2 * f + j
                                for k in range(HALVES):
                                    last = nc.tensor.matmul(bank[u][:, j * D:(j + 1) * D], w1[:, k, c * P:(c + 1) * P], xt[:, u, k, :],
                                                            start=(k == 0), stop=(k == HALVES - 1))
                            last.then_inc(s_ff, 1)
                    for u, n in units(r):
                        pe.wait_ge(s_ffc, r * (UNROLL * FF_ROUNDS) + ((FF_ROUNDS - 1) * UNROLL + u + 1))
                        for i in range(PAIR):
                            for c in range(NF):
                                last = nc.tensor.matmul(bank[u][:, i * D:(i + 1) * D], fft[:, u, c, i * P:(i + 1) * P], w2[:, c, :],
                                                        start=(c == 0), stop=(c == NF - 1))
                        last.then_inc(s_o2, 1)


def relation_features(nc, io, dram, keep):
    B, SUB = 8, 32
    with ExitStack() as stack:
        space = Space(nc, stack, "rel")
        sb, sem = space.sb, space.sem
        w = sb("w", [P, HALVES, REL, P])
        x = sb("x", [P, UNROLL, PAIR, D])
        xt = sb("xt", [P, UNROLL, HALVES, PAIR * P])
        out = sb("out", [P, UNROLL, PAIR, REL, D])
        bank = [space.ps(f"bank{u}", [P, 512]) for u in range(8)]
        ln = Normalise(space, "ln", keep["eps"])
        s_x, s_sent = space.sems("s_x", UNROLL), space.sems("s_sent", UNROLL)
        s_w, s_free, s_xn, s_xt, s_xtc, s_mm, s_dve, s_act, s_zero = (
            sem(n) for n in ("s_w", "s_free", "s_xn", "s_xt", "s_xtc", "s_mm", "s_dve", "s_act", "s_zero"))
        tiles = pair_rows(dram["x2"])
        to = dram["rel_feat"].rearrange("(r t p) d -> p t r d", r=REL, p=P)
        pieces = [(i, a, g) for i in range(PAIR) for a in range(HALVES) for g in range(2)]

        def landing(u, p):
            i, a, g = pieces[p]
            return out[:, u, i, 4 * g:4 * g + 4, a * P:(a + 1) * P]

        def product(p):
            return bank[p % 4][:, :].rearrange("p (r o) -> p r o", r=4)

        with nc.Block() as block:

            @block.sync
            def _(sp):
                sp.wait_ge(s_zero, 1)
                weight = io["L1_gnn_weight"].rearrange("r (b i o) -> b i r o", b=B, i=SUB)
                for b in range(B):
                    lo = (b % 4) * SUB
                    sp.dma_start(w[lo:lo + SUB, b // 4, :, lo:lo + SUB], weight[b]).then_inc(s_w, 16)
                with sp.Fori(0, ROUNDS) as r:
                    for u, n in units(r):
                        sp.wait_ge(s_free, n)
                        sp.dma_start(x[:, u, :, :], tiles[:, pair_of(r, u), :]).then_inc(s_x[u], 16)
                    for u, n in units(r):
                        sp.wait_ge(s_dve, r * (4 * UNROLL) + (4 * u + 4 + 2))
                        sp.wait_ge(s_act, r * (4 * UNROLL) + (4 * u + 4 + 2))
                        for i in range(PAIR):
                            sp.dma_start(to[:, bass.ds(r * (UNROLL * PAIR) + u * PAIR + i, 1), :, :].rearrange("p t r d -> p (t r) d"),
                                         out[:, u, i, :, :]).then_inc(s_sent[u], 16)
                    for u, n in units(r):
                        sp.wait_ge(s_sent[u], r * 32 + 32)
                        sp.sem_inc(s_free, 1)

            @block.vector
            def _(dve):
                dve.sem_inc(s_free, UNROLL)
                dve.sem_inc(s_dve, 2)
                nc.vector.memset(w[:, :, :, :], 0.0).then_inc(s_zero, 1)
                with dve.Fori(0, ROUNDS) as r:
                    for u, n in units(r):
                        dve.wait_ge(s_x[u], r * 16 + 16)
                        ln.statistics(nc, u, n, x[:, u])
                    for u, n in units(r):
                        ln.aggregate(nc, u, n)
                    for u, n in units(r):
                        ln.invert(nc, u, n)
                    for u, n in units(r):
                        ln.scale(nc, u, n, x[:, u], x[:, u]).then_inc(s_xn, 1)
                    for u, n in units(r):
                        dve.wait_ge(s_free, n)
                        for p in range(0, 8, 2):
                            dve.wait_ge(s_mm, r * (8 * UNROLL) + (8 * u + p + 1))
                            nc.vector.tensor_copy(landing(u, p), product(p)).then_inc(s_dve, 1)

            @block.scalar
            def _(act):
                act.sem_inc(s_act, 2)
                with act.Fori(0, ROUNDS) as r:
                    for u, n in units(r):
                        ln.root(nc, u, n)
                    for u, n in units(r):
                        act.wait_ge(s_xt, n)
                        nc.scalar.copy(xt[:, u].rearrange("p a n -> p (a n)"), bank[4 + u % 4][:, :]).then_inc(s_xtc, 1)
                    for u, n in units(r):
                        act.wait_ge(s_free, n)
                        for p in range(1, 8, 2):
                            act.wait_ge(s_mm, r * (8 * UNROLL) + (8 * u + p + 1))
                            nc.scalar.copy(landing(u, p), product(p)).then_inc(s_act, 1)

            @block.tensor
            def _(pe):
                pe.wait_ge(s_w, 16 * B)
                with pe.Fori(0, ROUNDS) as r:
                    for u, n in units(r):
                        pe.wait_ge(s_xn, n)
                        if u >= 4:
                            pe.wait_ge(s_xtc, n - 4)
                        transpose_pair(nc, bank[4 + u % 4], x[:, u], keep["ident"]).then_inc(s_xt, 1)
                    for u, n in units(r):
                        pe.wait_ge(s_xtc, n)
                        for p, (i, a, g) in enumerate(pieces):
                            pe.wait_ge((s_dve, s_act)[p % 2], r * (4 * UNROLL) + (4 * u + p // 2 + 1))
                            nc.tensor.matmul(bank[p % 4][:, :], xt[:, u, a, i * P:(i + 1) * P],
                                             w[:, a, 4 * g:4 * g + 4, :].rearrange("p r o -> p (r o)"), start=True, stop=True).then_inc(s_mm, 1)


def mix_cfg(io, dram, layer):
    names = ["W1", "b1", "W2", "b2", "ln1_g", "ln1_b", "ln2_g", "ln2_b"]
    names += ["Wqkv"] if layer else ["Wq", "Wk", "Wv", "bq", "bk", "bv", "Wo", "bo"]
    cfg = {"Wqkv": None, "Wo": None} | {n: io[f"L{layer}_mix_{n}"] for n in names}
    x, out, ff = (("x0", "x1", L0_FF), ("x2", "x3", L1_FF))[layer]
    return cfg | {"tag": f"mix{layer}", "x": dram[x], "out": dram[out], "ff": ff}


def expert_mixture(nc, io, dram, keep, hidden):
    E = MOE_E
    EPS = 1e-3
    with ExitStack() as stack:
        space = Space(nc, stack, "moe")
        sb, sem = space.sb, space.sem
        w = [sb(f"w{j}", [P, E, HALVES, D]) for j in range(3)]
        wr = sb("wr", [P, HALVES, E])
        br = sb("br", [P, E])
        bo = sb("bo", [E, D])
        par_rows = sb("par_rows", [E * HALVES, 2, 5, P])
        par = sb("par", [P, 2, 5, E * HALVES])
        gain, shift = sb("gain", [P, 2, E * HALVES]), sb("shift", [P, 2, E * HALVES])
        bn_eps = sb("bn_eps", [P, 1])
        x = sb("x", [P, 2, PAIR, D])
        h = sb("h", [P, 2, PAIR, D])
        xn = sb("xn", [P, 2, PAIR, D])
        xt = sb("xt", [P, HALVES, PAIR * P])
        h1, h2 = sb("h1", [P, 2, HALVES, PAIR * P]), sb("h2", [P, 2, HALVES, PAIR * P])
        logit = sb("logit", [P, PAIR, E])
        top = sb("top", [P, PAIR])
        gate = sb("gate", [P, 2, PAIR, E])
        gate_t = sb("gate_t", [E, PAIR, P])
        bank1 = [space.ps(f"first{i}", [P, 512]) for i in range(2)]
        bank2 = [space.ps(f"second{i}", [P, 512]) for i in range(2)]
        bank3 = [space.ps(f"third{i}", [P, 512]) for i in range(2)]
        bank_x, bank_g = space.ps("turn", [P, 512]), space.ps("route", [P, 512])
        stats, mv = sb("stats", [P, PAIR, 6]), sb("mv", [P, PAIR, 2])
        std = sb("std", [P, PAIR])
        s_x, s_sent = space.sems("s_x", 2), space.sems("s_sent", 2)
        (s_w, s_free, s_dve, s_std_in, s_std, s_xn, s_xt, s_xtc, s_l1, s_h1, s_l2, s_h2, s_l3, s_acc, s_route, s_logit, s_exp, s_gate,
         s_turn, s_gate_t, s_bias, s_done, s_var, s_par, s_root, s_scale) = (
            sem(n) for n in ("s_w", "s_free", "s_dve", "s_std_in", "s_std", "s_xn", "s_xt", "s_xtc", "s_l1", "s_h1", "s_l2", "s_h2",
                             "s_l3", "s_acc", "s_route", "s_logit", "s_exp", "s_gate", "s_turn", "s_gate_t", "s_bias", "s_done",
                             "s_var", "s_par", "s_root", "s_scale"))
        tiles, out_tiles = pair_rows(dram["x1"]), pair_rows(dram["x2"])
        loads = [(w[j][:, :, :, :], io[f"L0_ffn_{n}"].rearrange("e (a p) n -> p e a n", p=P)) for j, n in enumerate(("W1", "W2", "Wo"))]
        loads += [(wr[:, :, :], io["L0_ffn_Wr"].rearrange("(a p) e -> p a e", p=P)), (br[:, :], rows_of(io["L0_ffn_br"])),
                  (bo[:, :], io["L0_ffn_bo"])]
        loads += [(par_rows[:, j, i, :], io[f"L0_ffn_{n}{j + 1}"].rearrange("e (a p) -> (e a) p", p=P))
                  for j in range(2) for i, n in enumerate(("b", "g", "be", "m", "v"))]
        N_U = UNITS

        def load(sp, s, pair):
            sp.dma_start(x[:, s, :, :], tiles[:, pair, :]).then_inc(s_x[s], 16)

        with nc.Block() as block:

            @block.sync
            def _(sp):
                with nc.allow_non_contiguous_dma(reason="small routing weights"):
                    for to, frm in loads:
                        sp.dma_start(to, frm).then_inc(s_w, 16)
                for s in range(2):
                    load(sp, s, slice(s * PAIR, (s + 1) * PAIR))
                def store(n, s, rows, sent):
                    sp.wait_ge(s_done, n)
                    sp.dma_start(out_tiles[:, rows, :], x[:, s, :, :]).then_inc(s_sent[s], 16)
                    sp.wait_ge(s_sent[s], sent)

                with sp.Fori(0, N_U // 2 - 1) as r:
                    for s in range(2):
                        store(r * 2 + s + 1, s, bass.ds(r * (2 * PAIR) + s * PAIR, PAIR), r * 16 + 16)
                        load(sp, s, bass.ds(r * (2 * PAIR) + (s + 2) * PAIR, PAIR))
                for k in range(N_U - 3, N_U):
                    store(k + 1, k % 2, slice(k * PAIR, (k + 1) * PAIR), 16 * (k // 2 + 1))
                    if k + 2 < N_U:
                        load(sp, k % 2, slice((k + 2) * PAIR, (k + 3) * PAIR))

            @block.vector
            def _(dve):
                c = Count(dve, s_dve)
                for j in range(2):
                    dve.wait_ge(s_par, j + 1)
                    last = nc.vector.tensor_copy(par[:, j], bank1[j][:, 0:5 * 16].rearrange("p (i e) -> p i e", i=5))
                c.done(last)
                c.done(nc.vector.memset(bn_eps[:, :], EPS))
                dve.sem_inc(s_var, 1)
                dve.wait_ge(s_root, 1)
                c.done(nc.vector.reciprocal(gain[:, :, :], shift[:, :, :]))
                c.done(nc.vector.tensor_tensor(gain[:, :, :], gain[:, :, :], par[:, :, 1, :], ALU.mult))
                c.done(nc.vector.tensor_tensor(shift[:, :, :], par[:, :, 0, :], par[:, :, 3, :], ALU.subtract))
                c.done(nc.vector.tensor_tensor(shift[:, :, :], shift[:, :, :], gain[:, :, :], ALU.mult))
                nc.vector.tensor_tensor(shift[:, :, :], shift[:, :, :], par[:, :, 2, :], ALU.add).then_inc(s_scale, 1)
                dve.wait_ge(s_w, 16 * len(loads))

                def front(n, s, loaded, pair):
                    dve.wait_ge(s_x[s], loaded)
                    c.done(nc.vector.tensor_tensor(x[:, s], x[:, s], hidden[:, pair, :], ALU.add))
                    for i in range(PAIR):
                        last = nc.vector.bn_stats(stats[:, i, :], x[:, s, i, :])
                    c.done(last)
                    dve.sem_inc(s_std_in, 1)
                    for i in range(PAIR):
                        last = nc.vector.bn_aggr(mv[:, i, :], stats[:, i, :])
                    last.then_inc(s_std_in, 1)
                    dve.wait_ge(s_std, n)
                    c.done(nc.vector.reciprocal(std[:, :], std[:, :]))
                    for i in range(PAIR):
                        last = nc.vector.tensor_scalar(xn[:, s, i, :], x[:, s, i, :], mv[:, i, 0:1], std[:, i:i + 1], ALU.subtract, ALU.mult)
                    last.then_inc(s_xn, 1)

                def route(n, s):
                    dve.wait_ge(s_route, n)
                    c.done(nc.vector.tensor_tensor(logit[:, :, :], bank_g[:, 0:PAIR * E].rearrange("p (i e) -> p i e", i=PAIR), both(br[:, :]),
                                                   ALU.add))
                    c.done(nc.vector.tensor_reduce(top[:, :], logit[:, :, :], AX.X, ALU.max))
                    nc.vector.tensor_tensor(logit[:, :, :], logit[:, :, :], top[:, :].unsqueeze(2).to_broadcast([P, PAIR, E]),
                                            ALU.subtract).then_inc(s_logit, 1)
                    dve.wait_ge(s_exp, n)
                    c.done(nc.vector.tensor_reduce(top[:, :], gate[:, s], AX.X, ALU.add))
                    c.done(nc.vector.reciprocal(top[:, :], top[:, :]))
                    nc.vector.tensor_tensor(gate[:, s], gate[:, s], top[:, :].unsqueeze(2).to_broadcast([P, PAIR, E]), ALU.mult).then_inc(s_gate, 1)
                    dve.wait_ge(s_turn, n)
                    nc.vector.tensor_copy(gate_t[:, :, :], bank_g[0:E, 0:PAIR * P].rearrange("e (i n) -> e i n", i=PAIR)).then_inc(s_gate_t, 1)
                    dve.wait_ge(s_bias, n)
                    c.done(nc.vector.tensor_tensor(x[:, s], x[:, s], bank_g[:, :].rearrange("p (i d) -> p i d", i=PAIR), ALU.add))

                def gather_expert(n_acc, s, e, done):
                    dve.wait_ge(s_l3, n_acc)
                    for i in range(PAIR):
                        last = nc.vector.scalar_tensor_tensor(x[:, s, i, :], bank3[e % 2][:, i * D:(i + 1) * D], gate[:, s, i, e:e + 1], x[:, s, i, :],
                                                              ALU.mult, ALU.add)
                    last.then_inc(s_acc, 1)
                    dve.wait_ge(s_acc, n_acc + 2)
                    if e == E - 1:
                        dve.sem_inc(s_done, 1)

                dve.sem_inc(s_acc, 2)
                front(1, 0, 16, slice(0, PAIR))
                FRONT, ROUTE = 3, 5
                with dve.Fori(0, N_U // 2) as r:
                    c.enter(r, 2 * (FRONT + ROUTE))
                    for s in range(2):
                        n = r * 2 + s + 1
                        route(n, s)
                        for e in range(E):
                            gather_expert(r * (2 * E) + (s * E + e + 1), s, e, None)
                            if e == 3:
                                front(n + 1, 1 - s, r * 16 + (16 if s == 0 else 32), bass.ds(r * (2 * PAIR) + (s + 1) * PAIR, PAIR))
                c.leave(N_U // 2)
                route(N_U, 0)
                for e in range(E):
                    gather_expert((N_U - 1) * E + e + 1, 0, e, None)

            @block.scalar
            def _(act):
                act.wait_ge(s_var, 1)
                nc.scalar.activation(shift[:, :, :], par[:, :, 4, :], ACT.Sqrt, bias=bn_eps[:, 0:1]).then_inc(s_root, 1)
                act.wait_ge(s_scale, 1)

                def front_root(n):
                    act.wait_ge(s_std_in, n * 2)
                    nc.scalar.activation(std[:, :], mv[:, :, 1], ACT.Sqrt, bias=keep["eps"][:, 0:1]).then_inc(s_std, 1)

                def turned(n):
                    act.wait_ge(s_xt, n)
                    nc.scalar.copy(xt[:, :, :].rearrange("p a n -> p (a n)"), bank_x[:, :]).then_inc(s_xtc, 1)

                def layer(j, m, e):
                    act.wait_ge((s_l1, s_l2)[j], m)
                    for a in range(HALVES):
                        q = e * HALVES + a
                        last = nc.scalar.activation((h1, h2)[j][:, e % 2, a, :], (bank1, bank2)[j][e % 2][:, a * D:(a + 1) * D], ACT.Relu,
                                                    bias=shift[:, j, q:q + 1], scale=gain[:, j, q:q + 1])
                    last.then_inc((s_h1, s_h2)[j], 1)

                def unit(n, s, m, last):
                    act.wait_ge(s_logit, n)
                    nc.scalar.activation(gate[:, s], logit[:, :, :], ACT.Exp).then_inc(s_exp, 1)
                    for e in range(E + 1):
                        if e < E:
                            layer(0, m + (e + 1), e)
                        if e >= 1:
                            layer(1, m + e, e - 1)
                        if e == 5 and not last:
                            front_root(n + 1)
                    if not last:
                        turned(n + 1)

                front_root(1)
                turned(1)
                with act.Fori(0, N_U // 2) as r:
                    for s in range(2):
                        unit(r * 2 + s + 1, s, r * (2 * E) + s * E, False)
                unit(N_U, 0, (N_U - 1) * E, True)

            @block.tensor
            def _(pe):
                pe.wait_ge(s_w, 16 * len(loads))
                for j in range(2):
                    for i in range(5):
                        last = nc.tensor.transpose(bank1[j][:, 16 * i:16 * i + 16], par_rows[:, j, i, :], keep["ident"][0:16, 0:16])
                    last.then_inc(s_par, 1)
                pe.wait_ge(s_scale, 1)

                def turn(n, s):
                    pe.wait_ge(s_xn, n)
                    transpose_pair(nc, bank_x, xn[:, s], keep["ident"]).then_inc(s_xt, 1)

                def wide(bank, weight, data):
                    for a in range(HALVES):
                        for k in range(HALVES):
                            last = nc.tensor.matmul(bank[:, a * D:(a + 1) * D], weight[:, k, a * P:(a + 1) * P], data[:, k, :],
                                                    start=(k == 0), stop=(k == HALVES - 1))
                    return last

                def unit(n, s, m, last_unit):
                    pe.wait_ge(s_xtc, n)
                    for i in range(PAIR):
                        for k in range(HALVES):
                            last = nc.tensor.matmul(bank_g[:, i * E:(i + 1) * E], xt[:, k, i * P:(i + 1) * P], wr[:, k, :],
                                                    start=(k == 0), stop=(k == HALVES - 1))
                    last.then_inc(s_route, 1)
                    for e in range(E + 2):
                        if e < E:
                            if e < 2:
                                pe.wait_ge(s_xtc, n)
                            wide(bank1[e % 2], w[0][:, e], xt[:, :, :]).then_inc(s_l1, 1)
                        if e == 1:
                            pe.wait_ge(s_gate, n)
                            for i in range(PAIR):
                                last = nc.tensor.transpose(bank_g[0:E, i * P:(i + 1) * P], gate[:, s, i, :], keep["ident"][:, :])
                            last.then_inc(s_turn, 1)
                        if 1 <= e <= E:
                            pe.wait_ge(s_h1, m + e)
                            wide(bank2[(e - 1) % 2], w[1][:, e - 1], h1[:, (e - 1) % 2]).then_inc(s_l2, 1)
                        if e == 2:
                            pe.wait_ge(s_gate_t, n)
                            for i in range(PAIR):
                                last = nc.tensor.matmul(bank_g[:, i * D:(i + 1) * D], gate_t[:, i, :], bo[:, :], start=True, stop=True)
                            last.then_inc(s_bias, 1)
                        if e == E - 1 and not last_unit:
                            turn(n + 1, 1 - s)
                        if e >= 2:
                            pe.wait_ge(s_h2, m + (e - 1))
                            pe.wait_ge(s_acc, m + (e - 1))
                            for i in range(PAIR):
                                for k in range(HALVES):
                                    last = nc.tensor.matmul(bank3[e % 2][:, i * D:(i + 1) * D], h2[:, e % 2, k, i * P:(i + 1) * P], w[2][:, e - 2, k, :],
                                                            start=(k == 0), stop=(k == HALVES - 1))
                            last.then_inc(s_l3, 1)

                turn(1, 0)
                with pe.Fori(0, N_U // 2) as r:
                    for s in range(2):
                        unit(r * 2 + s + 1, s, r * (2 * E) + s * E, False)
                unit(N_U, 0, (N_U - 1) * E, True)


def slice_attention(nc, io, dram, keep, out):
    J = INNER // P
    with ExitStack() as stack:
        space = Space(nc, stack, "ffn")
        sb = space.sb
        slice_t = sb("slice_t", [P, N_TILES, INNER])
        sums = sb("sums", [P, HALVES, INNER])
        total = sb("total", [P, INNER])
        spread = sb("spread", [P, J, D])
        slice_weights(nc, io, dram, keep, slice_t, sums, total)
        slice_tokens(nc, io, keep, sums, total, spread)
        slice_output(nc, io, dram, slice_t, spread, out)


def slice_weights(nc, io, dram, keep, slice_t, sums, total):
    H, G = 8, 64
    J = INNER // P
    U = UNROLL
    with ExitStack() as stack:
        space = Space(nc, stack, "slw")
        sb, sem = space.sb, space.sem
        w_x = sb("w_x", [P, HALVES, INNER])
        w_xt = sb("w_xt", [P, J, D])
        w_slice = sb("w_slice", [P, P])
        b_xt = sb("b_xt", [P, J])
        b_xt_wide = sb("b_xt_wide", [P, J, P])
        b_slice = sb("b_slice", [P, G])
        inv_temp = sb("inv_temp", [P, H])
        w_logit = sb("w_logit", [P, HALVES, INNER])
        b_logit = sb("b_logit", [P, INNER])
        x = sb("x", [P, U, PAIR, D])
        xt = sb("xt", [P, U, HALVES, PAIR * P])
        sw = sb("sw", [P, U, INNER])
        top = sb("top", [P, U, H])
        den = sb("den", [P, U, H])
        nothing = sb("nothing", [P, P])
        bank = [space.ps(f"bank{u}", [P, 512]) for u in range(U)]
        sum_bank = [space.ps(f"sum_bank{a}", [P, 512]) for a in range(HALVES)]
        ln = Normalise(space, "ln", keep["eps"])
        s_x = space.sems("s_x", U)
        (s_w, s_dve, s_zero, s_wt, s_wtc, s_wl, s_ready, s_xn, s_xt, s_xtc, s_lg, s_lb, s_mx, s_sub, s_exp, s_sm, s_rc, s_sw, s_swt,
         s_swtc, s_total, s_sums) = (
            sem(n) for n in ("s_w", "s_dve", "s_zero", "s_wt", "s_wtc", "s_wl", "s_ready", "s_xn", "s_xt", "s_xtc", "s_lg", "s_lb",
                             "s_mx", "s_sub", "s_exp", "s_sm", "s_rc", "s_sw", "s_swt", "s_swtc", "s_total", "s_sums"))
        tiles = pair_rows(dram["x3"])
        loads = [(w_x[:, :, :], io["L1_ffn_W_x"].rearrange("(a p) n -> p a n", p=P)),
                 (w_slice[0:G, 0:G], io["L1_ffn_W_slice"]), (w_slice[G:P, G:P], io["L1_ffn_W_slice"]),
                 (b_xt[:, :], io["L1_ffn_b_x"].rearrange("(j p) -> p j", p=P)),
                 (b_slice[:, :], rows_of(io["L1_ffn_b_slice"])),
                 (inv_temp[:, :], rows_of(io["L1_ffn_temperature"].rearrange("a h b c -> (a h b c)")))]

        def at(r, i, u):
            return r * (PAIR * U) + (i * U + u + 1)

        def heads(ap):
            return ap.rearrange("p (h g) -> p h g", h=H)

        def by_head(ap):
            return ap.unsqueeze(2).to_broadcast([P, H, G])

        with nc.Block() as block:

            @block.sync
            def _(sp):
                sp.wait_ge(s_zero, 1)
                with nc.allow_non_contiguous_dma(reason="bias by partition"):
                    for to, frm in loads:
                        sp.dma_start(to, frm).then_inc(s_w, 16)
                with sp.Fori(0, ROUNDS) as r:
                    for u in range(U):
                        sp.wait_ge(s_swt, r * (PAIR * U) + (U + u + 1))
                        sp.dma_start(x[:, u, :, :], tiles[:, pair_of(r, u), :]).then_inc(s_x[u], 16)

            @block.vector
            def _(dve):
                c = Count(dve, s_dve)
                nc.vector.memset(w_slice[:, :], 0.0)
                nc.vector.memset(nothing[:, :], 0.0)
                nc.vector.memset(total[:, :], 0.0).then_inc(s_zero, 1)
                dve.wait_ge(s_w, 16 * len(loads))
                for j in range(J):
                    last = nc.vector.tensor_copy(b_xt_wide[:, j, :], b_xt[:, j:j + 1].to_broadcast([P, P]))
                c.done(nc.vector.tensor_scalar(inv_temp[:, :], inv_temp[:, :], 0.1, 5.0, ALU.max, ALU.min))
                c.done(nc.vector.reciprocal(inv_temp[:, :], inv_temp[:, :]))
                for a in range(HALVES):
                    dve.wait_ge(s_wt, a + 1)
                    nc.vector.tensor_copy(w_xt[:, :, a * P:(a + 1) * P], bank[a][:, :].rearrange("p (j i) -> p j i", j=J)).then_inc(s_wtc, 1)
                dve.wait_ge(s_wl, 1)
                for a in range(HALVES):
                    nc.vector.tensor_tensor(heads(w_logit[:, a, :]), heads(bank[a][:, :]), by_head(inv_temp[:, :]), ALU.mult)
                c.done(nc.vector.tensor_tensor(heads(b_logit[:, :]), heads(bank[2][:, :]), b_slice[:, :].unsqueeze(1).to_broadcast([P, H, G]),
                                               ALU.add))
                nc.vector.tensor_tensor(heads(b_logit[:, :]), heads(b_logit[:, :]), by_head(inv_temp[:, :]), ALU.mult).then_inc(s_ready, 1)
                dve.wait_ge(s_ready, 1)
                with dve.Fori(0, ROUNDS) as r:
                    for u, n in units(r):
                        dve.wait_ge(s_x[u], r * 16 + 16)
                        ln.statistics(nc, u, n, x[:, u])
                    for u, n in units(r):
                        ln.aggregate(nc, u, n)
                    for u, n in units(r):
                        ln.invert(nc, u, n)
                    for u, n in units(r):
                        ln.scale(nc, u, n, x[:, u], x[:, u]).then_inc(s_xn, 1)
                    for i in range(PAIR):
                        for u in range(U):
                            dve.wait_ge(s_lg, at(r, i, u))
                            dve.wait_ge(s_total, at(r, i, u))
                            nc.vector.tensor_tensor(sw[:, u], bank[u][:, :], b_logit[:, :], ALU.add).then_inc(s_lb, 1)
                        for u in range(U):
                            dve.wait_ge(s_lb, at(r, i, u))
                            nc.vector.tensor_reduce(top[:, u], heads(sw[:, u]), AX.X, ALU.max).then_inc(s_mx, 1)
                        for u in range(U):
                            dve.wait_ge(s_mx, at(r, i, u))
                            nc.vector.tensor_tensor(heads(sw[:, u]), heads(sw[:, u]), by_head(top[:, u]), ALU.subtract).then_inc(s_sub, 1)
                        for u in range(U):
                            dve.wait_ge(s_exp, at(r, i, u))
                            nc.vector.tensor_reduce(den[:, u], heads(sw[:, u]), AX.X, ALU.add).then_inc(s_sm, 1)
                        for u in range(U):
                            dve.wait_ge(s_sm, at(r, i, u))
                            nc.vector.reciprocal(den[:, u], den[:, u]).then_inc(s_rc, 1)
                        for u in range(U):
                            dve.wait_ge(s_rc, at(r, i, u))
                            nc.vector.scalar_tensor_tensor(heads(sw[:, u]), heads(sw[:, u]),
                                                           keep["mask"][:, bass.ds(r * (U * PAIR) + u * PAIR + i, 1)], by_head(den[:, u]),
                                                           ALU.mult, ALU.mult).then_inc(s_sw, 1)
                dve.wait_ge(s_sums, 1)
                for a in range(HALVES):
                    nc.vector.tensor_copy(sums[:, a, :], sum_bank[a][:, :])

            @block.gpsimd
            def _(pool):
                pool.sem_inc(s_total, U)
                with pool.Fori(0, ROUNDS) as r:
                    for i in range(PAIR):
                        for u in range(U):
                            pool.wait_ge(s_sw, at(r, i, u))
                            pool.wait_ge(s_total, at(r, i, u) + (U - 1))
                            nc.gpsimd.tensor_tensor(total[:, :], total[:, :], sw[:, u], ALU.add).then_inc(s_total, 1)

            @block.scalar
            def _(act):
                act.sem_inc(s_swtc, PAIR * U)
                with act.Fori(0, ROUNDS) as r:
                    for u, n in units(r):
                        ln.root(nc, u, n)
                    for u, n in units(r):
                        act.wait_ge(s_xt, n)
                        nc.scalar.copy(xt[:, u].rearrange("p a n -> p (a n)"), bank[u][:, :]).then_inc(s_xtc, 1)
                    for i in range(PAIR):
                        for u in range(U):
                            act.wait_ge(s_sub, at(r, i, u))
                            nc.scalar.activation(sw[:, u], sw[:, u], ACT.Exp).then_inc(s_exp, 1)
                        for u in range(U):
                            act.wait_ge(s_swt, at(r, i, u) + PAIR * U)
                            nc.scalar.copy(slice_t[:, bass.ds(r * (U * PAIR) + u * PAIR + i, 1), :].rearrange("p t n -> p (t n)"),
                                           bank[u][:, :]).then_inc(s_swtc, 1)

            @block.tensor
            def _(pe):
                pe.sem_inc(s_swt, PAIR * U)
                pe.wait_ge(s_w, 16 * len(loads))
                for a in range(HALVES):
                    for j in range(J):
                        last = nc.tensor.transpose(bank[a][:, j * P:(j + 1) * P], w_x[:, a, j * P:(j + 1) * P], keep["ident"][:, :])
                    last.then_inc(s_wt, 1)
                pe.wait_ge(s_wtc, 2)
                for a in range(HALVES):
                    for j in range(J):
                        nc.tensor.matmul(bank[a][:, j * P:(j + 1) * P], w_xt[:, j, a * P:(a + 1) * P], w_slice[:, :], start=True, stop=True)
                for j in range(J):
                    last = nc.tensor.matmul(bank[2][:, j * P:(j + 1) * P], b_xt_wide[:, j, :], w_slice[:, :], start=True, stop=True)
                last.then_inc(s_wl, 1)
                pe.wait_ge(s_ready, 1)
                for a in range(HALVES):
                    nc.tensor.matmul(sum_bank[a][:, :], nothing[:, :], w_logit[:, 0, :], start=True, stop=False)
                with pe.Fori(0, ROUNDS) as r:
                    for u, n in units(r):
                        pe.wait_ge(s_xn, n)
                        pe.wait_ge(s_swtc, r * (PAIR * U) + (U + u + 1))
                        transpose_pair(nc, bank[u], x[:, u], keep["ident"]).then_inc(s_xt, 1)
                    for i in range(PAIR):
                        for u, n in units(r):
                            if i == 0:
                                pe.wait_ge(s_xtc, n)
                            else:
                                pe.wait_ge(s_swtc, at(r, 0, u) + PAIR * U)
                            for a in range(HALVES):
                                last = nc.tensor.matmul(bank[u][:, :], xt[:, u, a, i * P:(i + 1) * P], w_logit[:, a, :],
                                                        start=(a == 0), stop=(a == HALVES - 1))
                            last.then_inc(s_lg, 1)
                        for u in range(U):
                            pe.wait_ge(s_sw, at(r, i, u))
                            for a in range(HALVES):
                                nc.tensor.matmul(sum_bank[a][:, :], x[:, u, i, a * P:(a + 1) * P], sw[:, u], start=False, stop=False)
                            for j in range(J):
                                last = nc.tensor.transpose(bank[u][:, j * P:(j + 1) * P], sw[:, u, j * P:(j + 1) * P], keep["ident"][:, :])
                            last.then_inc(s_swt, 1)
                for a in range(HALVES):
                    last = nc.tensor.matmul(sum_bank[a][:, :], nothing[:, :], w_logit[:, 0, :], start=False, stop=True)
                last.then_inc(s_sums, 1)


def slice_tokens(nc, io, keep, sums, total, spread):
    G = DH = 64
    J = INNER // P
    with ExitStack() as stack:
        space = Space(nc, stack, "slt")
        sb, sem = space.sb, space.sem
        w_fx = sb("w_fx", [P, HALVES, INNER])
        w_out = sb("w_out", [P, J, D])
        b_fxt = sb("b_fxt", [P, J])
        w_head = [sb(f"w_{n}", [P, P]) for n in "qkv"]
        ones = sb("ones", [P, P])
        same = sb("same", [P, P])
        other = sb("other", [P, P])
        norm = sb("norm", [P, INNER])
        inv_norm = sb("inv_norm", [P, INNER])
        token_t = sb("token_t", [P, INNER])
        head_t = [sb(f"{n}_t", [P, INNER]) for n in "qkv"]
        attn, attn_t = sb("attn", [P, INNER]), sb("attn_t", [P, INNER])
        top = sb("top", [P, J])
        value_out = sb("value_out", [P, J, D])
        bank = [space.ps(f"bank{i}", [P, 512]) for i in range(8)]
        s_w, s_dve, s_zero, s_norm, s_token, s_heads, s_qkv, s_copied, s_score, s_vw, s_vwc, s_sub, s_exp, s_attn, s_turn, s_out = (
            sem(n) for n in ("s_w", "s_dve", "s_zero", "s_norm", "s_token", "s_heads", "s_qkv", "s_copied", "s_score", "s_vw", "s_vwc",
                             "s_sub", "s_exp", "s_attn", "s_turn", "s_out"))
        loads = [(w_fx[:, :, :], io["L1_ffn_W_fx"].rearrange("(a p) n -> p a n", p=P)),
                 (w_out[:, :, :], io["L1_ffn_W_out"].rearrange("(j p) n -> p j n", p=P)),
                 (b_fxt[:, :], io["L1_ffn_b_fx"].rearrange("(j p) -> p j", p=P))]
        loads += [(w_head[i][h * DH:(h + 1) * DH, h * DH:(h + 1) * DH], io[f"L1_ffn_W_{n}"]) for i, n in enumerate("qkv") for h in range(2)]

        def pairs(ap):
            return ap.rearrange("p (j g) -> p j g", j=J)

        with nc.Block() as block:

            @block.sync
            def _(sp):
                sp.wait_ge(s_zero, 1)
                with nc.allow_non_contiguous_dma(reason="bias by partition"):
                    for to, frm in loads:
                        sp.dma_start(to, frm).then_inc(s_w, 16)

            @block.vector
            def _(dve):
                c = Count(dve, s_dve)
                for w in w_head:
                    nc.vector.memset(w[:, :], 0.0)
                nc.vector.memset(ones[:, :], 1.0)
                c.done(nc.vector.memset(same[:, :], 0.0))
                for h in range(2):
                    last = nc.vector.memset(same[h * G:(h + 1) * G, h * G:(h + 1) * G], 1.0)
                c.done(last)
                nc.vector.tensor_scalar(other[:, :], same[:, :], -1.0, BIG, ALU.add, ALU.mult).then_inc(s_zero, 1)
                dve.wait_ge(s_norm, 1)
                nc.vector.tensor_copy(norm[:, :], bank[0][:, :])
                c.done(nc.vector.tensor_scalar(inv_norm[:, :], bank[0][:, :], 1e-5, None, ALU.add))
                c.done(nc.vector.reciprocal(inv_norm[:, :], inv_norm[:, :]))
                dve.wait_ge(s_w, 16 * len(loads))
                dve.wait_ge(s_token, 1)
                for j in range(J):
                    cols = slice(j * P, (j + 1) * P)
                    last = nc.vector.scalar_tensor_tensor(token_t[:, cols], norm[:, cols], b_fxt[:, j:j + 1], bank[1][:, cols], ALU.mult, ALU.add)
                c.done(last)
                c.done(nc.vector.tensor_tensor(token_t[:, :], token_t[:, :], inv_norm[:, :], ALU.mult))
                nc.vector.tensor_tensor(pairs(token_t[:, :]), pairs(token_t[:, :]), same[:, :].unsqueeze(1).to_broadcast([P, J, P]),
                                        ALU.mult).then_inc(s_heads, 1)
                dve.wait_ge(s_qkv, 1)
                for i in range(3):
                    last = nc.vector.tensor_copy(head_t[i][:, :], bank[2 + i][:, :])
                last.then_inc(s_copied, 1)
                dve.wait_ge(s_vw, 1)
                for j in range(J):
                    last = nc.vector.tensor_copy(value_out[:, j, :], bank[6 + j // 2][:, (j % 2) * D:(j % 2 + 1) * D])
                last.then_inc(s_vwc, 1)
                dve.wait_ge(s_score, 1)
                c.done(nc.vector.scalar_tensor_tensor(pairs(attn[:, :]), pairs(bank[5][:, :]), DH ** -0.5,
                                                      other[:, :].unsqueeze(1).to_broadcast([P, J, P]), ALU.mult, ALU.add))
                c.done(nc.vector.tensor_reduce(top[:, :], pairs(attn[:, :]), AX.X, ALU.max))
                nc.vector.tensor_tensor(pairs(attn[:, :]), pairs(attn[:, :]), top[:, :].unsqueeze(2).to_broadcast([P, J, P]),
                                        ALU.subtract).then_inc(s_sub, 1)
                dve.wait_ge(s_exp, 1)
                c.done(nc.vector.tensor_reduce(top[:, :], pairs(attn[:, :]), AX.X, ALU.add))
                c.done(nc.vector.reciprocal(top[:, :], top[:, :]))
                nc.vector.tensor_tensor(pairs(attn[:, :]), pairs(attn[:, :]), top[:, :].unsqueeze(2).to_broadcast([P, J, P]),
                                        ALU.mult).then_inc(s_attn, 1)
                dve.wait_ge(s_turn, 1)
                nc.vector.tensor_copy(attn_t[:, :], bank[0][:, :]).then_inc(s_turn, 1)
                dve.wait_ge(s_out, 1)
                for j in range(J):
                    nc.vector.tensor_copy(spread[:, j, :], bank[2 + j // 2][:, (j % 2) * D:(j % 2 + 1) * D])

            @block.scalar
            def _(act):
                act.wait_ge(s_sub, 1)
                nc.scalar.activation(attn[:, :], attn[:, :], ACT.Exp).then_inc(s_exp, 1)

            @block.tensor
            def _(pe):
                pe.wait_ge(s_zero, 1)
                nc.tensor.matmul(bank[0][:, :], ones[:, :], total[:, :], start=True, stop=True).then_inc(s_norm, 1)
                pe.wait_ge(s_w, 16 * len(loads))
                for j in range(J):
                    cols = slice(j * P, (j + 1) * P)
                    for a in range(HALVES):
                        last = nc.tensor.matmul(bank[1][:, cols], w_fx[:, a, cols], sums[:, a, cols], start=(a == 0), stop=(a == HALVES - 1))
                last.then_inc(s_token, 1)
                pe.wait_ge(s_heads, 1)
                for i in range(3):
                    last = nc.tensor.matmul(bank[2 + i][:, :], w_head[i][:, :], token_t[:, :], start=True, stop=True)
                last.then_inc(s_qkv, 1)
                pe.wait_ge(s_copied, 1)
                q_t, k_t, v_t = head_t
                for j in range(J):
                    cols = slice(j * P, (j + 1) * P)
                    last = nc.tensor.matmul(bank[6 + j // 2][:, (j % 2) * D:(j % 2 + 1) * D], v_t[:, cols], w_out[:, j, :], start=True, stop=True)
                last.then_inc(s_vw, 1)
                for j in range(J):
                    cols = slice(j * P, (j + 1) * P)
                    last = nc.tensor.matmul(bank[5][:, cols], q_t[:, cols], k_t[:, cols], start=True, stop=True)
                last.then_inc(s_score, 1)
                pe.wait_ge(s_attn, 1)
                for j in range(J):
                    cols = slice(j * P, (j + 1) * P)
                    last = nc.tensor.transpose(bank[0][:, cols], attn[:, cols], keep["ident"][:, :])
                last.then_inc(s_turn, 1)
                pe.wait_ge(s_turn, 2)
                pe.wait_ge(s_vwc, 1)
                for j in range(J):
                    cols = slice(j * P, (j + 1) * P)
                    last = nc.tensor.matmul(bank[2 + j // 2][:, (j % 2) * D:(j % 2 + 1) * D], attn_t[:, cols], value_out[:, j, :],
                                            start=True, stop=True)
                last.then_inc(s_out, 1)


def slice_output(nc, io, dram, slice_t, spread, out):
    J = INNER // P
    with ExitStack() as stack:
        space = Space(nc, stack, "slo")
        sb, sem = space.sb, space.sem
        b_out = sb("b_out", [P, D])
        x = sb("x", [P, UNROLL, PAIR, D])
        lhs = sb("lhs", [P, UNROLL, PAIR, INNER])
        bank = [space.ps(f"bank{u}", [P, 512]) for u in range(UNROLL)]
        s_x, s_sent = space.sems("s_x", UNROLL), space.sems("s_sent", UNROLL)
        s_w, s_free, s_lhs, s_bias, s_mm, s_done = (sem(n) for n in ("s_w", "s_free", "s_lhs", "s_bias", "s_mm", "s_done"))
        tiles = pair_rows(dram["x3"])
        whole = out[0:LAST_TILE * P, :].rearrange("(t p) d -> p t d", p=P)
        rest = N_NODES - LAST_TILE * P
        with nc.Block() as block:

            @block.sync
            def _(sp):
                sp.dma_start(b_out[:, :], rows_of(io["L1_ffn_b_out"])).then_inc(s_w, 16)

                def load(u, rows):
                    sp.dma_start(x[:, u, :, :], tiles[:, rows, :]).then_inc(s_x[u], 16)

                with sp.Fori(0, ROUNDS - 1) as r:
                    for u, n in units(r):
                        sp.wait_ge(s_free, n)
                        load(u, pair_of(r, u))
                    for u, n in units(r):
                        sp.wait_ge(s_done, n)
                        sp.dma_start(whole[:, pair_of(r, u), :], x[:, u, :, :]).then_inc(s_sent[u], 16)
                    for u, n in units(r):
                        sp.wait_ge(s_sent[u], r * 16 + 16)
                        sp.sem_inc(s_free, 1)
                r = ROUNDS - 1
                for u in range(UNROLL):
                    sp.wait_ge(s_free, r * UNROLL + u + 1)
                    load(u, slice((r * UNROLL + u) * PAIR, (r * UNROLL + u + 1) * PAIR))
                for u in range(UNROLL):
                    t = (r * UNROLL + u) * PAIR
                    sp.wait_ge(s_done, r * UNROLL + u + 1)
                    if t < LAST_TILE:
                        sp.dma_start(whole[:, t:t + PAIR, :], x[:, u, :, :]).then_inc(s_sent[u], 16)
                    else:
                        sp.dma_start(out[LAST_TILE * P:, :], x[0:rest, u, 0, :]).then_inc(s_sent[u], 16)
                for u in range(UNROLL):
                    sp.wait_ge(s_sent[u], 16 * ROUNDS)

            @block.gpsimd
            def _(pool):
                pool.sem_inc(s_free, UNROLL)
                pool.wait_ge(s_w, 16)
                with pool.Fori(0, ROUNDS) as r:
                    for u, n in units(r):
                        pool.wait_ge(s_x[u], r * 16 + 16)
                        nc.gpsimd.tensor_tensor(x[:, u], x[:, u], both(b_out[:, :]), ALU.add).then_inc(s_bias, 1)

            @block.scalar
            def _(act):
                with act.Fori(0, ROUNDS) as r:
                    for u, n in units(r):
                        act.wait_ge(s_mm, n)
                        nc.scalar.copy(lhs[:, u], slice_t[:, pair_of(r, u), :]).then_inc(s_lhs, 1)

            @block.tensor
            def _(pe):
                pe.sem_inc(s_mm, UNROLL)
                with pe.Fori(0, ROUNDS) as r:
                    for u, n in units(r):
                        pe.wait_ge(s_lhs, n)
                        pe.wait_ge(s_free, n)
                        for i in range(PAIR):
                            for j in range(J):
                                last = nc.tensor.matmul(bank[u][:, i * D:(i + 1) * D], lhs[:, u, i, j * P:(j + 1) * P], spread[:, j, :],
                                                        start=(j == 0), stop=(j == J - 1))
                        last.then_inc(s_mm, 1)

            @block.vector
            def _(dve):
                with dve.Fori(0, ROUNDS) as r:
                    for u, n in units(r):
                        dve.wait_ge(s_bias, n)
                        dve.wait_ge(s_mm, n + UNROLL)
                        nc.vector.tensor_tensor(x[:, u], x[:, u], bank[u][:, :].rearrange("p (i d) -> p i d", i=PAIR), ALU.add).then_inc(s_done, 1)


def scratch(nc):
    shapes = {"x0": ((N_PAD, D), F32), "x1": ((N_PAD, D), F32), "x2": ((N_PAD, D), F32), "x3": ((N_PAD, D), F32),
              "first": ((STEPS_PAD * P, 8), F32), "seg_max": ((STEPS_PAD * P, GAT_HEADS), F32),
              "flags": ((P, 5 * BLOCKS * P), F32), "any_reset": ((P, 2 * BLOCKS * 8), F32),
              "feat": ((N_PAD, GAT_ROW), F32), "score": ((N_PAD, GAT_HEADS), F32), "rel_feat": ((REL * N_PAD, D), F32)}
    shapes |= {f"{n}_rows": ((CHUNKS, P), I32) for n in ("src", "dst", "prev", "next", "kind")}
    shapes["weight_rows"] = ((CHUNKS, P), F32)
    return {n: nc.dram_tensor(f"scratch_{n}", s, dt).ap() for n, (s, dt) in shapes.items()}


def build(nc, io, out):
    dram = scratch(nc)
    with ExitStack() as stack:
        sb = Space(nc, stack, "keep").sb
        keep = {"ident": sb("ident", [P, P]), "iota_row": sb("iota_row", [P, P]),
                "src_tab": sb("src_tab", [P, STEPS_PAD], I32), "rel_tab": sb("rel_tab", [P, STEPS_PAD], I32),
                "wt_tab": sb("wt_tab", [P, STEPS_PAD]), "dst_tab": sb("dst_tab", [P, STEPS_PAD]),
                "eps": sb("eps", [P, 1]), "mask": sb("mask", [P, N_TILES]), "same_head": sb("same_head", [P, P]),
                "head_of": sb("head_of", [P, P // MIX_DIM]), "tile_row": sb("tile_row", [1, STEPS_PAD], I32),
                "first_pos": sb("first_pos", [P, N_TILES], I32)}
        gathers = Gathers(nc)
        build_tables(nc, io, dram, keep, gathers)
        mix(nc, io, dram, keep, 0)
        with ExitStack() as inner:
            hidden = Space(nc, inner, "layer0").sb("hidden", [P, N_TILES, D])
            gnn_input(nc, io, dram, keep, hidden)
            for layer in range(GAT_LAYERS):
                graph_attention(nc, io, dram, keep, gathers, layer, hidden)
            expert_mixture(nc, io, dram, keep, hidden)
        relation_features(nc, io, dram, keep)
        with ExitStack() as inner:
            acc = Space(nc, inner, "layer1").sb("acc", [P, N_TILES, D])
            add_messages(nc, keep, gathers, "rm", dram["rel_feat"], D, keep["rel_tab"], acc, edge_weight=keep["wt_tab"])
            mix(nc, io, dram, keep, 1, added=acc)
        slice_attention(nc, io, dram, keep, out)


def mix(nc, io, dram, keep, layer, added=None):
    cfg = mix_cfg(io, dram, layer)
    with ExitStack() as stack:
        kv_sum = Space(nc, stack, f"mix{layer}").sb("kv_sum", [P, HALVES, P + 1])
        linear_attention_sums(nc, io, dram, keep, cfg, kv_sum)
        linear_attention(nc, io, dram, keep, cfg, kv_sum, added)


def graph_attention(nc, io, dram, keep, gathers, layer, hidden):
    with ExitStack() as stack:
        sb = Space(nc, stack, f"gat{layer}").sb
        weights = sb("weights", [P, STEPS_PAD, GAT_HEADS])
        self_weight = sb("self_weight", [P, N_TILES, GAT_HEADS])
        with ExitStack() as inner:
            scores = Space(nc, inner, f"gat{layer}").sb("scores", [P, N_TILES, 2 * GAT_HEADS])
            gat_project(nc, io, dram, keep, layer, hidden, scores)
            gat_softmax(nc, dram, keep, gathers, layer, scores, weights, self_weight)
        acc = sb("acc", [P, N_TILES, GAT_ROW])
        add_messages(nc, keep, gathers, f"gm{layer}", dram["feat"], GAT_ROW, keep["src_tab"], acc, weights=weights)
        gat_finish(nc, io, dram, keep, layer, hidden, acc, self_weight)


def kernel(**inputs):
    import concourse.bacc as _bacc
    from concourse.bass_utils import run_bass_kernel_spmd as _run

    nc = _bacc.Bacc("TRN2", target_bir_lowering=False, num_devices=1)
    arrays, io = {}, {}
    for name in _INS:
        a = np.ascontiguousarray(inputs[name])
        arrays[f"in_{name}"] = a
        io[name] = nc.dram_tensor(f"in_{name}", a.shape, mybir.dt.from_np(a.dtype), kind="ExternalInput").ap()
    out = nc.dram_tensor("out", (N_NODES, D), F32, kind="ExternalOutput").ap()
    build(nc, io, out)
    r = _run(nc, [arrays], core_ids=[0])
    return r.results[0]["out"]
```

```python
from contextlib import ExitStack

import numpy as np

import concourse.bass as bass
from concourse import mybir

F32 = mybir.dt.float32
I32 = mybir.dt.int32
ALU = mybir.AluOpType
ACT = mybir.ActivationFunctionType
AX = mybir.AxisListType

P = 128
N_NODES = 6250
N_EDGES = 100000
D = 256
HALVES = D // P
N_TILES = 50
N_PAD = N_TILES * P
LAST_TILE = N_NODES // P
PAIR = 2
UNITS = N_TILES // PAIR
UNROLL = 5
ROUNDS = UNITS // UNROLL
GAT_LAYERS, GAT_HEADS, GAT_DIM = 3, 4, 64
MIX_DIM = 32
GAT_ROW = D + GAT_HEADS
GAT_SUM = GAT_ROW + GAT_HEADS
LN_EPS = 1e-5
BIG = 2.0 ** 100
OUT_OF_RANGE = 1 << 20

CHUNKS = -(-N_EDGES // P)
STEPS = CHUNKS + LAST_TILE
WINDOW = 28
WINDOW_BUFS = 3
WINDOWS = -(-STEPS // (WINDOW * WINDOW_BUFS)) * WINDOW_BUFS
STEPS_RUN = WINDOWS * WINDOW
SLOTS = 24
STEP_ROUNDS = STEPS_RUN // SLOTS
assert STEP_ROUNDS * SLOTS == STEPS_RUN
BLOCKS = -(-STEPS_RUN // P)
STEPS_PAD = BLOCKS * P


class Count:

    def __init__(self, engine, sem):
        self.engine, self.sem, self.base, self.n = engine, sem, 0, 0

    def done(self, instruction):
        instruction.then_inc(self.sem, 1)
        self.n += 1
        self.engine.wait_ge(self.sem, self.base + self.n)

    def enter(self, i, per):
        self.before, self.per = self.base + self.n, per
        self.base, self.n = self.before + i * per, 0

    def leave(self, trips):
        assert self.n == self.per, (self.n, self.per)
        self.base, self.n = self.before + trips * self.per, 0


FIRST_SEM, LAST_SEM = 100, 229
GATHER_SEMS = 26


class Space:

    def __init__(self, nc, stack, tag, gathers=None):
        self.nc, self.stack, self.tag, self.next, self.gathers = nc, stack, tag, FIRST_SEM, gathers
        stack.callback(self.close)

    def close(self):
        if self.next > FIRST_SEM:
            self.nc.all_engine_barrier(sems_to_clear=range(FIRST_SEM, self.next))

    def sb(self, name, shape, dt=F32):
        return self.stack.enter_context(self.nc.sbuf_tensor(f"{self.tag}_{name}", shape, dt))

    def ps(self, name, shape, dt=F32):
        return self.stack.enter_context(self.nc.psum_tensor(f"{self.tag}_{name}", shape, dt))

    def sem(self, name):
        assert self.next <= LAST_SEM
        self.next += 1
        return self.stack.enter_context(self.nc.semaphore(f"{self.tag}_{name}", num=self.next - 1))

    def sems(self, name, n):
        return [self.sem(f"{name}{i}") for i in range(n)]


class Gathers:

    def __init__(self, nc):
        self.sems = [nc.alloc_semaphore(f"gather{i}", num=LAST_SEM + 1 + i) for i in range(GATHER_SEMS)]
        self.had = [0] * GATHER_SEMS

    def start(self, slots):
        return [(self.sems[i], self.had[i]) for i in slots]

    def count(self, slots, dmas):
        for i in slots:
            self.had[i] += 16 * dmas


def rows_of(vector):
    return vector.partition_broadcast(P)


def build_tables(nc, io, dram, keep, gathers):
    with ExitStack() as stack:
        sp_ = Space(nc, stack, "tab")
        sb, ps, sem = sp_.sb, sp_.ps, sp_.sem
        ident, iota_row = keep["ident"], keep["iota_row"]
        pad_int = sb("pad_int", [1, 4, P], I32)
        zeros = sb("zeros", [P, D])
        minus_big = sb("minus_big", [P, 2048])
        iota_int = sb("iota_int", [P, P], I32)
        chunk_int = sb("chunk_int", [1, CHUNKS], I32)
        chunk_no = sb("chunk_no", [1, CHUNKS])
        step_int = sb("step_int", [P, BLOCKS], I32)
        step_no = sb("step_no", [P, BLOCKS])
        node_int = sb("node_int", [P, N_TILES], I32)
        node_no = sb("node_no", [P, N_TILES])
        ones = sb("ones", [1, P])
        ends = sb("ends", [1, 2, CHUNKS], I32)
        path = sb("path", [1, 2, CHUNKS])
        tile_int = sb("tile_int", [1, CHUNKS], I32)
        path_all = sb("path_all", [P, 2, CHUNKS])
        junk = sb("junk", [P, CHUNKS])
        chunk_of = sb("chunk_of", [P, BLOCKS])
        chunk_idx = sb("chunk_idx", [P, BLOCKS], I32)
        tile_of = sb("tile_of", [P, BLOCKS])
        tile_clip = sb("tile_clip", [P, BLOCKS])
        first_of = sb("first_of", [P, BLOCKS])
        raw = sb("raw", [P, 5, BLOCKS, P], I32)
        weight = sb("weight", [P, BLOCKS, P])
        as_f = sb("as_f", [P, 5, BLOCKS, P])
        rel = sb("rel", [P, BLOCKS, P])
        low = sb("low", [P, BLOCKS, P])
        valid = sb("valid", [P, BLOCKS, P])
        flags = sb("flags", [P, 5, BLOCKS, P])
        differs = sb("differs", [P, BLOCKS, P])
        zero_row = sb("zero_row", [P, P])
        step_min = sb("step_min", [P, 2, BLOCKS])
        cross_row = sb("cross_row", [1, STEPS_PAD])
        node_chunk = sb("node_chunk", [P, N_TILES])
        node_chunk_idx = sb("node_chunk_idx", [P, N_TILES], I32)
        node_rows = sb("node_rows", [P, UNROLL, P], I32)
        node_stage = sb("node_stage", [P, UNROLL], I32)
        node_rows_f = sb("node_rows_f", [P, UNROLL, P])
        before = sb("before", [P, N_TILES])
        has = sb("has", [P, N_TILES])
        position = sb("position", [P, N_TILES])
        bank = [ps(f"bank{i}", [P, 512]) for i in range(8)]
        s_pads, s_fill, s_consts, s_iota = sem("pads"), sem("fill"), sem("consts"), sem("iota")
        s_flat, s_ends, s_path, s_bcast = sem("flat"), sem("ends"), sem("path"), sem("bcast")
        s_index, s_rows, s_dve, s_tabs, s_psum = sem("index"), gathers.start([UNROLL])[0][0], sem("dve"), sem("tabs"), sem("psum")
        s_nidx, s_ncopy, s_nused, s_const = sem("nidx"), sem("ncopy"), sem("nused"), sem("const")
        s_nrow = [s for s, _ in gathers.start(range(UNROLL))]
        s_flags = sem("flags")

        src, dst, kind, wt = io["src"], io["dst"], io["edge_type_8"], io["edge_weight"]
        names = ["src", "dst", "prev", "next", "kind"]
        flat = {n: dram[f"{n}_rows"].rearrange("c e -> (c e)") for n in names + ["weight"]}
        tail = CHUNKS * P - N_EDGES
        n_flat = 13
        n_fill = 1 + 1 + 2 * BLOCKS

        def line(ap):
            return ap.rearrange("(a n) -> a n", a=1)

        gathers.count(range(UNROLL), N_TILES // UNROLL)
        gathers.count([UNROLL], 6 * BLOCKS)
        with nc.Block() as block:

            @block.gpsimd
            def _(pool):
                nc.gpsimd.memset(pad_int[:, 0, :], 0)
                nc.gpsimd.memset(pad_int[:, 1, :], OUT_OF_RANGE)
                nc.gpsimd.memset(pad_int[:, 2, :], -2)
                nc.gpsimd.memset(zeros[:, :], 0.0)
                nc.gpsimd.memset(minus_big[:, :], -BIG).then_inc(s_pads, 1)
                nc.gpsimd.memset(ident[:, :], 0.0)
                nc.gpsimd.memset(ones[:, :], 1.0)
                nc.gpsimd.memset(keep["eps"][:, :], LN_EPS)
                nc.gpsimd.memset(zero_row[:, :], 0.0)
                nc.gpsimd.iota(chunk_int[:, :], [[1, CHUNKS]], base=0, channel_multiplier=0)
                nc.gpsimd.iota(step_int[:, :], [[P, BLOCKS]], base=0, channel_multiplier=1)
                nc.gpsimd.iota(node_int[:, :], [[P, N_TILES]], base=0, channel_multiplier=1)
                nc.gpsimd.iota(iota_int[:, :], [[1, P]], base=0, channel_multiplier=0).then_inc(s_iota, 1)
                pool.wait_ge(s_iota, 1)
                nc.gpsimd.affine_select(out=ident[:, :], in_=ident[:, :], compare_op=ALU.not_equal, fill=1.0,
                                        base=0, pattern=[[-1, P]], channel_multiplier=1).then_inc(s_consts, 1)
                pool.wait_ge(s_index, 1)
                pool.wait_ge(s_flat, 16 * n_flat)
                for b in range(BLOCKS):
                    for j, n in enumerate(names):
                        nc.gpsimd.indirect_dma_start(
                            out=raw[:, j, b, :], out_offset=None, in_=dram[f"{n}_rows"],
                            in_offset=bass.IndirectOffsetOnAxis(ap=chunk_idx[:, b:b + 1], axis=0)).then_inc(s_rows, 16)
                    nc.gpsimd.indirect_dma_start(
                        out=weight[:, b, :], out_offset=None, in_=dram["weight_rows"],
                        in_offset=bass.IndirectOffsetOnAxis(ap=chunk_idx[:, b:b + 1], axis=0)).then_inc(s_rows, 16)
                with pool.Fori(0, N_TILES // UNROLL) as r:
                    pool.wait_ge(s_nidx, r * UNROLL + UNROLL)
                    pool.wait_ge(s_nused, r * UNROLL + UNROLL)
                    nc.gpsimd.tensor_copy(node_stage[:, :], node_chunk_idx[:, bass.ts(r, UNROLL)]).then_inc(s_ncopy, 1)
                    pool.wait_ge(s_ncopy, r + 1)
                    pool.sem_inc(s_const, 1)
                    for u in range(UNROLL):
                        nc.gpsimd.indirect_dma_start(
                            out=node_rows[:, u, :], out_offset=None, in_=dram["dst_rows"],
                            in_offset=bass.IndirectOffsetOnAxis(ap=node_stage[:, u:u + 1], axis=0)).then_inc(s_nrow[u], 16)

            @block.sync
            def _(sp):
                sp.wait_ge(s_pads, 1)
                for n, ap, pad in (("src", src, 0), ("dst", dst, 1), ("kind", kind, 0)):
                    sp.dma_start(line(flat[n][0:N_EDGES]), line(ap)).then_inc(s_flat, 16)
                    sp.dma_start(line(flat[n][N_EDGES:]), pad_int[:, pad, 0:tail]).then_inc(s_flat, 16)
                sp.dma_start(line(flat["weight"][0:N_EDGES]), line(wt)).then_inc(s_flat, 16)
                sp.dma_start(line(flat["weight"][N_EDGES:]), zeros[0:1, 0:tail]).then_inc(s_flat, 16)
                sp.dma_start(line(flat["prev"][0:1]), pad_int[:, 2, 0:1]).then_inc(s_flat, 16)
                sp.dma_start(line(flat["prev"][1:N_EDGES + 1]), line(dst)).then_inc(s_flat, 16)
                sp.dma_start(line(flat["prev"][N_EDGES + 1:]), pad_int[:, 2, 0:tail - 1]).then_inc(s_flat, 16)
                sp.dma_start(line(flat["next"][0:N_EDGES - 1]), line(dst[1:])).then_inc(s_flat, 16)
                sp.dma_start(line(flat["next"][N_EDGES - 1:]), pad_int[:, 2, 0:tail + 1]).then_inc(s_flat, 16)
                sp.dma_start(dram["x0"][0:N_NODES, :], io["x"]).then_inc(s_fill, 16)
                rest = N_PAD - N_NODES
                assert rest <= 2 * P
                sp.dma_start(dram["x0"][N_NODES:N_NODES + rest // 2, :], zeros[0:rest // 2, :]).then_inc(s_fill, 16)
                sp.dma_start(dram["x0"][N_NODES + rest // 2:, :], zeros[0:rest - rest // 2, :]).then_inc(s_fill, 16)
                for b in range(BLOCKS):
                    sp.dma_start(dram["first"][b * P * P:(b + 1) * P * P, :].rearrange("(p e) q -> p (e q)", p=P),
                                 minus_big[:, 0:P * GAT_HEADS]).then_inc(s_fill, 16)
                sp.wait_ge(s_flat, 16 * n_flat)
                with nc.allow_non_contiguous_dma(reason="one destination per chunk"):
                    sp.dma_start(ends[:, 0, :], dram["dst_rows"][:, 0:1].rearrange("c e -> e c")).then_inc(s_ends, 16)
                    sp.dma_start(ends[:, 1, :], dram["dst_rows"][:, P - 1:P].rearrange("c e -> e c")).then_inc(s_ends, 16)
                sp.wait_ge(s_flags, 1)
                by_head = dram["flags"].rearrange("(b p h) f e -> h p f b e", p=P, h=GAT_HEADS)
                for h in range(GAT_HEADS):
                    for f in range(5):
                        sp.dma_start(by_head[h][:, f], flags[:, f, :, :]).then_inc(s_fill, 16)
                with nc.allow_non_contiguous_dma(reason="one flag per step"):
                    for f, e in ((0, P - 1), (1, 0)):
                        sp.dma_start(dram["resets"][f].rearrange("(b p) -> p b", p=P), flags[:, 2 + f, :, e]).then_inc(s_fill, 16)
                sp.wait_ge(s_fill, 16 * (3 + BLOCKS + 5 * GAT_HEADS + 2))

            @block.vector
            def _(dve):
                dve.sem_inc(s_nused, UNROLL)
                c = Count(dve, s_dve)
                nc.vector.memset(keep["same_head"][:, :], 0.0)
                c.done(nc.vector.memset(keep["head_of"][:, :], 0.0))
                for h in range(P // MIX_DIM):
                    rows = slice(h * MIX_DIM, (h + 1) * MIX_DIM)
                    nc.vector.memset(keep["same_head"][rows, rows], 1.0)
                    nc.vector.memset(keep["head_of"][rows, h:h + 1], 1.0)
                dve.wait_ge(s_iota, 1)
                nc.vector.tensor_copy(chunk_no[:, :], chunk_int[:, :])
                nc.vector.tensor_copy(step_no[:, :], step_int[:, :])
                nc.vector.tensor_copy(node_no[:, :], node_int[:, :])
                c.done(nc.vector.tensor_copy(iota_row[:, :], iota_int[:, :]))
                nc.vector.tensor_scalar(keep["mask"][:, :], node_no[:, :], float(N_NODES), None, ALU.is_lt)
                dve.wait_ge(s_ends, 32)
                c.done(nc.vector.tensor_single_scalar(tile_int[:, :], ends[:, 0, :], 7, ALU.arith_shift_right))
                c.done(nc.vector.tensor_copy(path[:, 0, :], tile_int[:, :]))
                nc.vector.tensor_copy(path[:, 1, :], ends[:, 1, :])
                nc.vector.tensor_tensor(path[:, 0, :], path[:, 0, :], chunk_no[:, :], ALU.add).then_inc(s_path, 1)
                dve.wait_ge(s_bcast, 1)
                half = CHUNKS // 2
                for f in range(2):
                    for h in range(2):
                        last = nc.vector.tensor_copy(path_all[:, f, h * half:(h + 1) * half], bank[2 * f + h][:, 0:half])
                c.done(last)
                for b in range(BLOCKS):
                    last = nc.vector.tensor_scalar(junk[:, 0:CHUNKS - 1], path_all[:, 0, 1:CHUNKS], step_no[:, b:b + 1],
                                                   0.0, ALU.is_le, ALU.add, accum_out=chunk_of[:, b:b + 1])
                    c.done(last)
                nc.vector.tensor_copy(chunk_idx[:, :], chunk_of[:, :]).then_inc(s_index, 1)
                c.done(nc.vector.tensor_tensor(tile_of[:, :], step_no[:, :], chunk_of[:, :], ALU.subtract))
                nc.vector.tensor_scalar(first_of[:, :], tile_of[:, :], float(P), None, ALU.mult)
                c.done(nc.vector.tensor_scalar(tile_clip[:, :], tile_of[:, :], float(LAST_TILE), None, ALU.min))
                with dve.Fori(0, N_TILES) as t:
                    c.enter(t, 1)
                    c.done(nc.vector.tensor_scalar(junk[:, :], path_all[:, 1, :], node_no[:, bass.ts(t, 1)], 0.0,
                                                   ALU.is_lt, ALU.add, accum_out=node_chunk[:, bass.ts(t, 1)]))
                    nc.vector.tensor_copy(node_chunk_idx[:, bass.ts(t, 1)], node_chunk[:, bass.ts(t, 1)]).then_inc(s_nidx, 1)
                c.leave(N_TILES)
                dve.wait_ge(s_rows, 16 * 6 * BLOCKS)
                c.done(nc.vector.tensor_copy(as_f[:, :, :, :].rearrange("p j b e -> p (j b e)"),
                                             raw[:, :, :, :].rearrange("p j b e -> p (j b e)")))
                for b in range(BLOCKS):
                    last = nc.vector.tensor_scalar(rel[:, b, :], as_f[:, 1, b, :], first_of[:, b:b + 1], None, ALU.subtract)
                c.done(last)
                c.done(nc.vector.tensor_scalar(low[:, :, :], rel[:, :, :], 0.0, None, ALU.is_ge))
                c.done(nc.vector.scalar_tensor_tensor(valid[:, :, :], rel[:, :, :], float(P), low[:, :, :], ALU.is_lt, ALU.mult))
                c.done(nc.vector.scalar_tensor_tensor(as_f[:, 4, :, :], as_f[:, 4, :, :], float(N_PAD), as_f[:, 0, :, :],
                                                      ALU.mult, ALU.add))
                c.done(nc.vector.tensor_scalar(flags[:, 4, :, :], valid[:, :, :], -1.0, BIG, ALU.add, ALU.mult))
                for f in range(2):
                    c.done(nc.vector.tensor_tensor(differs[:, :, :], as_f[:, 1, :, :], as_f[:, 2 + f, :, :], ALU.not_equal))
                    c.done(nc.vector.tensor_tensor(differs[:, :, :], differs[:, :, :], valid[:, :, :], ALU.mult))
                    c.done(nc.vector.tensor_scalar(flags[:, f, :, :], differs[:, :, :], -BIG, None, ALU.mult))
                for b in range(BLOCKS):
                    nc.vector.tensor_tensor_scan(flags[:, 2, b, :], zero_row[:, :], flags[:, 0, b, :], 0.0, ALU.add, ALU.min)
                    last = nc.vector.tensor_tensor_scan(flags[:, 3, b, ::-1], zero_row[:, :], flags[:, 1, b, ::-1], 0.0,
                                                        ALU.add, ALU.min)
                c.done(last)
                c.done(nc.vector.tensor_scalar(differs[:, :, :], valid[:, :, :], -1.0, -float(OUT_OF_RANGE), ALU.add, ALU.mult))
                c.done(nc.vector.tensor_tensor(differs[:, :, :], differs[:, :, :], rel[:, :, :], ALU.add))
                c.done(nc.vector.tensor_reduce(step_min[:, 0, :], differs[:, :, :], AX.X, ALU.min))
                c.done(nc.vector.scalar_tensor_tensor(differs[:, :, :], flags[:, 0], OUT_OF_RANGE / BIG, differs[:, :, :], ALU.mult, ALU.add))
                c.done(nc.vector.tensor_reduce(step_min[:, 1, :], differs[:, :, :], AX.X, ALU.min))
                c.done(nc.vector.scalar_tensor_tensor(step_min[:, 1, :], step_min[:, 1, :], float(OUT_OF_RANGE), step_min[:, 0, :],
                                                      ALU.add, ALU.is_equal))
                nc.vector.scalar_tensor_tensor(step_min[:, 0, :], step_min[:, 1, :], float(OUT_OF_RANGE), step_min[:, 0, :],
                                               ALU.mult, ALU.add).then_inc(s_flags, 1)
                tables = (keep["src_tab"], keep["rel_tab"], keep["wt_tab"], keep["dst_tab"])
                for i in range(4 * BLOCKS):
                    j, b = i // BLOCKS, i % BLOCKS
                    dve.wait_ge(s_psum, i + 1)
                    nc.vector.tensor_copy(tables[j][:, b * P:(b + 1) * P], bank[i % 8][:, 0:P]).then_inc(s_tabs, 1)
                for b in range(BLOCKS):
                    dve.wait_ge(s_psum, 4 * BLOCKS + 1 + b)
                    nc.vector.tensor_copy(keep["tile_row"][:, b * P:(b + 1) * P], bank[b % 8][0:1, 128:256])
                    last = nc.vector.tensor_copy(cross_row[:, b * P:(b + 1) * P], bank[b % 8][0:1, 256:384])
                last.then_inc(s_tabs, 1)
                dve.wait_ge(s_psum, 5 * BLOCKS + 1)
                c.done(nc.vector.tensor_scalar(keep["cross"][:, :], bank[7][:, 0:WINDOWS], node_no[:, 0:1], None, ALU.is_equal))
                with dve.Fori(0, N_TILES // UNROLL) as r:
                    c.enter(r, 3 * UNROLL)
                    for u in range(UNROLL):
                        dve.wait_ge(s_nrow[u], r * 16 + 16)
                        c.done(nc.vector.tensor_copy(node_rows_f[:, u, :], node_rows[:, u, :]))
                        dve.sem_inc(s_nused, 1)
                        c.done(nc.vector.tensor_scalar(junk[:, 0:P], node_rows_f[:, u, :], node_no[:, bass.ds(r * UNROLL + u, 1)],
                                                       0.0, ALU.is_lt, ALU.add, accum_out=before[:, bass.ds(r * UNROLL + u, 1)]))
                        c.done(nc.vector.tensor_scalar(junk[:, 0:P], node_rows_f[:, u, :], node_no[:, bass.ds(r * UNROLL + u, 1)],
                                                       0.0, ALU.is_equal, ALU.max, accum_out=has[:, bass.ds(r * UNROLL + u, 1)]))
                c.leave(N_TILES // UNROLL)
                c.done(nc.vector.scalar_tensor_tensor(position[:, :], node_chunk[:, :], float(P), before[:, :], ALU.mult, ALU.add))
                nc.vector.tensor_scalar(keep["absent"][:, :], has[:, :], -1.0, BIG, ALU.add, ALU.mult)
                c.done(nc.vector.scalar_tensor_tensor(position[:, :], has[:, :], -float(OUT_OF_RANGE), position[:, :],
                                                      ALU.mult, ALU.add))
                for t in range(N_TILES):
                    last = nc.vector.tensor_scalar(position[:, t:t + 1], position[:, t:t + 1], float(OUT_OF_RANGE + P * t), None,
                                                   ALU.add)
                c.done(last)
                c.done(nc.vector.tensor_copy(keep["first_pos"][:, :], position[:, :]))

            @block.tensor
            def _(pe):
                pe.wait_ge(s_path, 1)
                pe.wait_ge(s_consts, 1)
                half = CHUNKS // 2
                for f in range(2):
                    for h in range(2):
                        last = nc.tensor.matmul(bank[2 * f + h][:, 0:half], ones[:, :], path[:, f, h * half:(h + 1) * half],
                                                start=True, stop=True)
                last.then_inc(s_bcast, 1)
                pe.wait_ge(s_flags, 1)
                sources = (as_f[:, 0], as_f[:, 4], weight, rel)
                for i in range(4 * BLOCKS):
                    j, b = i // BLOCKS, i % BLOCKS
                    if i >= 8:
                        pe.wait_ge(s_tabs, i - 7)
                    nc.tensor.transpose(bank[i % 8][:, 0:P], sources[j][:, b, :], ident[:, :]).then_inc(s_psum, 1)
                pe.wait_ge(s_tabs, 4 * BLOCKS)
                for b in range(BLOCKS):
                    nc.tensor.matmul(bank[b % 8][0:1, 128:256], tile_clip[:, b:b + 1], ident[:, :], start=True, stop=True)
                    nc.tensor.matmul(bank[b % 8][0:1, 256:384], step_min[:, 0, b:b + 1], ident[:, :],
                                     start=True, stop=True).then_inc(s_psum, 1)
                pe.wait_ge(s_tabs, 4 * BLOCKS + 1)
                nc.tensor.matmul(bank[7][:, 0:WINDOWS], ones[:, :], cross_row[:, 0:STEPS_RUN:WINDOW], start=True, stop=True).then_inc(s_psum, 1)



REL = 8
L0_FF, L1_FF = 1024, 256
MOE_E = 8
INNER = 512

_INS = ['x', 'src', 'dst', 'edge_type_8', 'edge_weight', 'L0_gnn_w_in', 'L0_gnn_b_in', 'L0_gnn_g_in', 'L0_gnn_bt_in',
        'L0_gnn_w_l', 'L0_gnn_a_s', 'L0_gnn_a_d', 'L0_gnn_b_l', 'L0_gnn_g_l', 'L0_gnn_bt_l',
        'L0_mix_Wq', 'L0_mix_bq', 'L0_mix_Wk', 'L0_mix_bk', 'L0_mix_Wv', 'L0_mix_bv', 'L0_mix_Wo', 'L0_mix_bo',
        'L0_mix_W1', 'L0_mix_b1', 'L0_mix_W2', 'L0_mix_b2', 'L0_mix_ln1_g', 'L0_mix_ln1_b', 'L0_mix_ln2_g', 'L0_mix_ln2_b',
        'L0_ffn_Wr', 'L0_ffn_br', 'L0_ffn_W1', 'L0_ffn_b1', 'L0_ffn_g1', 'L0_ffn_be1', 'L0_ffn_m1', 'L0_ffn_v1',
        'L0_ffn_W2', 'L0_ffn_b2', 'L0_ffn_g2', 'L0_ffn_be2', 'L0_ffn_m2', 'L0_ffn_v2', 'L0_ffn_Wo', 'L0_ffn_bo',
        'L1_gnn_weight', 'L1_mix_Wqkv', 'L1_mix_ln1_g', 'L1_mix_ln1_b', 'L1_mix_W1', 'L1_mix_b1', 'L1_mix_W2', 'L1_mix_b2',
        'L1_mix_ln2_g', 'L1_mix_ln2_b', 'L1_ffn_W_fx', 'L1_ffn_b_fx', 'L1_ffn_W_x', 'L1_ffn_b_x', 'L1_ffn_W_slice',
        'L1_ffn_b_slice', 'L1_ffn_W_q', 'L1_ffn_W_k', 'L1_ffn_W_v', 'L1_ffn_W_out', 'L1_ffn_b_out', 'L1_ffn_temperature']


class Normalise:

    def __init__(self, space, tag, eps):
        self.stats = space.sb(f"{tag}_stats", [P, UNROLL, PAIR, 6])
        self.mv = space.sb(f"{tag}_mv", [P, UNROLL, PAIR, 2])
        self.std = space.sb(f"{tag}_std", [P, UNROLL, PAIR])
        self.rstd = space.sb(f"{tag}_rstd", [P, UNROLL, PAIR])
        self.eps = eps
        self.s_stats, self.s_mv = space.sem(f"{tag}_s_stats"), space.sem(f"{tag}_s_mv")
        self.s_go = space.sem(f"{tag}_s_go")
        self.s_std, self.s_rstd = space.sem(f"{tag}_s_std"), space.sem(f"{tag}_s_rstd")

    def statistics(self, nc, u, n, data):
        for i in range(PAIR):
            last = nc.vector.bn_stats(self.stats[:, u, i, :], data[:, i, :])
        last.then_inc(self.s_stats, 1)

    def aggregate(self, nc, u, n):
        nc.vector.wait_ge(self.s_stats, n)
        nc.vector.sem_inc(self.s_go, 1)
        for i in range(PAIR):
            last = nc.vector.bn_aggr(self.mv[:, u, i, :], self.stats[:, u, i, :])
        last.then_inc(self.s_mv, 1)

    def root(self, nc, u, n):
        nc.scalar.wait_ge(self.s_mv, n)
        nc.scalar.activation(self.std[:, u, :], self.mv[:, u, :, 1], ACT.Sqrt, bias=self.eps[:, 0:1]).then_inc(self.s_std, 1)

    def invert(self, nc, u, n):
        nc.vector.wait_ge(self.s_std, n)
        nc.vector.reciprocal(self.rstd[:, u, :], self.std[:, u, :]).then_inc(self.s_rstd, 1)

    def scale(self, nc, u, n, out, data):
        nc.vector.wait_ge(self.s_rstd, n)
        for i in range(PAIR):
            last = nc.vector.tensor_scalar(out[:, i, :], data[:, i, :], self.mv[:, u, i, 0:1], self.rstd[:, u, i:i + 1],
                                           ALU.subtract, ALU.mult)
        return last


def transpose_pair(nc, bank, data, ident):
    for i in range(PAIR):
        for a in range(HALVES):
            last = nc.tensor.transpose(bank[:, a * D + i * P:a * D + i * P + P], data[:, i, a * P:(a + 1) * P], ident[:, :])
    return last


def project_pair(nc, bank, data_t, weight):
    for i in range(PAIR):
        for a in range(HALVES):
            last = nc.tensor.matmul(bank[:, i * D:(i + 1) * D], data_t[:, a, i * P:(i + 1) * P], weight[:, a, :],
                                    start=(a == 0), stop=(a == HALVES - 1))
    return last


def pair_rows(ap):
    return ap.rearrange("(t p) d -> p t d", p=P)


def both(rows):
    return rows.unsqueeze(1).to_broadcast([P, PAIR, rows.shape[-1]])


def gnn_input(nc, io, dram, keep):
    with ExitStack() as stack:
        space = Space(nc, stack, "gin")
        sb, sem = space.sb, space.sem
        w = sb("w", [P, HALVES, D])
        rows = {n: sb(n, [P, D]) for n in ("b_in", "g_in", "bt_in")}
        x = sb("x", [P, UNROLL, PAIR, D])
        xn = sb("xn", [P, UNROLL, PAIR, D])
        xt = sb("xt", [P, UNROLL, HALVES, PAIR * P])
        y = sb("y", [P, UNROLL, PAIR, D])
        neg = sb("neg", [P, UNROLL, PAIR, D])
        bank = [space.ps(f"bank{u}", [P, 512]) for u in range(UNROLL)]
        ln0, ln1 = Normalise(space, "ln0", keep["eps"]), Normalise(space, "ln1", keep["eps"])
        s_w, s_x, s_sent, s_free = sem("s_w"), space.sems("s_x", UNROLL), space.sems("s_sent", UNROLL), sem("s_free")
        s_out = sem("s_out")
        s_xn, s_xt, s_xtc, s_y, s_yb, s_yn = (sem(n) for n in ("s_xn", "s_xt", "s_xtc", "s_y", "s_yb", "s_yn"))
        s_yg, s_ya, s_neg, s_exp, s_pos = (sem(n) for n in ("s_yg", "s_ya", "s_neg", "s_exp", "s_pos"))
        tiles, hidden = pair_rows(dram["x0"]), pair_rows(dram["hidden"])
        with nc.Block() as block:

            @block.sync
            def _(sp):
                sp.dma_start(w[:, :, :], io["L0_gnn_w_in"].rearrange("(a p) n -> p a n", p=P)).then_inc(s_w, 16)
                for n, t in rows.items():
                    sp.dma_start(t[:, :], rows_of(io[f"L0_gnn_{n}"])).then_inc(s_w, 16)
                with sp.Fori(0, ROUNDS) as r:
                    for u in range(UNROLL):
                        n = r * UNROLL + u + 1
                        sp.wait_ge(s_free, n)
                        sp.dma_start(x[:, u, :, :], tiles[:, bass.ds(r * (UNROLL * PAIR) + u * PAIR, PAIR), :]).then_inc(s_x[u], 16)
                    for u in range(UNROLL):
                        sp.wait_ge(s_out, r * UNROLL + u + 1)
                        sp.dma_start(hidden[:, bass.ds(r * (UNROLL * PAIR) + u * PAIR, PAIR), :], y[:, u, :, :]).then_inc(s_sent[u], 16)
                    for u in range(UNROLL):
                        sp.wait_ge(s_sent[u], r * 16 + 16)
                        sp.sem_inc(s_free, 1)

            @block.vector
            def _(dve):
                dve.sem_inc(s_free, UNROLL)
                dve.wait_ge(s_w, 64)
                with dve.Fori(0, ROUNDS) as r:
                    at = lambda u: r * UNROLL + u + 1
                    for u in range(UNROLL):
                        dve.wait_ge(s_x[u], r * 16 + 16)
                        ln0.statistics(nc, u, at(u), x[:, u])
                    for u in range(UNROLL):
                        ln0.aggregate(nc, u, at(u))
                    for u in range(UNROLL):
                        ln0.invert(nc, u, at(u))
                    for u in range(UNROLL):
                        ln0.scale(nc, u, at(u), xn[:, u], x[:, u]).then_inc(s_xn, 1)
                    for u in range(UNROLL):
                        dve.wait_ge(s_y, at(u))
                        nc.vector.tensor_tensor(y[:, u], bank[u][:, :].rearrange("p (i d) -> p i d", i=PAIR), both(rows["b_in"][:, :]),
                                                ALU.add).then_inc(s_yb, 1)
                    for u in range(UNROLL):
                        dve.wait_ge(s_yb, at(u))
                        ln1.statistics(nc, u, at(u), y[:, u])
                    for u in range(UNROLL):
                        ln1.aggregate(nc, u, at(u))
                    for u in range(UNROLL):
                        ln1.invert(nc, u, at(u))
                    for u in range(UNROLL):
                        ln1.scale(nc, u, at(u), y[:, u], y[:, u]).then_inc(s_yn, 1)
                    for u in range(UNROLL):
                        dve.wait_ge(s_ya, at(u))
                        nc.vector.tensor_scalar(neg[:, u], y[:, u], 0.0, None, ALU.min).then_inc(s_neg, 1)
                    for u in range(UNROLL):
                        nc.vector.tensor_scalar(y[:, u], y[:, u], 0.0, -1.0, ALU.max, ALU.add).then_inc(s_pos, 1)
                    for u in range(UNROLL):
                        dve.wait_ge(s_exp, at(u))
                        dve.wait_ge(s_pos, at(u))
                        nc.vector.tensor_tensor(y[:, u], y[:, u], neg[:, u], ALU.add).then_inc(s_out, 1)

            @block.scalar
            def _(act):
                with act.Fori(0, ROUNDS) as r:
                    at = lambda u: r * UNROLL + u + 1
                    for u in range(UNROLL):
                        ln0.root(nc, u, at(u))
                    for u in range(UNROLL):
                        act.wait_ge(s_xt, at(u))
                        nc.scalar.copy(xt[:, u].rearrange("p a n -> p (a n)"), bank[u][:, :]).then_inc(s_xtc, 1)
                    for u in range(UNROLL):
                        ln1.root(nc, u, at(u))
                    for u in range(UNROLL):
                        act.wait_ge(s_neg, at(u))
                        nc.scalar.activation(neg[:, u], neg[:, u], ACT.Exp).then_inc(s_exp, 1)

            @block.tensor
            def _(pe):
                pe.wait_ge(s_w, 64)
                with pe.Fori(0, ROUNDS) as r:
                    at = lambda u: r * UNROLL + u + 1
                    for u in range(UNROLL):
                        pe.wait_ge(s_xn, at(u))
                        transpose_pair(nc, bank[u], xn[:, u], keep["ident"]).then_inc(s_xt, 1)
                    for u in range(UNROLL):
                        pe.wait_ge(s_xtc, at(u))
                        project_pair(nc, bank[u], xt[:, u], w).then_inc(s_y, 1)

            @block.gpsimd
            def _(pool):
                pool.wait_ge(s_w, 64)
                with pool.Fori(0, ROUNDS) as r:
                    at = lambda u: r * UNROLL + u + 1
                    for u in range(UNROLL):
                        pool.wait_ge(s_yn, at(u))
                        nc.gpsimd.tensor_tensor(y[:, u], y[:, u], both(rows["g_in"][:, :]), ALU.mult).then_inc(s_yg, 1)
                        pool.wait_ge(s_yg, at(u))
                        nc.gpsimd.tensor_tensor(y[:, u], y[:, u], both(rows["bt_in"][:, :]), ALU.add).then_inc(s_ya, 1)


def gat_project(nc, io, dram, keep, layer, scores):
    with ExitStack() as stack:
        space = Space(nc, stack, f"gp{layer}")
        sb, sem = space.sb, space.sem
        w = sb("w", [P, HALVES, D])
        a = sb("a", [P, 2, D])
        prod = sb("prod", [P, HALVES, 2, D])
        wa = sb("wa", [P, HALVES, 2 * GAT_HEADS])
        h = sb("h", [P, UNROLL, PAIR, D])
        ht = sb("ht", [P, UNROLL, HALVES, PAIR * P])
        row = sb("row", [P, UNROLL, PAIR, GAT_ROW])
        bank = [space.ps(f"bank{u}", [P, 512]) for u in range(UNROLL)]
        score_bank = [space.ps(f"score_bank{i}", [P, 512]) for i in range(3)]
        s_w, s_prod, s_wa, s_ht, s_htc = (sem(n) for n in ("s_w", "s_prod", "s_wa", "s_ht", "s_htc"))
        s_h = space.sems("s_h", UNROLL)
        s_mm, s_row, s_sc, s_sent, s_used = sem("s_mm"), sem("s_row"), sem("s_sc"), space.sems("s_sent", UNROLL), sem("s_used")
        feat, hidden = pair_rows(dram["feat"]), pair_rows(dram["hidden"])
        with nc.Block() as block:

            @block.sync
            def _(sp):
                sp.dma_start(w[:, :, :], io["L0_gnn_w_l"][layer].rearrange("(a p) n -> p a n", p=P)).then_inc(s_w, 16)
                for j, n in enumerate(("a_s", "a_d")):
                    sp.dma_start(a[:, j, :], rows_of(io[f"L0_gnn_{n}"][layer].rearrange("h d -> (h d)"))).then_inc(s_w, 16)
                sp.sem_inc(s_used, UNROLL)
                with sp.Fori(0, ROUNDS) as r:
                    for u in range(UNROLL):
                        sp.wait_ge(s_used, r * UNROLL + u + 1)
                        sp.dma_start(h[:, u, :, :], hidden[:, bass.ds(r * (UNROLL * PAIR) + u * PAIR, PAIR), :]).then_inc(s_h[u], 16)
                    for u in range(UNROLL):
                        n = r * UNROLL + u + 1
                        sp.wait_ge(s_row, n + UNROLL)
                        sp.wait_ge(s_sc, n + UNROLL)
                        sp.dma_start(feat[:, bass.ds(r * (UNROLL * PAIR) + u * PAIR, PAIR), :], row[:, u, :, :]).then_inc(s_sent[u], 16)
                    for u in range(UNROLL):
                        sp.wait_ge(s_sent[u], r * 16 + 16)
                        sp.sem_inc(s_used, 1)

            @block.vector
            def _(dve):
                dve.sem_inc(s_sc, UNROLL)
                dve.wait_ge(s_w, 48)
                for i in range(HALVES):
                    for j in range(2):
                        last = nc.vector.tensor_tensor(prod[:, i, j, :], w[:, i, :], a[:, j, :], ALU.mult)
                last.then_inc(s_prod, 1)
                dve.wait_ge(s_prod, 1)
                nc.vector.tensor_reduce(wa[:, :, :].rearrange("p i s -> p (i s)"),
                                        prod[:, :, :, :].rearrange("p i j (h d) -> p (i j h) d", d=GAT_DIM), AX.X, ALU.add).then_inc(s_wa, 1)
                with dve.Fori(0, ROUNDS) as r:
                    for u in range(UNROLL):
                        n = r * UNROLL + u + 1
                        pair = bass.ds(r * (UNROLL * PAIR) + u * PAIR, PAIR)
                        dve.wait_ge(s_mm, n)
                        dve.wait_ge(s_used, n)
                        sc = score_bank[u % 3][:, 0:16].rearrange("p (i s) -> p i s", i=PAIR)
                        nc.vector.tensor_copy(row[:, u, :, D:], sc[:, :, 0:GAT_HEADS])
                        nc.vector.tensor_copy(scores[:, pair, :], sc).then_inc(s_sc, 1)

            @block.scalar
            def _(act):
                act.sem_inc(s_row, UNROLL)
                with act.Fori(0, ROUNDS) as r:
                    for u in range(UNROLL):
                        n = r * UNROLL + u + 1
                        act.wait_ge(s_ht, n)
                        nc.scalar.copy(ht[:, u].rearrange("p a n -> p (a n)"), bank[u][:, :]).then_inc(s_htc, 1)
                    for u in range(UNROLL):
                        n = r * UNROLL + u + 1
                        act.wait_ge(s_mm, n)
                        act.wait_ge(s_used, n)
                        nc.scalar.copy(row[:, u, :, 0:D], bank[u][:, :].rearrange("p (i d) -> p i d", i=PAIR)).then_inc(s_row, 1)

            @block.tensor
            def _(pe):
                pe.wait_ge(s_wa, 1)
                with pe.Fori(0, ROUNDS) as r:
                    for u in range(UNROLL):
                        pe.wait_ge(s_h[u], r * 16 + 16)
                        transpose_pair(nc, bank[u], h[:, u], keep["ident"]).then_inc(s_ht, 1)
                    for u in range(UNROLL):
                        pe.wait_ge(s_htc, r * UNROLL + u + 1)
                        project_pair(nc, bank[u], ht[:, u], w)
                        pe.wait_ge(s_sc, r * UNROLL + (4, 5, 3, 6, 7)[u])
                        for i in range(PAIR):
                            c = 8 * i
                            for k in range(HALVES):
                                last = nc.tensor.matmul(score_bank[u % 3][:, c:c + 8], ht[:, u, k, i * P:(i + 1) * P], wa[:, k, :],
                                                        start=(k == 0), stop=(k == HALVES - 1))
                        last.then_inc(s_mm, 1)


def gat_spread(nc, dram, keep, gathers, layer, scores, d_edge):
    H = GAT_HEADS
    R = N_TILES // UNROLL
    with ExitStack() as stack:
        space = Space(nc, stack, f"sp{layer}")
        sb, sem = space.sb, space.sem
        starts = sb("starts", [P, 2, BLOCKS, P])
        resets = sb("resets", [1, STEPS_PAD])
        seg = sb("seg", [P, BLOCKS, P, H])
        carry_row = sb("carry_row", [1, H, STEPS_PAD])
        chain = sb("chain", [1, H, STEPS_PAD + 1])
        carry = sb("carry", [P, BLOCKS, H])
        node_score = sb("node_score", [P, UNROLL, H])
        node_pos = sb("node_pos", [P, UNROLL], I32)
        bank = [space.ps(f"bank{i}", [P, 512]) for i in range(8)]
        s_sent = gathers.start(range(UNROLL))
        gathers.count(range(UNROLL), R)
        s_load, s_copy, s_free, s_dummy, s_seg, s_dve, s_last, s_row, s_chain, s_col, s_spread, s_turn, s_out = (
            sem(n) for n in ("s_load", "s_copy", "s_free", "s_dummy", "s_seg", "s_dve", "s_last", "s_row", "s_chain", "s_col", "s_spread",
                             "s_turn", "s_out"))
        first = dram["first"].rearrange("(b p e) q -> p b (e q)", p=P, e=P)
        flags = dram["flags"].rearrange("(b p h) f e -> h p f b e", p=P, h=H)[0]

        with nc.Block() as block:

            @block.gpsimd
            def _(pool):
                with pool.Fori(0, R) as r:
                    pool.wait_ge(s_free, r * UNROLL + UNROLL)
                    nc.gpsimd.tensor_copy(node_score[:, :, :], scores[:, bass.ts(r, UNROLL), H:])
                    nc.gpsimd.tensor_copy(node_pos[:, :], keep["first_pos"][:, bass.ts(r, UNROLL)]).then_inc(s_copy, 1)
                    pool.wait_ge(s_copy, r + 1)
                    pool.sem_inc(s_dummy, 1)
                    for u in range(UNROLL):
                        nc.gpsimd.indirect_dma_start(
                            out=dram["first"], out_offset=bass.IndirectOffsetOnAxis(ap=node_pos[:, u:u + 1], axis=0),
                            in_=node_score[:, u, :], in_offset=None, bounds_check=STEPS_PAD * P - 1,
                            oob_is_err=False).then_inc(s_sent[u][0], 16)

            @block.sync
            def _(sp):
                sp.dma_start(starts[:, 0], flags[:, 0]).then_inc(s_load, 16)
                sp.dma_start(starts[:, 1], flags[:, 2]).then_inc(s_load, 16)
                sp.dma_start(resets[:, :], dram["resets"][0:1, :]).then_inc(s_load, 16)
                sp.sem_inc(s_free, UNROLL)
                with sp.Fori(0, R) as r:
                    for u in range(UNROLL):
                        sp.wait_ge(s_sent[u][0], r * 16 + (s_sent[u][1] + 16))
                        sp.sem_inc(s_free, 1)
                sp.wait_ge(s_free, UNROLL + N_TILES)
                sp.dma_start(seg[:, :, :, :].rearrange("p b e q -> p b (e q)"), first).then_inc(s_seg, 16)

            @block.vector
            def _(dve):
                c = Count(dve, s_dve)
                c.done(nc.vector.memset(chain[:, :, 0:1], -BIG))
                dve.wait_ge(s_load, 48)
                dve.wait_ge(s_seg, 16)
                for b in range(BLOCKS):
                    for h in range(H):
                        last = nc.vector.tensor_tensor_scan(seg[:, b, :, h], starts[:, 0, b, :], seg[:, b, :, h], -BIG, ALU.add, ALU.max)
                    last.then_inc(s_last, 1)
                for b in range(BLOCKS):
                    dve.wait_ge(s_row, b + 1)
                    last = nc.vector.tensor_copy(carry_row[:, :, b * P:(b + 1) * P], bank[b][0:1, :].rearrange("o (h k) -> o h k", h=H))
                c.done(last)
                for h in range(H):
                    last = nc.vector.tensor_tensor_scan(chain[:, h, 1:], resets[:, :], carry_row[:, h, :], -BIG, ALU.add, ALU.max)
                last.then_inc(s_chain, 1)
                dve.wait_ge(s_col, 1)
                c.done(nc.vector.tensor_copy(carry[:, :, :], bank[7][:, 0:BLOCKS * H].rearrange("p (b h) -> p b h", b=BLOCKS)))
                for b in range(BLOCKS):
                    for h in range(H):
                        last = nc.vector.scalar_tensor_tensor(seg[:, b, :, h], starts[:, 1, b, :], carry[:, b, h:h + 1], seg[:, b, :, h],
                                                              ALU.add, ALU.max)
                    last.then_inc(s_spread, 1)
                for b in range(BLOCKS):
                    dve.wait_ge(s_turn, b + 1)
                    nc.vector.tensor_copy(d_edge[:, b * P:(b + 1) * P, :].rearrange("p k h -> p h k"),
                                          bank[b][:, :].rearrange("p (h k) -> p h k", h=H))

            @block.tensor
            def _(pe):
                ident = keep["ident"]
                for b in range(BLOCKS):
                    pe.wait_ge(s_last, b + 1)
                    for h in range(H):
                        last = nc.tensor.transpose(bank[b][0:1, h * P:(h + 1) * P], seg[:, b, P - 1:P, h], ident[:, :])
                    last.then_inc(s_row, 1)
                pe.wait_ge(s_chain, 1)
                for b in range(BLOCKS):
                    for h in range(H):
                        q = b * H + h
                        last = nc.tensor.transpose(bank[7][:, q:q + 1], chain[:, h, b * P:(b + 1) * P], ident[0:1, 0:1])
                last.then_inc(s_col, 1)
                for b in range(BLOCKS):
                    pe.wait_ge(s_spread, b + 1)
                    for h in range(H):
                        last = nc.tensor.transpose(bank[b][:, h * P:(h + 1) * P], seg[:, b, :, h], ident[:, :])
                    last.then_inc(s_turn, 1)




def add_messages(nc, keep, gathers, table, acc):
    GROUP = 4
    BANKS = 8
    LAG = 3
    with ExitStack() as stack:
        space = Space(nc, stack, "rm")
        sb, sem = space.sb, space.sem
        got = sb("got", [P, SLOTS, D])
        idx = sb("idx", [P, SLOTS], I32)
        onehot = sb("onehot", [P, SLOTS, P])
        bank = [space.ps(f"bank{u}", [P, 512]) for u in range(BANKS)]
        s_got, s_idx, s_dummy = gathers.start(range(SLOTS)), sem("s_idx"), sem("s_dummy")
        gathers.count(range(SLOTS), STEP_ROUNDS)
        s_hot, s_sum, s_acc, s_zero = sem("s_hot"), sem("s_sum"), sem("s_acc"), sem("s_zero")
        with nc.Block() as block:

            @block.gpsimd
            def _(pool):
                with pool.Fori(0, STEP_ROUNDS) as r:
                    for q in range(SLOTS // GROUP):
                        group = slice(q * GROUP, (q + 1) * GROUP)
                        pool.wait_ge(s_sum, r * SLOTS + (q + 1) * GROUP)
                        nc.gpsimd.tensor_copy(idx[:, group], keep["rel_tab"][:, bass.ds(r * SLOTS + q * GROUP, GROUP)]).then_inc(s_idx, 1)
                        pool.wait_ge(s_idx, r * (SLOTS // GROUP) + q + 1)
                        pool.sem_inc(s_dummy, 1)
                        for u in range(q * GROUP, (q + 1) * GROUP):
                            nc.gpsimd.indirect_dma_start(
                                out=got[:, u, :], out_offset=None, in_=table,
                                in_offset=bass.IndirectOffsetOnAxis(ap=idx[:, u:u + 1], axis=0)).then_inc(s_got[u][0], 16)

            @block.vector
            def _(dve):
                dve.sem_inc(s_acc, BANKS)
                nc.vector.memset(acc[:, :, :], 0.0).then_inc(s_zero, 1)
                dve.wait_ge(s_zero, 1)

                def prepare(r, u):
                    k = bass.ds(r * SLOTS + u, 1)
                    dve.wait_ge(s_sum, r * SLOTS + u + 1)
                    nc.vector.tensor_scalar(onehot[:, u, :], keep["iota_row"][:, :], keep["dst_tab"][:, k], keep["wt_tab"][:, k],
                                            ALU.is_equal, ALU.mult).then_inc(s_hot, 1)

                def add(r, u, tile):
                    n = r * SLOTS + u + 1
                    dve.wait_ge(s_sum, n + SLOTS)
                    dve.wait_ge(s_acc, n + BANKS - 1)
                    rows = acc[:, bass.ds(tile, 1), :].rearrange("p t d -> p (t d)")
                    nc.vector.tensor_tensor(rows, rows, bank[u % BANKS][:, 0:D], ALU.add).then_inc(s_acc, 1)

                with dve.Fori(0, STEP_ROUNDS) as r:
                    _, tiles = nc.values_load_multi_w_load_instructions(
                        keep["tile_row"][0:1, bass.ds(r * SLOTS, SLOTS)], engines=[mybir.EngineType.DVE], min_val=0,
                        max_val=LAST_TILE)
                    for u in range(SLOTS + LAG):
                        if u < SLOTS:
                            prepare(r, u)
                        if u >= LAG:
                            add(r, u - LAG, tiles[u - LAG])

            @block.tensor
            def _(pe):
                pe.sem_inc(s_sum, SLOTS)
                with pe.Fori(0, STEP_ROUNDS) as r:
                    for u in range(SLOTS):
                        n = r * SLOTS + u + 1
                        pe.wait_ge(s_hot, n)
                        pe.wait_ge(s_acc, n)
                        pe.wait_ge(s_got[u][0], r * 16 + (s_got[u][1] + 16))
                        nc.tensor.matmul(bank[u % BANKS][:, 0:D], onehot[:, u, :], got[:, u, :], start=True, stop=True).then_inc(s_sum, 1)


def gat_messages(nc, dram, keep, gathers, layer, d_edge, acc):
    W, H, B = WINDOW, GAT_HEADS, WINDOW_BUFS
    WH = W * H
    GROUP = 7
    HOTS = W // 2
    BANKS = 4
    LAG = 3
    assert W % GROUP == 0 and W % BANKS == 0
    DVE_AT = dict(zip((0, 4, 8, 12, 16, 20, 25), "ABCDEFG"))
    PE_AT = dict(zip((1, 5, 9, 13, 17, 22), "ABCDEF"))
    ACT_AT = dict(zip((18, 21), "EF"))
    with ExitStack() as stack:
        space = Space(nc, stack, f"gm{layer}")
        sb, sem = space.sb, space.sem
        got = sb("got", [P, B, W, GAT_SUM])
        idx = sb("idx", [P, B, W], I32)
        flags = sb("flags", [WH, B, 5, P])
        resets = sb("resets", [1, B, 2, W])
        onehot = sb("onehot", [P, HOTS, P])
        e = sb("e", [P, W, H])
        seg, top, weight, last_top = (sb(n, [WH, P]) for n in ("seg", "top", "weight", "last_top"))
        chain = sb("chain", [1, 2, W + 1, H])
        carry = sb("carry", [WH, 2])
        fall = sb("fall", [1, H])
        rescale = sb("rescale", [P, H])
        ones = sb("ones", [1, P])
        bank = [space.ps(f"bank{i}", [P, 512]) for i in range(BANKS)]
        bank_e, bank_c, bank_w = (space.ps(n, [P, 512]) for n in ("bank_e", "bank_c", "bank_w"))
        s_got = gathers.start(range(B))
        gathers.count(range(B), (WINDOWS // B) * W)
        s_flags = space.sems("s_flags", B)
        names = ("s_idx", "s_dummy", "s_hot", "s_scaled", "s_sum", "s_acc", "s_zero", "s_dve", "s_e", "s_et", "s_fwd", "s_fwd_row",
                 "s_chain", "s_carry", "s_back", "s_back_row", "s_back_chain", "s_back_carry", "s_fall", "s_factor", "s_diff", "s_exp",
                 "s_last", "s_turn", "s_weights", "s_rescale", "s_rescaled", "s_used", "s_turns")
        (s_idx, s_dummy, s_hot, s_scaled, s_sum, s_acc, s_zero, s_dve, s_e, s_et, s_fwd, s_fwd_row, s_chain, s_carry, s_back, s_back_row,
         s_back_chain, s_back_carry, s_fall, s_factor, s_diff, s_exp, s_last, s_turn, s_weights, s_rescale, s_rescaled, s_used, s_turns) = (
            sem(n) for n in names)
        ident = keep["ident"]
        flag_rows = dram["flags"].rearrange("k f e -> k (f e)")
        AHEAD = B * W

        def windows(r):
            return [((r, c), (r, c - 1)) for c in range(1, B + 1)]

        def number(w):
            return w[0] * B + w[1]

        def loaded(w, per):
            return w[0] * per + (w[1] // B + 1) * per

        def program(engine, softmax_part, sum_step, at):
            def both_parts(w, v):
                for i in range(W):
                    if w is not None and i in at:
                        softmax_part(at[i], w)
                    if v is not None:
                        sum_step(v, i)

            both_parts((0, 0), None)
            with engine.Fori(0, WINDOWS // B - 1) as r:
                for w, v in windows(r):
                    both_parts(w, v)
            end = WINDOWS // B - 1
            for w, v in windows(end)[:-1]:
                both_parts(w, v)
            both_parts(None, (end, B - 1))

        with nc.Block() as block:

            @block.gpsimd
            def _(pool):
                with pool.Fori(0, WINDOWS // B) as r:
                    for b in range(B):
                        w = r * B + b
                        for g in range(W // GROUP):
                            group = slice(g * GROUP, (g + 1) * GROUP)
                            pool.wait_ge(s_sum, w * W + (g + 1) * GROUP)
                            nc.gpsimd.tensor_copy(idx[:, b, group], keep["src_tab"][:, bass.ds(w * W + g * GROUP, GROUP)]).then_inc(s_idx, 1)
                            pool.wait_ge(s_idx, w * (W // GROUP) + (g + 1))
                            pool.sem_inc(s_dummy, 1)
                            for k in range(g * GROUP, (g + 1) * GROUP):
                                nc.gpsimd.indirect_dma_start(
                                    out=got[:, b, k, 0:GAT_ROW], out_offset=None, in_=dram["feat"],
                                    in_offset=bass.IndirectOffsetOnAxis(ap=idx[:, b, k:k + 1], axis=0)).then_inc(s_got[b][0], 16)

            @block.sync
            def _(sp):
                with sp.Fori(0, WINDOWS // B) as r:
                    for b in range(B):
                        sp.wait_ge(s_used, r * B + b + 1)
                        sp.dma_start(flags[:, b].rearrange("k f e -> k (f e)"), flag_rows[bass.ds(r * (B * WH) + b * WH, WH), :]).then_inc(s_flags[b], 16)
                        sp.dma_start(resets[:, b, :, :].rearrange("o f k -> o f k"),
                                     dram["resets"][:, bass.ds(r * (B * W) + b * W, W)].unsqueeze(0)).then_inc(s_flags[b], 16)

            @block.vector
            def _(dve):
                dve.sem_inc(s_acc, BANKS)
                dve.sem_inc(s_used, B)
                nc.vector.memset(chain[:, :, :, :], -BIG)
                nc.vector.memset(ones[:, :], 1.0)
                nc.vector.memset(acc[:, :, :], 0.0).then_inc(s_zero, 1)
                dve.wait_ge(s_zero, 1)
                PER = 9
                c = Count(dve, s_dve)
                tiles = {}

                def softmax_part(name, w):
                    n, b = number(w) + 1, w[1] % B
                    if name == "A":
                        c.base, c.n = number(w) * PER, 0
                        dve.wait_ge(s_got[b][0], loaded(w, 16 * W) + s_got[b][1])
                        c.done(nc.vector.tensor_tensor(e[:, :, :], got[:, b, :, D:GAT_ROW], d_edge[:, bass.ds(number(w) * W, W), :], ALU.add))
                        nc.vector.scalar_tensor_tensor(e[:, :, :], e[:, :, :], 0.2, e[:, :, :], ALU.mult, ALU.max).then_inc(s_e, 1)
                    elif name == "B":
                        dve.wait_ge(s_et, n)
                        dve.wait_ge(s_flags[b], loaded(w, 32))
                        c.done(nc.vector.tensor_tensor(seg[:, :], bank_e[0:WH, 0:P], flags[:, b, 4, :], ALU.add))
                        nc.vector.tensor_tensor_scan(seg[:, :], flags[:, b, 0, :], seg[:, :], -BIG, ALU.add, ALU.max).then_inc(s_fwd, 1)
                    elif name == "C":
                        dve.wait_ge(s_fwd_row, n)
                        for h in range(H):
                            last = nc.vector.tensor_tensor_scan(chain[:, 0, 1:, h], resets[:, b, 0, :], bank_c[0:1, h:WH:H], chain[:, 0, 0:1, h],
                                                                ALU.add, ALU.max)
                        last.then_inc(s_chain, 1)
                    elif name == "D":
                        dve.wait_ge(s_carry, n)
                        c.done(nc.vector.tensor_copy(carry[:, 0:1], bank_c[0:WH, 256:257]))
                        c.done(nc.vector.scalar_tensor_tensor(seg[:, :], flags[:, b, 2, :], carry[:, 0:1], seg[:, :], ALU.add, ALU.max))
                        nc.vector.tensor_tensor_scan(top[:, ::-1], flags[:, b, 1, ::-1], seg[:, ::-1], -BIG, ALU.add, ALU.max).then_inc(s_back, 1)
                    elif name == "E":
                        dve.wait_ge(s_back_row, n)
                        for h in range(H):
                            last = nc.vector.tensor_tensor_scan(chain[:, 1, W - 1::-1, h], resets[:, b, 1, ::-1], bank_c[0:1, WH - H + h::-H][:, 0:W],
                                                                -BIG, ALU.add, ALU.max)
                        last.then_inc(s_back_chain, 1)
                        dve.wait_ge(s_back_chain, n)
                        c.done(nc.vector.tensor_tensor(fall[:, :], chain[:, 0, 0, :], chain[:, 1, 0, :], ALU.subtract))
                        nc.vector.tensor_scalar(fall[:, :], fall[:, :], 0.0, None, ALU.min).then_inc(s_fall, 1)
                        c.done(nc.vector.tensor_copy(chain[:, 0, 0, :], chain[:, 0, W, :]))
                    elif name == "F":
                        dve.wait_ge(s_back_carry, n)
                        c.done(nc.vector.tensor_copy(carry[:, 1:2], bank_c[0:WH, 256:257]))
                        c.done(nc.vector.scalar_tensor_tensor(top[:, :], flags[:, b, 3, :], carry[:, 1:2], top[:, :], ALU.add, ALU.max))
                        c.done(nc.vector.tensor_tensor(weight[:, :], bank_e[0:WH, 0:P], top[:, :], ALU.subtract))
                        nc.vector.tensor_scalar(weight[:, :], weight[:, :], 0.0, None, ALU.min).then_inc(s_diff, 1)
                        nc.vector.scalar_tensor_tensor(last_top[:, :], flags[:, b, 1, :], -1.0 / BIG, top[:, :], ALU.mult, ALU.mult).then_inc(s_last, 1)
                        dve.wait_ge(s_last, n)
                        dve.sem_inc(s_used, 1)
                    else:
                        assert c.n == PER
                        dve.wait_ge(s_turn, n)
                        nc.vector.tensor_copy(got[:, b, :, D:].rearrange("p k (j h) -> p j k h", j=2),
                                              bank_w[:, 0:2 * WH].rearrange("p (j k h) -> p j k h", j=2, h=H)).then_inc(s_weights, 1)
                        nc.vector.tensor_scalar(rescale[:, :], bank_w[:, 2 * WH:2 * WH + H], -1.0, keep["cross"][:, bass.ds(number(w), 1)],
                                                ALU.add, ALU.mult).then_inc(s_rescale, 1)

                def sum_step(v, i):
                    n = number(v) * W + i

                    def rows(tile, cols):
                        return acc[:, bass.ds(tile, 1), cols].rearrange("p t d -> p (t d)")

                    def add(j):
                        m = number(v) * W + j
                        dve.wait_ge(s_sum, m + (1 + AHEAD))
                        dve.wait_ge(s_acc, m + BANKS)
                        a = rows(tiles[j], slice(0, GAT_SUM))
                        nc.vector.tensor_tensor(a, a, bank[j % BANKS][:, 0:GAT_SUM], ALU.add).then_inc(s_acc, 1)

                    if i == 0:
                        _, loaded_tiles = nc.values_load_multi_w_load_instructions(
                            keep["tile_row"][0:1, bass.ds(number(v) * W, W)], engines=[mybir.EngineType.DVE], min_val=0, max_val=LAST_TILE)
                        tiles.update(enumerate(loaded_tiles))
                        dve.wait_ge(s_rescale, number(v) + 1)
                        dve.wait_ge(s_acc, n + BANKS)
                        f = rows(tiles[0], slice(0, D)).rearrange("p (h d) -> p h d", h=H)
                        nc.vector.scalar_tensor_tensor(f, rescale[:, :].unsqueeze(2).to_broadcast([P, H, GAT_DIM]), 1.0, f, ALU.add, ALU.mult)
                        s = rows(tiles[0], slice(D, GAT_ROW))
                        nc.vector.scalar_tensor_tensor(s, rescale[:, :], 1.0, s, ALU.add, ALU.mult).then_inc(s_rescaled, 1)
                    dve.wait_ge(s_sum, n + (1 + AHEAD - HOTS))
                    nc.vector.tensor_scalar(onehot[:, i % HOTS, :], keep["iota_row"][:, :], keep["dst_tab"][:, bass.ds(n, 1)], None,
                                            ALU.is_equal).then_inc(s_hot, 1)
                    if i == LAG:
                        dve.wait_ge(s_rescaled, number(v) + 1)
                    if i >= LAG:
                        add(i - LAG)
                    if i == W - 1:
                        for j in range(W - LAG, W):
                            add(j)

                program(dve, softmax_part, sum_step, DVE_AT)

            @block.scalar
            def _(act):
                def softmax_part(name, w):
                    n = number(w) + 1
                    if name == "E":
                        act.wait_ge(s_fall, n)
                        nc.scalar.activation(fall[:, :], fall[:, :], ACT.Exp).then_inc(s_factor, 1)
                    else:
                        act.wait_ge(s_diff, n)
                        nc.scalar.activation(weight[:, :], weight[:, :], ACT.Exp).then_inc(s_exp, 1)

                def sum_step(v, i):
                    b = v[1] % B
                    if i == 0:
                        act.wait_ge(s_weights, number(v) + 1)
                    for h in range(H):
                        rows = got[:, b, i, h * GAT_DIM:(h + 1) * GAT_DIM]
                        last = nc.scalar.activation(rows, rows, ACT.Copy, scale=got[:, b, i, D + h:D + h + 1])
                    last.then_inc(s_scaled, 1)

                program(act, softmax_part, sum_step, ACT_AT)

            @block.tensor
            def _(pe):
                def softmax_part(name, w):
                    n = number(w) + 1
                    if name == "A":
                        pe.wait_ge(s_e, n)
                        nc.tensor.transpose(bank_e[0:WH, 0:P], e[:, :, :].rearrange("p k h -> p (k h)"), ident[:, :]).then_inc(s_et, 1)
                    elif name == "B":
                        pe.wait_ge(s_fwd, n)
                        nc.tensor.transpose(bank_c[0:1, 0:WH], seg[:, P - 1:P], ident[0:WH, 0:WH]).then_inc(s_fwd_row, 1)
                    elif name == "C":
                        pe.wait_ge(s_chain, n)
                        pe.sem_inc(s_turns, 1)
                        nc.tensor.transpose(bank_c[0:WH, 256:257], chain[:, 0, 0:W, :].rearrange("o k h -> o (k h)"), ident[0:1, 0:1]).then_inc(s_carry, 1)
                    elif name == "D":
                        pe.wait_ge(s_back, n)
                        nc.tensor.transpose(bank_c[0:1, 0:WH], top[:, 0:1], ident[0:WH, 0:WH]).then_inc(s_back_row, 1)
                    elif name == "E":
                        pe.wait_ge(s_back_chain, n)
                        pe.sem_inc(s_turns, 1)
                        nc.tensor.transpose(bank_c[0:WH, 256:257], chain[:, 1, 1:, :].rearrange("o k h -> o (k h)"), ident[0:1, 0:1]).then_inc(s_back_carry, 1)
                    else:
                        pe.wait_ge(s_factor, n)
                        nc.tensor.matmul(bank_w[:, 2 * WH:2 * WH + H], ones[:, :], fall[:, :], start=True, stop=True)
                        pe.wait_ge(s_last, n)
                        nc.tensor.transpose(bank_w[:, WH:2 * WH], last_top[:, :], ident[0:WH, 0:WH])
                        pe.wait_ge(s_exp, n)
                        nc.tensor.transpose(bank_w[:, 0:WH], weight[:, :], ident[0:WH, 0:WH]).then_inc(s_turn, 1)

                def sum_step(v, i):
                    n = number(v) * W + i
                    pe.wait_ge(s_hot, n + 1)
                    pe.wait_ge(s_scaled, n + 1)
                    pe.wait_ge(s_acc, n + 1)
                    nc.tensor.matmul(bank[i % BANKS][:, 0:GAT_SUM], onehot[:, i % HOTS, :], got[:, v[1] % B, i, :],
                                     start=True, stop=True).then_inc(s_sum, 1)

                pe.sem_inc(s_sum, AHEAD)
                program(pe, softmax_part, sum_step, PE_AT)


def gat_finish(nc, io, dram, keep, layer, scores, acc):
    H = GAT_HEADS
    with ExitStack() as stack:
        space = Space(nc, stack, f"gf{layer}")
        sb, sem = space.sb, space.sem
        rows = {n: sb(n, [P, D]) for n in ("b_l", "g_l", "bt_l")}
        feat = sb("feat", [P, UNROLL, PAIR, D])
        h = sb("h", [P, UNROLL, PAIR, D])
        y = sb("y", [P, UNROLL, PAIR, D])
        neg = sb("neg", [P, UNROLL, PAIR, D])
        e_self, e_top, of_edges, of_self, den = (sb(n, [P, N_TILES, H]) for n in ("e_self", "e_top", "of_edges", "of_self", "den"))
        ln = Normalise(space, "ln", keep["eps"])
        names = ("s_w", "s_free", "s_self", "s_sum", "s_y", "s_yb", "s_neg", "s_pos", "s_exp", "s_elu", "s_yn", "s_yg", "s_ya", "s_dve",
                 "s_fall", "s_factors", "s_done")
        (s_w, s_free, s_self, s_sum, s_y, s_yb, s_neg, s_pos, s_exp, s_elu, s_yn, s_yg, s_ya, s_dve, s_fall, s_factors, s_done) = (
            sem(n) for n in names)
        s_feat, s_sent = space.sems("s_feat", UNROLL), space.sems("s_sent", UNROLL)
        tiles, hidden = pair_rows(dram["feat"]), pair_rows(dram["hidden"])

        def pair(r, u):
            return bass.ds(r * (UNROLL * PAIR) + u * PAIR, PAIR)

        def heads(ap):
            return ap.rearrange("p i (h d) -> p i h d", h=H)

        def one_tile(ap):
            return ap.rearrange("p (h d) -> p h d", h=H)

        def spread(ap, t):
            return ap[:, t, :].rearrange("p t h -> p (t h)").unsqueeze(2).to_broadcast([P, H, GAT_DIM])

        with nc.Block() as block:

            @block.sync
            def _(sp):
                for n, t in rows.items():
                    sp.dma_start(t[:, :], rows_of(io[f"L0_gnn_{n}"][layer])).then_inc(s_w, 16)
                with sp.Fori(0, ROUNDS) as r:
                    for u in range(UNROLL):
                        sp.wait_ge(s_free, r * UNROLL + u + 1)
                        sp.dma_start(feat[:, u, :, :], tiles[:, pair(r, u), 0:D]).then_inc(s_feat[u], 16)
                        sp.dma_start(h[:, u, :, :], hidden[:, pair(r, u), :]).then_inc(s_feat[u], 16)
                    for u in range(UNROLL):
                        sp.wait_ge(s_done, r * UNROLL + u + 1)
                        sp.dma_start(hidden[:, pair(r, u), :], h[:, u, :, :]).then_inc(s_sent[u], 16)
                    for u in range(UNROLL):
                        sp.wait_ge(s_sent[u], r * 16 + 16)
                        sp.sem_inc(s_free, 1)

            @block.gpsimd
            def _(pool):
                pool.wait_ge(s_w, 48)
                pool.wait_ge(s_factors, 2)
                with pool.Fori(0, ROUNDS) as r:
                    at = lambda u: r * UNROLL + u + 1
                    for u in range(UNROLL):
                        pool.wait_ge(s_feat[u], r * 32 + 32)
                        for i in range(PAIR):
                            t = bass.ds(r * (UNROLL * PAIR) + u * PAIR + i, 1)
                            last = nc.gpsimd.tensor_tensor(one_tile(feat[:, u, i]), one_tile(feat[:, u, i]), spread(of_self, t), ALU.mult)
                        last.then_inc(s_self, 1)
                    for u in range(UNROLL):
                        pool.wait_ge(s_self, at(u))
                        nc.gpsimd.tensor_tensor(feat[:, u], feat[:, u], both(rows["b_l"][:, :]), ALU.add).then_inc(s_sum, 1)
                    for u in range(UNROLL):
                        pool.wait_ge(s_yn, at(u))
                        nc.gpsimd.tensor_tensor(y[:, u], y[:, u], both(rows["g_l"][:, :]), ALU.mult).then_inc(s_yg, 1)
                    for u in range(UNROLL):
                        pool.wait_ge(s_yg, at(u))
                        nc.gpsimd.tensor_tensor(y[:, u], y[:, u], both(rows["bt_l"][:, :]), ALU.add).then_inc(s_ya, 1)

            @block.vector
            def _(dve):
                c = Count(dve, s_dve)
                dve.sem_inc(s_free, UNROLL)
                c.done(nc.vector.tensor_tensor(e_self[:, :, :], scores[:, :, 0:H], scores[:, :, H:], ALU.add))
                c.done(nc.vector.scalar_tensor_tensor(e_self[:, :, :], e_self[:, :, :], 0.2, e_self[:, :, :], ALU.mult, ALU.max))
                c.done(nc.vector.tensor_tensor(of_edges[:, :, :], acc[:, :, GAT_ROW:], keep["absent"][:, :].unsqueeze(2).to_broadcast([P, N_TILES, H]),
                                               ALU.add))
                c.done(nc.vector.tensor_tensor(e_top[:, :, :], of_edges[:, :, :], e_self[:, :, :], ALU.max))
                nc.vector.tensor_tensor(of_edges[:, :, :], of_edges[:, :, :], e_top[:, :, :], ALU.subtract)
                nc.vector.tensor_tensor(of_self[:, :, :], e_self[:, :, :], e_top[:, :, :], ALU.subtract).then_inc(s_fall, 1)
                dve.wait_ge(s_factors, 1)
                c.done(nc.vector.tensor_tensor(den[:, :, :], acc[:, :, D:GAT_ROW], of_edges[:, :, :], ALU.mult))
                c.done(nc.vector.scalar_tensor_tensor(den[:, :, :], den[:, :, :], 1e-16, of_self[:, :, :], ALU.add, ALU.add))
                c.done(nc.vector.reciprocal(den[:, :, :], den[:, :, :]))
                nc.vector.tensor_tensor(of_edges[:, :, :], of_edges[:, :, :], den[:, :, :], ALU.mult)
                c.done(nc.vector.tensor_tensor(of_self[:, :, :], of_self[:, :, :], den[:, :, :], ALU.mult))
                dve.sem_inc(s_factors, 1)
                with dve.Fori(0, ROUNDS) as r:
                    at = lambda u: r * UNROLL + u + 1
                    for u in range(UNROLL):
                        dve.wait_ge(s_free, at(u))
                        for i in range(PAIR):
                            t = bass.ds(r * (UNROLL * PAIR) + u * PAIR + i, 1)
                            last = nc.vector.tensor_tensor(one_tile(y[:, u, i]), one_tile(acc[:, t, 0:D].rearrange("p t d -> p (t d)")), spread(of_edges, t), ALU.mult)
                        last.then_inc(s_y, 1)
                    for u in range(UNROLL):
                        dve.wait_ge(s_y, at(u))
                        dve.wait_ge(s_sum, at(u))
                        nc.vector.tensor_tensor(y[:, u], y[:, u], feat[:, u], ALU.add).then_inc(s_yb, 1)
                    for u in range(UNROLL):
                        dve.wait_ge(s_yb, at(u))
                        nc.vector.tensor_scalar(neg[:, u], y[:, u], 0.0, None, ALU.min).then_inc(s_neg, 1)
                    for u in range(UNROLL):
                        nc.vector.tensor_scalar(y[:, u], y[:, u], 0.0, -1.0, ALU.max, ALU.add).then_inc(s_pos, 1)
                    for u in range(UNROLL):
                        dve.wait_ge(s_exp, at(u))
                        dve.wait_ge(s_pos, at(u))
                        nc.vector.tensor_tensor(y[:, u], y[:, u], neg[:, u], ALU.add).then_inc(s_elu, 1)
                    for u in range(UNROLL):
                        dve.wait_ge(s_elu, at(u))
                        ln.statistics(nc, u, at(u), y[:, u])
                    for u in range(UNROLL):
                        ln.aggregate(nc, u, at(u))
                    for u in range(UNROLL):
                        ln.invert(nc, u, at(u))
                    for u in range(UNROLL):
                        ln.scale(nc, u, at(u), y[:, u], y[:, u]).then_inc(s_yn, 1)
                    for u in range(UNROLL):
                        dve.wait_ge(s_ya, at(u))
                        nc.vector.tensor_tensor(h[:, u], h[:, u], y[:, u], ALU.add).then_inc(s_done, 1)

            @block.scalar
            def _(act):
                act.wait_ge(s_fall, 1)
                nc.scalar.activation(of_edges[:, :, :], of_edges[:, :, :], ACT.Exp)
                nc.scalar.activation(of_self[:, :, :], of_self[:, :, :], ACT.Exp).then_inc(s_factors, 1)
                with act.Fori(0, ROUNDS) as r:
                    at = lambda u: r * UNROLL + u + 1
                    for u in range(UNROLL):
                        act.wait_ge(s_neg, at(u))
                        nc.scalar.activation(neg[:, u], neg[:, u], ACT.Exp).then_inc(s_exp, 1)
                    for u in range(UNROLL):
                        ln.root(nc, u, at(u))


def pair_of(r, u):
    return bass.ds(r * (UNROLL * PAIR) + u * PAIR, PAIR)


def units(r):
    return [(u, r * UNROLL + u + 1) for u in range(UNROLL)]


def linear_attention_sums(nc, io, dram, keep, cfg, kv_sum):
    with ExitStack() as stack:
        space = Space(nc, stack, cfg["tag"] + "a")
        sb, sem = space.sb, space.sem
        wk, wv = sb("wk", [P, HALVES, D]), sb("wv", [P, HALVES, D])
        raw = sb("raw", [P, 4, D])
        bk, bv = sb("bk", [P, D]), sb("bv", [P, D])
        x = sb("x", [P, UNROLL, PAIR, D])
        xt = sb("xt", [P, UNROLL, HALVES, PAIR * P])
        k = sb("k", [P, UNROLL, PAIR, D])
        neg = sb("neg", [P, UNROLL, PAIR, D])
        v = sb("v", [P, UNROLL, PAIR, D])
        va = sb("va", [P, UNROLL, PAIR, HALVES, P + 1])
        bank = [space.ps(f"bank{u}", [P, 512]) for u in range(UNROLL)]
        ln = Normalise(space, "ln", keep["eps"])
        s_x = space.sems("s_x", UNROLL)
        (s_w, s_free, s_xn, s_xt, s_xtc, s_k, s_kb, s_neg, s_exp, s_phi, s_v, s_vb, s_va, s_kv, s_zero, s_turn, s_turned) = (
            sem(n) for n in ("s_w", "s_free", "s_xn", "s_xt", "s_xtc", "s_k", "s_kb", "s_neg", "s_exp", "s_phi", "s_v", "s_vb",
                             "s_va", "s_kv", "s_zero", "s_turn", "s_turned"))
        tiles = pair_rows(cfg["x"])
        turned = cfg["Wqkv"] is not None
        n_w = 1 if turned else 4

        with nc.Block() as block:

            @block.sync
            def _(sp):
                if turned:
                    sp.dma_start(raw[:, :, :], cfg["Wqkv"][D:3 * D, :].rearrange("(b p) i -> p b i", p=P)).then_inc(s_w, 16)
                else:
                    sp.dma_start(wk[:, :, :], cfg["Wk"].rearrange("(a p) n -> p a n", p=P)).then_inc(s_w, 16)
                    sp.dma_start(wv[:, :, :], cfg["Wv"].rearrange("(a p) n -> p a n", p=P)).then_inc(s_w, 16)
                    sp.dma_start(bk[:, :], rows_of(cfg["bk"])).then_inc(s_w, 16)
                    sp.dma_start(bv[:, :], rows_of(cfg["bv"])).then_inc(s_w, 16)
                with sp.Fori(0, ROUNDS) as r:
                    for u, n in units(r):
                        sp.wait_ge(s_free, n)
                        sp.dma_start(x[:, u, :, :], tiles[:, pair_of(r, u), :]).then_inc(s_x[u], 16)

            @block.vector
            def _(dve):
                dve.sem_inc(s_free, UNROLL)
                if turned:
                    nc.vector.memset(bk[:, :], 0.0)
                    nc.vector.memset(bv[:, :], 0.0)
                nc.vector.memset(kv_sum[:, :, :], 0.0).then_inc(s_zero, 1)
                dve.wait_ge(s_zero, 1)
                dve.wait_ge(s_w, 16 * n_w)
                with dve.Fori(0, ROUNDS) as r:
                    for u, n in units(r):
                        dve.wait_ge(s_x[u], r * 16 + 16)
                        ln.statistics(nc, u, n, x[:, u])
                    for u, n in units(r):
                        ln.aggregate(nc, u, n)
                    for u, n in units(r):
                        ln.invert(nc, u, n)
                    for u, n in units(r):
                        ln.scale(nc, u, n, x[:, u], x[:, u]).then_inc(s_xn, 1)
                    for u, n in units(r):
                        dve.wait_ge(s_k, n)
                        nc.vector.tensor_tensor(k[:, u], bank[u][:, :].rearrange("p (i d) -> p i d", i=PAIR), both(bk[:, :]),
                                                ALU.add).then_inc(s_kb, 1)
                    for u, n in units(r):
                        dve.wait_ge(s_kb, n)
                        nc.vector.tensor_scalar(neg[:, u], k[:, u], 0.0, None, ALU.min).then_inc(s_neg, 1)
                    for u, n in units(r):
                        dve.wait_ge(s_v, n)
                        nc.vector.tensor_tensor(v[:, u], bank[u][:, :].rearrange("p (i d) -> p i d", i=PAIR), both(bv[:, :]),
                                                ALU.add).then_inc(s_vb, 1)
                    for u, n in units(r):
                        dve.wait_ge(s_exp, n)
                        nc.vector.scalar_tensor_tensor(k[:, u], k[:, u], 0.0, neg[:, u], ALU.max, ALU.add).then_inc(s_phi, 1)
                    for u, n in units(r):
                        dve.wait_ge(s_kv, n)
                        dve.wait_ge(s_free, n + UNROLL - 1)
                        nc.vector.tensor_tensor(kv_sum[:, :, :], kv_sum[:, :, :],
                                                bank[u][:, 0:HALVES * (P + 1)].rearrange("p (a d) -> p a d", a=HALVES),
                                                ALU.add).then_inc(s_free, 1)

            @block.scalar
            def _(act):
                if turned:
                    for j in range(4):
                        act.wait_ge(s_turn, j + 1)
                        w, a = (wk, wv)[j // 2], j % 2
                        nc.scalar.copy(w[:, :, a * P:(a + 1) * P], bank[j][:, 0:2 * P].rearrange("p (k n) -> p k n", k=HALVES)).then_inc(s_turned, 1)
                with act.Fori(0, ROUNDS) as r:
                    for u, n in units(r):
                        ln.root(nc, u, n)
                    for u, n in units(r):
                        act.wait_ge(s_xt, n)
                        nc.scalar.copy(xt[:, u].rearrange("p a n -> p (a n)"), bank[u][:, :]).then_inc(s_xtc, 1)
                    for u, n in units(r):
                        act.wait_ge(s_neg, n)
                        nc.scalar.activation(neg[:, u], neg[:, u], ACT.Exp).then_inc(s_exp, 1)
                    for u, n in units(r):
                        act.wait_ge(s_vb, n)
                        for i in range(PAIR):
                            mask = keep["mask"][:, bass.ds(r * (UNROLL * PAIR) + u * PAIR + i, 1)]
                            nc.scalar.activation(va[:, u, i, :, 0:P], v[:, u, i, :].rearrange("p (a d) -> p a d", a=HALVES), ACT.Copy,
                                                 scale=mask)
                            last = nc.scalar.copy(va[:, u, i, :, P:P + 1], mask.unsqueeze(1).to_broadcast([P, HALVES, 1]))
                        last.then_inc(s_va, 1)

            @block.tensor
            def _(pe):
                pe.wait_ge(s_w, 16 * n_w)
                if turned:
                    for j in range(4):
                        for h in range(HALVES):
                            last = nc.tensor.transpose(bank[j][:, h * P:(h + 1) * P], raw[:, j, h * P:(h + 1) * P], keep["ident"][:, :])
                        last.then_inc(s_turn, 1)
                    pe.wait_ge(s_turned, 4)
                with pe.Fori(0, ROUNDS) as r:
                    for u, n in units(r):
                        pe.wait_ge(s_xn, n)
                        transpose_pair(nc, bank[u], x[:, u], keep["ident"]).then_inc(s_xt, 1)
                    for u, n in units(r):
                        pe.wait_ge(s_xtc, n)
                        project_pair(nc, bank[u], xt[:, u], wk).then_inc(s_k, 1)
                    for u, n in units(r):
                        pe.wait_ge(s_kb, n)
                        project_pair(nc, bank[u], xt[:, u], wv).then_inc(s_v, 1)
                    for u, n in units(r):
                        pe.wait_ge(s_phi, n)
                        pe.wait_ge(s_va, n)
                        for a in range(HALVES):
                            for i in range(PAIR):
                                last = nc.tensor.matmul(bank[u][:, a * (P + 1):(a + 1) * (P + 1)], k[:, u, i, a * P:(a + 1) * P],
                                                        va[:, u, i, a, :], start=(i == 0), stop=(i == PAIR - 1))
                        last.then_inc(s_kv, 1)


def linear_attention(nc, io, dram, keep, cfg, kv_sum, added=None):
    ff = cfg["ff"]
    NF = ff // P
    turned = cfg["Wqkv"] is not None
    has_out = cfg["Wo"] is not None
    ACT_FF = ACT.Gelu if turned else ACT.Relu
    with ExitStack() as stack:
        space = Space(nc, stack, cfg["tag"] + "b")
        sb, sem = space.sb, space.sem
        wq, w1, w2 = sb("wq", [P, HALVES, D]), sb("w1", [P, HALVES, ff]), sb("w2", [P, NF, D])
        wo = sb("wo", [P, HALVES, D])
        raw = sb("raw", [P, 6, D])
        bq, b1 = sb("bq", [P, HALVES]), sb("b1", [P, NF])
        rows = {n: sb(n, [P, D]) for n in ("bo", "b2", "ln1_g", "ln1_b", "ln2_g", "ln2_b")}
        kv = sb("kv", [P, HALVES, P])
        ks = sb("ks", [P, HALVES, 4])
        x = sb("x", [P, UNROLL, PAIR, D])
        xn = sb("xn", [P, UNROLL, PAIR, D])
        xt = sb("xt", [P, UNROLL, HALVES, PAIR * P])
        neg = sb("neg", [P, UNROLL, HALVES, PAIR * P])
        y = sb("y", [P, UNROLL, PAIR, D])
        z = sb("z", [P, UNROLL, PAIR * 8])
        fft = sb("fft", [P, UNROLL, NF, PAIR * P])
        bank = [space.ps(f"bank{u}", [P, 512]) for u in range(UNROLL)]
        ln0, ln1, ln2 = (Normalise(space, f"ln{i}", keep["eps"]) for i in range(3))
        s_x, s_sent = space.sems("s_x", UNROLL), space.sems("s_sent", UNROLL)
        (s_w, s_free, s_xn, s_xt, s_xtc, s_q, s_neg, s_pos, s_exp, s_phi, s_den, s_z0, s_z, s_num, s_att, s_att_t, s_att_c, s_o,
         s_ob, s_y, s_yn, s_yg, s_y1, s_y1t, s_y1c, s_ff, s_ffc, s_o2, s_o2b, s_y2, s_y2n, s_y2g, s_y2a, s_add, s_kv, s_turn,
         s_turned, s_done) = (
            sem(n) for n in ("s_w", "s_free", "s_xn", "s_xt", "s_xtc", "s_q", "s_neg", "s_pos", "s_exp", "s_phi", "s_den", "s_z0",
                             "s_z", "s_num", "s_att", "s_att_t", "s_att_c", "s_o", "s_ob", "s_y", "s_yn", "s_yg", "s_y1", "s_y1t",
                             "s_y1c", "s_ff", "s_ffc", "s_o2", "s_o2b", "s_y2", "s_y2n", "s_y2g", "s_y2a", "s_add", "s_kv",
                             "s_turn", "s_turned", "s_done"))
        tiles, out_tiles = pair_rows(cfg["x"]), pair_rows(cfg["out"])
        FF_ROUNDS = NF // 2
        loads = []
        if turned:
            loads += [(raw[:, 0:2], cfg["Wqkv"][0:D, :].rearrange("(b p) i -> p b i", p=P)),
                      (raw[:, 2:4], cfg["W1"].rearrange("(b p) i -> p b i", p=P)),
                      (raw[:, 4:6], cfg["W2"].rearrange("(b p) i -> p b i", p=P))]
        else:
            loads += [(wq[:, :, :], cfg["Wq"].rearrange("(a p) n -> p a n", p=P)),
                      (w1[:, :, :], cfg["W1"].rearrange("(a p) n -> p a n", p=P)),
                      (w2[:, :, :], cfg["W2"].rearrange("(a p) n -> p a n", p=P)),
                      (wo[:, :, :], cfg["Wo"].rearrange("(a p) n -> p a n", p=P)),
                      (bq[:, :], cfg["bq"].rearrange("(a p) -> p a", p=P)),
                      (rows["bo"][:, :], rows_of(cfg["bo"]))]
        loads += [(b1[:, :], cfg["b1"].rearrange("(a p) -> p a", p=P))]
        loads += [(rows[n][:, :], rows_of(cfg[n])) for n in ("b2", "ln1_g", "ln1_b", "ln2_g", "ln2_b")]

        def node_rows(u):
            return bank[u][:, :].rearrange("p (i d) -> p i d", i=PAIR)

        def by_head(ap):
            return ap.rearrange("p i (h d) -> p (i h) d", d=32)

        with nc.Block() as block:

            @block.sync
            def _(sp):
                with nc.allow_non_contiguous_dma(reason="biases by partition"):
                    for to, frm in loads:
                        sp.dma_start(to, frm).then_inc(s_w, 16)
                with sp.Fori(0, ROUNDS) as r:
                    for u, n in units(r):
                        sp.wait_ge(s_free, n)
                        sp.dma_start(x[:, u, :, :], tiles[:, pair_of(r, u), :]).then_inc(s_x[u], 16)
                    for u, n in units(r):
                        sp.wait_ge(s_done, n)
                        sp.dma_start(out_tiles[:, pair_of(r, u), :], x[:, u, :, :]).then_inc(s_sent[u], 16)
                    for u, n in units(r):
                        sp.wait_ge(s_sent[u], r * 16 + 16)
                        sp.sem_inc(s_free, 1)

            @block.vector
            def _(dve):
                dve.sem_inc(s_free, UNROLL)
                if turned:
                    nc.vector.memset(bq[:, :], 0.0)
                dve.wait_ge(s_w, 16 * len(loads))
                for a in range(HALVES):
                    nc.vector.tensor_tensor(kv[:, a, :], kv_sum[:, a, 0:P], keep["same_head"][:, :], ALU.mult)
                    last = nc.vector.tensor_scalar(ks[:, a, :], keep["head_of"][:, :], kv_sum[:, a, P:P + 1], None, ALU.mult)
                last.then_inc(s_kv, 1)
                with dve.Fori(0, ROUNDS) as r:
                    for u, n in units(r):
                        dve.wait_ge(s_x[u], r * 16 + 16)
                        ln0.statistics(nc, u, n, x[:, u])
                    for u, n in units(r):
                        ln0.aggregate(nc, u, n)
                    for u, n in units(r):
                        ln0.invert(nc, u, n)
                    for u, n in units(r):
                        ln0.scale(nc, u, n, xn[:, u], x[:, u]).then_inc(s_xn, 1)
                    for u, n in units(r):
                        dve.wait_ge(s_q, n)
                        for a in range(HALVES):
                            last = nc.vector.tensor_scalar(neg[:, u, a], bank[u][:, a * D:(a + 1) * D], bq[:, a:a + 1], 0.0, ALU.add,
                                                           ALU.min)
                        last.then_inc(s_neg, 1)
                        for a in range(HALVES):
                            last = nc.vector.tensor_scalar(xt[:, u, a], bank[u][:, a * D:(a + 1) * D], bq[:, a:a + 1], 0.0, ALU.add,
                                                           ALU.max)
                        last.then_inc(s_pos, 1)
                    for u, n in units(r):
                        dve.wait_ge(s_exp, n)
                        dve.wait_ge(s_pos, n)
                        nc.vector.tensor_tensor(xt[:, u], xt[:, u], neg[:, u], ALU.add).then_inc(s_phi, 1)
                    for u, n in units(r):
                        dve.wait_ge(s_den, n)
                        nc.vector.tensor_scalar(z[:, u, :], bank[u][:, 0:PAIR * 8], 1e-6, None, ALU.add).then_inc(s_z0, 1)
                    for u, n in units(r):
                        dve.wait_ge(s_z0, n)
                        nc.vector.reciprocal(z[:, u, :], z[:, u, :]).then_inc(s_z, 1)
                    for u, n in units(r):
                        dve.wait_ge(s_num, n)
                        dve.wait_ge(s_z, n)
                        nc.vector.tensor_tensor(by_head(y[:, u]), by_head(node_rows(u)),
                                                z[:, u, :].unsqueeze(2).to_broadcast([P, PAIR * 8, 32]), ALU.mult).then_inc(s_att, 1)
                    if has_out:
                        for u, n in units(r):
                            dve.wait_ge(s_o, n)
                            nc.vector.tensor_tensor(y[:, u], node_rows(u), both(rows["bo"][:, :]), ALU.add).then_inc(s_ob, 1)
                    for u, n in units(r):
                        dve.wait_ge(s_ob if has_out else s_att, n)
                        nc.vector.tensor_tensor(y[:, u], y[:, u], xn[:, u], ALU.add).then_inc(s_y, 1)
                    for u, n in units(r):
                        dve.wait_ge(s_y, n)
                        ln1.statistics(nc, u, n, y[:, u])
                    for u, n in units(r):
                        ln1.aggregate(nc, u, n)
                    for u, n in units(r):
                        ln1.invert(nc, u, n)
                    for u, n in units(r):
                        ln1.scale(nc, u, n, y[:, u], y[:, u]).then_inc(s_yn, 1)
                    for u, n in units(r):
                        dve.wait_ge(s_o2, n)
                        nc.vector.tensor_tensor(xn[:, u], node_rows(u), both(rows["b2"][:, :]), ALU.add).then_inc(s_o2b, 1)
                    for u, n in units(r):
                        dve.wait_ge(s_o2b, n)
                        nc.vector.tensor_tensor(y[:, u], y[:, u], xn[:, u], ALU.add).then_inc(s_y2, 1)
                    for u, n in units(r):
                        dve.wait_ge(s_y2, n)
                        ln2.statistics(nc, u, n, y[:, u])
                    for u, n in units(r):
                        ln2.aggregate(nc, u, n)
                    for u, n in units(r):
                        ln2.invert(nc, u, n)
                    for u, n in units(r):
                        ln2.scale(nc, u, n, y[:, u], y[:, u]).then_inc(s_y2n, 1)
                    if added is not None:
                        for u, n in units(r):
                            nc.vector.tensor_tensor(x[:, u], x[:, u], added[:, pair_of(r, u), 0:D], ALU.add).then_inc(s_add, 1)
                    for u, n in units(r):
                        dve.wait_ge(s_y2a, n)
                        if added is not None:
                            dve.wait_ge(s_add, n)
                        nc.vector.tensor_tensor(x[:, u], x[:, u], y[:, u], ALU.add).then_inc(s_done, 1)

            @block.gpsimd
            def _(pool):
                pool.wait_ge(s_w, 16 * len(loads))
                with pool.Fori(0, ROUNDS) as r:
                    for s_in, g, s_mid, b, s_out in ((s_yn, "ln1_g", s_yg, "ln1_b", s_y1), (s_y2n, "ln2_g", s_y2g, "ln2_b", s_y2a)):
                        for u, n in units(r):
                            pool.wait_ge(s_in, n)
                            nc.gpsimd.tensor_tensor(y[:, u], y[:, u], both(rows[g][:, :]), ALU.mult).then_inc(s_mid, 1)
                            pool.wait_ge(s_mid, n)
                            nc.gpsimd.tensor_tensor(y[:, u], y[:, u], both(rows[b][:, :]), ALU.add).then_inc(s_out, 1)

            @block.scalar
            def _(act):
                if turned:
                    for j in range(6):
                        w, a = (wq, w1, w2)[j // 2], j % 2
                        act.wait_ge(s_turn, j + 1)
                        nc.scalar.copy(w[:, :, a * P:(a + 1) * P], bank[j % UNROLL][:, 0:2 * P].rearrange("p (k n) -> p k n", k=HALVES)).then_inc(s_turned, 1)
                with act.Fori(0, ROUNDS) as r:
                    for u, n in units(r):
                        ln0.root(nc, u, n)
                    for u, n in units(r):
                        act.wait_ge(s_xt, n)
                        nc.scalar.copy(xt[:, u].rearrange("p a n -> p (a n)"), bank[u][:, :]).then_inc(s_xtc, 1)
                    for u, n in units(r):
                        act.wait_ge(s_neg, n)
                        nc.scalar.activation(neg[:, u], neg[:, u], ACT.Exp).then_inc(s_exp, 1)
                    if has_out:
                        for u, n in units(r):
                            act.wait_ge(s_att_t, n)
                            nc.scalar.copy(xt[:, u].rearrange("p a n -> p (a n)"), bank[u][:, :]).then_inc(s_att_c, 1)
                    for u, n in units(r):
                        ln1.root(nc, u, n)
                    for u, n in units(r):
                        act.wait_ge(s_y1t, n)
                        nc.scalar.copy(xt[:, u].rearrange("p a n -> p (a n)"), bank[u][:, :]).then_inc(s_y1c, 1)
                    for f in range(FF_ROUNDS):
                        for u, n in units(r):
                            act.wait_ge(s_ff, r * (UNROLL * FF_ROUNDS) + (f * UNROLL + u + 1))
                            for j in range(2):
                                c = 2 * f + j
                                last = nc.scalar.activation(fft[:, u, c], bank[u][:, j * D:(j + 1) * D], ACT_FF, bias=b1[:, c:c + 1])
                            last.then_inc(s_ffc, 1)
                    for u, n in units(r):
                        ln2.root(nc, u, n)

            @block.tensor
            def _(pe):
                pe.wait_ge(s_w, 16 * len(loads))
                if turned:
                    for j in range(6):
                        if j >= UNROLL:
                            pe.wait_ge(s_turned, j - UNROLL + 1)
                        for h in range(HALVES):
                            last = nc.tensor.transpose(bank[j % UNROLL][:, h * P:(h + 1) * P], raw[:, j, h * P:(h + 1) * P], keep["ident"][:, :])
                        last.then_inc(s_turn, 1)
                    pe.wait_ge(s_turned, 6)
                pe.wait_ge(s_kv, 1)
                with pe.Fori(0, ROUNDS) as r:
                    for u, n in units(r):
                        pe.wait_ge(s_xn, n)
                        transpose_pair(nc, bank[u], xn[:, u], keep["ident"]).then_inc(s_xt, 1)
                    for u, n in units(r):
                        pe.wait_ge(s_xtc, n)
                        for a in range(HALVES):
                            for k in range(HALVES):
                                last = nc.tensor.matmul(bank[u][:, a * D:(a + 1) * D], wq[:, k, a * P:(a + 1) * P], xt[:, u, k, :],
                                                        start=(k == 0), stop=(k == HALVES - 1))
                        last.then_inc(s_q, 1)
                    for u, n in units(r):
                        pe.wait_ge(s_phi, n)
                        for i in range(PAIR):
                            for a in range(HALVES):
                                c = 8 * i + 4 * a
                                last = nc.tensor.matmul(bank[u][:, c:c + 4], xt[:, u, a, i * P:(i + 1) * P], ks[:, a, :], start=True, stop=True)
                        last.then_inc(s_den, 1)
                    for u, n in units(r):
                        pe.wait_ge(s_z0, n)
                        for i in range(PAIR):
                            for a in range(HALVES):
                                c = i * D + a * P
                                last = nc.tensor.matmul(bank[u][:, c:c + P], xt[:, u, a, i * P:(i + 1) * P], kv[:, a, :], start=True, stop=True)
                        last.then_inc(s_num, 1)
                    if has_out:
                        for u, n in units(r):
                            pe.wait_ge(s_att, n)
                            transpose_pair(nc, bank[u], y[:, u], keep["ident"]).then_inc(s_att_t, 1)
                        for u, n in units(r):
                            pe.wait_ge(s_att_c, n)
                            project_pair(nc, bank[u], xt[:, u], wo).then_inc(s_o, 1)
                    for u, n in units(r):
                        pe.wait_ge(s_y1, n)
                        transpose_pair(nc, bank[u], y[:, u], keep["ident"]).then_inc(s_y1t, 1)
                    for f in range(FF_ROUNDS):
                        for u, n in units(r):
                            if f == 0:
                                pe.wait_ge(s_y1c, n)
                            else:
                                pe.wait_ge(s_ffc, r * (UNROLL * FF_ROUNDS) + ((f - 1) * UNROLL + u + 1))
                            for j in range(2):
                                c = 2 * f + j
                                for k in range(HALVES):
                                    last = nc.tensor.matmul(bank[u][:, j * D:(j + 1) * D], w1[:, k, c * P:(c + 1) * P], xt[:, u, k, :],
                                                            start=(k == 0), stop=(k == HALVES - 1))
                            last.then_inc(s_ff, 1)
                    for u, n in units(r):
                        pe.wait_ge(s_ffc, r * (UNROLL * FF_ROUNDS) + ((FF_ROUNDS - 1) * UNROLL + u + 1))
                        for i in range(PAIR):
                            for c in range(NF):
                                last = nc.tensor.matmul(bank[u][:, i * D:(i + 1) * D], fft[:, u, c, i * P:(i + 1) * P], w2[:, c, :],
                                                        start=(c == 0), stop=(c == NF - 1))
                        last.then_inc(s_o2, 1)


def relation_features(nc, io, dram, keep):
    B, SUB = 8, 32
    with ExitStack() as stack:
        space = Space(nc, stack, "rel")
        sb, sem = space.sb, space.sem
        w = sb("w", [P, HALVES, REL, P])
        x = sb("x", [P, UNROLL, PAIR, D])
        xt = sb("xt", [P, UNROLL, HALVES, PAIR * P])
        out = sb("out", [P, UNROLL, PAIR, REL, D])
        bank = [space.ps(f"bank{u}", [P, 512]) for u in range(8)]
        ln = Normalise(space, "ln", keep["eps"])
        s_x, s_sent = space.sems("s_x", UNROLL), space.sems("s_sent", UNROLL)
        s_w, s_free, s_xn, s_xt, s_xtc, s_mm, s_dve, s_act, s_zero = (
            sem(n) for n in ("s_w", "s_free", "s_xn", "s_xt", "s_xtc", "s_mm", "s_dve", "s_act", "s_zero"))
        tiles = pair_rows(dram["x2"])
        to = dram["rel_feat"].rearrange("(r t p) d -> p t r d", r=REL, p=P)
        pieces = [(i, a, g) for i in range(PAIR) for a in range(HALVES) for g in range(2)]

        def landing(u, p):
            i, a, g = pieces[p]
            return out[:, u, i, 4 * g:4 * g + 4, a * P:(a + 1) * P]

        def product(p):
            return bank[p % 4][:, :].rearrange("p (r o) -> p r o", r=4)

        with nc.Block() as block:

            @block.sync
            def _(sp):
                sp.wait_ge(s_zero, 1)
                weight = io["L1_gnn_weight"].rearrange("r (b i o) -> b i r o", b=B, i=SUB)
                for b in range(B):
                    lo = (b % 4) * SUB
                    sp.dma_start(w[lo:lo + SUB, b // 4, :, lo:lo + SUB], weight[b]).then_inc(s_w, 16)
                with sp.Fori(0, ROUNDS) as r:
                    for u, n in units(r):
                        sp.wait_ge(s_free, n)
                        sp.dma_start(x[:, u, :, :], tiles[:, pair_of(r, u), :]).then_inc(s_x[u], 16)
                    for u, n in units(r):
                        sp.wait_ge(s_dve, r * (4 * UNROLL) + (4 * u + 4 + 2))
                        sp.wait_ge(s_act, r * (4 * UNROLL) + (4 * u + 4 + 2))
                        for i in range(PAIR):
                            sp.dma_start(to[:, bass.ds(r * (UNROLL * PAIR) + u * PAIR + i, 1), :, :].rearrange("p t r d -> p (t r) d"),
                                         out[:, u, i, :, :]).then_inc(s_sent[u], 16)
                    for u, n in units(r):
                        sp.wait_ge(s_sent[u], r * 32 + 32)
                        sp.sem_inc(s_free, 1)

            @block.vector
            def _(dve):
                dve.sem_inc(s_free, UNROLL)
                dve.sem_inc(s_dve, 2)
                nc.vector.memset(w[:, :, :, :], 0.0).then_inc(s_zero, 1)
                with dve.Fori(0, ROUNDS) as r:
                    for u, n in units(r):
                        dve.wait_ge(s_x[u], r * 16 + 16)
                        ln.statistics(nc, u, n, x[:, u])
                    for u, n in units(r):
                        ln.aggregate(nc, u, n)
                    for u, n in units(r):
                        ln.invert(nc, u, n)
                    for u, n in units(r):
                        ln.scale(nc, u, n, x[:, u], x[:, u]).then_inc(s_xn, 1)
                    for u, n in units(r):
                        dve.wait_ge(s_free, n)
                        for p in range(0, 8, 2):
                            dve.wait_ge(s_mm, r * (8 * UNROLL) + (8 * u + p + 1))
                            nc.vector.tensor_copy(landing(u, p), product(p)).then_inc(s_dve, 1)

            @block.scalar
            def _(act):
                act.sem_inc(s_act, 2)
                with act.Fori(0, ROUNDS) as r:
                    for u, n in units(r):
                        ln.root(nc, u, n)
                    for u, n in units(r):
                        act.wait_ge(s_xt, n)
                        nc.scalar.copy(xt[:, u].rearrange("p a n -> p (a n)"), bank[4 + u % 4][:, :]).then_inc(s_xtc, 1)
                    for u, n in units(r):
                        act.wait_ge(s_free, n)
                        for p in range(1, 8, 2):
                            act.wait_ge(s_mm, r * (8 * UNROLL) + (8 * u + p + 1))
                            nc.scalar.copy(landing(u, p), product(p)).then_inc(s_act, 1)

            @block.tensor
            def _(pe):
                pe.wait_ge(s_w, 16 * B)
                with pe.Fori(0, ROUNDS) as r:
                    for u, n in units(r):
                        pe.wait_ge(s_xn, n)
                        if u >= 4:
                            pe.wait_ge(s_xtc, n - 4)
                        transpose_pair(nc, bank[4 + u % 4], x[:, u], keep["ident"]).then_inc(s_xt, 1)
                    for u, n in units(r):
                        pe.wait_ge(s_xtc, n)
                        for p, (i, a, g) in enumerate(pieces):
                            pe.wait_ge((s_dve, s_act)[p % 2], r * (4 * UNROLL) + (4 * u + p // 2 + 1))
                            nc.tensor.matmul(bank[p % 4][:, :], xt[:, u, a, i * P:(i + 1) * P],
                                             w[:, a, 4 * g:4 * g + 4, :].rearrange("p r o -> p (r o)"), start=True, stop=True).then_inc(s_mm, 1)


def mix_cfg(io, dram, layer):
    names = ["W1", "b1", "W2", "b2", "ln1_g", "ln1_b", "ln2_g", "ln2_b"]
    names += ["Wqkv"] if layer else ["Wq", "Wk", "Wv", "bq", "bk", "bv", "Wo", "bo"]
    cfg = {"Wqkv": None, "Wo": None} | {n: io[f"L{layer}_mix_{n}"] for n in names}
    x, out, ff = (("x0", "x1", L0_FF), ("x2", "x3", L1_FF))[layer]
    return cfg | {"tag": f"mix{layer}", "x": dram[x], "out": dram[out], "ff": ff}


def expert_mixture(nc, io, dram, keep):
    E = MOE_E
    EPS = 1e-3
    with ExitStack() as stack:
        space = Space(nc, stack, "moe")
        sb, sem = space.sb, space.sem
        w = [sb(f"w{j}", [P, E, HALVES, D]) for j in range(3)]
        wr = sb("wr", [P, HALVES, E])
        br = sb("br", [P, E])
        bo = sb("bo", [E, D])
        par_rows = sb("par_rows", [E * HALVES, 2, 5, P])
        par = sb("par", [P, 2, 5, E * HALVES])
        gain, shift = sb("gain", [P, 2, E * HALVES]), sb("shift", [P, 2, E * HALVES])
        bn_eps = sb("bn_eps", [P, 1])
        x = sb("x", [P, 2, PAIR, D])
        h = sb("h", [P, 2, PAIR, D])
        xn = sb("xn", [P, 2, PAIR, D])
        xt = sb("xt", [P, HALVES, PAIR * P])
        h1, h2 = sb("h1", [P, 2, HALVES, PAIR * P]), sb("h2", [P, 2, HALVES, PAIR * P])
        logit = sb("logit", [P, PAIR, E])
        top = sb("top", [P, PAIR])
        gate = sb("gate", [P, 2, PAIR, E])
        gate_t = sb("gate_t", [E, PAIR, P])
        bank1 = [space.ps(f"first{i}", [P, 512]) for i in range(2)]
        bank2 = [space.ps(f"second{i}", [P, 512]) for i in range(2)]
        bank3 = [space.ps(f"third{i}", [P, 512]) for i in range(2)]
        bank_x, bank_g = space.ps("turn", [P, 512]), space.ps("route", [P, 512])
        stats, mv = sb("stats", [P, PAIR, 6]), sb("mv", [P, PAIR, 2])
        std = sb("std", [P, PAIR])
        s_x, s_sent = space.sems("s_x", 2), space.sems("s_sent", 2)
        (s_w, s_free, s_dve, s_std_in, s_std, s_xn, s_xt, s_xtc, s_l1, s_h1, s_l2, s_h2, s_l3, s_acc, s_route, s_logit, s_exp, s_gate,
         s_turn, s_gate_t, s_bias, s_done, s_var, s_par, s_root, s_scale) = (
            sem(n) for n in ("s_w", "s_free", "s_dve", "s_std_in", "s_std", "s_xn", "s_xt", "s_xtc", "s_l1", "s_h1", "s_l2", "s_h2",
                             "s_l3", "s_acc", "s_route", "s_logit", "s_exp", "s_gate", "s_turn", "s_gate_t", "s_bias", "s_done",
                             "s_var", "s_par", "s_root", "s_scale"))
        tiles, out_tiles = pair_rows(dram["x1"]), pair_rows(dram["x2"])
        hidden = pair_rows(dram["hidden"])
        loads = [(w[j][:, :, :, :], io[f"L0_ffn_{n}"].rearrange("e (a p) n -> p e a n", p=P)) for j, n in enumerate(("W1", "W2", "Wo"))]
        loads += [(wr[:, :, :], io["L0_ffn_Wr"].rearrange("(a p) e -> p a e", p=P)), (br[:, :], rows_of(io["L0_ffn_br"])),
                  (bo[:, :], io["L0_ffn_bo"])]
        loads += [(par_rows[:, j, i, :], io[f"L0_ffn_{n}{j + 1}"].rearrange("e (a p) -> (e a) p", p=P))
                  for j in range(2) for i, n in enumerate(("b", "g", "be", "m", "v"))]
        N_U = UNITS

        def load(sp, s, pair):
            sp.dma_start(x[:, s, :, :], tiles[:, pair, :]).then_inc(s_x[s], 16)
            sp.dma_start(h[:, s, :, :], hidden[:, pair, :]).then_inc(s_x[s], 16)

        with nc.Block() as block:

            @block.sync
            def _(sp):
                with nc.allow_non_contiguous_dma(reason="small routing weights"):
                    for to, frm in loads:
                        sp.dma_start(to, frm).then_inc(s_w, 16)
                for s in range(2):
                    load(sp, s, slice(s * PAIR, (s + 1) * PAIR))
                def store(n, s, rows, sent):
                    sp.wait_ge(s_done, n)
                    sp.dma_start(out_tiles[:, rows, :], x[:, s, :, :]).then_inc(s_sent[s], 16)
                    sp.wait_ge(s_sent[s], sent)

                with sp.Fori(0, N_U // 2 - 1) as r:
                    for s in range(2):
                        store(r * 2 + s + 1, s, bass.ds(r * (2 * PAIR) + s * PAIR, PAIR), r * 16 + 16)
                        load(sp, s, bass.ds(r * (2 * PAIR) + (s + 2) * PAIR, PAIR))
                for k in range(N_U - 3, N_U):
                    store(k + 1, k % 2, slice(k * PAIR, (k + 1) * PAIR), 16 * (k // 2 + 1))
                    if k + 2 < N_U:
                        load(sp, k % 2, slice((k + 2) * PAIR, (k + 3) * PAIR))

            @block.vector
            def _(dve):
                c = Count(dve, s_dve)
                for j in range(2):
                    dve.wait_ge(s_par, j + 1)
                    last = nc.vector.tensor_copy(par[:, j], bank1[j][:, 0:5 * 16].rearrange("p (i e) -> p i e", i=5))
                c.done(last)
                c.done(nc.vector.memset(bn_eps[:, :], EPS))
                dve.sem_inc(s_var, 1)
                dve.wait_ge(s_root, 1)
                c.done(nc.vector.reciprocal(gain[:, :, :], shift[:, :, :]))
                c.done(nc.vector.tensor_tensor(gain[:, :, :], gain[:, :, :], par[:, :, 1, :], ALU.mult))
                c.done(nc.vector.tensor_tensor(shift[:, :, :], par[:, :, 0, :], par[:, :, 3, :], ALU.subtract))
                c.done(nc.vector.tensor_tensor(shift[:, :, :], shift[:, :, :], gain[:, :, :], ALU.mult))
                nc.vector.tensor_tensor(shift[:, :, :], shift[:, :, :], par[:, :, 2, :], ALU.add).then_inc(s_scale, 1)
                dve.wait_ge(s_w, 16 * len(loads))

                def front(n, s, loaded):
                    dve.wait_ge(s_x[s], loaded)
                    c.done(nc.vector.tensor_tensor(x[:, s], x[:, s], h[:, s], ALU.add))
                    for i in range(PAIR):
                        last = nc.vector.bn_stats(stats[:, i, :], x[:, s, i, :])
                    c.done(last)
                    dve.sem_inc(s_std_in, 1)
                    for i in range(PAIR):
                        last = nc.vector.bn_aggr(mv[:, i, :], stats[:, i, :])
                    last.then_inc(s_std_in, 1)
                    dve.wait_ge(s_std, n)
                    c.done(nc.vector.reciprocal(std[:, :], std[:, :]))
                    for i in range(PAIR):
                        last = nc.vector.tensor_scalar(xn[:, s, i, :], x[:, s, i, :], mv[:, i, 0:1], std[:, i:i + 1], ALU.subtract, ALU.mult)
                    last.then_inc(s_xn, 1)

                def route(n, s):
                    dve.wait_ge(s_route, n)
                    c.done(nc.vector.tensor_tensor(logit[:, :, :], bank_g[:, 0:PAIR * E].rearrange("p (i e) -> p i e", i=PAIR), both(br[:, :]),
                                                   ALU.add))
                    c.done(nc.vector.tensor_reduce(top[:, :], logit[:, :, :], AX.X, ALU.max))
                    nc.vector.tensor_tensor(logit[:, :, :], logit[:, :, :], top[:, :].unsqueeze(2).to_broadcast([P, PAIR, E]),
                                            ALU.subtract).then_inc(s_logit, 1)
                    dve.wait_ge(s_exp, n)
                    c.done(nc.vector.tensor_reduce(top[:, :], gate[:, s], AX.X, ALU.add))
                    c.done(nc.vector.reciprocal(top[:, :], top[:, :]))
                    nc.vector.tensor_tensor(gate[:, s], gate[:, s], top[:, :].unsqueeze(2).to_broadcast([P, PAIR, E]), ALU.mult).then_inc(s_gate, 1)
                    dve.wait_ge(s_turn, n)
                    nc.vector.tensor_copy(gate_t[:, :, :], bank_g[0:E, 0:PAIR * P].rearrange("e (i n) -> e i n", i=PAIR)).then_inc(s_gate_t, 1)
                    dve.wait_ge(s_bias, n)
                    c.done(nc.vector.tensor_tensor(x[:, s], x[:, s], bank_g[:, :].rearrange("p (i d) -> p i d", i=PAIR), ALU.add))

                def gather_expert(n_acc, s, e, done):
                    dve.wait_ge(s_l3, n_acc)
                    for i in range(PAIR):
                        last = nc.vector.scalar_tensor_tensor(x[:, s, i, :], bank3[e % 2][:, i * D:(i + 1) * D], gate[:, s, i, e:e + 1], x[:, s, i, :],
                                                              ALU.mult, ALU.add)
                    last.then_inc(s_acc, 1)
                    dve.wait_ge(s_acc, n_acc + 2)
                    if e == E - 1:
                        dve.sem_inc(s_done, 1)

                dve.sem_inc(s_acc, 2)
                front(1, 0, 32)
                FRONT, ROUTE = 3, 5
                with dve.Fori(0, N_U // 2) as r:
                    c.enter(r, 2 * (FRONT + ROUTE))
                    for s in range(2):
                        n = r * 2 + s + 1
                        route(n, s)
                        for e in range(E):
                            gather_expert(r * (2 * E) + (s * E + e + 1), s, e, None)
                            if e == 3:
                                front(n + 1, 1 - s, r * 32 + (32 if s == 0 else 64))
                c.leave(N_U // 2)
                route(N_U, 0)
                for e in range(E):
                    gather_expert((N_U - 1) * E + e + 1, 0, e, None)

            @block.scalar
            def _(act):
                act.wait_ge(s_var, 1)
                nc.scalar.activation(shift[:, :, :], par[:, :, 4, :], ACT.Sqrt, bias=bn_eps[:, 0:1]).then_inc(s_root, 1)
                act.wait_ge(s_scale, 1)

                def front_root(n):
                    act.wait_ge(s_std_in, n * 2)
                    nc.scalar.activation(std[:, :], mv[:, :, 1], ACT.Sqrt, bias=keep["eps"][:, 0:1]).then_inc(s_std, 1)

                def turned(n):
                    act.wait_ge(s_xt, n)
                    nc.scalar.copy(xt[:, :, :].rearrange("p a n -> p (a n)"), bank_x[:, :]).then_inc(s_xtc, 1)

                def layer(j, m, e):
                    act.wait_ge((s_l1, s_l2)[j], m)
                    for a in range(HALVES):
                        q = e * HALVES + a
                        last = nc.scalar.activation((h1, h2)[j][:, e % 2, a, :], (bank1, bank2)[j][e % 2][:, a * D:(a + 1) * D], ACT.Relu,
                                                    bias=shift[:, j, q:q + 1], scale=gain[:, j, q:q + 1])
                    last.then_inc((s_h1, s_h2)[j], 1)

                def unit(n, s, m, last):
                    act.wait_ge(s_logit, n)
                    nc.scalar.activation(gate[:, s], logit[:, :, :], ACT.Exp).then_inc(s_exp, 1)
                    for e in range(E + 1):
                        if e < E:
                            layer(0, m + (e + 1), e)
                        if e >= 1:
                            layer(1, m + e, e - 1)
                        if e == 5 and not last:
                            front_root(n + 1)
                    if not last:
                        turned(n + 1)

                front_root(1)
                turned(1)
                with act.Fori(0, N_U // 2) as r:
                    for s in range(2):
                        unit(r * 2 + s + 1, s, r * (2 * E) + s * E, False)
                unit(N_U, 0, (N_U - 1) * E, True)

            @block.tensor
            def _(pe):
                pe.wait_ge(s_w, 16 * len(loads))
                for j in range(2):
                    for i in range(5):
                        last = nc.tensor.transpose(bank1[j][:, 16 * i:16 * i + 16], par_rows[:, j, i, :], keep["ident"][0:16, 0:16])
                    last.then_inc(s_par, 1)
                pe.wait_ge(s_scale, 1)

                def turn(n, s):
                    pe.wait_ge(s_xn, n)
                    transpose_pair(nc, bank_x, xn[:, s], keep["ident"]).then_inc(s_xt, 1)

                def wide(bank, weight, data):
                    for a in range(HALVES):
                        for k in range(HALVES):
                            last = nc.tensor.matmul(bank[:, a * D:(a + 1) * D], weight[:, k, a * P:(a + 1) * P], data[:, k, :],
                                                    start=(k == 0), stop=(k == HALVES - 1))
                    return last

                def unit(n, s, m, last_unit):
                    pe.wait_ge(s_xtc, n)
                    for i in range(PAIR):
                        for k in range(HALVES):
                            last = nc.tensor.matmul(bank_g[:, i * E:(i + 1) * E], xt[:, k, i * P:(i + 1) * P], wr[:, k, :],
                                                    start=(k == 0), stop=(k == HALVES - 1))
                    last.then_inc(s_route, 1)
                    for e in range(E + 2):
                        if e < E:
                            if e < 2:
                                pe.wait_ge(s_xtc, n)
                            wide(bank1[e % 2], w[0][:, e], xt[:, :, :]).then_inc(s_l1, 1)
                        if e == 1:
                            pe.wait_ge(s_gate, n)
                            for i in range(PAIR):
                                last = nc.tensor.transpose(bank_g[0:E, i * P:(i + 1) * P], gate[:, s, i, :], keep["ident"][:, :])
                            last.then_inc(s_turn, 1)
                        if 1 <= e <= E:
                            pe.wait_ge(s_h1, m + e)
                            wide(bank2[(e - 1) % 2], w[1][:, e - 1], h1[:, (e - 1) % 2]).then_inc(s_l2, 1)
                        if e == 2:
                            pe.wait_ge(s_gate_t, n)
                            for i in range(PAIR):
                                last = nc.tensor.matmul(bank_g[:, i * D:(i + 1) * D], gate_t[:, i, :], bo[:, :], start=True, stop=True)
                            last.then_inc(s_bias, 1)
                        if e == E - 1 and not last_unit:
                            turn(n + 1, 1 - s)
                        if e >= 2:
                            pe.wait_ge(s_h2, m + (e - 1))
                            pe.wait_ge(s_acc, m + (e - 1))
                            for i in range(PAIR):
                                for k in range(HALVES):
                                    last = nc.tensor.matmul(bank3[e % 2][:, i * D:(i + 1) * D], h2[:, e % 2, k, i * P:(i + 1) * P], w[2][:, e - 2, k, :],
                                                            start=(k == 0), stop=(k == HALVES - 1))
                            last.then_inc(s_l3, 1)

                turn(1, 0)
                with pe.Fori(0, N_U // 2) as r:
                    for s in range(2):
                        unit(r * 2 + s + 1, s, r * (2 * E) + s * E, False)
                unit(N_U, 0, (N_U - 1) * E, True)


def slice_attention(nc, io, dram, keep, out):
    J = INNER // P
    with ExitStack() as stack:
        space = Space(nc, stack, "ffn")
        sb = space.sb
        slice_t = sb("slice_t", [P, N_TILES, INNER])
        sums = sb("sums", [P, HALVES, INNER])
        total = sb("total", [P, INNER])
        spread = sb("spread", [P, J, D])
        slice_weights(nc, io, dram, keep, slice_t, sums, total)
        slice_tokens(nc, io, keep, sums, total, spread)
        slice_output(nc, io, dram, slice_t, spread, out)


def slice_weights(nc, io, dram, keep, slice_t, sums, total):
    H, G = 8, 64
    J = INNER // P
    U = UNROLL
    with ExitStack() as stack:
        space = Space(nc, stack, "slw")
        sb, sem = space.sb, space.sem
        w_x = sb("w_x", [P, HALVES, INNER])
        w_xt = sb("w_xt", [P, J, D])
        w_slice = sb("w_slice", [P, P])
        b_xt = sb("b_xt", [P, J])
        b_xt_wide = sb("b_xt_wide", [P, J, P])
        b_slice = sb("b_slice", [P, G])
        inv_temp = sb("inv_temp", [P, H])
        w_logit = sb("w_logit", [P, HALVES, INNER])
        b_logit = sb("b_logit", [P, INNER])
        x = sb("x", [P, U, PAIR, D])
        xt = sb("xt", [P, U, HALVES, PAIR * P])
        sw = sb("sw", [P, U, INNER])
        top = sb("top", [P, U, H])
        den = sb("den", [P, U, H])
        nothing = sb("nothing", [P, P])
        bank = [space.ps(f"bank{u}", [P, 512]) for u in range(U)]
        sum_bank = [space.ps(f"sum_bank{a}", [P, 512]) for a in range(HALVES)]
        ln = Normalise(space, "ln", keep["eps"])
        s_x = space.sems("s_x", U)
        (s_w, s_dve, s_zero, s_wt, s_wtc, s_wl, s_ready, s_xn, s_xt, s_xtc, s_lg, s_lb, s_mx, s_sub, s_exp, s_sm, s_rc, s_sw, s_swt,
         s_swtc, s_total, s_sums) = (
            sem(n) for n in ("s_w", "s_dve", "s_zero", "s_wt", "s_wtc", "s_wl", "s_ready", "s_xn", "s_xt", "s_xtc", "s_lg", "s_lb",
                             "s_mx", "s_sub", "s_exp", "s_sm", "s_rc", "s_sw", "s_swt", "s_swtc", "s_total", "s_sums"))
        tiles = pair_rows(dram["x3"])
        loads = [(w_x[:, :, :], io["L1_ffn_W_x"].rearrange("(a p) n -> p a n", p=P)),
                 (w_slice[0:G, 0:G], io["L1_ffn_W_slice"]), (w_slice[G:P, G:P], io["L1_ffn_W_slice"]),
                 (b_xt[:, :], io["L1_ffn_b_x"].rearrange("(j p) -> p j", p=P)),
                 (b_slice[:, :], rows_of(io["L1_ffn_b_slice"])),
                 (inv_temp[:, :], rows_of(io["L1_ffn_temperature"].rearrange("a h b c -> (a h b c)")))]

        def at(r, i, u):
            return r * (PAIR * U) + (i * U + u + 1)

        def heads(ap):
            return ap.rearrange("p (h g) -> p h g", h=H)

        def by_head(ap):
            return ap.unsqueeze(2).to_broadcast([P, H, G])

        with nc.Block() as block:

            @block.sync
            def _(sp):
                sp.wait_ge(s_zero, 1)
                with nc.allow_non_contiguous_dma(reason="bias by partition"):
                    for to, frm in loads:
                        sp.dma_start(to, frm).then_inc(s_w, 16)
                with sp.Fori(0, ROUNDS) as r:
                    for u in range(U):
                        sp.wait_ge(s_swt, r * (PAIR * U) + (U + u + 1))
                        sp.dma_start(x[:, u, :, :], tiles[:, pair_of(r, u), :]).then_inc(s_x[u], 16)

            @block.vector
            def _(dve):
                c = Count(dve, s_dve)
                nc.vector.memset(w_slice[:, :], 0.0)
                nc.vector.memset(nothing[:, :], 0.0)
                nc.vector.memset(total[:, :], 0.0).then_inc(s_zero, 1)
                dve.wait_ge(s_w, 16 * len(loads))
                for j in range(J):
                    last = nc.vector.tensor_copy(b_xt_wide[:, j, :], b_xt[:, j:j + 1].to_broadcast([P, P]))
                c.done(nc.vector.tensor_scalar(inv_temp[:, :], inv_temp[:, :], 0.1, 5.0, ALU.max, ALU.min))
                c.done(nc.vector.reciprocal(inv_temp[:, :], inv_temp[:, :]))
                for a in range(HALVES):
                    dve.wait_ge(s_wt, a + 1)
                    nc.vector.tensor_copy(w_xt[:, :, a * P:(a + 1) * P], bank[a][:, :].rearrange("p (j i) -> p j i", j=J)).then_inc(s_wtc, 1)
                dve.wait_ge(s_wl, 1)
                for a in range(HALVES):
                    nc.vector.tensor_tensor(heads(w_logit[:, a, :]), heads(bank[a][:, :]), by_head(inv_temp[:, :]), ALU.mult)
                c.done(nc.vector.tensor_tensor(heads(b_logit[:, :]), heads(bank[2][:, :]), b_slice[:, :].unsqueeze(1).to_broadcast([P, H, G]),
                                               ALU.add))
                nc.vector.tensor_tensor(heads(b_logit[:, :]), heads(b_logit[:, :]), by_head(inv_temp[:, :]), ALU.mult).then_inc(s_ready, 1)
                dve.wait_ge(s_ready, 1)
                with dve.Fori(0, ROUNDS) as r:
                    for u, n in units(r):
                        dve.wait_ge(s_x[u], r * 16 + 16)
                        ln.statistics(nc, u, n, x[:, u])
                    for u, n in units(r):
                        ln.aggregate(nc, u, n)
                    for u, n in units(r):
                        ln.invert(nc, u, n)
                    for u, n in units(r):
                        ln.scale(nc, u, n, x[:, u], x[:, u]).then_inc(s_xn, 1)
                    for i in range(PAIR):
                        for u in range(U):
                            dve.wait_ge(s_lg, at(r, i, u))
                            dve.wait_ge(s_total, at(r, i, u))
                            nc.vector.tensor_tensor(sw[:, u], bank[u][:, :], b_logit[:, :], ALU.add).then_inc(s_lb, 1)
                        for u in range(U):
                            dve.wait_ge(s_lb, at(r, i, u))
                            nc.vector.tensor_reduce(top[:, u], heads(sw[:, u]), AX.X, ALU.max).then_inc(s_mx, 1)
                        for u in range(U):
                            dve.wait_ge(s_mx, at(r, i, u))
                            nc.vector.tensor_tensor(heads(sw[:, u]), heads(sw[:, u]), by_head(top[:, u]), ALU.subtract).then_inc(s_sub, 1)
                        for u in range(U):
                            dve.wait_ge(s_exp, at(r, i, u))
                            nc.vector.tensor_reduce(den[:, u], heads(sw[:, u]), AX.X, ALU.add).then_inc(s_sm, 1)
                        for u in range(U):
                            dve.wait_ge(s_sm, at(r, i, u))
                            nc.vector.reciprocal(den[:, u], den[:, u]).then_inc(s_rc, 1)
                        for u in range(U):
                            dve.wait_ge(s_rc, at(r, i, u))
                            nc.vector.scalar_tensor_tensor(heads(sw[:, u]), heads(sw[:, u]),
                                                           keep["mask"][:, bass.ds(r * (U * PAIR) + u * PAIR + i, 1)], by_head(den[:, u]),
                                                           ALU.mult, ALU.mult).then_inc(s_sw, 1)
                dve.wait_ge(s_sums, 1)
                for a in range(HALVES):
                    nc.vector.tensor_copy(sums[:, a, :], sum_bank[a][:, :])

            @block.gpsimd
            def _(pool):
                pool.sem_inc(s_total, U)
                with pool.Fori(0, ROUNDS) as r:
                    for i in range(PAIR):
                        for u in range(U):
                            pool.wait_ge(s_sw, at(r, i, u))
                            pool.wait_ge(s_total, at(r, i, u) + (U - 1))
                            nc.gpsimd.tensor_tensor(total[:, :], total[:, :], sw[:, u], ALU.add).then_inc(s_total, 1)

            @block.scalar
            def _(act):
                act.sem_inc(s_swtc, PAIR * U)
                with act.Fori(0, ROUNDS) as r:
                    for u, n in units(r):
                        ln.root(nc, u, n)
                    for u, n in units(r):
                        act.wait_ge(s_xt, n)
                        nc.scalar.copy(xt[:, u].rearrange("p a n -> p (a n)"), bank[u][:, :]).then_inc(s_xtc, 1)
                    for i in range(PAIR):
                        for u in range(U):
                            act.wait_ge(s_sub, at(r, i, u))
                            nc.scalar.activation(sw[:, u], sw[:, u], ACT.Exp).then_inc(s_exp, 1)
                        for u in range(U):
                            act.wait_ge(s_swt, at(r, i, u) + PAIR * U)
                            nc.scalar.copy(slice_t[:, bass.ds(r * (U * PAIR) + u * PAIR + i, 1), :].rearrange("p t n -> p (t n)"),
                                           bank[u][:, :]).then_inc(s_swtc, 1)

            @block.tensor
            def _(pe):
                pe.sem_inc(s_swt, PAIR * U)
                pe.wait_ge(s_w, 16 * len(loads))
                for a in range(HALVES):
                    for j in range(J):
                        last = nc.tensor.transpose(bank[a][:, j * P:(j + 1) * P], w_x[:, a, j * P:(j + 1) * P], keep["ident"][:, :])
                    last.then_inc(s_wt, 1)
                pe.wait_ge(s_wtc, 2)
                for a in range(HALVES):
                    for j in range(J):
                        nc.tensor.matmul(bank[a][:, j * P:(j + 1) * P], w_xt[:, j, a * P:(a + 1) * P], w_slice[:, :], start=True, stop=True)
                for j in range(J):
                    last = nc.tensor.matmul(bank[2][:, j * P:(j + 1) * P], b_xt_wide[:, j, :], w_slice[:, :], start=True, stop=True)
                last.then_inc(s_wl, 1)
                pe.wait_ge(s_ready, 1)
                for a in range(HALVES):
                    nc.tensor.matmul(sum_bank[a][:, :], nothing[:, :], w_logit[:, 0, :], start=True, stop=False)
                with pe.Fori(0, ROUNDS) as r:
                    for u, n in units(r):
                        pe.wait_ge(s_xn, n)
                        pe.wait_ge(s_swtc, r * (PAIR * U) + (U + u + 1))
                        transpose_pair(nc, bank[u], x[:, u], keep["ident"]).then_inc(s_xt, 1)
                    for i in range(PAIR):
                        for u, n in units(r):
                            if i == 0:
                                pe.wait_ge(s_xtc, n)
                            else:
                                pe.wait_ge(s_swtc, at(r, 0, u) + PAIR * U)
                            for a in range(HALVES):
                                last = nc.tensor.matmul(bank[u][:, :], xt[:, u, a, i * P:(i + 1) * P], w_logit[:, a, :],
                                                        start=(a == 0), stop=(a == HALVES - 1))
                            last.then_inc(s_lg, 1)
                        for u in range(U):
                            pe.wait_ge(s_sw, at(r, i, u))
                            for a in range(HALVES):
                                nc.tensor.matmul(sum_bank[a][:, :], x[:, u, i, a * P:(a + 1) * P], sw[:, u], start=False, stop=False)
                            for j in range(J):
                                last = nc.tensor.transpose(bank[u][:, j * P:(j + 1) * P], sw[:, u, j * P:(j + 1) * P], keep["ident"][:, :])
                            last.then_inc(s_swt, 1)
                for a in range(HALVES):
                    last = nc.tensor.matmul(sum_bank[a][:, :], nothing[:, :], w_logit[:, 0, :], start=False, stop=True)
                last.then_inc(s_sums, 1)


def slice_tokens(nc, io, keep, sums, total, spread):
    G = DH = 64
    J = INNER // P
    with ExitStack() as stack:
        space = Space(nc, stack, "slt")
        sb, sem = space.sb, space.sem
        w_fx = sb("w_fx", [P, HALVES, INNER])
        w_out = sb("w_out", [P, J, D])
        b_fxt = sb("b_fxt", [P, J])
        w_head = [sb(f"w_{n}", [P, P]) for n in "qkv"]
        ones = sb("ones", [P, P])
        same = sb("same", [P, P])
        other = sb("other", [P, P])
        norm = sb("norm", [P, INNER])
        inv_norm = sb("inv_norm", [P, INNER])
        token_t = sb("token_t", [P, INNER])
        head_t = [sb(f"{n}_t", [P, INNER]) for n in "qkv"]
        attn, attn_t = sb("attn", [P, INNER]), sb("attn_t", [P, INNER])
        top = sb("top", [P, J])
        value_out = sb("value_out", [P, J, D])
        bank = [space.ps(f"bank{i}", [P, 512]) for i in range(8)]
        s_w, s_dve, s_zero, s_norm, s_token, s_heads, s_qkv, s_copied, s_score, s_vw, s_vwc, s_sub, s_exp, s_attn, s_turn, s_out = (
            sem(n) for n in ("s_w", "s_dve", "s_zero", "s_norm", "s_token", "s_heads", "s_qkv", "s_copied", "s_score", "s_vw", "s_vwc",
                             "s_sub", "s_exp", "s_attn", "s_turn", "s_out"))
        loads = [(w_fx[:, :, :], io["L1_ffn_W_fx"].rearrange("(a p) n -> p a n", p=P)),
                 (w_out[:, :, :], io["L1_ffn_W_out"].rearrange("(j p) n -> p j n", p=P)),
                 (b_fxt[:, :], io["L1_ffn_b_fx"].rearrange("(j p) -> p j", p=P))]
        loads += [(w_head[i][h * DH:(h + 1) * DH, h * DH:(h + 1) * DH], io[f"L1_ffn_W_{n}"]) for i, n in enumerate("qkv") for h in range(2)]

        def pairs(ap):
            return ap.rearrange("p (j g) -> p j g", j=J)

        with nc.Block() as block:

            @block.sync
            def _(sp):
                sp.wait_ge(s_zero, 1)
                with nc.allow_non_contiguous_dma(reason="bias by partition"):
                    for to, frm in loads:
                        sp.dma_start(to, frm).then_inc(s_w, 16)

            @block.vector
            def _(dve):
                c = Count(dve, s_dve)
                for w in w_head:
                    nc.vector.memset(w[:, :], 0.0)
                nc.vector.memset(ones[:, :], 1.0)
                c.done(nc.vector.memset(same[:, :], 0.0))
                for h in range(2):
                    last = nc.vector.memset(same[h * G:(h + 1) * G, h * G:(h + 1) * G], 1.0)
                c.done(last)
                nc.vector.tensor_scalar(other[:, :], same[:, :], -1.0, BIG, ALU.add, ALU.mult).then_inc(s_zero, 1)
                dve.wait_ge(s_norm, 1)
                nc.vector.tensor_copy(norm[:, :], bank[0][:, :])
                c.done(nc.vector.tensor_scalar(inv_norm[:, :], bank[0][:, :], 1e-5, None, ALU.add))
                c.done(nc.vector.reciprocal(inv_norm[:, :], inv_norm[:, :]))
                dve.wait_ge(s_w, 16 * len(loads))
                dve.wait_ge(s_token, 1)
                for j in range(J):
                    cols = slice(j * P, (j + 1) * P)
                    last = nc.vector.scalar_tensor_tensor(token_t[:, cols], norm[:, cols], b_fxt[:, j:j + 1], bank[1][:, cols], ALU.mult, ALU.add)
                c.done(last)
                c.done(nc.vector.tensor_tensor(token_t[:, :], token_t[:, :], inv_norm[:, :], ALU.mult))
                nc.vector.tensor_tensor(pairs(token_t[:, :]), pairs(token_t[:, :]), same[:, :].unsqueeze(1).to_broadcast([P, J, P]),
                                        ALU.mult).then_inc(s_heads, 1)
                dve.wait_ge(s_qkv, 1)
                for i in range(3):
                    last = nc.vector.tensor_copy(head_t[i][:, :], bank[2 + i][:, :])
                last.then_inc(s_copied, 1)
                dve.wait_ge(s_vw, 1)
                for j in range(J):
                    last = nc.vector.tensor_copy(value_out[:, j, :], bank[6 + j // 2][:, (j % 2) * D:(j % 2 + 1) * D])
                last.then_inc(s_vwc, 1)
                dve.wait_ge(s_score, 1)
                c.done(nc.vector.scalar_tensor_tensor(pairs(attn[:, :]), pairs(bank[5][:, :]), DH ** -0.5,
                                                      other[:, :].unsqueeze(1).to_broadcast([P, J, P]), ALU.mult, ALU.add))
                c.done(nc.vector.tensor_reduce(top[:, :], pairs(attn[:, :]), AX.X, ALU.max))
                nc.vector.tensor_tensor(pairs(attn[:, :]), pairs(attn[:, :]), top[:, :].unsqueeze(2).to_broadcast([P, J, P]),
                                        ALU.subtract).then_inc(s_sub, 1)
                dve.wait_ge(s_exp, 1)
                c.done(nc.vector.tensor_reduce(top[:, :], pairs(attn[:, :]), AX.X, ALU.add))
                c.done(nc.vector.reciprocal(top[:, :], top[:, :]))
                nc.vector.tensor_tensor(pairs(attn[:, :]), pairs(attn[:, :]), top[:, :].unsqueeze(2).to_broadcast([P, J, P]),
                                        ALU.mult).then_inc(s_attn, 1)
                dve.wait_ge(s_turn, 1)
                nc.vector.tensor_copy(attn_t[:, :], bank[0][:, :]).then_inc(s_turn, 1)
                dve.wait_ge(s_out, 1)
                for j in range(J):
                    nc.vector.tensor_copy(spread[:, j, :], bank[2 + j // 2][:, (j % 2) * D:(j % 2 + 1) * D])

            @block.scalar
            def _(act):
                act.wait_ge(s_sub, 1)
                nc.scalar.activation(attn[:, :], attn[:, :], ACT.Exp).then_inc(s_exp, 1)

            @block.tensor
            def _(pe):
                pe.wait_ge(s_zero, 1)
                nc.tensor.matmul(bank[0][:, :], ones[:, :], total[:, :], start=True, stop=True).then_inc(s_norm, 1)
                pe.wait_ge(s_w, 16 * len(loads))
                for j in range(J):
                    cols = slice(j * P, (j + 1) * P)
                    for a in range(HALVES):
                        last = nc.tensor.matmul(bank[1][:, cols], w_fx[:, a, cols], sums[:, a, cols], start=(a == 0), stop=(a == HALVES - 1))
                last.then_inc(s_token, 1)
                pe.wait_ge(s_heads, 1)
                for i in range(3):
                    last = nc.tensor.matmul(bank[2 + i][:, :], w_head[i][:, :], token_t[:, :], start=True, stop=True)
                last.then_inc(s_qkv, 1)
                pe.wait_ge(s_copied, 1)
                q_t, k_t, v_t = head_t
                for j in range(J):
                    cols = slice(j * P, (j + 1) * P)
                    last = nc.tensor.matmul(bank[6 + j // 2][:, (j % 2) * D:(j % 2 + 1) * D], v_t[:, cols], w_out[:, j, :], start=True, stop=True)
                last.then_inc(s_vw, 1)
                for j in range(J):
                    cols = slice(j * P, (j + 1) * P)
                    last = nc.tensor.matmul(bank[5][:, cols], q_t[:, cols], k_t[:, cols], start=True, stop=True)
                last.then_inc(s_score, 1)
                pe.wait_ge(s_attn, 1)
                for j in range(J):
                    cols = slice(j * P, (j + 1) * P)
                    last = nc.tensor.transpose(bank[0][:, cols], attn[:, cols], keep["ident"][:, :])
                last.then_inc(s_turn, 1)
                pe.wait_ge(s_turn, 2)
                pe.wait_ge(s_vwc, 1)
                for j in range(J):
                    cols = slice(j * P, (j + 1) * P)
                    last = nc.tensor.matmul(bank[2 + j // 2][:, (j % 2) * D:(j % 2 + 1) * D], attn_t[:, cols], value_out[:, j, :],
                                            start=True, stop=True)
                last.then_inc(s_out, 1)


def slice_output(nc, io, dram, slice_t, spread, out):
    J = INNER // P
    with ExitStack() as stack:
        space = Space(nc, stack, "slo")
        sb, sem = space.sb, space.sem
        b_out = sb("b_out", [P, D])
        x = sb("x", [P, UNROLL, PAIR, D])
        lhs = sb("lhs", [P, UNROLL, PAIR, INNER])
        bank = [space.ps(f"bank{u}", [P, 512]) for u in range(UNROLL)]
        s_x, s_sent = space.sems("s_x", UNROLL), space.sems("s_sent", UNROLL)
        s_w, s_free, s_lhs, s_bias, s_mm, s_done = (sem(n) for n in ("s_w", "s_free", "s_lhs", "s_bias", "s_mm", "s_done"))
        tiles = pair_rows(dram["x3"])
        whole = out[0:LAST_TILE * P, :].rearrange("(t p) d -> p t d", p=P)
        rest = N_NODES - LAST_TILE * P
        with nc.Block() as block:

            @block.sync
            def _(sp):
                sp.dma_start(b_out[:, :], rows_of(io["L1_ffn_b_out"])).then_inc(s_w, 16)

                def load(u, rows):
                    sp.dma_start(x[:, u, :, :], tiles[:, rows, :]).then_inc(s_x[u], 16)

                with sp.Fori(0, ROUNDS - 1) as r:
                    for u, n in units(r):
                        sp.wait_ge(s_free, n)
                        load(u, pair_of(r, u))
                    for u, n in units(r):
                        sp.wait_ge(s_done, n)
                        sp.dma_start(whole[:, pair_of(r, u), :], x[:, u, :, :]).then_inc(s_sent[u], 16)
                    for u, n in units(r):
                        sp.wait_ge(s_sent[u], r * 16 + 16)
                        sp.sem_inc(s_free, 1)
                r = ROUNDS - 1
                for u in range(UNROLL):
                    sp.wait_ge(s_free, r * UNROLL + u + 1)
                    load(u, slice((r * UNROLL + u) * PAIR, (r * UNROLL + u + 1) * PAIR))
                for u in range(UNROLL):
                    t = (r * UNROLL + u) * PAIR
                    sp.wait_ge(s_done, r * UNROLL + u + 1)
                    if t < LAST_TILE:
                        sp.dma_start(whole[:, t:t + PAIR, :], x[:, u, :, :]).then_inc(s_sent[u], 16)
                    else:
                        sp.dma_start(out[LAST_TILE * P:, :], x[0:rest, u, 0, :]).then_inc(s_sent[u], 16)
                for u in range(UNROLL):
                    sp.wait_ge(s_sent[u], 16 * ROUNDS)

            @block.gpsimd
            def _(pool):
                pool.sem_inc(s_free, UNROLL)
                pool.wait_ge(s_w, 16)
                with pool.Fori(0, ROUNDS) as r:
                    for u, n in units(r):
                        pool.wait_ge(s_x[u], r * 16 + 16)
                        nc.gpsimd.tensor_tensor(x[:, u], x[:, u], both(b_out[:, :]), ALU.add).then_inc(s_bias, 1)

            @block.scalar
            def _(act):
                with act.Fori(0, ROUNDS) as r:
                    for u, n in units(r):
                        act.wait_ge(s_mm, n)
                        nc.scalar.copy(lhs[:, u], slice_t[:, pair_of(r, u), :]).then_inc(s_lhs, 1)

            @block.tensor
            def _(pe):
                pe.sem_inc(s_mm, UNROLL)
                with pe.Fori(0, ROUNDS) as r:
                    for u, n in units(r):
                        pe.wait_ge(s_lhs, n)
                        pe.wait_ge(s_free, n)
                        for i in range(PAIR):
                            for j in range(J):
                                last = nc.tensor.matmul(bank[u][:, i * D:(i + 1) * D], lhs[:, u, i, j * P:(j + 1) * P], spread[:, j, :],
                                                        start=(j == 0), stop=(j == J - 1))
                        last.then_inc(s_mm, 1)

            @block.vector
            def _(dve):
                with dve.Fori(0, ROUNDS) as r:
                    for u, n in units(r):
                        dve.wait_ge(s_bias, n)
                        dve.wait_ge(s_mm, n + UNROLL)
                        nc.vector.tensor_tensor(x[:, u], x[:, u], bank[u][:, :].rearrange("p (i d) -> p i d", i=PAIR), ALU.add).then_inc(s_done, 1)


def scratch(nc):
    shapes = {"x0": ((N_PAD, D), F32), "x1": ((N_PAD, D), F32), "x2": ((N_PAD, D), F32), "x3": ((N_PAD, D), F32),
              "first": ((STEPS_PAD * P, GAT_HEADS), F32), "hidden": ((N_PAD, D), F32),
              "flags": ((STEPS_PAD * GAT_HEADS, 5, P), F32), "resets": ((2, STEPS_PAD), F32),
              "feat": ((N_PAD, GAT_ROW), F32), "rel_feat": ((REL * N_PAD, D), F32)}
    shapes |= {f"{n}_rows": ((CHUNKS, P), I32) for n in ("src", "dst", "prev", "next", "kind")}
    shapes["weight_rows"] = ((CHUNKS, P), F32)
    return {n: nc.dram_tensor(f"scratch_{n}", s, dt).ap() for n, (s, dt) in shapes.items()}


def build(nc, io, out):
    dram = scratch(nc)
    with ExitStack() as stack:
        sb = Space(nc, stack, "keep").sb
        keep = {"ident": sb("ident", [P, P]), "iota_row": sb("iota_row", [P, P]),
                "src_tab": sb("src_tab", [P, STEPS_PAD], I32), "rel_tab": sb("rel_tab", [P, STEPS_PAD], I32),
                "wt_tab": sb("wt_tab", [P, STEPS_PAD]), "dst_tab": sb("dst_tab", [P, STEPS_PAD]),
                "eps": sb("eps", [P, 1]), "mask": sb("mask", [P, N_TILES]), "same_head": sb("same_head", [P, P]),
                "head_of": sb("head_of", [P, P // MIX_DIM]), "tile_row": sb("tile_row", [1, STEPS_PAD], I32),
                "first_pos": sb("first_pos", [P, N_TILES], I32), "cross": sb("cross", [P, WINDOWS]),
                "absent": sb("absent", [P, N_TILES])}
        gathers = Gathers(nc)
        build_tables(nc, io, dram, keep, gathers)
        mix(nc, io, dram, keep, 0)
        gnn_input(nc, io, dram, keep)
        for layer in range(GAT_LAYERS):
            graph_attention(nc, io, dram, keep, gathers, layer)
        expert_mixture(nc, io, dram, keep)
        relation_features(nc, io, dram, keep)
        with ExitStack() as inner:
            acc = Space(nc, inner, "layer1").sb("acc", [P, N_TILES, D])
            add_messages(nc, keep, gathers, dram["rel_feat"], acc)
            mix(nc, io, dram, keep, 1, added=acc)
        slice_attention(nc, io, dram, keep, out)


def mix(nc, io, dram, keep, layer, added=None):
    cfg = mix_cfg(io, dram, layer)
    with ExitStack() as stack:
        kv_sum = Space(nc, stack, f"mix{layer}").sb("kv_sum", [P, HALVES, P + 1])
        linear_attention_sums(nc, io, dram, keep, cfg, kv_sum)
        linear_attention(nc, io, dram, keep, cfg, kv_sum, added)


def graph_attention(nc, io, dram, keep, gathers, layer):
    with ExitStack() as stack:
        sb = Space(nc, stack, f"gat{layer}").sb
        scores = sb("scores", [P, N_TILES, 2 * GAT_HEADS])
        gat_project(nc, io, dram, keep, layer, scores)
        acc = sb("acc", [P, N_TILES, GAT_SUM])
        with ExitStack() as inner:
            d_edge = Space(nc, inner, f"gat{layer}").sb("d_edge", [P, STEPS_PAD, GAT_HEADS])
            gat_spread(nc, dram, keep, gathers, layer, scores, d_edge)
            gat_messages(nc, dram, keep, gathers, layer, d_edge, acc)
        gat_finish(nc, io, dram, keep, layer, scores, acc)


def kernel(**inputs):
    import concourse.bacc as _bacc
    from concourse.bass_utils import run_bass_kernel_spmd as _run

    nc = _bacc.Bacc("TRN2", target_bir_lowering=False, num_devices=1)
    arrays, io = {}, {}
    for name in _INS:
        a = np.ascontiguousarray(inputs[name])
        arrays[f"in_{name}"] = a
        io[name] = nc.dram_tensor(f"in_{name}", a.shape, mybir.dt.from_np(a.dtype), kind="ExternalInput").ap()
    out = nc.dram_tensor("out", (N_NODES, D), F32, kind="ExternalOutput").ap()
    build(nc, io, out)
    r = _run(nc, [arrays], core_ids=[0])
    return r.results[0]["out"]
```

```python
from contextlib import ExitStack

import numpy as np

import concourse.bass as bass
from concourse import mybir

F32 = mybir.dt.float32
F32R = mybir.dt.float32r
I32 = mybir.dt.int32
ALU = mybir.AluOpType
ACT = mybir.ActivationFunctionType
AX = mybir.AxisListType

P = 128
N_NODES = 6250
N_EDGES = 100000
D = 256
HALVES = D // P
N_TILES = 50
N_PAD = N_TILES * P
LAST_TILE = N_NODES // P
PAIR = 2
UNITS = N_TILES // PAIR
UNROLL = 5
ROUNDS = UNITS // UNROLL
GAT_LAYERS, GAT_HEADS, GAT_DIM = 3, 4, 64
MIX_DIM = 32
GAT_ROW = D + GAT_HEADS
GAT_SUM = GAT_ROW + GAT_HEADS
LN_EPS = 1e-5
BIG = 2.0 ** 100
OUT_OF_RANGE = 1 << 20

CHUNKS = -(-N_EDGES // P)
STEPS = CHUNKS + LAST_TILE
WINDOW = 28
WINDOW_BUFS = 3
WINDOWS = -(-STEPS // (WINDOW * WINDOW_BUFS)) * WINDOW_BUFS
STEPS_RUN = WINDOWS * WINDOW
SLOTS = 24
STEP_ROUNDS = STEPS_RUN // SLOTS
assert STEP_ROUNDS * SLOTS == STEPS_RUN
BLOCKS = -(-STEPS_RUN // P)
STEPS_PAD = BLOCKS * P


class Count:

    def __init__(self, engine, sem):
        self.engine, self.sem, self.base, self.n = engine, sem, 0, 0

    def done(self, instruction):
        instruction.then_inc(self.sem, 1)
        self.n += 1
        self.engine.wait_ge(self.sem, self.base + self.n)

    def enter(self, i, per):
        self.before, self.per = self.base + self.n, per
        self.base, self.n = self.before + i * per, 0

    def leave(self, trips):
        assert self.n == self.per, (self.n, self.per)
        self.base, self.n = self.before + trips * self.per, 0


FIRST_SEM, LAST_SEM = 100, 229
GATHER_SEMS = 26


class Space:

    def __init__(self, nc, stack, tag, gathers=None):
        self.nc, self.stack, self.tag, self.next, self.gathers = nc, stack, tag, FIRST_SEM, gathers
        stack.callback(self.close)

    def close(self):
        if self.next > FIRST_SEM:
            self.nc.all_engine_barrier(sems_to_clear=range(FIRST_SEM, self.next))

    def sb(self, name, shape, dt=F32):
        return self.stack.enter_context(self.nc.sbuf_tensor(f"{self.tag}_{name}", shape, dt))

    def ps(self, name, shape, dt=F32):
        return self.stack.enter_context(self.nc.psum_tensor(f"{self.tag}_{name}", shape, dt))

    def sem(self, name):
        assert self.next <= LAST_SEM
        self.next += 1
        return self.stack.enter_context(self.nc.semaphore(f"{self.tag}_{name}", num=self.next - 1))

    def sems(self, name, n):
        return [self.sem(f"{name}{i}") for i in range(n)]


class Gathers:

    def __init__(self, nc):
        self.sems = [nc.alloc_semaphore(f"gather{i}", num=LAST_SEM + 1 + i) for i in range(GATHER_SEMS)]
        self.had = [0] * GATHER_SEMS

    def start(self, slots):
        return [(self.sems[i], self.had[i]) for i in slots]

    def count(self, slots, dmas):
        for i in slots:
            self.had[i] += 16 * dmas


def rows_of(vector):
    return vector.partition_broadcast(P)


def build_tables(nc, io, dram, keep, gathers):
    with ExitStack() as stack:
        sp_ = Space(nc, stack, "tab")
        sb, ps, sem = sp_.sb, sp_.ps, sp_.sem
        ident, iota_row = keep["ident"], keep["iota_row"]
        pad_int = sb("pad_int", [1, 4, P], I32)
        zeros = sb("zeros", [P, D])
        minus_big = sb("minus_big", [P, 2048])
        iota_int = sb("iota_int", [P, P], I32)
        chunk_int = sb("chunk_int", [1, CHUNKS], I32)
        chunk_no = sb("chunk_no", [1, CHUNKS])
        step_int = sb("step_int", [P, BLOCKS], I32)
        step_no = sb("step_no", [P, BLOCKS])
        node_int = sb("node_int", [P, N_TILES], I32)
        node_no = sb("node_no", [P, N_TILES])
        ones = sb("ones", [1, P])
        ends = sb("ends", [1, 2, CHUNKS], I32)
        path = sb("path", [1, 2, CHUNKS])
        tile_int = sb("tile_int", [1, CHUNKS], I32)
        path_all = sb("path_all", [P, 2, CHUNKS])
        junk = sb("junk", [P, CHUNKS])
        chunk_of = sb("chunk_of", [P, BLOCKS])
        chunk_idx = sb("chunk_idx", [P, BLOCKS], I32)
        tile_of = sb("tile_of", [P, BLOCKS])
        tile_clip = sb("tile_clip", [P, BLOCKS])
        first_of = sb("first_of", [P, BLOCKS])
        raw = sb("raw", [P, 5, BLOCKS, P], I32)
        weight = sb("weight", [P, BLOCKS, P])
        as_f = sb("as_f", [P, 5, BLOCKS, P])
        rel = sb("rel", [P, BLOCKS, P])
        low = sb("low", [P, BLOCKS, P])
        valid = sb("valid", [P, BLOCKS, P])
        flags = sb("flags", [P, 5, BLOCKS, P])
        differs = sb("differs", [P, BLOCKS, P])
        zero_row = sb("zero_row", [P, P])
        step_min = sb("step_min", [P, 2, BLOCKS])
        cross_row = sb("cross_row", [1, STEPS_PAD])
        node_chunk = sb("node_chunk", [P, N_TILES])
        node_chunk_idx = sb("node_chunk_idx", [P, N_TILES], I32)
        node_rows = sb("node_rows", [P, UNROLL, P], I32)
        node_stage = sb("node_stage", [P, UNROLL], I32)
        node_rows_f = sb("node_rows_f", [P, UNROLL, P])
        before = sb("before", [P, N_TILES])
        has = sb("has", [P, N_TILES])
        position = sb("position", [P, N_TILES])
        bank = [ps(f"bank{i}", [P, 512]) for i in range(8)]
        s_pads, s_fill, s_consts, s_iota = sem("pads"), sem("fill"), sem("consts"), sem("iota")
        s_flat, s_ends, s_path, s_bcast = sem("flat"), sem("ends"), sem("path"), sem("bcast")
        s_index, s_rows, s_dve, s_tabs, s_psum = sem("index"), gathers.start([UNROLL])[0][0], sem("dve"), sem("tabs"), sem("psum")
        s_nidx, s_ncopy, s_nused, s_const = sem("nidx"), sem("ncopy"), sem("nused"), sem("const")
        s_nrow = [s for s, _ in gathers.start(range(UNROLL))]
        s_flags = sem("flags")

        src, dst, kind, wt = io["src"], io["dst"], io["edge_type_8"], io["edge_weight"]
        names = ["src", "dst", "prev", "next", "kind"]
        flat = {n: dram[f"{n}_rows"].rearrange("c e -> (c e)") for n in names + ["weight"]}
        tail = CHUNKS * P - N_EDGES
        n_flat = 13
        n_fill = 1 + 1 + 2 * BLOCKS

        def line(ap):
            return ap.rearrange("(a n) -> a n", a=1)

        gathers.count(range(UNROLL), N_TILES // UNROLL)
        gathers.count([UNROLL], 6 * BLOCKS)
        with nc.Block() as block:

            @block.gpsimd
            def _(pool):
                nc.gpsimd.memset(pad_int[:, 0, :], 0)
                nc.gpsimd.memset(pad_int[:, 1, :], OUT_OF_RANGE)
                nc.gpsimd.memset(pad_int[:, 2, :], -2)
                nc.gpsimd.memset(zeros[:, :], 0.0)
                nc.gpsimd.memset(minus_big[:, :], -BIG).then_inc(s_pads, 1)
                nc.gpsimd.memset(ident[:, :], 0.0)
                nc.gpsimd.memset(ones[:, :], 1.0)
                nc.gpsimd.memset(keep["eps"][:, :], LN_EPS)
                nc.gpsimd.memset(zero_row[:, :], 0.0)
                nc.gpsimd.iota(chunk_int[:, :], [[1, CHUNKS]], base=0, channel_multiplier=0)
                nc.gpsimd.iota(step_int[:, :], [[P, BLOCKS]], base=0, channel_multiplier=1)
                nc.gpsimd.iota(node_int[:, :], [[P, N_TILES]], base=0, channel_multiplier=1)
                nc.gpsimd.iota(iota_int[:, :], [[1, P]], base=0, channel_multiplier=0).then_inc(s_iota, 1)
                pool.wait_ge(s_iota, 1)
                nc.gpsimd.affine_select(out=ident[:, :], in_=ident[:, :], compare_op=ALU.not_equal, fill=1.0,
                                        base=0, pattern=[[-1, P]], channel_multiplier=1).then_inc(s_consts, 1)
                pool.wait_ge(s_index, 1)
                pool.wait_ge(s_flat, 16 * n_flat)
                for b in range(BLOCKS):
                    for j, n in enumerate(names):
                        nc.gpsimd.indirect_dma_start(
                            out=raw[:, j, b, :], out_offset=None, in_=dram[f"{n}_rows"],
                            in_offset=bass.IndirectOffsetOnAxis(ap=chunk_idx[:, b:b + 1], axis=0)).then_inc(s_rows, 16)
                    nc.gpsimd.indirect_dma_start(
                        out=weight[:, b, :], out_offset=None, in_=dram["weight_rows"],
                        in_offset=bass.IndirectOffsetOnAxis(ap=chunk_idx[:, b:b + 1], axis=0)).then_inc(s_rows, 16)
                with pool.Fori(0, N_TILES // UNROLL) as r:
                    pool.wait_ge(s_nidx, r * UNROLL + UNROLL)
                    pool.wait_ge(s_nused, r * UNROLL + UNROLL)
                    nc.gpsimd.tensor_copy(node_stage[:, :], node_chunk_idx[:, bass.ts(r, UNROLL)]).then_inc(s_ncopy, 1)
                    pool.wait_ge(s_ncopy, r + 1)
                    pool.sem_inc(s_const, 1)
                    for u in range(UNROLL):
                        nc.gpsimd.indirect_dma_start(
                            out=node_rows[:, u, :], out_offset=None, in_=dram["dst_rows"],
                            in_offset=bass.IndirectOffsetOnAxis(ap=node_stage[:, u:u + 1], axis=0)).then_inc(s_nrow[u], 16)

            @block.sync
            def _(sp):
                sp.wait_ge(s_pads, 1)
                for n, ap, pad in (("src", src, 0), ("dst", dst, 1), ("kind", kind, 0)):
                    sp.dma_start(line(flat[n][0:N_EDGES]), line(ap)).then_inc(s_flat, 16)
                    sp.dma_start(line(flat[n][N_EDGES:]), pad_int[:, pad, 0:tail]).then_inc(s_flat, 16)
                sp.dma_start(line(flat["weight"][0:N_EDGES]), line(wt)).then_inc(s_flat, 16)
                sp.dma_start(line(flat["weight"][N_EDGES:]), zeros[0:1, 0:tail]).then_inc(s_flat, 16)
                sp.dma_start(line(flat["prev"][0:1]), pad_int[:, 2, 0:1]).then_inc(s_flat, 16)
                sp.dma_start(line(flat["prev"][1:N_EDGES + 1]), line(dst)).then_inc(s_flat, 16)
                sp.dma_start(line(flat["prev"][N_EDGES + 1:]), pad_int[:, 2, 0:tail - 1]).then_inc(s_flat, 16)
                sp.dma_start(line(flat["next"][0:N_EDGES - 1]), line(dst[1:])).then_inc(s_flat, 16)
                sp.dma_start(line(flat["next"][N_EDGES - 1:]), pad_int[:, 2, 0:tail + 1]).then_inc(s_flat, 16)
                sp.dma_start(dram["x0"][0:N_NODES, :], io["x"]).then_inc(s_fill, 16)
                rest = N_PAD - N_NODES
                assert rest <= 2 * P
                sp.dma_start(dram["x0"][N_NODES:N_NODES + rest // 2, :], zeros[0:rest // 2, :]).then_inc(s_fill, 16)
                sp.dma_start(dram["x0"][N_NODES + rest // 2:, :], zeros[0:rest - rest // 2, :]).then_inc(s_fill, 16)
                for b in range(BLOCKS):
                    sp.dma_start(dram["first"][b * P * P:(b + 1) * P * P, :].rearrange("(p e) q -> p (e q)", p=P),
                                 minus_big[:, 0:P * GAT_HEADS]).then_inc(s_fill, 16)
                sp.wait_ge(s_flat, 16 * n_flat)
                with nc.allow_non_contiguous_dma(reason="one destination per chunk"):
                    sp.dma_start(ends[:, 0, :], dram["dst_rows"][:, 0:1].rearrange("c e -> e c")).then_inc(s_ends, 16)
                    sp.dma_start(ends[:, 1, :], dram["dst_rows"][:, P - 1:P].rearrange("c e -> e c")).then_inc(s_ends, 16)
                sp.wait_ge(s_flags, 1)
                by_head = dram["flags"].rearrange("(b p h) f e -> h p f b e", p=P, h=GAT_HEADS)
                for h in range(GAT_HEADS):
                    for f in range(5):
                        sp.dma_start(by_head[h][:, f], flags[:, f, :, :]).then_inc(s_fill, 16)
                with nc.allow_non_contiguous_dma(reason="one flag per step"):
                    for f, e in ((0, P - 1), (1, 0)):
                        sp.dma_start(dram["resets"][f].rearrange("(b p) -> p b", p=P), flags[:, 2 + f, :, e]).then_inc(s_fill, 16)
                sp.wait_ge(s_fill, 16 * (3 + BLOCKS + 5 * GAT_HEADS + 2))

            @block.vector
            def _(dve):
                dve.sem_inc(s_nused, UNROLL)
                c = Count(dve, s_dve)
                nc.vector.memset(keep["same_head"][:, :], 0.0)
                c.done(nc.vector.memset(keep["head_of"][:, :], 0.0))
                for h in range(P // MIX_DIM):
                    rows = slice(h * MIX_DIM, (h + 1) * MIX_DIM)
                    nc.vector.memset(keep["same_head"][rows, rows], 1.0)
                    nc.vector.memset(keep["head_of"][rows, h:h + 1], 1.0)
                dve.wait_ge(s_iota, 1)
                nc.vector.tensor_copy(chunk_no[:, :], chunk_int[:, :])
                nc.vector.tensor_copy(step_no[:, :], step_int[:, :])
                nc.vector.tensor_copy(node_no[:, :], node_int[:, :])
                c.done(nc.vector.tensor_copy(iota_row[:, :], iota_int[:, :]))
                nc.vector.tensor_scalar(keep["mask"][:, :], node_no[:, :], float(N_NODES), None, ALU.is_lt)
                dve.wait_ge(s_ends, 32)
                c.done(nc.vector.tensor_single_scalar(tile_int[:, :], ends[:, 0, :], 7, ALU.arith_shift_right))
                c.done(nc.vector.tensor_copy(path[:, 0, :], tile_int[:, :]))
                nc.vector.tensor_copy(path[:, 1, :], ends[:, 1, :])
                nc.vector.tensor_tensor(path[:, 0, :], path[:, 0, :], chunk_no[:, :], ALU.add).then_inc(s_path, 1)
                dve.wait_ge(s_bcast, 1)
                half = CHUNKS // 2
                for f in range(2):
                    for h in range(2):
                        last = nc.vector.tensor_copy(path_all[:, f, h * half:(h + 1) * half], bank[2 * f + h][:, 0:half])
                c.done(last)
                for b in range(BLOCKS):
                    last = nc.vector.tensor_scalar(junk[:, 0:CHUNKS - 1], path_all[:, 0, 1:CHUNKS], step_no[:, b:b + 1],
                                                   0.0, ALU.is_le, ALU.add, accum_out=chunk_of[:, b:b + 1])
                    c.done(last)
                nc.vector.tensor_copy(chunk_idx[:, :], chunk_of[:, :]).then_inc(s_index, 1)
                c.done(nc.vector.tensor_tensor(tile_of[:, :], step_no[:, :], chunk_of[:, :], ALU.subtract))
                nc.vector.tensor_scalar(first_of[:, :], tile_of[:, :], float(P), None, ALU.mult)
                c.done(nc.vector.tensor_scalar(tile_clip[:, :], tile_of[:, :], float(LAST_TILE), None, ALU.min))
                with dve.Fori(0, N_TILES) as t:
                    c.enter(t, 1)
                    c.done(nc.vector.tensor_scalar(junk[:, :], path_all[:, 1, :], node_no[:, bass.ts(t, 1)], 0.0,
                                                   ALU.is_lt, ALU.add, accum_out=node_chunk[:, bass.ts(t, 1)]))
                    nc.vector.tensor_copy(node_chunk_idx[:, bass.ts(t, 1)], node_chunk[:, bass.ts(t, 1)]).then_inc(s_nidx, 1)
                c.leave(N_TILES)
                dve.wait_ge(s_rows, 16 * 6 * BLOCKS)
                c.done(nc.vector.tensor_copy(as_f[:, :, :, :].rearrange("p j b e -> p (j b e)"),
                                             raw[:, :, :, :].rearrange("p j b e -> p (j b e)")))
                for b in range(BLOCKS):
                    last = nc.vector.tensor_scalar(rel[:, b, :], as_f[:, 1, b, :], first_of[:, b:b + 1], None, ALU.subtract)
                c.done(last)
                c.done(nc.vector.tensor_scalar(low[:, :, :], rel[:, :, :], 0.0, None, ALU.is_ge))
                c.done(nc.vector.scalar_tensor_tensor(valid[:, :, :], rel[:, :, :], float(P), low[:, :, :], ALU.is_lt, ALU.mult))
                c.done(nc.vector.scalar_tensor_tensor(as_f[:, 4, :, :], as_f[:, 4, :, :], float(N_PAD), as_f[:, 0, :, :],
                                                      ALU.mult, ALU.add))
                c.done(nc.vector.tensor_scalar(flags[:, 4, :, :], valid[:, :, :], -1.0, BIG, ALU.add, ALU.mult))
                for f in range(2):
                    c.done(nc.vector.tensor_tensor(differs[:, :, :], as_f[:, 1, :, :], as_f[:, 2 + f, :, :], ALU.not_equal))
                    c.done(nc.vector.tensor_tensor(differs[:, :, :], differs[:, :, :], valid[:, :, :], ALU.mult))
                    c.done(nc.vector.tensor_scalar(flags[:, f, :, :], differs[:, :, :], -BIG, None, ALU.mult))
                for b in range(BLOCKS):
                    nc.vector.tensor_tensor_scan(flags[:, 2, b, :], zero_row[:, :], flags[:, 0, b, :], 0.0, ALU.add, ALU.min)
                    last = nc.vector.tensor_tensor_scan(flags[:, 3, b, ::-1], zero_row[:, :], flags[:, 1, b, ::-1], 0.0,
                                                        ALU.add, ALU.min)
                c.done(last)
                c.done(nc.vector.tensor_scalar(differs[:, :, :], valid[:, :, :], -1.0, -float(OUT_OF_RANGE), ALU.add, ALU.mult))
                c.done(nc.vector.tensor_tensor(differs[:, :, :], differs[:, :, :], rel[:, :, :], ALU.add))
                c.done(nc.vector.tensor_reduce(step_min[:, 0, :], differs[:, :, :], AX.X, ALU.min))
                c.done(nc.vector.scalar_tensor_tensor(differs[:, :, :], flags[:, 0], OUT_OF_RANGE / BIG, differs[:, :, :], ALU.mult, ALU.add))
                c.done(nc.vector.tensor_reduce(step_min[:, 1, :], differs[:, :, :], AX.X, ALU.min))
                c.done(nc.vector.scalar_tensor_tensor(step_min[:, 1, :], step_min[:, 1, :], float(OUT_OF_RANGE), step_min[:, 0, :],
                                                      ALU.add, ALU.is_equal))
                nc.vector.scalar_tensor_tensor(step_min[:, 0, :], step_min[:, 1, :], float(OUT_OF_RANGE), step_min[:, 0, :],
                                               ALU.mult, ALU.add).then_inc(s_flags, 1)
                tables = (keep["src_tab"], keep["rel_tab"], keep["wt_tab"], keep["dst_tab"])
                for i in range(4 * BLOCKS):
                    j, b = i // BLOCKS, i % BLOCKS
                    dve.wait_ge(s_psum, i + 1)
                    nc.vector.tensor_copy(tables[j][:, b * P:(b + 1) * P], bank[i % 8][:, 0:P]).then_inc(s_tabs, 1)
                for b in range(BLOCKS):
                    dve.wait_ge(s_psum, 4 * BLOCKS + 1 + b)
                    nc.vector.tensor_copy(keep["tile_row"][:, b * P:(b + 1) * P], bank[b % 8][0:1, 128:256])
                    last = nc.vector.tensor_copy(cross_row[:, b * P:(b + 1) * P], bank[b % 8][0:1, 256:384])
                last.then_inc(s_tabs, 1)
                dve.wait_ge(s_psum, 5 * BLOCKS + 1)
                c.done(nc.vector.tensor_scalar(keep["cross"][:, :], bank[7][:, 0:WINDOWS], node_no[:, 0:1], None, ALU.is_equal))
                with dve.Fori(0, N_TILES // UNROLL) as r:
                    c.enter(r, 3 * UNROLL)
                    for u in range(UNROLL):
                        dve.wait_ge(s_nrow[u], r * 16 + 16)
                        c.done(nc.vector.tensor_copy(node_rows_f[:, u, :], node_rows[:, u, :]))
                        dve.sem_inc(s_nused, 1)
                        c.done(nc.vector.tensor_scalar(junk[:, 0:P], node_rows_f[:, u, :], node_no[:, bass.ds(r * UNROLL + u, 1)],
                                                       0.0, ALU.is_lt, ALU.add, accum_out=before[:, bass.ds(r * UNROLL + u, 1)]))
                        c.done(nc.vector.tensor_scalar(junk[:, 0:P], node_rows_f[:, u, :], node_no[:, bass.ds(r * UNROLL + u, 1)],
                                                       0.0, ALU.is_equal, ALU.max, accum_out=has[:, bass.ds(r * UNROLL + u, 1)]))
                c.leave(N_TILES // UNROLL)
                c.done(nc.vector.scalar_tensor_tensor(position[:, :], node_chunk[:, :], float(P), before[:, :], ALU.mult, ALU.add))
                nc.vector.tensor_scalar(keep["absent"][:, :], has[:, :], -1.0, BIG, ALU.add, ALU.mult)
                c.done(nc.vector.scalar_tensor_tensor(position[:, :], has[:, :], -float(OUT_OF_RANGE), position[:, :],
                                                      ALU.mult, ALU.add))
                for t in range(N_TILES):
                    last = nc.vector.tensor_scalar(position[:, t:t + 1], position[:, t:t + 1], float(OUT_OF_RANGE + P * t), None,
                                                   ALU.add)
                c.done(last)
                c.done(nc.vector.tensor_copy(keep["first_pos"][:, :], position[:, :]))

            @block.tensor
            def _(pe):
                pe.wait_ge(s_path, 1)
                pe.wait_ge(s_consts, 1)
                half = CHUNKS // 2
                for f in range(2):
                    for h in range(2):
                        last = nc.tensor.matmul(bank[2 * f + h][:, 0:half], ones[:, :], path[:, f, h * half:(h + 1) * half],
                                                start=True, stop=True)
                last.then_inc(s_bcast, 1)
                pe.wait_ge(s_flags, 1)
                sources = (as_f[:, 0], as_f[:, 4], weight, rel)
                for i in range(4 * BLOCKS):
                    j, b = i // BLOCKS, i % BLOCKS
                    if i >= 8:
                        pe.wait_ge(s_tabs, i - 7)
                    nc.tensor.transpose(bank[i % 8][:, 0:P], sources[j][:, b, :], ident[:, :]).then_inc(s_psum, 1)
                pe.wait_ge(s_tabs, 4 * BLOCKS)
                for b in range(BLOCKS):
                    nc.tensor.matmul(bank[b % 8][0:1, 128:256], tile_clip[:, b:b + 1], ident[:, :], start=True, stop=True)
                    nc.tensor.matmul(bank[b % 8][0:1, 256:384], step_min[:, 0, b:b + 1], ident[:, :],
                                     start=True, stop=True).then_inc(s_psum, 1)
                pe.wait_ge(s_tabs, 4 * BLOCKS + 1)
                nc.tensor.matmul(bank[7][:, 0:WINDOWS], ones[:, :], cross_row[:, 0:STEPS_RUN:WINDOW], start=True, stop=True).then_inc(s_psum, 1)



REL = 8
L0_FF, L1_FF = 1024, 256
MOE_E = 8
INNER = 512

_INS = ['x', 'src', 'dst', 'edge_type_8', 'edge_weight', 'L0_gnn_w_in', 'L0_gnn_b_in', 'L0_gnn_g_in', 'L0_gnn_bt_in',
        'L0_gnn_w_l', 'L0_gnn_a_s', 'L0_gnn_a_d', 'L0_gnn_b_l', 'L0_gnn_g_l', 'L0_gnn_bt_l',
        'L0_mix_Wq', 'L0_mix_bq', 'L0_mix_Wk', 'L0_mix_bk', 'L0_mix_Wv', 'L0_mix_bv', 'L0_mix_Wo', 'L0_mix_bo',
        'L0_mix_W1', 'L0_mix_b1', 'L0_mix_W2', 'L0_mix_b2', 'L0_mix_ln1_g', 'L0_mix_ln1_b', 'L0_mix_ln2_g', 'L0_mix_ln2_b',
        'L0_ffn_Wr', 'L0_ffn_br', 'L0_ffn_W1', 'L0_ffn_b1', 'L0_ffn_g1', 'L0_ffn_be1', 'L0_ffn_m1', 'L0_ffn_v1',
        'L0_ffn_W2', 'L0_ffn_b2', 'L0_ffn_g2', 'L0_ffn_be2', 'L0_ffn_m2', 'L0_ffn_v2', 'L0_ffn_Wo', 'L0_ffn_bo',
        'L1_gnn_weight', 'L1_mix_Wqkv', 'L1_mix_ln1_g', 'L1_mix_ln1_b', 'L1_mix_W1', 'L1_mix_b1', 'L1_mix_W2', 'L1_mix_b2',
        'L1_mix_ln2_g', 'L1_mix_ln2_b', 'L1_ffn_W_fx', 'L1_ffn_b_fx', 'L1_ffn_W_x', 'L1_ffn_b_x', 'L1_ffn_W_slice',
        'L1_ffn_b_slice', 'L1_ffn_W_q', 'L1_ffn_W_k', 'L1_ffn_W_v', 'L1_ffn_W_out', 'L1_ffn_b_out', 'L1_ffn_temperature']


class Normalise:

    def __init__(self, space, tag, eps):
        self.stats = space.sb(f"{tag}_stats", [P, UNROLL, PAIR, 6])
        self.mv = space.sb(f"{tag}_mv", [P, UNROLL, PAIR, 2])
        self.std = space.sb(f"{tag}_std", [P, UNROLL, PAIR])
        self.rstd = space.sb(f"{tag}_rstd", [P, UNROLL, PAIR])
        self.eps = eps
        self.s_stats, self.s_mv = space.sem(f"{tag}_s_stats"), space.sem(f"{tag}_s_mv")
        self.s_go = space.sem(f"{tag}_s_go")
        self.s_std, self.s_rstd = space.sem(f"{tag}_s_std"), space.sem(f"{tag}_s_rstd")
        self.s_centred = space.sem(f"{tag}_s_centred")

    def statistics(self, nc, u, n, data):
        for i in range(PAIR):
            last = nc.vector.bn_stats(self.stats[:, u, i, :], data[:, i, :])
        last.then_inc(self.s_stats, 1)

    def aggregate(self, nc, u, n):
        nc.vector.wait_ge(self.s_stats, n)
        nc.vector.sem_inc(self.s_go, 1)
        for i in range(PAIR):
            last = nc.vector.bn_aggr(self.mv[:, u, i, :], self.stats[:, u, i, :])
        last.then_inc(self.s_mv, 1)

    def root(self, nc, u, n):
        nc.scalar.wait_ge(self.s_mv, n)
        nc.scalar.activation(self.std[:, u, :], self.mv[:, u, :, 1], ACT.Sqrt, bias=self.eps[:, 0:1]).then_inc(self.s_std, 1)

    def invert(self, nc, u, n):
        nc.vector.wait_ge(self.s_std, n)
        nc.vector.reciprocal(self.rstd[:, u, :], self.std[:, u, :]).then_inc(self.s_rstd, 1)

    def scale(self, nc, u, n, out, data):
        nc.vector.wait_ge(self.s_rstd, n)
        for i in range(PAIR):
            last = nc.vector.tensor_scalar(out[:, i, :], data[:, i, :], self.mv[:, u, i, 0:1], self.rstd[:, u, i:i + 1],
                                           ALU.subtract, ALU.mult)
        return last

    def centre(self, nc, u, n, out, data, gain):
        nc.vector.wait_ge(self.s_mv, n)
        for i in range(PAIR):
            last = nc.vector.scalar_tensor_tensor(out[:, i, :], data[:, i, :], self.mv[:, u, i, 0:1], gain[:, :], ALU.subtract, ALU.mult)
        last.then_inc(self.s_centred, 1)

    def finish(self, nc, u, n, out, shift):
        nc.vector.wait_ge(self.s_rstd, n)
        nc.vector.wait_ge(self.s_centred, n)
        for i in range(PAIR):
            last = nc.vector.scalar_tensor_tensor(out[:, i, :], out[:, i, :], self.rstd[:, u, i:i + 1], shift[:, :], ALU.mult, ALU.add)
        return last


def transpose_pair(nc, bank, data, ident):
    for i in range(PAIR):
        for a in range(HALVES):
            last = nc.tensor.transpose(bank[:, a * D + i * P:a * D + i * P + P], data[:, i, a * P:(a + 1) * P], ident[:, :])
    return last


def project_pair(nc, bank, data_t, weight):
    for i in range(PAIR):
        for a in range(HALVES):
            last = nc.tensor.matmul(bank[:, i * D:(i + 1) * D], data_t[:, a, i * P:(i + 1) * P], weight[:, a, :],
                                    start=(a == 0), stop=(a == HALVES - 1))
    return last


def pair_rows(ap):
    return ap.rearrange("(t p) d -> p t d", p=P)


def both(rows):
    return rows.unsqueeze(1).to_broadcast([P, PAIR, rows.shape[-1]])


def rounds(engine, part, first, body, last):
    for name in first:
        part(name, (0, 0))
    with engine.Fori(0, ROUNDS - 1) as r:
        for name, ahead in body:
            part(name, (r, ahead))
    for name in last:
        part(name, (ROUNDS - 1, 0))


def loads_ahead(sp, part, loads, stores):
    for q in range(2):
        for name in loads:
            part(name, (0, q))
    with sp.Fori(0, ROUNDS - 2) as r:
        for name in stores:
            part(name, (r, 0))
        for name in loads:
            part(name, (r, 2))
    for q in (2, 1):
        for name in stores:
            part(name, (ROUNDS - q, 0))


def slots(r):
    return [(u, r[0] * UNROLL + (r[1] * UNROLL + u + 1)) for u in range(UNROLL)]


def times(r, per):
    return r[0] * per + (r[1] + 1) * per


def pair_at(r, u):
    return bass.ds(r[0] * (UNROLL * PAIR) + (r[1] * UNROLL + u) * PAIR, PAIR)


class Ring:

    def __init__(self, banks, stages, ahead=()):
        self.banks, self.names, self.left, self.ahead = banks, list(stages), list(stages.values()), ahead

    def place(self, name, u):
        s, size = self.names.index(name) * UNROLL + u, len(self.banks)
        before, rounds_back = [q for q in range(s) if q % size == s % size], 0
        if not before:
            before, rounds_back = [q for q in range(len(self.names) * UNROLL) if q % size == s % size], 1
        q = before[-1]
        shift = (self.names[q // UNROLL] in self.ahead) - (name in self.ahead)
        return self.banks[s % size], self.left[q // UNROLL], (rounds_back - shift) * UNROLL + u - q % UNROLL

    def bank(self, name, u):
        return self.place(name, u)[0]

    def enter(self, pe, name, u, n):
        bank, left, behind = self.place(name, u)
        pe.wait_ge(left, n + (UNROLL - behind))
        return bank


class Projection:

    def __init__(self, nc, space, io, dram, keep, gathers, layer, scores):
        sb, sem = space.sb, space.sem
        self.nc, self.io, self.layer, self.scores, self.ident = nc, io, layer, scores, keep["ident"]
        self.w = sb("w_l", [P, HALVES, D])
        self.a = sb("a", [P, 2, D])
        self.prod = sb("prod", [P, HALVES, 2, D])
        self.wa = sb("wa", [P, HALVES, 2 * GAT_HEADS])
        self.ht = sb("ht", [P, UNROLL, HALVES, PAIR * P])
        self.row = sb("row", [P, UNROLL, PAIR, GAT_ROW])
        self.score_bank = [space.ps(f"score_bank{i}", [P, 512]) for i in range(2)]
        self.s_w, self.s_prod, self.s_wa, self.s_ht, self.s_htc, self.s_mm, self.s_row, self.s_sc, self.s_used = (
            sem(n) for n in ("p_w", "p_prod", "p_wa", "p_ht", "p_htc", "p_mm", "p_row", "p_sc", "p_used"))
        self.s_sent = space.sems("p_sent", UNROLL)
        self.first, self.first_pos = dram["first"], keep["first_pos"]
        self.node_score = sb("node_score", [P, UNROLL * PAIR, GAT_HEADS])
        self.node_pos = sb("node_pos", [P, UNROLL * PAIR], I32)
        self.s_copy, self.s_dummy, self.s_landed = (sem(n) for n in ("p_copy", "p_dummy", "p_landed"))
        self.s_scatter = gathers.start(range(UNROLL))
        gathers.count(range(UNROLL), N_TILES // UNROLL)
        self.ring = Ring([space.ps(f"p_ring{i}", [P, 512]) for i in range(3)], {"turn": self.s_htc, "project": self.s_row})
        self.feat = pair_rows(dram["feat"][layer % 2])

    def start_sp(self, sp):
        sp.dma_start(self.w[:, :, :], self.io["L0_gnn_w_l"][self.layer].rearrange("(a p) n -> p a n", p=P)).then_inc(self.s_w, 16)
        for j, n in enumerate(("a_s", "a_d")):
            sp.dma_start(self.a[:, j, :], rows_of(self.io[f"L0_gnn_{n}"][self.layer].rearrange("h d -> (h d)"))).then_inc(self.s_w, 16)
        sp.sem_inc(self.s_used, UNROLL)

    def start_dve(self, dve):
        nc = self.nc
        dve.sem_inc(self.s_sc, UNROLL)
        dve.wait_ge(self.s_w, 48)
        for i in range(HALVES):
            for j in range(2):
                last = nc.vector.tensor_tensor(self.prod[:, i, j, :], self.w[:, i, :], self.a[:, j, :], ALU.mult)
        last.then_inc(self.s_prod, 1)
        dve.wait_ge(self.s_prod, 1)
        nc.vector.tensor_reduce(self.wa[:, :, :].rearrange("p i s -> p (i s)"),
                                self.prod[:, :, :, :].rearrange("p i j (h d) -> p (i j h) d", d=GAT_DIM), AX.X, ALU.add).then_inc(self.s_wa, 1)

    def start_act(self, act):
        act.sem_inc(self.s_htc, UNROLL)
        act.sem_inc(self.s_row, UNROLL)

    def start_pe(self, pe):
        pe.wait_ge(self.s_wa, 1)

    def turn_pe(self, pe, u, n, data):
        bank = self.ring.enter(pe, "turn", u, n)
        transpose_pair(self.nc, bank, data, self.ident).then_inc(self.s_ht, 1)

    def turn_act(self, act, u, n):
        act.wait_ge(self.s_ht, n)
        self.nc.scalar.copy(self.ht[:, u].rearrange("p a n -> p (a n)"), self.ring.bank("turn", u)[:, :]).then_inc(self.s_htc, 1)

    def project_pe(self, pe, u, n):
        bank = self.ring.enter(pe, "project", u, n)
        pe.wait_ge(self.s_htc, n + UNROLL)
        project_pair(self.nc, bank, self.ht[:, u], self.w)
        pe.wait_ge(self.s_sc, n + UNROLL - (1, 3, 2, 2, 2)[u])
        for i in range(PAIR):
            c = 8 * i
            for k in range(HALVES):
                last = self.nc.tensor.matmul(self.score_bank[u % 2][:, c:c + 8], self.ht[:, u, k, i * P:(i + 1) * P], self.wa[:, k, :],
                                             start=(k == 0), stop=(k == HALVES - 1))
        last.then_inc(self.s_mm, 1)

    def project_act(self, act, u, n):
        act.wait_ge(self.s_mm, n)
        act.wait_ge(self.s_used, n)
        self.nc.scalar.copy(self.row[:, u, :, 0:D], self.ring.bank("project", u)[:, :].rearrange("p (i d) -> p i d", i=PAIR)).then_inc(self.s_row, 1)

    def project_dve(self, dve, u, n, pair):
        dve.wait_ge(self.s_mm, n)
        dve.wait_ge(self.s_used, n)
        sc = self.score_bank[u % 2][:, 0:16].rearrange("p (i s) -> p i s", i=PAIR)
        self.nc.vector.tensor_copy(self.row[:, u, :, D:], sc[:, :, 0:GAT_HEADS])
        self.nc.vector.tensor_copy(self.scores[:, pair, :], sc).then_inc(self.s_sc, 1)

    def send(self, sp, u, n, pair):
        sp.wait_ge(self.s_row, n + UNROLL)
        sp.wait_ge(self.s_sc, n + UNROLL)
        sp.dma_start(self.feat[:, pair, :], self.row[:, u, :, :]).then_inc(self.s_sent[u], 16)

    def sent(self, sp, u, r):
        sp.wait_ge(self.s_sent[u], times(r, 16))
        sp.sem_inc(self.s_used, 1)
        sp.wait_ge(self.s_scatter[u][0], times(r, 16 * PAIR) + self.s_scatter[u][1])
        sp.sem_inc(self.s_landed, 1)

    def start_pool(self, pool):
        pool.sem_inc(self.s_landed, UNROLL)

    def scatter_pool(self, pool, r):
        nc = self.nc
        n = r[0] * UNROLL + (r[1] + 1) * UNROLL
        tiles = bass.ds(r[0] * (UNROLL * PAIR) + r[1] * (UNROLL * PAIR), UNROLL * PAIR)
        pool.wait_ge(self.s_landed, n)
        pool.wait_ge(self.s_sc, n + UNROLL)
        nc.gpsimd.tensor_copy(self.node_score[:, :, :], self.scores[:, tiles, GAT_HEADS:])
        nc.gpsimd.tensor_copy(self.node_pos[:, :], self.first_pos[:, tiles]).then_inc(self.s_copy, 1)
        pool.wait_ge(self.s_copy, r[0] + (r[1] + 1))
        pool.sem_inc(self.s_dummy, 1)
        for t in range(UNROLL * PAIR):
            nc.gpsimd.indirect_dma_start(
                out=self.first, out_offset=bass.IndirectOffsetOnAxis(ap=self.node_pos[:, t:t + 1], axis=0),
                in_=self.node_score[:, t, :], in_offset=None, bounds_check=STEPS_PAD * P - 1,
                oob_is_err=False).then_inc(self.s_scatter[t // PAIR][0], 16)


class Elu:

    def __init__(self, space, tag):
        self.pos, self.neg = space.sb(f"{tag}_pos", [P, UNROLL, PAIR, D]), space.sb(f"{tag}_neg", [P, UNROLL, PAIR, D])
        self.s_neg, self.s_exp = space.sem(f"{tag}_s_neg"), space.sem(f"{tag}_s_exp")

    def parts(self, nc, u, n, y):
        nc.scalar.activation(self.pos[:, u], y, ACT.Relu)
        nc.scalar.activation(self.neg[:, u], y, ACT.Relu, scale=-1.0).then_inc(self.s_neg, 1)

    def exponent(self, nc, u, n):
        nc.scalar.wait_ge(self.s_neg, n)
        nc.scalar.activation(self.neg[:, u], self.neg[:, u], ACT.Exp, scale=-1.0).then_inc(self.s_exp, 1)

    def total(self, nc, u, n, out):
        nc.vector.wait_ge(self.s_exp, n)
        return nc.vector.scalar_tensor_tensor(out, self.neg[:, u], -1.0, self.pos[:, u], ALU.add, ALU.add)


def gnn_input(nc, io, dram, keep, gathers, scores):
    FIRST, LAST = ["norm0", "turn0", "project0"], ["turn", "project"]
    BODY = [("norm0", 1), ("turn", 0), ("turn0", 1), ("project", 0), ("project0", 1)]
    with ExitStack() as stack:
        space = Space(nc, stack, "gin")
        sb, sem = space.sb, space.sem
        w = sb("w", [P, HALVES, D])
        rows = {n: sb(n, [P, D]) for n in ("b_in", "g_in", "bt_in")}
        x = sb("x", [P, UNROLL, PAIR, D])
        xn = sb("xn", [P, UNROLL, PAIR, D])
        xt = sb("xt", [P, UNROLL, HALVES, PAIR * P])
        y = sb("y", [P, UNROLL, PAIR, D])
        h = sb("h", [P, UNROLL, PAIR, D])
        ln0, ln1 = Normalise(space, "ln0", keep["eps"]), Normalise(space, "ln1", keep["eps"])
        elu = Elu(space, "elu")
        project = Projection(nc, space, io, dram, keep, gathers, 0, scores)
        s_w, s_x, s_sent = sem("s_w"), space.sems("s_x", UNROLL), space.sems("s_sent", UNROLL)
        s_stored, s_xn, s_xt, s_xtc, s_y, s_yb, s_ya, s_h = (
            sem(n) for n in ("s_stored", "s_xn", "s_xt", "s_xtc", "s_y", "s_yb", "s_ya", "s_h"))
        ring = Ring([space.ps(f"ring{i}", [P, 512]) for i in range(3)], {"turn0": s_xtc, "project0": s_yb})
        tiles, hidden = pair_rows(dram["x0"]), pair_rows(dram["hidden"])
        with nc.Block() as block:

            @block.sync
            def _(sp):
                sp.dma_start(w[:, :, :], io["L0_gnn_w_in"].rearrange("(a p) n -> p a n", p=P)).then_inc(s_w, 16)
                for n, t in rows.items():
                    sp.dma_start(t[:, :], rows_of(io[f"L0_gnn_{n}"])).then_inc(s_w, 16)
                project.start_sp(sp)
                sp.sem_inc(s_stored, UNROLL)

                def part(name, r):
                    for u, n in slots(r):
                        if name == "load":
                            sp.wait_ge(s_xn, n)
                            sp.dma_start(x[:, u, :, :], tiles[:, pair_at(r, u), :]).then_inc(s_x[u], 16)
                        elif name == "store":
                            sp.wait_ge(s_h, n)
                            sp.dma_start(hidden[:, pair_at(r, u), :], h[:, u, :, :]).then_inc(s_sent[u], 16)
                        elif name == "send":
                            project.send(sp, u, n, pair_at(r, u))
                        else:
                            sp.wait_ge(s_sent[u], times(r, 16))
                            sp.sem_inc(s_stored, 1)
                            project.sent(sp, u, r)

                loads_ahead(sp, part, ["load"], ["store", "send", "done"])

            @block.vector
            def _(dve):
                dve.sem_inc(s_xn, UNROLL)
                dve.sem_inc(s_yb, UNROLL)
                dve.wait_ge(s_w, 64)
                project.start_dve(dve)

                def part(name, r):
                    if name == "norm0":
                        for u, n in slots(r):
                            dve.wait_ge(s_x[u], times(r, 16))
                            ln0.statistics(nc, u, n, x[:, u])
                        for u, n in slots(r):
                            ln0.aggregate(nc, u, n)
                        for u, n in slots(r):
                            ln0.invert(nc, u, n)
                        for u, n in slots(r):
                            ln0.scale(nc, u, n, xn[:, u], x[:, u]).then_inc(s_xn, 1)
                    elif name == "project0":
                        for u, n in slots(r):
                            dve.wait_ge(s_y, n)
                            nc.vector.tensor_tensor(y[:, u], ring.bank(name, u)[:, :].rearrange("p (i d) -> p i d", i=PAIR), both(rows["b_in"][:, :]),
                                                    ALU.add).then_inc(s_yb, 1)
                        for u, n in slots(r):
                            dve.wait_ge(s_yb, n + UNROLL)
                            ln1.statistics(nc, u, n, y[:, u])
                        for u, n in slots(r):
                            ln1.aggregate(nc, u, n)
                        for u, n in slots(r):
                            ln1.centre(nc, u, n, y[:, u], y[:, u], rows["g_in"])
                        for u, n in slots(r):
                            ln1.invert(nc, u, n)
                        for u, n in slots(r):
                            ln1.finish(nc, u, n, y[:, u], rows["bt_in"]).then_inc(s_ya, 1)
                        for u, n in slots(r):
                            dve.wait_ge(s_stored, n)
                            elu.total(nc, u, n, h[:, u]).then_inc(s_h, 1)
                    elif name == "project":
                        for u, n in slots(r):
                            project.project_dve(dve, u, n, pair_at(r, u))

                rounds(dve, part, FIRST, BODY, LAST)

            @block.scalar
            def _(act):
                act.sem_inc(s_xtc, UNROLL)
                project.start_act(act)

                def part(name, r):
                    for u, n in slots(r):
                        if name == "norm0":
                            ln0.root(nc, u, n)
                        elif name == "turn0":
                            act.wait_ge(s_xt, n)
                            nc.scalar.copy(xt[:, u].rearrange("p a n -> p (a n)"), ring.bank(name, u)[:, :]).then_inc(s_xtc, 1)
                        elif name == "project0":
                            ln1.root(nc, u, n)
                        elif name == "turn":
                            project.turn_act(act, u, n)
                        else:
                            project.project_act(act, u, n)
                    if name == "project0":
                        for u, n in slots(r):
                            act.wait_ge(s_ya, n)
                            elu.parts(nc, u, n, y[:, u])
                        for u, n in slots(r):
                            elu.exponent(nc, u, n)

                rounds(act, part, FIRST, BODY, LAST)

            @block.gpsimd
            def _(pool):
                project.start_pool(pool)

                def part(name, r):
                    if name == "project":
                        project.scatter_pool(pool, r)

                rounds(pool, part, FIRST, BODY, LAST)

            @block.tensor
            def _(pe):
                pe.wait_ge(s_w, 64)
                project.start_pe(pe)

                def part(name, r):
                    for u, n in slots(r):
                        if name == "turn0":
                            pe.wait_ge(s_xn, n + UNROLL)
                            bank = ring.enter(pe, name, u, n)
                            transpose_pair(nc, bank, xn[:, u], keep["ident"]).then_inc(s_xt, 1)
                        elif name == "project0":
                            bank = ring.enter(pe, name, u, n)
                            pe.wait_ge(s_xtc, n + UNROLL)
                            project_pair(nc, bank, xt[:, u], w).then_inc(s_y, 1)
                        elif name == "turn":
                            pe.wait_ge(s_h, n)
                            project.turn_pe(pe, u, n, h[:, u])
                        elif name == "project":
                            project.project_pe(pe, u, n)

                rounds(pe, part, FIRST, BODY, LAST)


def rounds_between(engine, part, first, body, last):
    def run(parts, at, k):
        before = 0
        for name, ahead, groups in parts + [(None, 0, 0)]:
            pairs = [((k[0], k[1], k[2] + q), p) for q in range(before) for p in range(Messages.GROUP // 2)]
            part(name, at(ahead), pairs)
            k, before = (k[0], k[1], k[2] + before), groups
        return k

    k = run([(name, 0, n) for name, n in first], lambda ahead: (0, 0), (0, 0, 0))[2]
    per = sum(n for _, _, n in body)
    with engine.Fori(0, ROUNDS - 1) as r:
        run(body, lambda ahead: (r, ahead), (r, per, k))
    run([(name, 0, n) for name, n in last], lambda ahead: (ROUNDS - 1, 0), (0, 0, k + per * (ROUNDS - 1)))


class Pace:

    def __init__(self, do_pair, turns):
        self.do_pair, self.turns = do_pair, turns

    def begin(self, name, pairs):
        self.pairs, self.done, self.turn, self.total = pairs, 0, 0, UNROLL * self.turns.get(name, 1)

    def slots(self, r):
        for u, n in slots(r):
            yield u, n
            self.turn += 1
            self.catch_up(len(self.pairs) * self.turn // self.total)

    def catch_up(self, n):
        while self.done < min(n, len(self.pairs)):
            self.do_pair(*self.pairs[self.done])
            self.done += 1

    def end(self):
        self.catch_up(len(self.pairs))


def next_group(at):
    return at[0], at[1], at[2] + 1


def groups_in(first, body, last):
    return sum(n for _, n in first) + (ROUNDS - 1) * sum(n for _, _, n in body) + sum(n for _, n in last)


class Messages:
    GROUP = 8
    SETS = 3
    BANKS = 2

    def __init__(self, nc, space, keep, gathers, table, acc, first_group, n_groups):
        sb, sem = space.sb, space.sem
        assert n_groups % self.SETS == 0
        self.nc, self.keep, self.table, self.acc, self.first_step, self.n_groups = nc, keep, table, acc, first_group * self.GROUP, n_groups
        n = self.GROUP * self.SETS
        self.got = sb("got", [P, n, D])
        self.idx = sb("idx", [P, n], I32)
        self.onehot = sb("onehot", [P, n, P])
        self.bank = [space.ps(f"m_bank{i}", [P, 512]) for i in range(self.BANKS)]
        self.s_got = gathers.start(range(n))
        gathers.count(range(n), n_groups // self.SETS)
        self.s_idx, self.s_dummy, self.s_hot, self.s_sum, self.s_acc = (sem(f"m_{n}") for n in ("idx", "dummy", "hot", "sum", "acc"))

    def number(self, at, per, add):
        r, groups, k = at
        return r * (groups * per) + (k * per + add)

    def step(self, at, j):
        return bass.ds(self.number(at, self.GROUP, j + self.first_step), 1)

    def slot(self, at, j):
        return at[2] % self.SETS * self.GROUP + j

    def pool(self, pool):
        nc, G, S = self.nc, self.GROUP, self.SETS
        with pool.Fori(0, self.n_groups // S) as r:
            for q in range(S):
                group = slice(q * G, (q + 1) * G)
                pool.wait_ge(self.s_sum, r * (S * G // 2) + (q + 1) * (G // 2))
                nc.gpsimd.tensor_copy(self.idx[:, group], self.keep["rel_tab"][:, bass.ds(r * (S * G) + (q * G + self.first_step), G)]).then_inc(self.s_idx, 1)
                pool.wait_ge(self.s_idx, r * S + (q + 1))
                pool.sem_inc(self.s_dummy, 1)
                for u in range(q * G, (q + 1) * G):
                    nc.gpsimd.indirect_dma_start(
                        out=self.got[:, u, :], out_offset=None, in_=self.table,
                        in_offset=bass.IndirectOffsetOnAxis(ap=self.idx[:, u:u + 1], axis=0)).then_inc(self.s_got[u][0], 16)

    def prepare(self, at, j):
        k = self.step(at, j)
        self.nc.vector.tensor_scalar(self.onehot[:, self.slot(at, j), :], self.keep["iota_row"][:, :], self.keep["dst_tab"][:, k],
                                     self.keep["wt_tab"][:, k], ALU.is_equal, ALU.mult).then_inc(self.s_hot, 1)

    def start_dve(self, dve):
        dve.sem_inc(self.s_acc, 2 * self.BANKS)
        for j in range(self.GROUP):
            self.prepare((0, 0, 0), j)

    def pair_dve(self, dve, at, p):
        nc, G = self.nc, self.GROUP
        if p == 0:
            _, self.tiles = nc.values_load_multi_w_load_instructions(
                self.keep["tile_row"][0:1, bass.ds(self.number(at, G, self.first_step), G)], engines=[mybir.EngineType.DVE], min_val=0,
                max_val=LAST_TILE, skip_runtime_bounds_check_because="build_tables keeps tiles at most LAST_TILE")
        dve.wait_ge(self.s_sum, self.number(at, G // 2, p + 1 + self.SETS * G // 2))
        for i in range(2):
            j = 2 * p + i
            dve.wait_ge(self.s_acc, self.number(at, G, j + 2 * self.BANKS))
            rows = self.acc[:, bass.ds(self.tiles[j], 1), :].rearrange("p t d -> p (t d)")
            nc.vector.tensor_tensor(rows, rows, self.bank[p % self.BANKS][:, i * D:(i + 1) * D], ALU.add).then_inc(self.s_acc, 1)
            self.prepare(next_group(at), j)

    def settle(self, dve, at, p):
        dve.wait_ge(self.s_acc, self.number(at, self.GROUP, 2 * p + 2 + 2 * self.BANKS))

    def wait_all(self, engine):
        engine.wait_ge(self.s_acc, 2 * self.BANKS + self.n_groups * self.GROUP)

    def start_pe(self, pe):
        pe.sem_inc(self.s_sum, self.SETS * self.GROUP // 2)

    def pair_pe(self, pe, at, p):
        G = self.GROUP
        pe.wait_ge(self.s_acc, self.number(at, G, 2 * p + 2))
        for i in range(2):
            u = self.slot(at, 2 * p + i)
            pe.wait_ge(self.s_hot, self.number(at, G, 2 * p + i + 1))
            sem, had = self.s_got[u]
            r, groups, k = at
            pe.wait_ge(sem, r * (groups // self.SETS * 16) + (k // self.SETS * 16 + 16 + had))
            last = self.nc.tensor.matmul(self.bank[p % self.BANKS][:, i * D:(i + 1) * D], self.onehot[:, u, :], self.got[:, u, :],
                                         start=True, stop=True)
        last.then_inc(self.s_sum, 1)


def gat_messages(nc, dram, keep, gathers, layer, acc):
    W, H, B = WINDOW, GAT_HEADS, WINDOW_BUFS
    WH = W * H
    GROUP = 14
    HOTS = W // 2
    BANKS = 4
    LAG = 3
    assert W % GROUP == 0 and W % BANKS == 0
    DVE_AT = dict(zip((0, 4, 8, 12, 16, 20, 25), "ABCDEFG"))
    PE_AT = dict(zip((1, 5, 9, 13, 17, 22), "ABCDEF"))
    ACT_AT = dict(zip((18, 21), "EF"))
    with ExitStack() as stack:
        space = Space(nc, stack, f"gm{layer}")
        sb, sem = space.sb, space.sem
        got = sb("got", [P, B, W, GAT_SUM])
        idx = sb("idx", [P, B, W], I32)
        d_edge = sb("d_edge", [P, STEPS_PAD, H])
        d_step = sb("d_step", [P, P, H])
        starts = sb("starts", [P, 2, P])
        start_row = sb("start_row", [1, P])
        d_chain = sb("d_chain", [1, H, P + 1])
        d_carry = sb("d_carry", [P, H])
        flags = sb("flags", [WH, B, 5, P])
        resets = sb("resets", [1, B, 2, W])
        onehot = sb("onehot", [P, HOTS, P])
        e = sb("e", [P, W, H])
        seg, top, weight, last_top = (sb(n, [WH, P]) for n in ("seg", "top", "weight", "last_top"))
        chain = sb("chain", [1, 2, W + 1, H])
        carry = sb("carry", [WH, 2])
        fall = sb("fall", [1, H])
        rescale = sb("rescale", [P, H])
        ones = sb("ones", [1, P])
        bank = [space.ps(f"bank{i}", [P, 512]) for i in range(BANKS)]
        bank_e, bank_c, bank_w = (space.ps(n, [P, 512]) for n in ("bank_e", "bank_c", "bank_w"))
        s_got = gathers.start(range(B))
        gathers.count(range(B), (WINDOWS // B) * W)
        s_block, s_spread_dve, s_d_last, s_d_row, s_d_chain, s_d_col, s_d_spread, s_d_turn, s_d_edge = (
            sem(n) for n in ("s_block", "s_spread_dve", "s_d_last", "s_d_row", "s_d_chain", "s_d_col", "s_d_spread",
                             "s_d_turn", "s_d_edge"))
        first = dram["first"].rearrange("(k e) q -> k (e q)", e=P)
        one_head = dram["flags"].rearrange("(k h) f e -> h k f e", h=H)[0]
        s_flags = space.sems("s_flags", B)
        names = ("s_idx", "s_dummy", "s_hot", "s_scaled", "s_sum", "s_acc", "s_zero", "s_dve", "s_e", "s_et", "s_fwd", "s_fwd_row",
                 "s_chain", "s_carry", "s_back", "s_back_row", "s_back_chain", "s_back_carry", "s_fall", "s_factor", "s_diff", "s_exp",
                 "s_last", "s_turn", "s_weights", "s_rescale", "s_rescaled", "s_used", "s_turns")
        (s_idx, s_dummy, s_hot, s_scaled, s_sum, s_acc, s_zero, s_dve, s_e, s_et, s_fwd, s_fwd_row, s_chain, s_carry, s_back, s_back_row,
         s_back_chain, s_back_carry, s_fall, s_factor, s_diff, s_exp, s_last, s_turn, s_weights, s_rescale, s_rescaled, s_used, s_turns) = (
            sem(n) for n in names)
        ident = keep["ident"]
        flag_rows = dram["flags"].rearrange("k f e -> k (f e)")
        AHEAD = B * W

        def windows(r):
            return [((r, c), (r, c - 1)) for c in range(1, B + 1)]

        def number(w):
            return w[0] * B + w[1]

        def loaded(w, per):
            return w[0] * per + (w[1] // B + 1) * per

        def program(engine, softmax_part, sum_step, at):
            def both_parts(w, v):
                for i in range(W):
                    if w is not None and i in at:
                        softmax_part(at[i], w)
                    if v is not None:
                        sum_step(v, i)

            both_parts((0, 0), None)
            with engine.Fori(0, WINDOWS // B - 1) as r:
                for w, v in windows(r):
                    both_parts(w, v)
            end = WINDOWS // B - 1
            for w, v in windows(end)[:-1]:
                both_parts(w, v)
            both_parts(None, (end, B - 1))

        with nc.Block() as block:

            @block.gpsimd
            def _(pool):
                with pool.Fori(0, WINDOWS // B) as r:
                    for b in range(B):
                        w = r * B + b
                        for g in range(W // GROUP):
                            group = slice(g * GROUP, (g + 1) * GROUP)
                            pool.wait_ge(s_sum, w * W + (g + 1) * GROUP)
                            nc.gpsimd.tensor_copy(idx[:, b, group], keep["src_tab"][:, bass.ds(w * W + g * GROUP, GROUP)]).then_inc(s_idx, 1)
                            pool.wait_ge(s_idx, w * (W // GROUP) + (g + 1))
                            pool.sem_inc(s_dummy, 1)
                            for k in range(g * GROUP, (g + 1) * GROUP):
                                nc.gpsimd.indirect_dma_start(
                                    out=got[:, b, k, 0:GAT_ROW], out_offset=None, in_=dram["feat"][layer % 2],
                                    in_offset=bass.IndirectOffsetOnAxis(ap=idx[:, b, k:k + 1], axis=0)).then_inc(s_got[b][0], 16)

            @block.sync
            def _(sp):
                with sp.Fori(0, BLOCKS) as k:
                    sp.wait_ge(s_d_turn, k + 1)
                    rows = bass.ds(k * P, P)
                    sp.dma_start(d_step[:, :, :].rearrange("p e q -> p (e q)"), first[rows, :]).then_inc(s_block, 16)
                    for j in range(2):
                        sp.dma_start(starts[:, j, :], one_head[rows, 2 * j, :]).then_inc(s_block, 16)
                    sp.dma_start(start_row[:, :], dram["resets"][0:1, rows]).then_inc(s_block, 16)
                with sp.Fori(0, WINDOWS // B) as r:
                    for b in range(B):
                        sp.wait_ge(s_used, r * B + b + 1)
                        sp.dma_start(flags[:, b].rearrange("k f e -> k (f e)"), flag_rows[bass.ds(r * (B * WH) + b * WH, WH), :]).then_inc(s_flags[b], 16)
                        sp.dma_start(resets[:, b, :, :].rearrange("o f k -> o f k"),
                                     dram["resets"][:, bass.ds(r * (B * W) + b * W, W)].unsqueeze(0)).then_inc(s_flags[b], 16)

            @block.vector
            def _(dve):
                dve.sem_inc(s_acc, BANKS)
                dve.sem_inc(s_used, B)
                nc.vector.memset(chain[:, :, :, :], -BIG)
                nc.vector.memset(d_chain[:, :, :], -BIG)
                nc.vector.memset(ones[:, :], 1.0)
                nc.vector.memset(acc[:, :, :], 0.0).then_inc(s_zero, 1)
                dve.wait_ge(s_zero, 1)
                with dve.Fori(0, BLOCKS) as k:
                    dve.wait_ge(s_block, k * 64 + 64)
                    for h in range(H):
                        last = nc.vector.tensor_tensor_scan(d_step[:, :, h], starts[:, 0, :], d_step[:, :, h], -BIG, ALU.add, ALU.max)
                    last.then_inc(s_d_last, 1)
                    dve.wait_ge(s_d_row, k + 1)
                    for h in range(H):
                        last = nc.vector.tensor_tensor_scan(d_chain[:, h, 1:], start_row[:, :], bank_c[0:1, h * P:(h + 1) * P], d_chain[:, h, 0:1],
                                                            ALU.add, ALU.max)
                    last.then_inc(s_d_chain, 1)
                    dve.wait_ge(s_d_col, k + 1)
                    nc.vector.tensor_copy(d_chain[:, :, 0:1], d_chain[:, :, P:P + 1])
                    nc.vector.tensor_copy(d_carry[:, :], bank_w[:, 0:H]).then_inc(s_spread_dve, 1)
                    dve.wait_ge(s_spread_dve, k + 1)
                    for h in range(H):
                        last = nc.vector.scalar_tensor_tensor(d_step[:, :, h], starts[:, 1, :], d_carry[:, h:h + 1], d_step[:, :, h], ALU.add, ALU.max)
                    last.then_inc(s_d_spread, 1)
                    dve.wait_ge(s_d_turn, k + 2)
                    nc.vector.tensor_copy(d_edge[:, bass.ts(k, P), :].rearrange("p k h -> p h k"),
                                          bank_e[:, :].rearrange("p (h k) -> p h k", h=H)).then_inc(s_d_edge, 1)
                dve.wait_ge(s_d_edge, BLOCKS)
                PER = 9
                c = Count(dve, s_dve)
                tiles = {}

                def softmax_part(name, w):
                    n, b = number(w) + 1, w[1] % B
                    if name == "A":
                        c.base, c.n = number(w) * PER, 0
                        dve.wait_ge(s_got[b][0], loaded(w, 16 * W) + s_got[b][1])
                        c.done(nc.vector.tensor_tensor(e[:, :, :], got[:, b, :, D:GAT_ROW], d_edge[:, bass.ds(number(w) * W, W), :], ALU.add))
                        nc.vector.scalar_tensor_tensor(e[:, :, :], e[:, :, :], 0.2, e[:, :, :], ALU.mult, ALU.max).then_inc(s_e, 1)
                    elif name == "B":
                        dve.wait_ge(s_et, n)
                        dve.wait_ge(s_flags[b], loaded(w, 32))
                        c.done(nc.vector.tensor_tensor(seg[:, :], bank_e[0:WH, 0:P], flags[:, b, 4, :], ALU.add))
                        nc.vector.tensor_tensor_scan(seg[:, :], flags[:, b, 0, :], seg[:, :], -BIG, ALU.add, ALU.max).then_inc(s_fwd, 1)
                    elif name == "C":
                        dve.wait_ge(s_fwd_row, n)
                        for h in range(H):
                            last = nc.vector.tensor_tensor_scan(chain[:, 0, 1:, h], resets[:, b, 0, :], bank_c[0:1, h:WH:H], chain[:, 0, 0:1, h],
                                                                ALU.add, ALU.max)
                        last.then_inc(s_chain, 1)
                    elif name == "D":
                        dve.wait_ge(s_carry, n)
                        c.done(nc.vector.tensor_copy(carry[:, 0:1], bank_c[0:WH, 256:257]))
                        c.done(nc.vector.scalar_tensor_tensor(seg[:, :], flags[:, b, 2, :], carry[:, 0:1], seg[:, :], ALU.add, ALU.max))
                        nc.vector.tensor_tensor_scan(top[:, ::-1], flags[:, b, 1, ::-1], seg[:, ::-1], -BIG, ALU.add, ALU.max).then_inc(s_back, 1)
                    elif name == "E":
                        dve.wait_ge(s_back_row, n)
                        for h in range(H):
                            last = nc.vector.tensor_tensor_scan(chain[:, 1, W - 1::-1, h], resets[:, b, 1, ::-1], bank_c[0:1, WH - H + h::-H][:, 0:W],
                                                                -BIG, ALU.add, ALU.max)
                        last.then_inc(s_back_chain, 1)
                        dve.wait_ge(s_back_chain, n)
                        c.done(nc.vector.tensor_tensor(fall[:, :], chain[:, 0, 0, :], chain[:, 1, 0, :], ALU.subtract))
                        nc.vector.tensor_scalar(fall[:, :], fall[:, :], 0.0, None, ALU.min).then_inc(s_fall, 1)
                        c.done(nc.vector.tensor_copy(chain[:, 0, 0, :], chain[:, 0, W, :]))
                    elif name == "F":
                        dve.wait_ge(s_back_carry, n)
                        c.done(nc.vector.tensor_copy(carry[:, 1:2], bank_c[0:WH, 256:257]))
                        c.done(nc.vector.scalar_tensor_tensor(top[:, :], flags[:, b, 3, :], carry[:, 1:2], top[:, :], ALU.add, ALU.max))
                        c.done(nc.vector.tensor_tensor(weight[:, :], bank_e[0:WH, 0:P], top[:, :], ALU.subtract))
                        nc.vector.tensor_scalar(weight[:, :], weight[:, :], 0.0, None, ALU.min).then_inc(s_diff, 1)
                        nc.vector.scalar_tensor_tensor(last_top[:, :], flags[:, b, 1, :], -1.0 / BIG, top[:, :], ALU.mult, ALU.mult).then_inc(s_last, 1)
                        dve.wait_ge(s_last, n)
                        dve.sem_inc(s_used, 1)
                    else:
                        assert c.n == PER
                        dve.wait_ge(s_turn, n)
                        nc.vector.tensor_copy(got[:, b, :, D:].rearrange("p k (j h) -> p j k h", j=2),
                                              bank_w[:, 0:2 * WH].rearrange("p (j k h) -> p j k h", j=2, h=H)).then_inc(s_weights, 1)
                        nc.vector.tensor_scalar(rescale[:, :], bank_w[:, 2 * WH:2 * WH + H], -1.0, keep["cross"][:, bass.ds(number(w), 1)],
                                                ALU.add, ALU.mult).then_inc(s_rescale, 1)

                def sum_step(v, i):
                    n = number(v) * W + i

                    def rows(tile, cols):
                        return acc[:, bass.ds(tile, 1), cols].rearrange("p t d -> p (t d)")

                    def add(j):
                        m = number(v) * W + j
                        dve.wait_ge(s_sum, m + (1 + AHEAD))
                        dve.wait_ge(s_acc, m + BANKS)
                        a = rows(tiles[j], slice(0, GAT_SUM))
                        nc.vector.tensor_tensor(a, a, bank[j % BANKS][:, 0:GAT_SUM], ALU.add).then_inc(s_acc, 1)

                    if i == 0:
                        _, loaded_tiles = nc.values_load_multi_w_load_instructions(
                            keep["tile_row"][0:1, bass.ds(number(v) * W, W)], engines=[mybir.EngineType.DVE], min_val=0, max_val=LAST_TILE,
                            skip_runtime_bounds_check_because="build_tables keeps tiles at most LAST_TILE")
                        tiles.update(enumerate(loaded_tiles))
                        dve.wait_ge(s_rescale, number(v) + 1)
                        dve.wait_ge(s_acc, n + BANKS)
                        f = rows(tiles[0], slice(0, D)).rearrange("p (h d) -> p h d", h=H)
                        nc.vector.scalar_tensor_tensor(f, rescale[:, :].unsqueeze(2).to_broadcast([P, H, GAT_DIM]), 1.0, f, ALU.add, ALU.mult)
                        s = rows(tiles[0], slice(D, GAT_ROW))
                        nc.vector.scalar_tensor_tensor(s, rescale[:, :], 1.0, s, ALU.add, ALU.mult).then_inc(s_rescaled, 1)
                    dve.wait_ge(s_sum, n + (1 + AHEAD - HOTS))
                    nc.vector.tensor_scalar(onehot[:, i % HOTS, :], keep["iota_row"][:, :], keep["dst_tab"][:, bass.ds(n, 1)], None,
                                            ALU.is_equal).then_inc(s_hot, 1)
                    if i == LAG:
                        dve.wait_ge(s_rescaled, number(v) + 1)
                    if i >= LAG:
                        add(i - LAG)
                    if i == W - 1:
                        for j in range(W - LAG, W):
                            add(j)

                program(dve, softmax_part, sum_step, DVE_AT)

            @block.scalar
            def _(act):
                def softmax_part(name, w):
                    n = number(w) + 1
                    if name == "E":
                        act.wait_ge(s_fall, n)
                        nc.scalar.activation(fall[:, :], fall[:, :], ACT.Exp).then_inc(s_factor, 1)
                    else:
                        act.wait_ge(s_diff, n)
                        nc.scalar.activation(weight[:, :], weight[:, :], ACT.Exp).then_inc(s_exp, 1)

                def sum_step(v, i):
                    b = v[1] % B
                    if i == 0:
                        act.wait_ge(s_weights, number(v) + 1)
                    for h in range(H):
                        rows = got[:, b, i, h * GAT_DIM:(h + 1) * GAT_DIM]
                        last = nc.scalar.activation(rows, rows, ACT.Copy, scale=got[:, b, i, D + h:D + h + 1])
                    last.then_inc(s_scaled, 1)

                program(act, softmax_part, sum_step, ACT_AT)

            @block.tensor
            def _(pe):
                def softmax_part(name, w):
                    n = number(w) + 1
                    if name == "A":
                        pe.wait_ge(s_e, n)
                        nc.tensor.transpose(bank_e[0:WH, 0:P], e[:, :, :].rearrange("p k h -> p (k h)"), ident[:, :]).then_inc(s_et, 1)
                    elif name == "B":
                        pe.wait_ge(s_fwd, n)
                        nc.tensor.transpose(bank_c[0:1, 0:WH], seg[:, P - 1:P], ident[0:WH, 0:WH]).then_inc(s_fwd_row, 1)
                    elif name == "C":
                        pe.wait_ge(s_chain, n)
                        pe.sem_inc(s_turns, 1)
                        nc.tensor.transpose(bank_c[0:WH, 256:257], chain[:, 0, 0:W, :].rearrange("o k h -> o (k h)"), ident[0:1, 0:1]).then_inc(s_carry, 1)
                    elif name == "D":
                        pe.wait_ge(s_back, n)
                        nc.tensor.transpose(bank_c[0:1, 0:WH], top[:, 0:1], ident[0:WH, 0:WH]).then_inc(s_back_row, 1)
                    elif name == "E":
                        pe.wait_ge(s_back_chain, n)
                        pe.sem_inc(s_turns, 1)
                        nc.tensor.transpose(bank_c[0:WH, 256:257], chain[:, 1, 1:, :].rearrange("o k h -> o (k h)"), ident[0:1, 0:1]).then_inc(s_back_carry, 1)
                    else:
                        pe.wait_ge(s_factor, n)
                        nc.tensor.matmul(bank_w[:, 2 * WH:2 * WH + H], ones[:, :], fall[:, :], start=True, stop=True)
                        pe.wait_ge(s_last, n)
                        nc.tensor.transpose(bank_w[:, WH:2 * WH], last_top[:, :], ident[0:WH, 0:WH])
                        pe.wait_ge(s_exp, n)
                        nc.tensor.transpose(bank_w[:, 0:WH], weight[:, :], ident[0:WH, 0:WH]).then_inc(s_turn, 1)

                def sum_step(v, i):
                    n = number(v) * W + i
                    pe.wait_ge(s_hot, n + 1)
                    pe.wait_ge(s_scaled, n + 1)
                    pe.wait_ge(s_acc, n + 1)
                    nc.tensor.matmul(bank[i % BANKS][:, 0:GAT_SUM], onehot[:, i % HOTS, :], got[:, v[1] % B, i, :],
                                     start=True, stop=True).then_inc(s_sum, 1)

                pe.sem_inc(s_sum, AHEAD)
                pe.sem_inc(s_d_turn, 1)
                with pe.Fori(0, BLOCKS) as k:
                    pe.wait_ge(s_d_last, k + 1)
                    for h in range(H):
                        last = nc.tensor.transpose(bank_c[0:1, h * P:(h + 1) * P], d_step[:, P - 1:P, h], ident[:, :])
                    last.then_inc(s_d_row, 1)
                    pe.wait_ge(s_d_chain, k + 1)
                    pe.sem_inc(s_turns, 1)
                    for h in range(H):
                        last = nc.tensor.transpose(bank_w[:, h:h + 1], d_chain[:, h, 0:P], ident[0:1, 0:1])
                    last.then_inc(s_d_col, 1)
                    pe.wait_ge(s_d_spread, k + 1)
                    for h in range(H):
                        last = nc.tensor.transpose(bank_e[:, h * P:(h + 1) * P], d_step[:, :, h], ident[:, :])
                    last.then_inc(s_d_turn, 1)
                program(pe, softmax_part, sum_step, PE_AT)


def gat_finish(nc, io, dram, keep, gathers, layer, scores, acc, last_layer):
    H = GAT_HEADS
    FIRST, LAST = ["sums", "norm"], ["turn", "project"]
    BODY = [("turn", 0), ("sums", 1), ("project", 0), ("norm", 1)]
    with ExitStack() as stack:
        space = Space(nc, stack, f"gf{layer}")
        sb, sem = space.sb, space.sem
        rows = {n: sb(n, [P, D]) for n in ("b_l", "g_l", "bt_l")}
        feat = sb("feat", [P, UNROLL, PAIR, D])
        old = sb("old", [P, UNROLL, PAIR, D])
        y = sb("y", [P, UNROLL, PAIR, D])
        h = sb("h", [P, UNROLL, PAIR, D])
        e_self, e_top, of_edges, of_self, den = (sb(n, [P, N_TILES, H]) for n in ("e_self", "e_top", "of_edges", "of_self", "den"))
        ln = Normalise(space, "ln", keep["eps"])
        elu = Elu(space, "elu")
        project = None if last_layer else Projection(nc, space, io, dram, keep, gathers, layer + 1, scores)
        s_w, s_sum, s_y, s_yb, s_elu, s_ya, s_h, s_dve, s_fall, s_factors, s_stored, s_self = (
            sem(n) for n in ("s_w", "s_sum", "s_y", "s_yb", "s_elu", "s_ya", "s_h", "s_dve", "s_fall", "s_factors", "s_stored",
                             "s_self"))
        s_feat, s_old, s_sent = space.sems("s_feat", UNROLL), space.sems("s_old", UNROLL), space.sems("s_sent", UNROLL)
        tiles, hidden = pair_rows(dram["feat"][layer % 2]), pair_rows(dram["hidden"])

        def one_tile(ap):
            return ap.rearrange("p (h d) -> p h d", h=H)

        def tile_at(r, u, i):
            return bass.ds(r[0] * (UNROLL * PAIR) + ((r[1] * UNROLL + u) * PAIR + i), 1)

        def spread(ap, t):
            return ap[:, t, :].rearrange("p t h -> p (t h)").unsqueeze(2).to_broadcast([P, H, GAT_DIM])

        with nc.Block() as block:

            @block.sync
            def _(sp):
                for n, t in rows.items():
                    sp.dma_start(t[:, :], rows_of(io[f"L0_gnn_{n}"][layer])).then_inc(s_w, 16)
                if project:
                    project.start_sp(sp)
                sp.sem_inc(s_stored, UNROLL)

                def part(name, r):
                    for u, n in slots(r):
                        if name == "feat":
                            sp.wait_ge(s_yb, n)
                            sp.dma_start(feat[:, u, :, :], tiles[:, pair_at(r, u), 0:D]).then_inc(s_feat[u], 16)
                        elif name == "old":
                            sp.wait_ge(s_h, n)
                            sp.dma_start(old[:, u, :, :], hidden[:, pair_at(r, u), :]).then_inc(s_old[u], 16)
                        elif name == "store":
                            sp.wait_ge(s_h, n + UNROLL)
                            sp.dma_start(hidden[:, pair_at(r, u), :], h[:, u, :, :]).then_inc(s_sent[u], 16)
                        elif name == "send":
                            project.send(sp, u, n, pair_at(r, u))
                        else:
                            sp.wait_ge(s_sent[u], times(r, 16))
                            sp.sem_inc(s_stored, 1)
                            if project:
                                project.sent(sp, u, r)

                loads_ahead(sp, part, ["feat", "old"], ["store", "send", "done"] if project else ["store", "done"])

            @block.gpsimd
            def _(pool):
                pool.wait_ge(s_w, 48)
                pool.wait_ge(s_factors, 2)
                if project:
                    project.start_pool(pool)

                def part(name, r):
                    for u, n in slots(r):
                        if name == "sums":
                            pool.wait_ge(s_feat[u], times(r, 16))
                            for i in range(PAIR):
                                last = nc.gpsimd.tensor_tensor(one_tile(feat[:, u, i]), one_tile(feat[:, u, i]), spread(of_self, tile_at(r, u, i)), ALU.mult)
                            last.then_inc(s_self, 1)
                            pool.wait_ge(s_self, n)
                            nc.gpsimd.tensor_tensor(feat[:, u], feat[:, u], both(rows["b_l"][:, :]), ALU.add).then_inc(s_sum, 1)
                    if name == "project" and project:
                        project.scatter_pool(pool, r)

                rounds(pool, part, FIRST, BODY, LAST)

            @block.vector
            def _(dve):
                c = Count(dve, s_dve)
                dve.sem_inc(s_yb, UNROLL)
                dve.sem_inc(s_h, UNROLL)
                c.done(nc.vector.tensor_tensor(e_self[:, :, :], scores[:, :, 0:H], scores[:, :, H:], ALU.add))
                c.done(nc.vector.scalar_tensor_tensor(e_self[:, :, :], e_self[:, :, :], 0.2, e_self[:, :, :], ALU.mult, ALU.max))
                c.done(nc.vector.tensor_tensor(of_edges[:, :, :], acc[:, :, GAT_ROW:], keep["absent"][:, :].unsqueeze(2).to_broadcast([P, N_TILES, H]),
                                               ALU.add))
                c.done(nc.vector.tensor_tensor(e_top[:, :, :], of_edges[:, :, :], e_self[:, :, :], ALU.max))
                nc.vector.tensor_tensor(of_edges[:, :, :], of_edges[:, :, :], e_top[:, :, :], ALU.subtract)
                nc.vector.tensor_tensor(of_self[:, :, :], e_self[:, :, :], e_top[:, :, :], ALU.subtract).then_inc(s_fall, 1)
                dve.wait_ge(s_factors, 1)
                c.done(nc.vector.tensor_tensor(den[:, :, :], acc[:, :, D:GAT_ROW], of_edges[:, :, :], ALU.mult))
                c.done(nc.vector.scalar_tensor_tensor(den[:, :, :], den[:, :, :], 1e-16, of_self[:, :, :], ALU.add, ALU.add))
                c.done(nc.vector.reciprocal(den[:, :, :], den[:, :, :]))
                nc.vector.tensor_tensor(of_edges[:, :, :], of_edges[:, :, :], den[:, :, :], ALU.mult)
                c.done(nc.vector.tensor_tensor(of_self[:, :, :], of_self[:, :, :], den[:, :, :], ALU.mult))
                dve.sem_inc(s_factors, 1)
                dve.wait_ge(s_w, 48)
                if project:
                    project.start_dve(dve)

                def part(name, r):
                    if name == "sums":
                        for u, n in slots(r):
                            dve.wait_ge(s_h, n)
                            for i in range(PAIR):
                                t = tile_at(r, u, i)
                                last = nc.vector.tensor_tensor(one_tile(y[:, u, i]), one_tile(acc[:, t, 0:D].rearrange("p t d -> p (t d)")),
                                                               spread(of_edges, t), ALU.mult)
                            last.then_inc(s_y, 1)
                        for u, n in slots(r):
                            dve.wait_ge(s_y, n)
                            dve.wait_ge(s_sum, n)
                            nc.vector.tensor_tensor(y[:, u], y[:, u], feat[:, u], ALU.add).then_inc(s_yb, 1)
                        for u, n in slots(r):
                            elu.total(nc, u, n, y[:, u]).then_inc(s_elu, 1)
                    elif name == "norm":
                        for u, n in slots(r):
                            dve.wait_ge(s_elu, n)
                            ln.statistics(nc, u, n, y[:, u])
                        for u, n in slots(r):
                            ln.aggregate(nc, u, n)
                        for u, n in slots(r):
                            ln.centre(nc, u, n, y[:, u], y[:, u], rows["g_l"])
                        for u, n in slots(r):
                            ln.invert(nc, u, n)
                        for u, n in slots(r):
                            ln.finish(nc, u, n, y[:, u], rows["bt_l"]).then_inc(s_ya, 1)
                        for u, n in slots(r):
                            dve.wait_ge(s_ya, n)
                            dve.wait_ge(s_old[u], times(r, 16))
                            dve.wait_ge(s_stored, n)
                            nc.vector.tensor_tensor(h[:, u], old[:, u], y[:, u], ALU.add).then_inc(s_h, 1)
                    elif name == "project" and project:
                        for u, n in slots(r):
                            project.project_dve(dve, u, n, pair_at(r, u))

                rounds(dve, part, FIRST, BODY, LAST)

            @block.scalar
            def _(act):
                act.wait_ge(s_fall, 1)
                nc.scalar.activation(of_edges[:, :, :], of_edges[:, :, :], ACT.Exp)
                nc.scalar.activation(of_self[:, :, :], of_self[:, :, :], ACT.Exp).then_inc(s_factors, 1)
                if project:
                    project.start_act(act)

                def part(name, r):
                    if name == "sums":
                        for u, n in slots(r):
                            act.wait_ge(s_yb, n + UNROLL)
                            elu.parts(nc, u, n, y[:, u])
                        for u, n in slots(r):
                            elu.exponent(nc, u, n)
                    for u, n in slots(r):
                        if name == "norm":
                            ln.root(nc, u, n)
                        elif name == "turn" and project:
                            project.turn_act(act, u, n)
                        elif name == "project" and project:
                            project.project_act(act, u, n)

                rounds(act, part, FIRST, BODY, LAST)

            @block.tensor
            def _(pe):
                if project is None:
                    return
                project.start_pe(pe)

                def part(name, r):
                    for u, n in slots(r):
                        if name == "turn":
                            pe.wait_ge(s_h, n + UNROLL)
                            project.turn_pe(pe, u, n, h[:, u])
                        elif name == "project":
                            project.project_pe(pe, u, n)

                rounds(pe, part, FIRST, BODY, LAST)


def pair_of(r, u):
    return bass.ds(r * (UNROLL * PAIR) + u * PAIR, PAIR)


def units(r):
    return [(u, r * UNROLL + u + 1) for u in range(UNROLL)]


SUMS_PARTS = ([("norm", 1), ("turn", 2)], [("k", 0, 1), ("v", 0, 1), ("norm", 1, 2), ("kv", 0, 1), ("turn", 1, 1)],
              [("k", 1), ("v", 1), ("kv", 1)])
SUMS_TURNS = {"norm": 4}


def linear_attention_sums(nc, io, dram, keep, cfg, kv_sum, messages_of=None):
    with ExitStack() as stack:
        space = Space(nc, stack, cfg["tag"] + "a")
        sb, sem = space.sb, space.sem
        wk, wv = sb("wk", [P, HALVES, D]), sb("wv", [P, HALVES, D])
        raw = sb("raw", [P, 4, D])
        bk, bv = sb("bk", [P, D]), sb("bv", [P, D])
        x = sb("x", [P, UNROLL, PAIR, D])
        xt = sb("xt", [P, UNROLL, HALVES, PAIR * P])
        k = sb("k", [P, UNROLL, PAIR, D])
        neg = sb("neg", [P, UNROLL, PAIR, D])
        v = sb("v", [P, UNROLL, PAIR, D])
        va = sb("va", [P, UNROLL, PAIR, HALVES, P + 1])
        bank = [space.ps(f"bank{u}", [P, 512]) for u in range(6)]
        messages = messages_of(space, groups_in(*SUMS_PARTS)) if messages_of else None
        ln = Normalise(space, "ln", keep["eps"])
        s_x = space.sems("s_x", UNROLL)
        (s_w, s_added, s_xn, s_xt, s_xtc, s_k, s_kb, s_neg, s_exp, s_phi, s_v, s_vb, s_va, s_kv, s_zero, s_turn, s_turned) = (
            sem(n) for n in ("s_w", "s_added", "s_xn", "s_xt", "s_xtc", "s_k", "s_kb", "s_neg", "s_exp", "s_phi", "s_v", "s_vb",
                             "s_va", "s_kv", "s_zero", "s_turn", "s_turned"))
        tiles = pair_rows(cfg["x"])
        turned = cfg["Wqkv"] is not None
        n_w = 1 if turned else 4
        ring = Ring(bank, {"k": s_kb, "v": s_vb, "kv": s_added, "turn": s_xtc}, ahead=["turn"])

        def node_rows(name, u):
            return ring.bank(name, u)[:, :].rearrange("p (i d) -> p i d", i=PAIR)

        def run(engine, part, pace=None):
            first, body, last = SUMS_PARTS
            if messages is None or pace is None:
                rounds(engine, part, [n for n, _ in first], [(n, a) for n, a, _ in body], [n for n, _ in last])
            else:
                def paced(name, r, pairs):
                    pace.begin(name, pairs)
                    if name:
                        part(name, r)
                    pace.end()

                rounds_between(engine, paced, first, body, last)

        with nc.Block() as block:

            @block.sync
            def _(sp):
                if turned:
                    sp.dma_start(raw[:, :, :], cfg["Wqkv"][D:3 * D, :].rearrange("(b p) i -> p b i", p=P)).then_inc(s_w, 16)
                else:
                    sp.dma_start(wk[:, :, :], cfg["Wk"].rearrange("(a p) n -> p a n", p=P)).then_inc(s_w, 16)
                    sp.dma_start(wv[:, :, :], cfg["Wv"].rearrange("(a p) n -> p a n", p=P)).then_inc(s_w, 16)
                    sp.dma_start(bk[:, :], rows_of(cfg["bk"])).then_inc(s_w, 16)
                    sp.dma_start(bv[:, :], rows_of(cfg["bv"])).then_inc(s_w, 16)
                with sp.Fori(0, ROUNDS) as r:
                    for u, n in units(r):
                        sp.wait_ge(s_xt, n)
                        sp.dma_start(x[:, u, :, :], tiles[:, pair_of(r, u), :]).then_inc(s_x[u], 16)

            @block.vector
            def _(dve):
                for left in ring.left:
                    dve.sem_inc(left, UNROLL)
                dve.sem_inc(s_xn, UNROLL)
                if turned:
                    nc.vector.memset(bk[:, :], 0.0)
                    nc.vector.memset(bv[:, :], 0.0)
                nc.vector.memset(kv_sum[:, :, :], 0.0).then_inc(s_zero, 1)
                dve.wait_ge(s_zero, 1)
                dve.wait_ge(s_w, 16 * n_w)

                pace = Pace(messages and (lambda at, p: messages.pair_dve(dve, at, p)), SUMS_TURNS)
                pace.begin(None, [])

                def part(name, r):
                    if name == "norm":
                        for u, n in pace.slots(r):
                            dve.wait_ge(s_x[u], times(r, 16))
                            ln.statistics(nc, u, n, x[:, u])
                        for u, n in pace.slots(r):
                            ln.aggregate(nc, u, n)
                        for u, n in pace.slots(r):
                            ln.invert(nc, u, n)
                        for u, n in pace.slots(r):
                            ln.scale(nc, u, n, x[:, u], x[:, u]).then_inc(s_xn, 1)
                    elif name == "k":
                        for u, n in pace.slots(r):
                            dve.wait_ge(s_k, n)
                            nc.vector.tensor_tensor(k[:, u], node_rows(name, u), both(bk[:, :]), ALU.add).then_inc(s_kb, 1)
                        for u, n in pace.slots(r):
                            dve.wait_ge(s_kb, n + UNROLL)
                            nc.vector.tensor_scalar(neg[:, u], k[:, u], 0.0, None, ALU.min).then_inc(s_neg, 1)
                    elif name == "v":
                        for u, n in pace.slots(r):
                            dve.wait_ge(s_v, n)
                            nc.vector.tensor_tensor(v[:, u], node_rows(name, u), both(bv[:, :]), ALU.add).then_inc(s_vb, 1)
                        for u, n in pace.slots(r):
                            dve.wait_ge(s_exp, n)
                            nc.vector.scalar_tensor_tensor(k[:, u], k[:, u], 0.0, neg[:, u], ALU.max, ALU.add).then_inc(s_phi, 1)
                    elif name == "kv":
                        for u, n in pace.slots(r):
                            dve.wait_ge(s_kv, n)
                            dve.wait_ge(s_added, n + UNROLL - 1)
                            nc.vector.tensor_tensor(kv_sum[:, :, :], kv_sum[:, :, :],
                                                    ring.bank(name, u)[:, 0:HALVES * (P + 1)].rearrange("p (a d) -> p a d", a=HALVES),
                                                    ALU.add).then_inc(s_added, 1)

                if messages:
                    messages.start_dve(dve)
                run(dve, part, pace)

            if messages:
                @block.gpsimd
                def _(pool):
                    messages.pool(pool)

            @block.scalar
            def _(act):
                if turned:
                    for j in range(4):
                        act.wait_ge(s_turn, j + 1)
                        w, a = (wk, wv)[j // 2], j % 2
                        nc.scalar.copy(w[:, :, a * P:(a + 1) * P], bank[j][:, 0:2 * P].rearrange("p (k n) -> p k n", k=HALVES)).then_inc(s_turned, 1)

                def part(name, r):
                    for u, n in slots(r):
                        if name == "norm":
                            ln.root(nc, u, n)
                        elif name == "turn":
                            act.wait_ge(s_xt, n + UNROLL)
                            nc.scalar.copy(xt[:, u].rearrange("p a n -> p (a n)"), ring.bank(name, u)[:, :]).then_inc(s_xtc, 1)
                        elif name == "k":
                            act.wait_ge(s_neg, n)
                            nc.scalar.activation(neg[:, u], neg[:, u], ACT.Exp).then_inc(s_exp, 1)
                        elif name == "v":
                            act.wait_ge(s_vb, n + UNROLL)
                            for i in range(PAIR):
                                mask = keep["mask"][:, bass.ds(r[0] * (UNROLL * PAIR) + ((r[1] * UNROLL + u) * PAIR + i), 1)]
                                nc.scalar.activation(va[:, u, i, :, 0:P], v[:, u, i, :].rearrange("p (a d) -> p a d", a=HALVES), ACT.Copy,
                                                     scale=mask)
                                last = nc.scalar.copy(va[:, u, i, :, P:P + 1], mask.unsqueeze(1).to_broadcast([P, HALVES, 1]))
                            last.then_inc(s_va, 1)

                run(act, part)

            @block.tensor
            def _(pe):
                pe.sem_inc(s_xt, UNROLL)
                pe.wait_ge(s_w, 16 * n_w)
                if turned:
                    for j in range(4):
                        for h in range(HALVES):
                            last = nc.tensor.transpose(bank[j][:, h * P:(h + 1) * P], raw[:, j, h * P:(h + 1) * P], keep["ident"][:, :])
                        last.then_inc(s_turn, 1)
                    pe.wait_ge(s_turned, 4)

                pace = Pace(messages and (lambda at, p: messages.pair_pe(pe, at, p)), {})
                pace.begin(None, [])

                def part(name, r):
                    for u, n in pace.slots(r):
                        if name in ring.names:
                            unit(name, r, u, n)

                def unit(name, r, u, n):
                    b = ring.enter(pe, name, u, n)
                    if name == "turn":
                        pe.wait_ge(s_xn, n + UNROLL)
                        transpose_pair(nc, b, x[:, u], keep["ident"]).then_inc(s_xt, 1)
                    elif name == "k":
                        pe.wait_ge(s_xtc, n + UNROLL)
                        project_pair(nc, b, xt[:, u], wk).then_inc(s_k, 1)
                    elif name == "v":
                        project_pair(nc, b, xt[:, u], wv).then_inc(s_v, 1)
                    else:
                        pe.wait_ge(s_phi, n)
                        pe.wait_ge(s_va, n)
                        for a in range(HALVES):
                            for i in range(PAIR):
                                last = nc.tensor.matmul(b[:, a * (P + 1):(a + 1) * (P + 1)], k[:, u, i, a * P:(a + 1) * P],
                                                        va[:, u, i, a, :], start=(i == 0), stop=(i == PAIR - 1))
                        last.then_inc(s_kv, 1)

                if messages:
                    messages.start_pe(pe)
                run(pe, part, pace)


def linear_attention(nc, io, dram, keep, cfg, kv_sum, added=None):
    ff = cfg["ff"]
    NF = ff // P
    turned = cfg["Wqkv"] is not None
    has_out = cfg["Wo"] is not None
    ACT_FF = ACT.Gelu if turned else ACT.Relu
    FF_ROUNDS = NF // 2
    RING = 3
    STAGES = ["turn", "q", "den", "num"] + (["att_turn", "out"] if has_out else [])
    FIRST = ["norm"] + STAGES + ["norm1", "bias"]
    LAST = ["y1_turn"] + [f"ff{f}" for f in range(FF_ROUNDS)] + ["ff_out", "tail"]
    if has_out:
        assert FF_ROUNDS == 4
        BODY = [("y1_turn", 0), ("ff0", 0), ("norm", 1), ("ff1", 0), ("turn", 1), ("q", 1), ("ff2", 0), ("den", 1), ("num", 1),
                ("att_turn", 1), ("ff3", 0), ("out", 1), ("norm1", 1), ("ff_out", 0), ("tail", 0), ("bias", 1)]
    else:
        assert FF_ROUNDS == 1
        BODY = [("y1_turn", 0), ("norm", 1), ("ff0", 0), ("turn", 1), ("q", 1), ("den", 1), ("ff_out", 0), ("num", 1), ("norm1", 1),
                ("tail", 0), ("bias", 1)]
    with ExitStack() as stack:
        space = Space(nc, stack, cfg["tag"] + "b")
        sb, sem = space.sb, space.sem
        wq, w1, w2 = sb("wq", [P, HALVES, D]), sb("w1", [P, HALVES, ff]), sb("w2", [P, NF, D])
        if has_out:
            wo = sb("wo", [P, HALVES, D])
        if turned:
            raw = sb("raw", [P, 6, D])
        bq, b1 = sb("bq", [P, HALVES]), sb("b1", [P, NF])
        rows = {n: sb(n, [P, D]) for n in ("bo", "b2", "ln1_g", "ln1_b", "ln2_g", "ln2_b")}
        kv = sb("kv", [P, HALVES, P])
        ks = sb("ks", [P, HALVES, 4])
        x = sb("x", [P, UNROLL, PAIR, D])
        xn = sb("xn", [P, UNROLL, PAIR, D])
        xt = sb("xt", [P, UNROLL, HALVES, PAIR * P])
        neg = sb("neg", [P, UNROLL, HALVES, PAIR * P])
        y = sb("y", [P, UNROLL, PAIR, D])
        z = sb("z", [P, UNROLL, PAIR * 8])
        y1 = sb("y1", [P, UNROLL, PAIR, D])
        y1t = sb("y1t", [P, UNROLL, HALVES, PAIR * P])
        y2 = sb("y2", [P, UNROLL, PAIR, D])
        fft = sb("fft", [P, UNROLL, NF, PAIR * P])
        xo = sb("xo", [P, UNROLL, PAIR, D])
        bank = [space.ps(f"bank{u}", [P, 512]) for u in range(UNROLL)]
        ring = [space.ps(f"ring{i}", [P, 512]) for i in range(RING)]
        ln0, ln1, ln2 = (Normalise(space, f"ln{i}", keep["eps"]) for i in range(3))
        s_x, s_xo, s_sent = space.sems("s_x", UNROLL), space.sems("s_xo", UNROLL), space.sems("s_sent", UNROLL)
        names = ("s_w", "s_xn", "s_xb", "s_xt", "s_xtc", "s_q", "s_neg", "s_pos", "s_exp", "s_phi", "s_den", "s_z0", "s_z", "s_num",
                 "s_att", "s_att_t", "s_att_c", "s_o", "s_y", "s_yn", "s_y1g", "s_y1", "s_y1t", "s_y1c", "s_y1b", "s_ff", "s_ffc",
                 "s_o2", "s_y2", "s_y2n", "s_y2g", "s_y2a", "s_stored", "s_kv", "s_turn", "s_turned", "s_done", "s_sum")
        (s_w, s_xn, s_xb, s_xt, s_xtc, s_q, s_neg, s_pos, s_exp, s_phi, s_den, s_z0, s_z, s_num, s_att, s_att_t, s_att_c, s_o, s_y, s_yn,
         s_y1g, s_y1, s_y1t, s_y1c, s_y1b, s_ff, s_ffc, s_o2, s_y2, s_y2n, s_y2g, s_y2a, s_stored, s_kv, s_turn, s_turned, s_done, s_sum) = (
            sem(n) for n in names)
        tiles, out_tiles = pair_rows(cfg["x"]), pair_rows(cfg["out"])
        loads = []
        if turned:
            loads += [(raw[:, 0:2], cfg["Wqkv"][0:D, :].rearrange("(b p) i -> p b i", p=P)),
                      (raw[:, 2:4], cfg["W1"].rearrange("(b p) i -> p b i", p=P)),
                      (raw[:, 4:6], cfg["W2"].rearrange("(b p) i -> p b i", p=P))]
        else:
            loads += [(wq[:, :, :], cfg["Wq"].rearrange("(a p) n -> p a n", p=P)),
                      (w1[:, :, :], cfg["W1"].rearrange("(a p) n -> p a n", p=P)),
                      (w2[:, :, :], cfg["W2"].rearrange("(a p) n -> p a n", p=P)),
                      (wo[:, :, :], cfg["Wo"].rearrange("(a p) n -> p a n", p=P)),
                      (bq[:, :], cfg["bq"].rearrange("(a p) -> p a", p=P)),
                      (rows["bo"][:, :], rows_of(cfg["bo"]))]
        loads += [(b1[:, :], cfg["b1"].rearrange("(a p) -> p a", p=P))]
        loads += [(rows[n][:, :], rows_of(cfg[n])) for n in ("b2", "ln1_g", "ln1_b", "ln2_g", "ln2_b")]

        ring = Ring(ring, {n: {"turn": s_xtc, "q": s_pos, "den": s_z0, "num": s_att, "att_turn": s_att_c, "out": s_y}[n] for n in STAGES})
        turn_of = ring.place

        def node_rows(b):
            return b[:, :].rearrange("p (i d) -> p i d", i=PAIR)

        def by_head(ap):
            return ap.rearrange("p i (h d) -> p (i h) d", d=MIX_DIM)

        with nc.Block() as block:

            @block.sync
            def _(sp):
                with nc.allow_non_contiguous_dma(reason="biases by partition"):
                    for to, frm in loads:
                        sp.dma_start(to, frm).then_inc(s_w, 16)

                def part(name, r):
                    for u, n in slots(r):
                        if name == "x":
                            sp.wait_ge(s_xn, n)
                            sp.dma_start(x[:, u, :, :], tiles[:, pair_at(r, u), :]).then_inc(s_x[u], 16)
                        elif name == "x_again":
                            sp.wait_ge(s_stored, n)
                            sp.dma_start(xo[:, u, :, :], tiles[:, pair_at(r, u), :]).then_inc(s_xo[u], 16)
                        elif name == "store":
                            sp.wait_ge(s_done, n + UNROLL)
                            sp.dma_start(out_tiles[:, pair_at(r, u), :], xo[:, u, :, :]).then_inc(s_sent[u], 16)
                        elif name == "stored":
                            sp.wait_ge(s_sent[u], times(r, 16))
                            sp.sem_inc(s_stored, 1)

                sp.sem_inc(s_stored, UNROLL)
                for name, q in (("x", 0), ("x_again", 0), ("x", 1)):
                    part(name, (0, q))
                with sp.Fori(0, ROUNDS - 2) as r:
                    for name, q in (("x", 2), ("store", 0), ("stored", 0), ("x_again", 1)):
                        part(name, (r, q))
                for name, q in (("store", 2), ("stored", 2), ("x_again", 1), ("store", 1), ("stored", 1)):
                    part(name, (ROUNDS - q, 0))

            @block.vector
            def _(dve):
                dve.sem_inc(s_xn, UNROLL)
                dve.sem_inc(s_pos, UNROLL)
                dve.sem_inc(s_z0, UNROLL)
                dve.sem_inc(s_att, UNROLL)
                dve.sem_inc(s_y, UNROLL)
                dve.sem_inc(s_y2, UNROLL)
                dve.sem_inc(s_done, UNROLL)
                if turned:
                    nc.vector.memset(bq[:, :], 0.0)
                dve.wait_ge(s_w, 16 * len(loads))
                for a in range(HALVES):
                    nc.vector.tensor_tensor(kv[:, a, :], kv_sum[:, a, 0:P], keep["same_head"][:, :], ALU.mult)
                    last = nc.vector.tensor_scalar(ks[:, a, :], keep["head_of"][:, :], kv_sum[:, a, P:P + 1], None, ALU.mult)
                last.then_inc(s_kv, 1)

                def part(name, r):
                    if name == "norm":
                        for u, n in slots(r):
                            dve.wait_ge(s_x[u], times(r, 16))
                            ln0.statistics(nc, u, n, x[:, u])
                        for u, n in slots(r):
                            ln0.aggregate(nc, u, n)
                        for u, n in slots(r):
                            ln0.invert(nc, u, n)
                        for u, n in slots(r):
                            ln0.scale(nc, u, n, xn[:, u], x[:, u]).then_inc(s_xn, 1)
                    elif name == "q":
                        for u, n in slots(r):
                            b = turn_of(name, u)[0]
                            dve.wait_ge(s_q, n)
                            for a in range(HALVES):
                                last = nc.vector.tensor_scalar(neg[:, u, a], b[:, a * D:(a + 1) * D], bq[:, a:a + 1], 0.0, ALU.add, ALU.min)
                            last.then_inc(s_neg, 1)
                            for a in range(HALVES):
                                last = nc.vector.tensor_scalar(xt[:, u, a], b[:, a * D:(a + 1) * D], bq[:, a:a + 1], 0.0, ALU.add, ALU.max)
                            last.then_inc(s_pos, 1)
                        for u, n in slots(r):
                            dve.wait_ge(s_exp, n)
                            dve.wait_ge(s_pos, n + UNROLL)
                            nc.vector.tensor_tensor(xt[:, u], xt[:, u], neg[:, u], ALU.add).then_inc(s_phi, 1)
                    elif name == "den":
                        for u, n in slots(r):
                            dve.wait_ge(s_den, n)
                            nc.vector.tensor_scalar(z[:, u, :], turn_of(name, u)[0][:, 0:PAIR * 8], 1e-6, None, ALU.add).then_inc(s_z0, 1)
                        for u, n in slots(r):
                            dve.wait_ge(s_z0, n + UNROLL)
                            nc.vector.reciprocal(z[:, u, :], z[:, u, :]).then_inc(s_z, 1)
                    elif name == "num":
                        for u, n in slots(r):
                            dve.wait_ge(s_num, n)
                            dve.wait_ge(s_z, n)
                            nc.vector.tensor_tensor(by_head(y[:, u]), by_head(node_rows(turn_of(name, u)[0])),
                                                    z[:, u, :].unsqueeze(2).to_broadcast([P, PAIR * 8, MIX_DIM]), ALU.mult).then_inc(s_att, 1)
                    elif name == "out":
                        for u, n in slots(r):
                            dve.wait_ge(s_o, n)
                            dve.wait_ge(s_xb, n)
                            nc.vector.tensor_tensor(y[:, u], node_rows(turn_of(name, u)[0]), xn[:, u], ALU.add).then_inc(s_y, 1)
                    elif name == "norm1":
                        if not has_out:
                            for u, n in slots(r):
                                dve.wait_ge(s_att, n + UNROLL)
                                nc.vector.tensor_tensor(y[:, u], y[:, u], xn[:, u], ALU.add).then_inc(s_y, 1)
                        for u, n in slots(r):
                            dve.wait_ge(s_y, n + UNROLL)
                            ln1.statistics(nc, u, n, y[:, u])
                        for u, n in slots(r):
                            ln1.aggregate(nc, u, n)
                        for u, n in slots(r):
                            dve.wait_ge(s_y1c, n)
                            dve.wait_ge(s_y1b, n)
                            ln1.centre(nc, u, n, y1[:, u], y[:, u], rows["ln1_g"])
                        for u, n in slots(r):
                            ln1.invert(nc, u, n)
                        for u, n in slots(r):
                            ln1.finish(nc, u, n, y1[:, u], rows["ln1_b"]).then_inc(s_y1, 1)
                    elif name == "ff_out":
                        for u, n in slots(r):
                            dve.wait_ge(s_o2, n)
                            dve.wait_ge(s_y1b, n + UNROLL)
                            nc.vector.tensor_tensor(y2[:, u], node_rows(bank[u]), y2[:, u], ALU.add).then_inc(s_y2, 1)
                    elif name == "tail":
                        for u, n in slots(r):
                            dve.wait_ge(s_y2, n + UNROLL)
                            ln2.statistics(nc, u, n, y2[:, u])
                        for u, n in slots(r):
                            ln2.aggregate(nc, u, n)
                        for u, n in slots(r):
                            ln2.centre(nc, u, n, y2[:, u], y2[:, u], rows["ln2_g"])
                        for u, n in slots(r):
                            ln2.invert(nc, u, n)
                        for u, n in slots(r):
                            ln2.finish(nc, u, n, y2[:, u], rows["ln2_b"]).then_inc(s_y2a, 1)
                        for u, n in slots(r):
                            dve.wait_ge(s_y2a, n)
                            if added is None:
                                dve.wait_ge(s_xo[u], times(r, 16))
                            else:
                                dve.wait_ge(s_sum, n)
                            nc.vector.tensor_tensor(xo[:, u], xo[:, u], y2[:, u], ALU.add).then_inc(s_done, 1)

                rounds(dve, part, FIRST, BODY, LAST)

            @block.gpsimd
            def _(pool):
                pool.sem_inc(s_y1b, UNROLL)
                pool.wait_ge(s_w, 16 * len(loads))

                def part(name, r):
                    for u, n in slots(r):
                        if name == "turn" and has_out:
                            pool.wait_ge(s_xt, n)
                            nc.gpsimd.tensor_tensor(xn[:, u], xn[:, u], both(rows["bo"][:, :]), ALU.add).then_inc(s_xb, 1)
                        elif name == "ff_out" and added is not None:
                            pool.wait_ge(s_xo[u], times(r, 16))
                            nc.gpsimd.tensor_tensor(xo[:, u], xo[:, u], added[:, pair_at(r, u), 0:D], ALU.add).then_inc(s_sum, 1)
                        elif name == "bias":
                            pool.wait_ge(s_y1, n)
                            pool.wait_ge(s_done, n)
                            nc.gpsimd.tensor_tensor(y2[:, u], y1[:, u], both(rows["b2"][:, :]), ALU.add).then_inc(s_y1b, 1)

                rounds(pool, part, FIRST, BODY, LAST)

            @block.scalar
            def _(act):
                act.sem_inc(s_xtc, UNROLL)
                act.sem_inc(s_att_c, UNROLL)
                act.sem_inc(s_y1c, UNROLL)
                if turned:
                    for j in range(6):
                        w, a = (wq, w1, w2)[j // 2], j % 2
                        act.wait_ge(s_turn, j + 1)
                        nc.scalar.copy(w[:, :, a * P:(a + 1) * P], bank[j % UNROLL][:, 0:2 * P].rearrange("p (k n) -> p k n", k=HALVES)).then_inc(s_turned, 1)

                def part(name, r):
                    for u, n in slots(r):
                        if name == "norm":
                            ln0.root(nc, u, n)
                        elif name == "turn":
                            act.wait_ge(s_xt, n)
                            nc.scalar.copy(xt[:, u].rearrange("p a n -> p (a n)"), turn_of(name, u)[0][:, :]).then_inc(s_xtc, 1)
                        elif name == "q":
                            act.wait_ge(s_neg, n)
                            nc.scalar.activation(neg[:, u], neg[:, u], ACT.Exp).then_inc(s_exp, 1)
                        elif name == "att_turn":
                            act.wait_ge(s_att_t, n)
                            nc.scalar.copy(xt[:, u].rearrange("p a n -> p (a n)"), turn_of(name, u)[0][:, :]).then_inc(s_att_c, 1)
                        elif name == "norm1":
                            ln1.root(nc, u, n)
                        elif name == "y1_turn":
                            act.wait_ge(s_y1t, n)
                            nc.scalar.copy(y1t[:, u].rearrange("p a n -> p (a n)"), bank[u][:, :]).then_inc(s_y1c, 1)
                        elif name.startswith("ff") and name != "ff_out":
                            f = int(name[2:])
                            act.wait_ge(s_ff, r[0] * (UNROLL * FF_ROUNDS) + (r[1] * UNROLL * FF_ROUNDS + f * UNROLL + u + 1))
                            for j in range(2):
                                c = 2 * f + j
                                last = nc.scalar.activation(fft[:, u, c], bank[u][:, j * D:(j + 1) * D], ACT_FF, bias=b1[:, c:c + 1])
                            last.then_inc(s_ffc, 1)
                        elif name == "tail":
                            ln2.root(nc, u, n)

                rounds(act, part, FIRST, BODY, LAST)

            @block.tensor
            def _(pe):
                pe.wait_ge(s_w, 16 * len(loads))
                if turned:
                    for j in range(6):
                        if j >= UNROLL:
                            pe.wait_ge(s_turned, j - UNROLL + 1)
                        for h in range(HALVES):
                            last = nc.tensor.transpose(bank[j % UNROLL][:, h * P:(h + 1) * P], raw[:, j, h * P:(h + 1) * P], keep["ident"][:, :])
                        last.then_inc(s_turn, 1)
                    pe.wait_ge(s_turned, 6)
                pe.wait_ge(s_kv, 1)

                def part(name, r):
                    for u, n in slots(r):
                        if name in STAGES:
                            b, left, behind = turn_of(name, u)
                            pe.wait_ge(left, n + (UNROLL - behind))
                        if name == "turn":
                            pe.wait_ge(s_xn, n + UNROLL)
                            transpose_pair(nc, b, xn[:, u], keep["ident"]).then_inc(s_xt, 1)
                        elif name == "q":
                            pe.wait_ge(s_xtc, n + UNROLL)
                            for a in range(HALVES):
                                for k in range(HALVES):
                                    last = nc.tensor.matmul(b[:, a * D:(a + 1) * D], wq[:, k, a * P:(a + 1) * P], xt[:, u, k, :],
                                                            start=(k == 0), stop=(k == HALVES - 1))
                            last.then_inc(s_q, 1)
                        elif name == "den":
                            pe.wait_ge(s_phi, n)
                            for i in range(PAIR):
                                for a in range(HALVES):
                                    c = 8 * i + 4 * a
                                    last = nc.tensor.matmul(b[:, c:c + 4], xt[:, u, a, i * P:(i + 1) * P], ks[:, a, :], start=True, stop=True)
                            last.then_inc(s_den, 1)
                        elif name == "num":
                            for i in range(PAIR):
                                for a in range(HALVES):
                                    c = i * D + a * P
                                    last = nc.tensor.matmul(b[:, c:c + P], xt[:, u, a, i * P:(i + 1) * P], kv[:, a, :], start=True, stop=True)
                            last.then_inc(s_num, 1)
                        elif name == "att_turn":
                            pe.wait_ge(s_att, n + UNROLL)
                            transpose_pair(nc, b, y[:, u], keep["ident"]).then_inc(s_att_t, 1)
                        elif name == "out":
                            pe.wait_ge(s_att_c, n + UNROLL)
                            project_pair(nc, b, xt[:, u], wo).then_inc(s_o, 1)
                        elif name == "y1_turn":
                            pe.wait_ge(s_y1, n)
                            pe.wait_ge(s_y2, n)
                            transpose_pair(nc, bank[u], y1[:, u], keep["ident"]).then_inc(s_y1t, 1)
                        elif name.startswith("ff") and name != "ff_out":
                            f = int(name[2:])
                            if f == 0:
                                pe.wait_ge(s_y1c, n + UNROLL)
                            else:
                                pe.wait_ge(s_ffc, r[0] * (UNROLL * FF_ROUNDS) + (r[1] * UNROLL * FF_ROUNDS + (f - 1) * UNROLL + u + 1))
                            for j in range(2):
                                c = 2 * f + j
                                for k in range(HALVES):
                                    last = nc.tensor.matmul(bank[u][:, j * D:(j + 1) * D], w1[:, k, c * P:(c + 1) * P], y1t[:, u, k, :],
                                                            start=(k == 0), stop=(k == HALVES - 1))
                            last.then_inc(s_ff, 1)
                        elif name == "ff_out":
                            pe.wait_ge(s_ffc, r[0] * (UNROLL * FF_ROUNDS) + (r[1] * UNROLL * FF_ROUNDS + (FF_ROUNDS - 1) * UNROLL + u + 1))
                            for i in range(PAIR):
                                for c in range(NF):
                                    last = nc.tensor.matmul(bank[u][:, i * D:(i + 1) * D], fft[:, u, c, i * P:(i + 1) * P], w2[:, c, :],
                                                            start=(c == 0), stop=(c == NF - 1))
                            last.then_inc(s_o2, 1)

                rounds(pe, part, FIRST, BODY, LAST)


LAYER1_PARTS = ([("norm", 2), ("turn", 1), ("q", 2), ("den", 1), ("num", 2), ("norm1", 0)],
                [("y1_turn", 0, 1), ("norm", 1, 2), ("ff0", 0, 1), ("turn", 1, 2), ("q", 1, 1), ("den", 1, 2), ("ff_out", 0, 1),
                 ("num", 1, 2), ("norm1", 1, 1), ("tail", 0, 2)],
                [("y1_turn", 2), ("ff0", 2), ("ff_out", 2), ("tail", 1)])
LAYER1_TURNS = {"norm": 4, "norm1": 5, "tail": 5}


def linear_attention_and_messages(nc, io, dram, keep, gathers, kv_sum, acc, first_group):
    cfg = mix_cfg(io, dram, 1)
    ff = cfg["ff"]
    NF = ff // P
    assert NF == 2
    first, body, last_parts = LAYER1_PARTS
    with ExitStack() as stack:
        space = Space(nc, stack, "mix1b")
        sb, sem = space.sb, space.sem
        wq, w1, w2 = sb("wq", [P, HALVES, D]), sb("w1", [P, HALVES, ff]), sb("w2", [P, NF, D])
        b1 = sb("b1", [P, NF])
        b2 = sb("b2", [1, D])
        ones = sb("ones", [1, P])
        rows = {n: sb(n, [P, D]) for n in ("ln1_g", "ln1_b", "ln2_g", "ln2_b")}
        kv = sb("kv", [P, HALVES, P])
        ks = sb("ks", [P, HALVES, 4])
        x = sb("x", [P, UNROLL, PAIR, D])
        xn = sb("xn", [P, UNROLL, PAIR, D])
        xt = sb("xt", [P, UNROLL, HALVES, PAIR * P])
        y = sb("y", [P, UNROLL, PAIR, D])
        neg = y
        z = sb("z", [P, UNROLL, PAIR * 8])
        y1 = sb("y1", [P, UNROLL, PAIR, D])
        y1t = sb("y1t", [P, UNROLL, HALVES, PAIR * P])
        raw = y1t[:, :, :, :].rearrange("p u a n -> p (u a) n")[:, 0:6]
        y2 = sb("y2", [P, UNROLL, PAIR, D])
        fft = sb("fft", [P, UNROLL, NF, PAIR * P])
        ln0, ln1, ln2 = (Normalise(space, f"ln{i}", keep["eps"]) for i in range(3))
        s_x, s_sent = space.sems("s_x", UNROLL), sem("s_sent")
        names = ("s_w", "s_xn", "s_xt", "s_xtc", "s_q", "s_neg", "s_pos", "s_exp", "s_phi", "s_den", "s_z0", "s_z", "s_num", "s_att", "s_y",
                 "s_y1", "s_y1t", "s_y1c", "s_ff", "s_ffc", "s_o2", "s_y2", "s_y2a", "s_done", "s_kv", "s_turn", "s_turned", "s_ones", "s_y1f")
        (s_w, s_xn, s_xt, s_xtc, s_q, s_neg, s_pos, s_exp, s_phi, s_den, s_z0, s_z, s_num, s_att, s_y,
         s_y1, s_y1t, s_y1c, s_ff, s_ffc, s_o2, s_y2, s_y2a, s_done, s_kv, s_turn, s_turned, s_ones, s_y1f) = (sem(n) for n in names)
        banks = [space.ps(f"bank{i}", [P, 512]) for i in range(6)]
        left = {"y1_turn": s_y1c, "ff0": s_ffc, "turn": s_xtc, "q": s_pos, "den": s_z0, "ff_out": s_y2, "num": s_att}
        assert list(left) == [n for n, _, _ in body if n in left]
        ring = Ring(banks, left, ahead=[n for n, ahead, _ in body if ahead and n in left])
        messages = Messages(nc, space, keep, gathers, dram["rel_feat"], acc, first_group, groups_in(*LAYER1_PARTS))
        tiles = pair_rows(cfg["x"])
        loads = [(raw[:, 0:2], cfg["Wqkv"][0:D, :].rearrange("(b p) i -> p b i", p=P)),
                 (raw[:, 2:4], cfg["W1"].rearrange("(b p) i -> p b i", p=P)),
                 (raw[:, 4:6], cfg["W2"].rearrange("(b p) i -> p b i", p=P)),
                 (b1[:, :], cfg["b1"].rearrange("(a p) -> p a", p=P)), (b2[:, :], cfg["b2"].unsqueeze(0))]
        loads += [(t[:, :], rows_of(cfg[n])) for n, t in rows.items()]

        def node_rows(name, u):
            return ring.bank(name, u)[:, :].rearrange("p (i d) -> p i d", i=PAIR)

        def by_head(ap):
            return ap.rearrange("p i (h d) -> p (i h) d", d=MIX_DIM)

        def plain(engine, part):
            rounds(engine, part, [n for n, _ in first], [(n, a) for n, a, _ in body], [n for n, _ in last_parts])

        def run(engine, part, pace):
            def paced(name, r, pairs):
                pace.begin(name, pairs)
                if name:
                    part(name, r)
                pace.end()

            rounds_between(engine, paced, *LAYER1_PARTS)

        with nc.Block() as block:

            @block.sync
            def _(sp):
                with nc.allow_non_contiguous_dma(reason="biases by partition"):
                    for to, frm in loads:
                        sp.dma_start(to, frm).then_inc(s_w, 16)
                with sp.Fori(0, ROUNDS) as r:
                    for u, n in slots((r, 0)):
                        sp.wait_ge(s_xn, n)
                        sp.dma_start(x[:, u, :, :], tiles[:, pair_at((r, 0), u), :]).then_inc(s_x[u], 16)
                sp.wait_ge(s_done, UNITS)
                messages.wait_all(sp)
                sp.dma_start(pair_rows(cfg["out"]), acc[:, :, :]).then_inc(s_sent, 16)
                sp.wait_ge(s_sent, 16)

            @block.gpsimd
            def _(pool):
                messages.pool(pool)

            @block.vector
            def _(dve):
                for s in (s_xn, s_z0, s_att, s_y2, s_y1f):
                    dve.sem_inc(s, UNROLL)
                nc.vector.memset(ones[:, :], 1.0).then_inc(s_ones, 1)
                for a in range(HALVES):
                    nc.vector.tensor_tensor(kv[:, a, :], kv_sum[:, a, 0:P], keep["same_head"][:, :], ALU.mult)
                    last = nc.vector.tensor_scalar(ks[:, a, :], keep["head_of"][:, :], kv_sum[:, a, P:P + 1], None, ALU.mult)
                last.then_inc(s_kv, 1)
                messages.start_dve(dve)
                dve.wait_ge(s_w, 16 * len(loads))

                pace = Pace(lambda at, p: messages.pair_dve(dve, at, p), LAYER1_TURNS)

                def part(name, r):
                    if name == "norm":
                        for u, n in pace.slots(r):
                            dve.wait_ge(s_x[u], times(r, 16))
                            ln0.statistics(nc, u, n, x[:, u])
                        for u, n in pace.slots(r):
                            ln0.aggregate(nc, u, n)
                        for u, n in pace.slots(r):
                            ln0.invert(nc, u, n)
                        for u, n in pace.slots(r):
                            ln0.scale(nc, u, n, xn[:, u], x[:, u]).then_inc(s_xn, 1)
                    elif name == "q":
                        for u, n in pace.slots(r):
                            dve.wait_ge(s_exp, n)
                            dve.wait_ge(s_pos, n + UNROLL)
                            nc.vector.tensor_tensor(xt[:, u], xt[:, u], neg[:, u], ALU.add).then_inc(s_phi, 1)
                    elif name == "den":
                        for u, n in pace.slots(r):
                            dve.wait_ge(s_den, n)
                            nc.vector.tensor_scalar(z[:, u, :], ring.bank(name, u)[:, 0:PAIR * 8], 1e-6, None, ALU.add).then_inc(s_z0, 1)
                        for u, n in pace.slots(r):
                            dve.wait_ge(s_z0, n + UNROLL)
                            nc.vector.reciprocal(z[:, u, :], z[:, u, :]).then_inc(s_z, 1)
                    elif name == "num":
                        for u, n in pace.slots(r):
                            dve.wait_ge(s_num, n)
                            dve.wait_ge(s_z, n)
                            nc.vector.tensor_tensor(by_head(y[:, u]), by_head(node_rows(name, u)),
                                                    z[:, u, :].unsqueeze(2).to_broadcast([P, PAIR * 8, MIX_DIM]), ALU.mult).then_inc(s_att, 1)
                        for u, n in pace.slots(r):
                            dve.wait_ge(s_att, n + UNROLL)
                            nc.vector.tensor_tensor(y[:, u], y[:, u], xn[:, u], ALU.add).then_inc(s_y, 1)
                    elif name == "norm1":
                        for u, n in pace.slots(r):
                            dve.wait_ge(s_y, n)
                            ln1.statistics(nc, u, n, y[:, u])
                        for u, n in pace.slots(r):
                            ln1.aggregate(nc, u, n)
                        for u, n in pace.slots(r):
                            dve.wait_ge(s_y1c, n)
                            ln1.centre(nc, u, n, y1[:, u], y[:, u], rows["ln1_g"])
                        for u, n in pace.slots(r):
                            ln1.invert(nc, u, n)
                        for u, n in pace.slots(r):
                            ln1.finish(nc, u, n, y1[:, u], rows["ln1_b"]).then_inc(s_y1, 1)
                            dve.sem_inc(s_y1f, 1)
                    elif name == "ff_out":
                        for u, n in pace.slots(r):
                            dve.wait_ge(s_o2, n)
                            nc.vector.tensor_tensor(y2[:, u], node_rows(name, u), y1[:, u], ALU.add).then_inc(s_y2, 1)
                    elif name == "tail":
                        for u, n in pace.slots(r):
                            dve.wait_ge(s_y2, n + UNROLL)
                            ln2.statistics(nc, u, n, y2[:, u])
                        for u, n in pace.slots(r):
                            ln2.aggregate(nc, u, n)
                        for u, n in pace.slots(r):
                            ln2.centre(nc, u, n, y2[:, u], y2[:, u], rows["ln2_g"])
                        for u, n in pace.slots(r):
                            ln2.invert(nc, u, n)
                        for u, n in pace.slots(r):
                            ln2.finish(nc, u, n, y2[:, u], rows["ln2_b"]).then_inc(s_y2a, 1)
                        pace.end()
                        if pace.pairs:
                            messages.settle(dve, *pace.pairs[-1])
                        for u, n in slots(r):
                            dve.wait_ge(s_y2a, n)
                            to = acc[:, pair_at(r, u), :]
                            nc.vector.tensor_tensor(to, to, y2[:, u], ALU.add).then_inc(s_done, 1)
                        dve.wait_ge(s_done, n)

                run(dve, part, pace)

            @block.scalar
            def _(act):
                for s in (s_xtc, s_pos, s_y1c, s_ffc):
                    act.sem_inc(s, UNROLL)
                for j in range(6):
                    w, a = (wq, w1, w2)[j // 2], j % 2
                    act.wait_ge(s_turn, j + 1)
                    nc.scalar.copy(w[:, :, a * P:(a + 1) * P], banks[j][:, 0:2 * P].rearrange("p (k n) -> p k n", k=HALVES)).then_inc(s_turned, 1)

                def part(name, r):
                    for u, n in slots(r):
                        if name == "norm":
                            ln0.root(nc, u, n)
                        elif name == "turn":
                            act.wait_ge(s_xt, n)
                            nc.scalar.copy(xt[:, u].rearrange("p a n -> p (a n)"), ring.bank(name, u)[:, :]).then_inc(s_xtc, 1)
                        elif name == "q":
                            act.wait_ge(s_q, n)
                            act.wait_ge(s_y1f, n)
                            flat = neg[:, u].rearrange("p i d -> p (i d)")
                            nc.scalar.activation(flat, ring.bank(name, u)[:, :], ACT.Relu, scale=-1.0).then_inc(s_neg, 1)
                            nc.scalar.activation(xt[:, u].rearrange("p a n -> p (a n)"), ring.bank(name, u)[:, :], ACT.Relu).then_inc(s_pos, 1)
                            act.wait_ge(s_neg, n)
                            nc.scalar.activation(neg[:, u], neg[:, u], ACT.Exp, scale=-1.0).then_inc(s_exp, 1)
                        elif name == "norm1":
                            ln1.root(nc, u, n)
                        elif name == "y1_turn":
                            act.wait_ge(s_y1t, n)
                            nc.scalar.copy(y1t[:, u].rearrange("p a n -> p (a n)"), ring.bank(name, u)[:, :]).then_inc(s_y1c, 1)
                        elif name == "ff0":
                            act.wait_ge(s_ff, n)
                            for c in range(NF):
                                last = nc.scalar.activation(fft[:, u, c], ring.bank(name, u)[:, c * D:(c + 1) * D], ACT.Gelu, bias=b1[:, c:c + 1])
                            last.then_inc(s_ffc, 1)
                        elif name == "tail":
                            ln2.root(nc, u, n)

                plain(act, part)

            @block.tensor
            def _(pe):
                pe.wait_ge(s_w, 16 * len(loads))
                for j in range(6):
                    for h in range(HALVES):
                        last = nc.tensor.transpose(banks[j][:, h * P:(h + 1) * P], raw[:, j, h * P:(h + 1) * P], keep["ident"][:, :])
                    last.then_inc(s_turn, 1)
                pe.wait_ge(s_turned, 6)
                pe.wait_ge(s_kv, 1)
                pe.wait_ge(s_ones, 1)
                messages.start_pe(pe)

                pace = Pace(lambda at, p: messages.pair_pe(pe, at, p), {})

                def part(name, r):
                    for u, n in pace.slots(r):
                        if name in ring.names:
                            unit(name, r, u, n)

                def unit(name, r, u, n):
                    if name == "ff_out" and isinstance(r[0], int):
                        pe.wait_ge(s_y1c, UNROLL + UNITS)
                        pe.wait_ge(s_ffc, UNROLL + UNITS)
                        b = ring.bank(name, u)
                    else:
                        b = ring.enter(pe, name, u, n)
                    if name == "turn":
                        pe.wait_ge(s_xn, n + UNROLL)
                        transpose_pair(nc, b, xn[:, u], keep["ident"]).then_inc(s_xt, 1)
                    elif name == "q":
                        pe.wait_ge(s_xtc, n + UNROLL)
                        for a in range(HALVES):
                            for k in range(HALVES):
                                last = nc.tensor.matmul(b[:, a * D:(a + 1) * D], wq[:, k, a * P:(a + 1) * P], xt[:, u, k, :],
                                                        start=(k == 0), stop=(k == HALVES - 1))
                        last.then_inc(s_q, 1)
                    elif name == "den":
                        pe.wait_ge(s_phi, n)
                        for i in range(PAIR):
                            for a in range(HALVES):
                                c = 8 * i + 4 * a
                                last = nc.tensor.matmul(b[:, c:c + 4], xt[:, u, a, i * P:(i + 1) * P], ks[:, a, :], start=True, stop=True)
                        last.then_inc(s_den, 1)
                    elif name == "num":
                        for i in range(PAIR):
                            for a in range(HALVES):
                                c = i * D + a * P
                                last = nc.tensor.matmul(b[:, c:c + P], xt[:, u, a, i * P:(i + 1) * P], kv[:, a, :], start=True, stop=True)
                        last.then_inc(s_num, 1)
                    elif name == "y1_turn":
                        pe.wait_ge(s_y1, n)
                        transpose_pair(nc, b, y1[:, u], keep["ident"]).then_inc(s_y1t, 1)
                    elif name == "ff0":
                        pe.wait_ge(s_y1c, n + UNROLL)
                        for c in range(NF):
                            for k in range(HALVES):
                                last = nc.tensor.matmul(b[:, c * D:(c + 1) * D], w1[:, k, c * P:(c + 1) * P], y1t[:, u, k, :],
                                                        start=(k == 0), stop=(k == HALVES - 1))
                        last.then_inc(s_ff, 1)
                    elif name == "ff_out":
                        pe.wait_ge(s_ffc, n + UNROLL)
                        for i in range(PAIR):
                            for c in range(NF):
                                nc.tensor.matmul(b[:, i * D:(i + 1) * D], fft[:, u, c, i * P:(i + 1) * P], w2[:, c, :], start=(c == 0), stop=False)
                            last = nc.tensor.matmul(b[:, i * D:(i + 1) * D], ones[:, :], b2[:, :], start=False, stop=True)
                        last.then_inc(s_o2, 1)

                run(pe, part, pace)


def relation_features(nc, io, dram, keep, acc):
    B, SUB = 8, 32
    FIRST, LAST = ["norm", "turn"], [f"unit{u}" for u in range(UNROLL)]
    BODY = [("unit0", 0), ("norm", 1)] + [(f"unit{u}", 0) for u in range(1, UNROLL)] + [("turn", 1)]
    BANKS = 4
    with ExitStack() as stack:
        space = Space(nc, stack, "rel")
        sb, sem = space.sb, space.sem
        w = sb("w", [P, HALVES, REL, P])
        x = sb("x", [P, UNROLL, PAIR, D])
        xt = sb("xt", [P, UNROLL, HALVES, PAIR * P])
        out = sb("out", [P, UNROLL, PAIR, REL, D])
        bank = [space.ps(f"bank{u}", [P, 512]) for u in range(BANKS)]
        ln = Normalise(space, "ln", keep["eps"])
        s_x, s_sent = space.sems("s_x", UNROLL), space.sems("s_sent", UNROLL)
        s_w, s_free, s_xn, s_xt, s_xtc, s_mm, s_out, s_zero, s_acc = (
            sem(n) for n in ("s_w", "s_free", "s_xn", "s_xt", "s_xtc", "s_mm", "s_out", "s_zero", "s_acc"))
        ring = Ring([space.ps(f"ring{i}", [P, 512]) for i in range(4)], {"turn": s_xtc})
        tiles = pair_rows(dram["x2"])
        to = dram["rel_feat"].rearrange("(r t p) d -> p t r d", r=REL, p=P)
        pieces = [(i, a, g) for i in range(PAIR) for a in range(HALVES) for g in range(2)]

        def piece_no(r, u, p):
            per = len(pieces)
            return r[0] * (per * UNROLL) + (per * (r[1] * UNROLL + u) + p + 1)

        with nc.Block() as block:

            @block.sync
            def _(sp):
                sp.wait_ge(s_zero, 1)
                weight = io["L1_gnn_weight"].rearrange("r (b i o) -> b i r o", b=B, i=SUB)
                for b in range(B):
                    lo = (b % 4) * SUB
                    sp.dma_start(w[lo:lo + SUB, b // 4, :, lo:lo + SUB], weight[b]).then_inc(s_w, 16)
                sp.sem_inc(s_free, UNROLL)

                def part(name, r):
                    for u, n in slots(r):
                        if name == "load":
                            sp.wait_ge(s_xt, n)
                            sp.dma_start(x[:, u, :, :], tiles[:, pair_at(r, u), :]).then_inc(s_x[u], 16)
                        elif name == "store":
                            sp.wait_ge(s_out, piece_no(r, u, len(pieces) - 1) + BANKS)
                            for i in range(PAIR):
                                t = bass.ds(r[0] * (UNROLL * PAIR) + ((r[1] * UNROLL + u) * PAIR + i), 1)
                                sp.dma_start(to[:, t, :, :].rearrange("p t r d -> p (t r) d"), out[:, u, i, :, :]).then_inc(s_sent[u], 16)
                        else:
                            sp.wait_ge(s_sent[u], times(r, 32))
                            sp.sem_inc(s_free, 1)

                sp.dma_start(acc[:, :, :], tiles).then_inc(s_acc, 16)
                loads_ahead(sp, part, ["load"], ["store", "done"])
                sp.wait_ge(s_acc, 16)

            @block.vector
            def _(dve):
                dve.sem_inc(s_xn, UNROLL)
                nc.vector.memset(w[:, :, :, :], 0.0).then_inc(s_zero, 1)

                def part(name, r):
                    if name == "norm":
                        for u, n in slots(r):
                            dve.wait_ge(s_x[u], times(r, 16))
                            ln.statistics(nc, u, n, x[:, u])
                        for u, n in slots(r):
                            ln.aggregate(nc, u, n)
                        for u, n in slots(r):
                            ln.invert(nc, u, n)
                        for u, n in slots(r):
                            ln.scale(nc, u, n, x[:, u], x[:, u]).then_inc(s_xn, 1)

                rounds(dve, part, FIRST, BODY, LAST)

            @block.scalar
            def _(act):
                act.sem_inc(s_out, BANKS)
                act.sem_inc(s_xtc, UNROLL)

                def part(name, r):
                    for u, n in slots(r):
                        if name == "norm":
                            ln.root(nc, u, n)
                        elif name == "turn":
                            act.wait_ge(s_xt, n + UNROLL)
                            nc.scalar.copy(xt[:, u].rearrange("p a n -> p (a n)"), ring.bank(name, u)[:, :]).then_inc(s_xtc, 1)
                        elif name == f"unit{u}":
                            act.wait_ge(s_free, n)
                            for p, (i, a, g) in enumerate(pieces):
                                act.wait_ge(s_mm, piece_no(r, u, p))
                                nc.scalar.copy(out[:, u, i, 4 * g:4 * g + 4, a * P:(a + 1) * P],
                                               bank[p % BANKS][:, :].rearrange("p (r o) -> p r o", r=4)).then_inc(s_out, 1)

                rounds(act, part, FIRST, BODY, LAST)

            @block.tensor
            def _(pe):
                pe.sem_inc(s_xt, UNROLL)
                pe.wait_ge(s_w, 16 * B)

                def part(name, r):
                    for u, n in slots(r):
                        if name == "turn":
                            pe.wait_ge(s_xn, n + UNROLL)
                            transpose_pair(nc, ring.enter(pe, name, u, n), x[:, u], keep["ident"]).then_inc(s_xt, 1)
                        elif name == f"unit{u}":
                            pe.wait_ge(s_xtc, n + UNROLL)
                            for p, (i, a, g) in enumerate(pieces):
                                pe.wait_ge(s_out, piece_no(r, u, p))
                                nc.tensor.matmul(bank[p % BANKS][:, :], xt[:, u, a, i * P:(i + 1) * P],
                                                 w[:, a, 4 * g:4 * g + 4, :].rearrange("p r o -> p (r o)"), start=True, stop=True).then_inc(s_mm, 1)

                rounds(pe, part, FIRST, BODY, LAST)


def mix_cfg(io, dram, layer):
    names = ["W1", "b1", "W2", "b2", "ln1_g", "ln1_b", "ln2_g", "ln2_b"]
    names += ["Wqkv"] if layer else ["Wq", "Wk", "Wv", "bq", "bk", "bv", "Wo", "bo"]
    cfg = {"Wqkv": None, "Wo": None} | {n: io[f"L{layer}_mix_{n}"] for n in names}
    x, out, ff = (("x0", "x1", L0_FF), ("x2", "x3", L1_FF))[layer]
    return cfg | {"tag": f"mix{layer}", "x": dram[x], "out": dram[out], "ff": ff}


def expert_mixture(nc, io, dram, keep):
    E = MOE_E
    EPS = 1e-3
    with ExitStack() as stack:
        space = Space(nc, stack, "moe")
        sb, sem = space.sb, space.sem
        w = [sb(f"w{j}", [P, E, HALVES, D]) for j in range(2)]
        w_high, w_low = ([sb(f"w_{n}{j}", [P, E, HALVES, D], F32R) for j in range(3)] for n in ("high", "low"))
        wr = sb("wr", [P, HALVES, E])
        br = sb("br", [P, E])
        bo = sb("bo", [E, D])
        par_rows = sb("par_rows", [E * HALVES, 2, 5, P])
        par = sb("par", [P, 2, 5, E * HALVES])
        gain, shift = sb("gain", [P, 2, E * HALVES]), sb("shift", [P, 2, E * HALVES])
        bn_eps = sb("bn_eps", [P, 1])
        x = sb("x", [P, 2, PAIR, D])
        h = sb("h", [P, 2, PAIR, D])
        xn = sb("xn", [P, 2, PAIR, D])
        xt = sb("xt", [P, HALVES, PAIR * P])
        xt_high, xt_low = (sb(f"xt_{n}", [P, HALVES, PAIR * P], F32R) for n in ("high", "low"))
        h1, h2 = sb("h1", [P, 2, HALVES, PAIR * P]), sb("h2", [P, 2, HALVES, PAIR * P])
        h1_high, h1_low, h2_high, h2_low = (sb(n, [P, 2, HALVES, PAIR * P], F32R) for n in ("h1_high", "h1_low", "h2_high", "h2_low"))
        logit = sb("logit", [P, PAIR, E])
        top = sb("top", [P, PAIR])
        gate = sb("gate", [P, 2, PAIR, E])
        gate_t = sb("gate_t", [E, PAIR, P])
        bank1 = [space.ps(f"first{i}", [P, 512]) for i in range(2)]
        bank2 = [space.ps(f"second{i}", [P, 512]) for i in range(2)]
        bank3 = [space.ps(f"third{i}", [P, 512]) for i in range(2)]
        bank_x, bank_g = space.ps("turn", [P, 512]), space.ps("route", [P, 512])
        stats, mv = sb("stats", [P, PAIR, 6]), sb("mv", [P, PAIR, 2])
        std = sb("std", [P, PAIR])
        s_x, s_sent = space.sems("s_x", 2), space.sems("s_sent", 2)
        s_wj = space.sems("s_wj", 3)
        s_and1, s_and2, s_cut1, s_cut2, s_andx, s_cutx, s_andw, s_cutw = (
            sem(n) for n in ("s_and1", "s_and2", "s_cut1", "s_cut2", "s_andx", "s_cutx", "s_andw", "s_cutw"))
        (s_w, s_free, s_dve, s_std_in, s_std, s_xn, s_xt, s_xtc, s_l1, s_h1, s_l2, s_h2, s_l3, s_acc, s_route, s_logit, s_exp, s_gate,
         s_turn, s_gate_t, s_bias, s_done, s_var, s_par, s_root, s_scale) = (
            sem(n) for n in ("s_w", "s_free", "s_dve", "s_std_in", "s_std", "s_xn", "s_xt", "s_xtc", "s_l1", "s_h1", "s_l2", "s_h2",
                             "s_l3", "s_acc", "s_route", "s_logit", "s_exp", "s_gate", "s_turn", "s_gate_t", "s_bias", "s_done",
                             "s_var", "s_par", "s_root", "s_scale"))
        tiles, out_tiles = pair_rows(dram["x1"]), pair_rows(dram["x2"])
        hidden = pair_rows(dram["hidden"])
        w_loads = [(w[j % 2][:, :, :, :], io[f"L0_ffn_{n}"].rearrange("e (a p) n -> p e a n", p=P)) for j, n in enumerate(("W1", "W2", "Wo"))]
        loads = [(wr[:, :, :], io["L0_ffn_Wr"].rearrange("(a p) e -> p a e", p=P)), (br[:, :], rows_of(io["L0_ffn_br"])),
                  (bo[:, :], io["L0_ffn_bo"])]
        loads += [(par_rows[:, j, i, :], io[f"L0_ffn_{n}{j + 1}"].rearrange("e (a p) -> (e a) p", p=P))
                  for j in range(2) for i, n in enumerate(("b", "g", "be", "m", "v"))]
        N_U = UNITS

        def load(sp, s, pair):
            sp.dma_start(x[:, s, :, :], tiles[:, pair, :]).then_inc(s_x[s], 16)
            sp.dma_start(h[:, s, :, :], hidden[:, pair, :]).then_inc(s_x[s], 16)

        def high_part(out, whole):
            return nc.vector.tensor_copy(out, whole)

        def low_part(out, whole, high):
            return nc.vector.tensor_tensor(out, whole, high.bitcast(F32), ALU.subtract)

        with nc.Block() as block:

            @block.sync
            def _(sp):
                with nc.allow_non_contiguous_dma(reason="small routing weights"):
                    for to, frm in loads:
                        sp.dma_start(to, frm).then_inc(s_w, 16)
                for s in range(2):
                    load(sp, s, slice(s * PAIR, (s + 1) * PAIR))
                for j, (to, frm) in enumerate(w_loads):
                    if j == 2:
                        sp.wait_ge(s_cutw, 1)
                    sp.dma_start(to, frm).then_inc(s_wj[j], 16)
                def store(n, s, rows, sent):
                    sp.wait_ge(s_done, n)
                    sp.dma_start(out_tiles[:, rows, :], x[:, s, :, :]).then_inc(s_sent[s], 16)
                    sp.wait_ge(s_sent[s], sent)

                with sp.Fori(0, N_U // 2 - 1) as r:
                    for s in range(2):
                        store(r * 2 + s + 1, s, bass.ds(r * (2 * PAIR) + s * PAIR, PAIR), r * 16 + 16)
                        load(sp, s, bass.ds(r * (2 * PAIR) + (s + 2) * PAIR, PAIR))
                for k in range(N_U - 3, N_U):
                    store(k + 1, k % 2, slice(k * PAIR, (k + 1) * PAIR), 16 * (k // 2 + 1))
                    if k + 2 < N_U:
                        load(sp, k % 2, slice((k + 2) * PAIR, (k + 3) * PAIR))

            @block.vector
            def _(dve):
                c = Count(dve, s_dve)
                for j in range(2):
                    dve.wait_ge(s_par, j + 1)
                    last = nc.vector.tensor_copy(par[:, j], bank1[j][:, 0:5 * 16].rearrange("p (i e) -> p i e", i=5))
                c.done(last)
                c.done(nc.vector.memset(bn_eps[:, :], EPS))
                dve.sem_inc(s_var, 1)
                dve.wait_ge(s_root, 1)
                c.done(nc.vector.reciprocal(gain[:, :, :], shift[:, :, :]))
                c.done(nc.vector.tensor_tensor(gain[:, :, :], gain[:, :, :], par[:, :, 1, :], ALU.mult))
                c.done(nc.vector.tensor_tensor(shift[:, :, :], par[:, :, 0, :], par[:, :, 3, :], ALU.subtract))
                c.done(nc.vector.tensor_tensor(shift[:, :, :], shift[:, :, :], gain[:, :, :], ALU.mult))
                nc.vector.tensor_tensor(shift[:, :, :], shift[:, :, :], par[:, :, 2, :], ALU.add).then_inc(s_scale, 1)
                dve.wait_ge(s_w, 16 * len(loads))

                def front_start(n, s, loaded):
                    dve.wait_ge(s_x[s], loaded)
                    c.done(nc.vector.tensor_tensor(x[:, s], x[:, s], h[:, s], ALU.add))
                    for i in range(PAIR):
                        last = nc.vector.bn_stats(stats[:, i, :], x[:, s, i, :])
                    c.done(last)
                    dve.sem_inc(s_std_in, 1)
                    for i in range(PAIR):
                        last = nc.vector.bn_aggr(mv[:, i, :], stats[:, i, :])
                    last.then_inc(s_std_in, 1)

                def front_end(n, s):
                    dve.wait_ge(s_std, n)
                    c.done(nc.vector.reciprocal(std[:, :], std[:, :]))
                    for i in range(PAIR):
                        last = nc.vector.tensor_scalar(xn[:, s, i, :], x[:, s, i, :], mv[:, i, 0:1], std[:, i:i + 1], ALU.subtract, ALU.mult)
                    last.then_inc(s_xn, 1)

                def cut_rows(n):
                    dve.wait_ge(s_xtc, n)
                    high_part(xt_high[:, :, :], xt[:, :, :]).then_inc(s_andx, 1)
                    dve.wait_ge(s_andx, n)
                    low_part(xt_low[:, :, :], xt[:, :, :], xt_high[:, :, :]).then_inc(s_cutx, 1)

                def cut_layer(j, m, e):
                    whole, high, low = ((h1, h1_high, h1_low), (h2, h2_high, h2_low))[j]
                    dve.wait_ge((s_h1, s_h2)[j], m)
                    high_part(high[:, e % 2], whole[:, e % 2]).then_inc((s_and1, s_and2)[j], 1)
                    dve.wait_ge((s_and1, s_and2)[j], m)
                    low_part(low[:, e % 2], whole[:, e % 2], high[:, e % 2]).then_inc((s_cut1, s_cut2)[j], 1)

                def gates(n, s):
                    dve.wait_ge(s_route, n)
                    c.done(nc.vector.tensor_tensor(logit[:, :, :], bank_g[:, 0:PAIR * E].rearrange("p (i e) -> p i e", i=PAIR), both(br[:, :]),
                                                   ALU.add))
                    c.done(nc.vector.tensor_reduce(top[:, :], logit[:, :, :], AX.X, ALU.max))
                    nc.vector.tensor_tensor(logit[:, :, :], logit[:, :, :], top[:, :].unsqueeze(2).to_broadcast([P, PAIR, E]),
                                            ALU.subtract).then_inc(s_logit, 1)
                    dve.wait_ge(s_exp, n)
                    c.done(nc.vector.tensor_reduce(top[:, :], gate[:, s], AX.X, ALU.add))
                    c.done(nc.vector.reciprocal(top[:, :], top[:, :]))
                    nc.vector.tensor_tensor(gate[:, s], gate[:, s], top[:, :].unsqueeze(2).to_broadcast([P, PAIR, E]), ALU.mult).then_inc(s_gate, 1)

                def turned_gates(n):
                    dve.wait_ge(s_turn, n)
                    nc.vector.tensor_copy(gate_t[:, :, :], bank_g[0:E, 0:PAIR * P].rearrange("e (i n) -> e i n", i=PAIR)).then_inc(s_gate_t, 1)

                def add_bias(n, s):
                    dve.wait_ge(s_bias, n)
                    c.done(nc.vector.tensor_tensor(x[:, s], x[:, s], bank_g[:, :].rearrange("p (i d) -> p i d", i=PAIR), ALU.add))

                def gather_expert(n_acc, s, e):
                    dve.wait_ge(s_l3, n_acc)
                    for i in range(PAIR):
                        last = nc.vector.scalar_tensor_tensor(x[:, s, i, :], bank3[e % 2][:, i * D:(i + 1) * D], gate[:, s, i, e:e + 1], x[:, s, i, :],
                                                              ALU.mult, ALU.add)
                    last.then_inc(s_acc, 1)
                    dve.wait_ge(s_acc, n_acc + 2)
                    if e == E - 1:
                        dve.sem_inc(s_done, 1)

                def unit(n, s, m, next_loaded):
                    gates(n, s)
                    for e in range(E + 2):
                        if e == E and next_loaded is not None:
                            cut_rows(n + 1)
                        if e < E:
                            cut_layer(0, m + (e + 1), e)
                        if e == 0:
                            turned_gates(n)
                        if e == 2:
                            add_bias(n, s)
                        if 1 <= e <= E:
                            cut_layer(1, m + e, e - 1)
                        if e >= 2:
                            gather_expert(m + (e - 1), s, e - 2)
                        if e == 4 and next_loaded is not None:
                            front_start(n + 1, 1 - s, next_loaded)
                        if e == 5 and next_loaded is not None:
                            front_end(n + 1, 1 - s)

                dve.sem_inc(s_acc, 2)
                front_start(1, 0, 32)
                front_end(1, 0)
                for j in range(3):
                    dve.wait_ge(s_wj[j], 16)
                    high_part(w_high[j][:, :, :, :], w[j % 2][:, :, :, :]).then_inc(s_andw, 1)
                    dve.wait_ge(s_andw, j + 1)
                    low_part(w_low[j][:, :, :, :], w[j % 2][:, :, :, :], w_high[j][:, :, :, :]).then_inc(s_cutw, 1)
                cut_rows(1)
                STEPS = 8
                with dve.Fori(0, N_U // 2) as r:
                    c.enter(r, 2 * STEPS)
                    for s in range(2):
                        unit(r * 2 + s + 1, s, r * (2 * E) + s * E, r * 32 + (32 if s == 0 else 64))
                c.leave(N_U // 2)
                unit(N_U, 0, (N_U - 1) * E, None)

            @block.scalar
            def _(act):
                act.wait_ge(s_var, 1)
                nc.scalar.activation(shift[:, :, :], par[:, :, 4, :], ACT.Sqrt, bias=bn_eps[:, 0:1]).then_inc(s_root, 1)
                act.wait_ge(s_scale, 1)

                def front_root(n):
                    act.wait_ge(s_std_in, n * 2)
                    nc.scalar.activation(std[:, :], mv[:, :, 1], ACT.Sqrt, bias=keep["eps"][:, 0:1]).then_inc(s_std, 1)

                def turned(n):
                    act.wait_ge(s_xt, n)
                    nc.scalar.copy(xt[:, :, :].rearrange("p a n -> p (a n)"), bank_x[:, :]).then_inc(s_xtc, 1)

                def layer(j, m, e):
                    act.wait_ge((s_l1, s_l2)[j], m)
                    for a in range(HALVES):
                        q = e * HALVES + a
                        last = nc.scalar.activation((h1, h2)[j][:, e % 2, a, :], (bank1, bank2)[j][e % 2][:, a * D:(a + 1) * D], ACT.Relu,
                                                    bias=shift[:, j, q:q + 1], scale=gain[:, j, q:q + 1])
                    last.then_inc((s_h1, s_h2)[j], 1)

                def unit(n, s, m, last):
                    act.wait_ge(s_logit, n)
                    nc.scalar.activation(gate[:, s], logit[:, :, :], ACT.Exp).then_inc(s_exp, 1)
                    for e in range(E + 1):
                        if e < E:
                            layer(0, m + (e + 1), e)
                        if e == E and not last:
                            turned(n + 1)
                        if e >= 1:
                            layer(1, m + e, e - 1)
                        if e == 4 and not last:
                            front_root(n + 1)

                front_root(1)
                turned(1)
                with act.Fori(0, N_U // 2) as r:
                    for s in range(2):
                        unit(r * 2 + s + 1, s, r * (2 * E) + s * E, False)
                unit(N_U, 0, (N_U - 1) * E, True)

            @block.tensor
            def _(pe):
                pe.wait_ge(s_w, 16 * len(loads))
                for j in range(2):
                    for i in range(5):
                        last = nc.tensor.transpose(bank1[j][:, 16 * i:16 * i + 16], par_rows[:, j, i, :], keep["ident"][0:16, 0:16])
                    last.then_inc(s_par, 1)
                pe.wait_ge(s_scale, 1)

                def turn(n, s):
                    pe.wait_ge(s_xn, n)
                    transpose_pair(nc, bank_x, xn[:, s], keep["ident"]).then_inc(s_xt, 1)

                def product(out, lhs, rhs):
                    passes = [(k, i, j) for k in range(HALVES) for i, j in ((0, 0), (0, 1), (1, 0))]
                    for p, (k, i, j) in enumerate(passes):
                        last = nc.tensor.matmul(out, lhs(k)[i], rhs(k)[j], start=(p == 0), stop=(p == len(passes) - 1))
                    return last

                def wide(bank, j, e, data):
                    for a in range(HALVES):
                        cols = slice(a * P, (a + 1) * P)
                        last = product(bank[:, a * D:(a + 1) * D], lambda k: [v[:, e, k, cols] for v in (w_high[j], w_low[j])],
                                       lambda k: [v[:, k, :] for v in data])
                    return last

                def unit(n, s, m, last_unit):
                    pe.wait_ge(s_xtc, n)
                    for i in range(PAIR):
                        for k in range(HALVES):
                            last = nc.tensor.matmul(bank_g[:, i * E:(i + 1) * E], xt[:, k, i * P:(i + 1) * P], wr[:, k, :],
                                                    start=(k == 0), stop=(k == HALVES - 1))
                    last.then_inc(s_route, 1)
                    for e in range(E + 2):
                        if e < E:
                            if e == 0:
                                pe.wait_ge(s_cutx, n)
                            wide(bank1[e % 2], 0, e, (xt_high, xt_low)).then_inc(s_l1, 1)
                        if e == 1:
                            pe.wait_ge(s_gate, n)
                            for i in range(PAIR):
                                last = nc.tensor.transpose(bank_g[0:E, i * P:(i + 1) * P], gate[:, s, i, :], keep["ident"][:, :])
                            last.then_inc(s_turn, 1)
                        if 1 <= e <= E:
                            pe.wait_ge(s_cut1, m + e)
                            wide(bank2[(e - 1) % 2], 1, e - 1, (h1_high[:, (e - 1) % 2], h1_low[:, (e - 1) % 2])).then_inc(s_l2, 1)
                        if e == 2:
                            pe.wait_ge(s_gate_t, n)
                            for i in range(PAIR):
                                last = nc.tensor.matmul(bank_g[:, i * D:(i + 1) * D], gate_t[:, i, :], bo[:, :], start=True, stop=True)
                            last.then_inc(s_bias, 1)
                        if e == E - 1 and not last_unit:
                            turn(n + 1, 1 - s)
                        if e >= 2:
                            pe.wait_ge(s_cut2, m + (e - 1))
                            pe.wait_ge(s_acc, m + (e - 1))
                            for i in range(PAIR):
                                cols = slice(i * P, (i + 1) * P)
                                last = product(bank3[e % 2][:, i * D:(i + 1) * D], lambda k: [v[:, e % 2, k, cols] for v in (h2_high, h2_low)],
                                               lambda k: [v[:, e - 2, k, :] for v in (w_high[2], w_low[2])])
                            last.then_inc(s_l3, 1)

                turn(1, 0)
                pe.wait_ge(s_cutw, 3)
                with pe.Fori(0, N_U // 2) as r:
                    for s in range(2):
                        unit(r * 2 + s + 1, s, r * (2 * E) + s * E, False)
                unit(N_U, 0, (N_U - 1) * E, True)


def slice_attention(nc, io, dram, keep, out):
    J = INNER // P
    with ExitStack() as stack:
        space = Space(nc, stack, "ffn")
        sb = space.sb
        slice_t = sb("slice_t", [P, N_TILES, INNER])
        sums = sb("sums", [P, HALVES, INNER])
        total = sb("total", [P, INNER])
        spread = sb("spread", [P, J, D])
        slice_weights(nc, io, dram, keep, slice_t, sums, total)
        slice_tokens(nc, io, keep, sums, total, spread)
        slice_output(nc, io, dram, slice_t, spread, out)


def slice_weights(nc, io, dram, keep, slice_t, sums, total):
    H, G = 8, 64
    J = INNER // P
    U = UNROLL
    FIRST, LAST = ["norm", "turn", "logit0", "copy"], ["logit1", "sum0", "sum1"]
    BODY = [("logit1", 0), ("norm", 1), ("sum0", 0), ("turn", 1), ("logit0", 1), ("sum1", 0), ("copy", 1)]
    with ExitStack() as stack:
        space = Space(nc, stack, "slw")
        sb, sem = space.sb, space.sem
        w_slice = sb("w_slice", [P, P])
        b_xt = sb("b_xt", [P, J])
        b_slice = sb("b_slice", [P, G])
        inv_temp = sb("inv_temp", [P, H])
        w_logit = sb("w_logit", [P, HALVES, INNER])
        b_logit = sb("b_logit", [P, INNER])
        x = sb("x", [P, U, PAIR, D])
        xt = sb("xt", [P, U, HALVES, PAIR * P])
        xn = sb("xn", [P, U, PAIR, D])
        xs = sb("xs", [P, U, PAIR, D])
        sw = sb("sw", [P, U, PAIR, INNER])
        w_x = sw[:, 0]
        w_xt = sw[:, 1].rearrange("p i n -> p (i n)").rearrange("p (j d) -> p j d", j=J)
        b_xt_wide = sw[:, 2, 0].rearrange("p (j q) -> p j q", j=J)
        top = sb("top", [P, U, PAIR, H])
        den = sb("den", [P, U, PAIR, H])
        nothing = sb("nothing", [P, P])
        sum_bank = [space.ps(f"sum_bank{a}", [P, 512]) for a in range(HALVES)]
        bank = [space.ps(f"bank{u}", [P, 512]) for u in range(6)]
        ln = Normalise(space, "ln", keep["eps"])
        s_x = space.sems("s_x", U)
        s_w, s_dve, s_zero, s_wt, s_wtc, s_wl, s_ready, s_xn, s_xt, s_xtc, s_copied, s_total, s_sums = (
            sem(n) for n in ("s_w", "s_dve", "s_zero", "s_wt", "s_wtc", "s_wl", "s_ready", "s_xn", "s_xt", "s_xtc", "s_copied", "s_total",
                             "s_sums"))
        s_lg, s_lb, s_mx, s_sub, s_exp, s_sm, s_rc, s_sw, s_swt, s_swtc, s_added = (
            space.sems(n, PAIR) for n in ("s_lg", "s_lb", "s_mx", "s_sub", "s_exp", "s_sm", "s_rc", "s_sw", "s_swt", "s_swtc", "s_added"))
        early = Ring(bank[0:3], {"turn": s_xtc, "logit0": s_lb[0]})
        late = Ring(bank[3:6], {"logit1": s_lb[1], "sum0": s_swtc[0], "sum1": s_swtc[1]})
        ring = {n: q for q in (early, late) for n in q.names}
        tiles = pair_rows(dram["x3"])
        loads = [(w_x[:, :, :], io["L1_ffn_W_x"].rearrange("(a p) n -> p a n", p=P)),
                 (w_slice[0:G, 0:G], io["L1_ffn_W_slice"]), (w_slice[G:P, G:P], io["L1_ffn_W_slice"]),
                 (b_xt[:, :], io["L1_ffn_b_x"].rearrange("(j p) -> p j", p=P)),
                 (b_slice[:, :], rows_of(io["L1_ffn_b_slice"])),
                 (inv_temp[:, :], rows_of(io["L1_ffn_temperature"].rearrange("a h b c -> (a h b c)")))]

        def tile_at(r, u, i):
            return bass.ds(r[0] * (U * PAIR) + ((r[1] * U + u) * PAIR + i), 1)

        def heads(ap):
            return ap.rearrange("p (h g) -> p h g", h=H)

        def by_head(ap):
            return ap.unsqueeze(2).to_broadcast([P, H, G])

        with nc.Block() as block:

            @block.sync
            def _(sp):
                sp.wait_ge(s_zero, 1)
                with nc.allow_non_contiguous_dma(reason="bias by partition"):
                    for to, frm in loads:
                        sp.dma_start(to, frm).then_inc(s_w, 16)
                with sp.Fori(0, ROUNDS) as r:
                    for u, n in units(r):
                        sp.wait_ge(s_xn, n)
                        sp.dma_start(x[:, u, :, :], tiles[:, pair_of(r, u), :]).then_inc(s_x[u], 16)

            @block.vector
            def _(dve):
                c = Count(dve, s_dve)
                nc.vector.memset(w_slice[:, :], 0.0)
                nc.vector.memset(nothing[:, :], 0.0)
                nc.vector.memset(total[:, :], 0.0).then_inc(s_zero, 1)
                dve.wait_ge(s_w, 16 * len(loads))
                for j in range(J):
                    last = nc.vector.tensor_copy(b_xt_wide[:, j, :], b_xt[:, j:j + 1].to_broadcast([P, P]))
                c.done(nc.vector.tensor_scalar(inv_temp[:, :], inv_temp[:, :], 0.1, 5.0, ALU.max, ALU.min))
                c.done(nc.vector.reciprocal(inv_temp[:, :], inv_temp[:, :]))
                for a in range(HALVES):
                    dve.wait_ge(s_wt, a + 1)
                    nc.vector.tensor_copy(w_xt[:, :, a * P:(a + 1) * P], bank[a][:, :].rearrange("p (j i) -> p j i", j=J)).then_inc(s_wtc, 1)
                dve.wait_ge(s_wl, 1)
                for a in range(HALVES):
                    nc.vector.tensor_tensor(heads(w_logit[:, a, :]), heads(bank[a][:, :]), by_head(inv_temp[:, :]), ALU.mult)
                c.done(nc.vector.tensor_tensor(heads(b_logit[:, :]), heads(bank[2][:, :]), b_slice[:, :].unsqueeze(1).to_broadcast([P, H, G]),
                                               ALU.add))
                nc.vector.tensor_tensor(heads(b_logit[:, :]), heads(b_logit[:, :]), by_head(inv_temp[:, :]), ALU.mult).then_inc(s_ready, 1)
                dve.wait_ge(s_ready, 1)
                dve.sem_inc(s_xn, U)
                for i in range(PAIR):
                    dve.sem_inc(s_lb[i], U)

                def part(name, r):
                    if name == "norm":
                        for u, n in slots(r):
                            dve.wait_ge(s_x[u], times(r, 16))
                            ln.statistics(nc, u, n, x[:, u])
                        for u, n in slots(r):
                            ln.aggregate(nc, u, n)
                        for u, n in slots(r):
                            ln.invert(nc, u, n)
                        for u, n in slots(r):
                            dve.wait_ge(s_copied, n)
                            ln.scale(nc, u, n, xn[:, u], x[:, u]).then_inc(s_xn, 1)
                    elif name in ("logit0", "logit1"):
                        i = int(name[-1])
                        for u, n in slots(r):
                            dve.wait_ge(s_lg[i], n)
                            dve.wait_ge(s_added[i], n)
                            nc.vector.tensor_tensor(sw[:, u, i], ring[name].bank(name, u)[:, :], b_logit[:, :], ALU.add).then_inc(s_lb[i], 1)
                        for u, n in slots(r):
                            dve.wait_ge(s_lb[i], n + U)
                            nc.vector.tensor_reduce(top[:, u, i], heads(sw[:, u, i]), AX.X, ALU.max).then_inc(s_mx[i], 1)
                        for u, n in slots(r):
                            dve.wait_ge(s_mx[i], n)
                            nc.vector.tensor_tensor(heads(sw[:, u, i]), heads(sw[:, u, i]), by_head(top[:, u, i]), ALU.subtract).then_inc(s_sub[i], 1)
                        for u, n in slots(r):
                            dve.wait_ge(s_exp[i], n)
                            nc.vector.tensor_reduce(den[:, u, i], heads(sw[:, u, i]), AX.X, ALU.add).then_inc(s_sm[i], 1)
                        for u, n in slots(r):
                            dve.wait_ge(s_sm[i], n)
                            nc.vector.reciprocal(den[:, u, i], den[:, u, i]).then_inc(s_rc[i], 1)
                        for u, n in slots(r):
                            dve.wait_ge(s_rc[i], n)
                            nc.vector.scalar_tensor_tensor(heads(sw[:, u, i]), heads(sw[:, u, i]), keep["mask"][:, tile_at(r, u, i)],
                                                           by_head(den[:, u, i]), ALU.mult, ALU.mult).then_inc(s_sw[i], 1)

                rounds(dve, part, FIRST, BODY, LAST)
                dve.wait_ge(s_sums, 1)
                for a in range(HALVES):
                    nc.vector.tensor_copy(sums[:, a, :], sum_bank[a][:, :])

            @block.gpsimd
            def _(pool):
                pool.sem_inc(s_total, 1)
                for i in range(PAIR):
                    pool.sem_inc(s_added[i], U)

                def part(name, r):
                    if name in ("sum0", "sum1"):
                        i = int(name[-1])
                        for u, n in slots(r):
                            pool.wait_ge(s_sw[i], n)
                            pool.wait_ge(s_total, r[0] * (PAIR * U) + (r[1] * PAIR * U + i * U + u + 1))
                            nc.gpsimd.tensor_tensor(total[:, :], total[:, :], sw[:, u, i], ALU.add).then_inc(s_total, 1)
                            pool.wait_ge(s_total, r[0] * (PAIR * U) + (r[1] * PAIR * U + i * U + u + 2))
                            pool.sem_inc(s_added[i], 1)

                rounds(pool, part, FIRST, BODY, LAST)

            @block.scalar
            def _(act):
                act.sem_inc(s_xtc, U)
                act.sem_inc(s_copied, U)
                for i in range(PAIR):
                    act.sem_inc(s_swtc[i], U)

                def part(name, r):
                    for u, n in slots(r):
                        if name == "norm":
                            ln.root(nc, u, n)
                        elif name == "turn":
                            act.wait_ge(s_xt, n)
                            nc.scalar.copy(xt[:, u].rearrange("p a n -> p (a n)"), early.bank(name, u)[:, :]).then_inc(s_xtc, 1)
                        elif name in ("logit0", "logit1"):
                            i = int(name[-1])
                            act.wait_ge(s_sub[i], n)
                            nc.scalar.activation(sw[:, u, i], sw[:, u, i], ACT.Exp).then_inc(s_exp[i], 1)
                        elif name in ("sum0", "sum1"):
                            i = int(name[-1])
                            act.wait_ge(s_swt[i], n + U)
                            nc.scalar.copy(slice_t[:, tile_at(r, u, i), :].rearrange("p t n -> p (t n)"), late.bank(name, u)[:, :]).then_inc(s_swtc[i], 1)
                        elif name == "copy":
                            act.wait_ge(s_xn, n + U)
                            act.wait_ge(s_swt[1], n)
                            nc.scalar.copy(xs[:, u], xn[:, u]).then_inc(s_copied, 1)

                rounds(act, part, FIRST, BODY, LAST)

            @block.tensor
            def _(pe):
                for i in range(PAIR):
                    pe.sem_inc(s_swt[i], U)
                pe.wait_ge(s_w, 16 * len(loads))
                for a in range(HALVES):
                    for j in range(J):
                        last = nc.tensor.transpose(bank[a][:, j * P:(j + 1) * P], w_x[:, a, j * P:(j + 1) * P], keep["ident"][:, :])
                    last.then_inc(s_wt, 1)
                pe.wait_ge(s_wtc, 2)
                for a in range(HALVES):
                    for j in range(J):
                        nc.tensor.matmul(bank[a][:, j * P:(j + 1) * P], w_xt[:, j, a * P:(a + 1) * P], w_slice[:, :], start=True, stop=True)
                for j in range(J):
                    last = nc.tensor.matmul(bank[2][:, j * P:(j + 1) * P], b_xt_wide[:, j, :], w_slice[:, :], start=True, stop=True)
                last.then_inc(s_wl, 1)
                pe.wait_ge(s_ready, 1)
                for a in range(HALVES):
                    nc.tensor.matmul(sum_bank[a][:, :], nothing[:, :], w_logit[:, 0, :], start=True, stop=False)

                def part(name, r):
                    for u, n in slots(r):
                        if name == "turn":
                            pe.wait_ge(s_xn, n + U)
                            transpose_pair(nc, early.enter(pe, name, u, n), xn[:, u], keep["ident"]).then_inc(s_xt, 1)
                        elif name in ("logit0", "logit1"):
                            i = int(name[-1])
                            b = ring[name].enter(pe, name, u, n)
                            pe.wait_ge(s_xtc, n + U)
                            for a in range(HALVES):
                                last = nc.tensor.matmul(b[:, :], xt[:, u, a, i * P:(i + 1) * P], w_logit[:, a, :],
                                                        start=(a == 0), stop=(a == HALVES - 1))
                            last.then_inc(s_lg[i], 1)
                        elif name in ("sum0", "sum1"):
                            i = int(name[-1])
                            pe.wait_ge(s_sw[i], n)
                            pe.wait_ge(s_copied, n + U)
                            for a in range(HALVES):
                                nc.tensor.matmul(sum_bank[a][:, :], xs[:, u, i, a * P:(a + 1) * P], sw[:, u, i], start=False, stop=False)
                            b = late.enter(pe, name, u, n)
                            for j in range(J):
                                last = nc.tensor.transpose(b[:, j * P:(j + 1) * P], sw[:, u, i, j * P:(j + 1) * P], keep["ident"][:, :])
                            last.then_inc(s_swt[i], 1)

                rounds(pe, part, FIRST, BODY, LAST)
                for a in range(HALVES):
                    last = nc.tensor.matmul(sum_bank[a][:, :], nothing[:, :], w_logit[:, 0, :], start=False, stop=True)
                last.then_inc(s_sums, 1)


def slice_tokens(nc, io, keep, sums, total, spread):
    G = DH = 64
    J = INNER // P
    with ExitStack() as stack:
        space = Space(nc, stack, "slt")
        sb, sem = space.sb, space.sem
        w_fx = sb("w_fx", [P, HALVES, INNER])
        w_out = sb("w_out", [P, J, D])
        b_fxt = sb("b_fxt", [P, J])
        w_head = [sb(f"w_{n}", [P, P]) for n in "qkv"]
        ones = sb("ones", [P, P])
        same = sb("same", [P, P])
        other = sb("other", [P, P])
        norm = sb("norm", [P, INNER])
        inv_norm = sb("inv_norm", [P, INNER])
        token_t = sb("token_t", [P, INNER])
        head_t = [sb(f"{n}_t", [P, INNER]) for n in "qkv"]
        attn, attn_t = sb("attn", [P, INNER]), sb("attn_t", [P, INNER])
        top = sb("top", [P, J])
        value_out = sb("value_out", [P, J, D])
        bank = [space.ps(f"bank{i}", [P, 512]) for i in range(8)]
        s_w, s_dve, s_zero, s_norm, s_token, s_heads, s_qkv, s_copied, s_score, s_vw, s_vwc, s_sub, s_exp, s_attn, s_turn, s_out = (
            sem(n) for n in ("s_w", "s_dve", "s_zero", "s_norm", "s_token", "s_heads", "s_qkv", "s_copied", "s_score", "s_vw", "s_vwc",
                             "s_sub", "s_exp", "s_attn", "s_turn", "s_out"))
        loads = [(w_fx[:, :, :], io["L1_ffn_W_fx"].rearrange("(a p) n -> p a n", p=P)),
                 (w_out[:, :, :], io["L1_ffn_W_out"].rearrange("(j p) n -> p j n", p=P)),
                 (b_fxt[:, :], io["L1_ffn_b_fx"].rearrange("(j p) -> p j", p=P))]
        loads += [(w_head[i][h * DH:(h + 1) * DH, h * DH:(h + 1) * DH], io[f"L1_ffn_W_{n}"]) for i, n in enumerate("qkv") for h in range(2)]

        def pairs(ap):
            return ap.rearrange("p (j g) -> p j g", j=J)

        with nc.Block() as block:

            @block.sync
            def _(sp):
                sp.wait_ge(s_zero, 1)
                with nc.allow_non_contiguous_dma(reason="bias by partition"):
                    for to, frm in loads:
                        sp.dma_start(to, frm).then_inc(s_w, 16)

            @block.vector
            def _(dve):
                c = Count(dve, s_dve)
                for w in w_head:
                    nc.vector.memset(w[:, :], 0.0)
                nc.vector.memset(ones[:, :], 1.0)
                c.done(nc.vector.memset(same[:, :], 0.0))
                for h in range(2):
                    last = nc.vector.memset(same[h * G:(h + 1) * G, h * G:(h + 1) * G], 1.0)
                c.done(last)
                nc.vector.tensor_scalar(other[:, :], same[:, :], -1.0, BIG, ALU.add, ALU.mult).then_inc(s_zero, 1)
                dve.wait_ge(s_norm, 1)
                nc.vector.tensor_copy(norm[:, :], bank[0][:, :])
                c.done(nc.vector.tensor_scalar(inv_norm[:, :], bank[0][:, :], 1e-5, None, ALU.add))
                c.done(nc.vector.reciprocal(inv_norm[:, :], inv_norm[:, :]))
                dve.wait_ge(s_w, 16 * len(loads))
                dve.wait_ge(s_token, 1)
                for j in range(J):
                    cols = slice(j * P, (j + 1) * P)
                    last = nc.vector.scalar_tensor_tensor(token_t[:, cols], norm[:, cols], b_fxt[:, j:j + 1], bank[1][:, cols], ALU.mult, ALU.add)
                c.done(last)
                c.done(nc.vector.tensor_tensor(token_t[:, :], token_t[:, :], inv_norm[:, :], ALU.mult))
                nc.vector.tensor_tensor(pairs(token_t[:, :]), pairs(token_t[:, :]), same[:, :].unsqueeze(1).to_broadcast([P, J, P]),
                                        ALU.mult).then_inc(s_heads, 1)
                dve.wait_ge(s_qkv, 1)
                for i in range(3):
                    last = nc.vector.tensor_copy(head_t[i][:, :], bank[2 + i][:, :])
                last.then_inc(s_copied, 1)
                dve.wait_ge(s_vw, 1)
                for j in range(J):
                    last = nc.vector.tensor_copy(value_out[:, j, :], bank[6 + j // 2][:, (j % 2) * D:(j % 2 + 1) * D])
                last.then_inc(s_vwc, 1)
                dve.wait_ge(s_score, 1)
                c.done(nc.vector.scalar_tensor_tensor(pairs(attn[:, :]), pairs(bank[5][:, :]), DH ** -0.5,
                                                      other[:, :].unsqueeze(1).to_broadcast([P, J, P]), ALU.mult, ALU.add))
                c.done(nc.vector.tensor_reduce(top[:, :], pairs(attn[:, :]), AX.X, ALU.max))
                nc.vector.tensor_tensor(pairs(attn[:, :]), pairs(attn[:, :]), top[:, :].unsqueeze(2).to_broadcast([P, J, P]),
                                        ALU.subtract).then_inc(s_sub, 1)
                dve.wait_ge(s_exp, 1)
                c.done(nc.vector.tensor_reduce(top[:, :], pairs(attn[:, :]), AX.X, ALU.add))
                c.done(nc.vector.reciprocal(top[:, :], top[:, :]))
                nc.vector.tensor_tensor(pairs(attn[:, :]), pairs(attn[:, :]), top[:, :].unsqueeze(2).to_broadcast([P, J, P]),
                                        ALU.mult).then_inc(s_attn, 1)
                dve.wait_ge(s_turn, 1)
                nc.vector.tensor_copy(attn_t[:, :], bank[0][:, :]).then_inc(s_turn, 1)
                dve.wait_ge(s_out, 1)
                for j in range(J):
                    nc.vector.tensor_copy(spread[:, j, :], bank[2 + j // 2][:, (j % 2) * D:(j % 2 + 1) * D])

            @block.scalar
            def _(act):
                act.wait_ge(s_sub, 1)
                nc.scalar.activation(attn[:, :], attn[:, :], ACT.Exp).then_inc(s_exp, 1)

            @block.tensor
            def _(pe):
                pe.wait_ge(s_zero, 1)
                nc.tensor.matmul(bank[0][:, :], ones[:, :], total[:, :], start=True, stop=True).then_inc(s_norm, 1)
                pe.wait_ge(s_w, 16 * len(loads))
                for j in range(J):
                    cols = slice(j * P, (j + 1) * P)
                    for a in range(HALVES):
                        last = nc.tensor.matmul(bank[1][:, cols], w_fx[:, a, cols], sums[:, a, cols], start=(a == 0), stop=(a == HALVES - 1))
                last.then_inc(s_token, 1)
                pe.wait_ge(s_heads, 1)
                for i in range(3):
                    last = nc.tensor.matmul(bank[2 + i][:, :], w_head[i][:, :], token_t[:, :], start=True, stop=True)
                last.then_inc(s_qkv, 1)
                pe.wait_ge(s_copied, 1)
                q_t, k_t, v_t = head_t
                for j in range(J):
                    cols = slice(j * P, (j + 1) * P)
                    last = nc.tensor.matmul(bank[6 + j // 2][:, (j % 2) * D:(j % 2 + 1) * D], v_t[:, cols], w_out[:, j, :], start=True, stop=True)
                last.then_inc(s_vw, 1)
                for j in range(J):
                    cols = slice(j * P, (j + 1) * P)
                    last = nc.tensor.matmul(bank[5][:, cols], q_t[:, cols], k_t[:, cols], start=True, stop=True)
                last.then_inc(s_score, 1)
                pe.wait_ge(s_attn, 1)
                for j in range(J):
                    cols = slice(j * P, (j + 1) * P)
                    last = nc.tensor.transpose(bank[0][:, cols], attn[:, cols], keep["ident"][:, :])
                last.then_inc(s_turn, 1)
                pe.wait_ge(s_turn, 2)
                pe.wait_ge(s_vwc, 1)
                for j in range(J):
                    cols = slice(j * P, (j + 1) * P)
                    last = nc.tensor.matmul(bank[2 + j // 2][:, (j % 2) * D:(j % 2 + 1) * D], attn_t[:, cols], value_out[:, j, :],
                                            start=True, stop=True)
                last.then_inc(s_out, 1)


def slice_output(nc, io, dram, slice_t, spread, out):
    J = INNER // P
    with ExitStack() as stack:
        space = Space(nc, stack, "slo")
        sb, sem = space.sb, space.sem
        b_out = sb("b_out", [P, D])
        x = sb("x", [P, UNROLL, PAIR, D])
        lhs = sb("lhs", [P, UNROLL, PAIR, INNER])
        bank = [space.ps(f"bank{u}", [P, 512]) for u in range(UNROLL)]
        s_x, s_sent = space.sems("s_x", UNROLL), space.sems("s_sent", UNROLL)
        s_w, s_free, s_lhs, s_bias, s_mm, s_done = (sem(n) for n in ("s_w", "s_free", "s_lhs", "s_bias", "s_mm", "s_done"))
        tiles = pair_rows(dram["x3"])
        whole = out[0:LAST_TILE * P, :].rearrange("(t p) d -> p t d", p=P)
        rest = N_NODES - LAST_TILE * P
        with nc.Block() as block:

            @block.sync
            def _(sp):
                sp.dma_start(b_out[:, :], rows_of(io["L1_ffn_b_out"])).then_inc(s_w, 16)

                def load(u, rows):
                    sp.dma_start(x[:, u, :, :], tiles[:, rows, :]).then_inc(s_x[u], 16)

                with sp.Fori(0, ROUNDS - 1) as r:
                    for u, n in units(r):
                        sp.wait_ge(s_free, n)
                        load(u, pair_of(r, u))
                    for u, n in units(r):
                        sp.wait_ge(s_done, n)
                        sp.dma_start(whole[:, pair_of(r, u), :], x[:, u, :, :]).then_inc(s_sent[u], 16)
                    for u, n in units(r):
                        sp.wait_ge(s_sent[u], r * 16 + 16)
                        sp.sem_inc(s_free, 1)
                r = ROUNDS - 1
                for u in range(UNROLL):
                    sp.wait_ge(s_free, r * UNROLL + u + 1)
                    load(u, slice((r * UNROLL + u) * PAIR, (r * UNROLL + u + 1) * PAIR))
                for u in range(UNROLL):
                    t = (r * UNROLL + u) * PAIR
                    sp.wait_ge(s_done, r * UNROLL + u + 1)
                    if t < LAST_TILE:
                        sp.dma_start(whole[:, t:t + PAIR, :], x[:, u, :, :]).then_inc(s_sent[u], 16)
                    else:
                        sp.dma_start(out[LAST_TILE * P:, :], x[0:rest, u, 0, :]).then_inc(s_sent[u], 16)
                for u in range(UNROLL):
                    sp.wait_ge(s_sent[u], 16 * ROUNDS)

            @block.gpsimd
            def _(pool):
                pool.sem_inc(s_free, UNROLL)
                pool.wait_ge(s_w, 16)
                with pool.Fori(0, ROUNDS) as r:
                    for u, n in units(r):
                        pool.wait_ge(s_x[u], r * 16 + 16)
                        nc.gpsimd.tensor_tensor(x[:, u], x[:, u], both(b_out[:, :]), ALU.add).then_inc(s_bias, 1)

            @block.scalar
            def _(act):
                with act.Fori(0, ROUNDS) as r:
                    for u, n in units(r):
                        act.wait_ge(s_mm, n)
                        nc.scalar.copy(lhs[:, u], slice_t[:, pair_of(r, u), :]).then_inc(s_lhs, 1)

            @block.tensor
            def _(pe):
                pe.sem_inc(s_mm, UNROLL)
                with pe.Fori(0, ROUNDS) as r:
                    for u, n in units(r):
                        pe.wait_ge(s_lhs, n)
                        pe.wait_ge(s_free, n)
                        for i in range(PAIR):
                            for j in range(J):
                                last = nc.tensor.matmul(bank[u][:, i * D:(i + 1) * D], lhs[:, u, i, j * P:(j + 1) * P], spread[:, j, :],
                                                        start=(j == 0), stop=(j == J - 1))
                        last.then_inc(s_mm, 1)

            @block.vector
            def _(dve):
                with dve.Fori(0, ROUNDS) as r:
                    for u, n in units(r):
                        dve.wait_ge(s_bias, n)
                        dve.wait_ge(s_mm, n + UNROLL)
                        nc.vector.tensor_tensor(x[:, u], x[:, u], bank[u][:, :].rearrange("p (i d) -> p i d", i=PAIR), ALU.add).then_inc(s_done, 1)


def scratch(nc):
    shapes = {"x0": ((N_PAD, D), F32), "x1": ((N_PAD, D), F32), "x2": ((N_PAD, D), F32), "x3": ((N_PAD, D), F32),
              "first": ((STEPS_PAD * P, GAT_HEADS), F32), "hidden": ((N_PAD, D), F32),
              "flags": ((STEPS_PAD * GAT_HEADS, 5, P), F32), "resets": ((2, STEPS_PAD), F32),
              "feat0": ((N_PAD, GAT_ROW), F32), "feat1": ((N_PAD, GAT_ROW), F32), "rel_feat": ((REL * N_PAD, D), F32)}
    shapes |= {f"{n}_rows": ((CHUNKS, P), I32) for n in ("src", "dst", "prev", "next", "kind")}
    shapes["weight_rows"] = ((CHUNKS, P), F32)
    dram = {n: nc.dram_tensor(f"scratch_{n}", s, dt).ap() for n, (s, dt) in shapes.items()}
    return dram | {"feat": [dram["feat0"], dram["feat1"]]}


def build(nc, io, out):
    dram = scratch(nc)
    with ExitStack() as stack:
        sb = Space(nc, stack, "keep").sb
        keep = {"ident": sb("ident", [P, P]), "iota_row": sb("iota_row", [P, P]),
                "src_tab": sb("src_tab", [P, STEPS_PAD], I32), "rel_tab": sb("rel_tab", [P, STEPS_PAD], I32),
                "wt_tab": sb("wt_tab", [P, STEPS_PAD]), "dst_tab": sb("dst_tab", [P, STEPS_PAD]),
                "eps": sb("eps", [P, 1]), "mask": sb("mask", [P, N_TILES]), "same_head": sb("same_head", [P, P]),
                "head_of": sb("head_of", [P, P // MIX_DIM]), "tile_row": sb("tile_row", [1, STEPS_PAD], I32),
                "first_pos": sb("first_pos", [P, N_TILES], I32), "cross": sb("cross", [P, WINDOWS]),
                "absent": sb("absent", [P, N_TILES])}
        gathers = Gathers(nc)
        build_tables(nc, io, dram, keep, gathers)
        mix(nc, io, dram, keep)
        with ExitStack() as inner:
            scores = Space(nc, inner, "gat").sb("scores", [P, N_TILES, 2 * GAT_HEADS])
            gnn_input(nc, io, dram, keep, gathers, scores)
            for layer in range(GAT_LAYERS):
                graph_attention(nc, io, dram, keep, gathers, layer, scores)
        expert_mixture(nc, io, dram, keep)
        relation_layer(nc, io, dram, keep, gathers)
        slice_attention(nc, io, dram, keep, out)


def mix(nc, io, dram, keep):
    cfg = mix_cfg(io, dram, 0)
    with ExitStack() as stack:
        kv_sum = Space(nc, stack, "mix0").sb("kv_sum", [P, HALVES, P + 1])
        linear_attention_sums(nc, io, dram, keep, cfg, kv_sum)
        linear_attention(nc, io, dram, keep, cfg, kv_sum)


def relation_layer(nc, io, dram, keep, gathers):
    with ExitStack() as stack:
        sb = Space(nc, stack, "layer1").sb
        acc = sb("acc", [P, N_TILES, D])
        kv_sum = sb("kv_sum", [P, HALVES, P + 1])
        relation_features(nc, io, dram, keep, acc)
        sums_groups = groups_in(*SUMS_PARTS)
        assert (sums_groups + groups_in(*LAYER1_PARTS)) * Messages.GROUP == STEPS_RUN
        linear_attention_sums(nc, io, dram, keep, mix_cfg(io, dram, 1), kv_sum,
                              lambda space, n: Messages(nc, space, keep, gathers, dram["rel_feat"], acc, 0, n))
        linear_attention_and_messages(nc, io, dram, keep, gathers, kv_sum, acc, sums_groups)


def graph_attention(nc, io, dram, keep, gathers, layer, scores):
    with ExitStack() as stack:
        acc = Space(nc, stack, f"gat{layer}").sb("acc", [P, N_TILES, GAT_SUM])
        gat_messages(nc, dram, keep, gathers, layer, acc)
        gat_finish(nc, io, dram, keep, gathers, layer, scores, acc, layer == GAT_LAYERS - 1)


def kernel(**inputs):
    import concourse.bacc as _bacc
    from concourse.bass_utils import run_bass_kernel_spmd as _run

    nc = _bacc.Bacc("TRN2", target_bir_lowering=False, num_devices=1)
    arrays, io = {}, {}
    for name in _INS:
        a = np.ascontiguousarray(inputs[name])
        arrays[f"in_{name}"] = a
        io[name] = nc.dram_tensor(f"in_{name}", a.shape, mybir.dt.from_np(a.dtype), kind="ExternalInput").ap()
    out = nc.dram_tensor("out", (N_NODES, D), F32, kind="ExternalOutput").ap()
    build(nc, io, out)
    r = _run(nc, [arrays], core_ids=[0])
    return r.results[0]["out"]
```
